# Optimizing a Trainium2 kernel written in Bass

```python
import numpy as np
import jax
import jax.numpy as jnp

def _softmax(x, axis=-1):
    return jax.nn.softmax(x, axis=axis)

def _gelu(x):
    return jax.nn.gelu(x, approximate=True)

def _silu(x):
    return jax.nn.silu(x)

def _sigmoid(x):
    return jax.nn.sigmoid(x)

def _layernorm(x, axis=-1, eps=1e-05):
    m = jnp.mean(x, axis=axis, keepdims=True)
    v = jnp.var(x, axis=axis, keepdims=True)
    return (x - m) / jnp.sqrt(v + eps)

def _scatter_add(tgt, idx, src, axis=0):
    return tgt.at[idx].add(src)

def _segment_sum(src, seg, n):
    return jax.ops.segment_sum(src, seg, n)
kernel_name = 'mk_perceiver_d2_seqx_r4_e2bc2f'

def setup_inputs(seed: int=0):
    np.random.seed(seed)
    _w = jnp.asarray

    def _rec_inputs():
        import jax
        import jax.numpy as jnp
        _rk = jax.random.key(seed)
        x = 7.22e-05 + 1 * jax.random.normal(jax.random.fold_in(_rk, 1), (1, 256, 512), jnp.float32)
        _lenS = 256 - jax.random.randint(jax.random.fold_in(_rk, 7), (1,), 0, max(1, 256 // 4) + 1, jnp.int32)
        _lenS2 = 4096 - jax.random.randint(jax.random.fold_in(_rk, 8), (1,), 0, max(1, 4096 // 4) + 1, jnp.int32)
        _ctx_512P = jax.random.normal(jax.random.fold_in(_rk, 11), (1, 16, 128), jnp.float32)
        _ctx_512c = jax.random.dirichlet(jax.random.fold_in(_rk, 511), 0.3 * jnp.ones((16,), jnp.float32), (1, 4096))
        _ctx_512t = jnp.einsum('bsk,bkd->bsd', _ctx_512c, _ctx_512P)
        _ctx_512t = _ctx_512t * jax.lax.rsqrt(jnp.mean(jnp.square(_ctx_512t)) + 1e-12) * 0.953939
        ctx_512 = -0.000514642 + 1.00011 * (_ctx_512t + 0.3 * jax.random.normal(jax.random.fold_in(_rk, 611), (1, 4096, 128), jnp.float32))
        return (x, ctx_512)
    x, ctx_512 = _rec_inputs()

    def _L0_xattn_setup():
        import jax, jax.numpy as jnp
        import numpy as np
        B, S, H, NH, L = (2, 512, 512, 16, 128)
        HD = H // NH
        key = jax.random.key(seed)
        k1, k2, k3, k4, k5 = jax.random.split(key, 5)
        scale = 0.02
        return {'q': jax.random.normal(k1, (B, S, H), dtype=jnp.float32), 'latent_kv': jax.random.normal(k2, (B, S, L), dtype=jnp.float32), 'Wq': jax.random.normal(k3, (H, H), dtype=jnp.float32) * scale, 'Wkv_expand': jax.random.normal(k4, (2 * H, L), dtype=jnp.float32) * scale, 'Wout': jax.random.normal(k5, (H, H), dtype=jnp.float32) * scale}
    _L0_xattn_all = _L0_xattn_setup()
    _L0_xattn_in = {k: v for k, v in _L0_xattn_all.items() if k in ('Wq', 'Wkv_expand', 'Wout')}
    del _L0_xattn_all

    def _L0_attn_setup():
        import jax, jax.numpy as jnp
        import numpy as np
        HIDDEN = 512
        HEAD_DIM = 128
        NUM_HEADS = 8
        NUM_HH = 2
        CONV = 4
        EPS = 1e-05
        KEY_DIM = NUM_HEADS * HEAD_DIM

        def _causal_conv_silu(x, w):
            y = jax.lax.conv_general_dilated(jnp.swapaxes(x, 1, 2), w, window_strides=(1,), padding=[(w.shape[-1] - 1, 0)], feature_group_count=w.shape[0], dimension_numbers=('NCH', 'OIH', 'NCH'))
            return jnp.swapaxes(jax.nn.silu(y), 1, 2)

        def _l2norm(x):
            n = jnp.sqrt(jnp.sum(x * x, axis=-1, keepdims=True))
            return x / jnp.maximum(n, 1e-12)

        def _reference_tuple_inner(x, Wq, Wk, Wv, Wb, Wa, A_log, dt_bias, conv_q_w, conv_k_w, conv_v_w, Wg, norm_w, Wo):
            B, L, _ = x.shape
            H, Dh, nh = (NUM_HEADS, HEAD_DIM, NUM_HH)
            q = _causal_conv_silu(x @ Wq, conv_q_w).reshape(B, L, H, Dh)
            k = _causal_conv_silu(x @ Wk, conv_k_w).reshape(B, L, nh, H, Dh)
            v = _causal_conv_silu(x @ Wv, conv_v_w).reshape(B, L, nh, H, Dh)
            q = _l2norm(q) / np.float32(np.sqrt(Dh))
            k = _l2norm(k)
            beta = 2.0 * jax.nn.sigmoid(x @ Wb).reshape(B, L, nh, H)
            g = -jnp.exp(A_log) * jax.nn.softplus(x @ Wa + dt_bias)

            def step(state, inp):
                q_t, k_t, v_t, b_t, g_t = inp
                state = state * jnp.exp(g_t)[..., None, None]
                for j in range(nh):
                    kj = k_t[:, j]
                    corr = jnp.einsum('bhk,bhkv->bhv', kj, state)
                    u = (v_t[:, j] - corr) * b_t[:, j][..., None]
                    state = state + jnp.einsum('bhk,bhv->bhkv', kj, u)
                o_t = jnp.einsum('bhk,bhkv->bhv', q_t, state)
                return (state, o_t)
            state0 = jnp.zeros((B, H, Dh, Dh), x.dtype)
            xs = (jnp.moveaxis(q, 1, 0), jnp.moveaxis(k, 1, 0), jnp.moveaxis(v, 1, 0), jnp.moveaxis(beta, 1, 0), jnp.moveaxis(g, 1, 0))
            state, o = jax.lax.scan(step, state0, xs)
            o = jnp.moveaxis(o, 0, 1)
            gate = (x @ Wg).reshape(B, L, H, Dh)
            o = o * jax.lax.rsqrt(jnp.mean(o * o, axis=-1, keepdims=True) + EPS)
            o = o * norm_w * jax.nn.silu(gate)
            out = o.reshape(B, L, H * Dh) @ Wo
            return (out, state)
        key = jax.random.key(seed)
        ks = jax.random.split(key, 14)
        B, L = (2, 128)
        s = 0.02
        x = jax.random.normal(ks[0], (B, L, HIDDEN), jnp.float32)
        Wq = jax.random.normal(ks[1], (HIDDEN, KEY_DIM), jnp.float32) * s
        Wk = jax.random.normal(ks[2], (HIDDEN, KEY_DIM * NUM_HH), jnp.float32) * s
        Wv = jax.random.normal(ks[3], (HIDDEN, KEY_DIM * NUM_HH), jnp.float32) * s
        Wb = jax.random.normal(ks[4], (HIDDEN, NUM_HEADS * NUM_HH), jnp.float32) * s
        Wa = jax.random.normal(ks[5], (HIDDEN, NUM_HEADS), jnp.float32) * s
        A_log = jnp.log(jax.random.uniform(ks[6], (NUM_HEADS,), jnp.float32, 0.001, 16.0))
        dt = jnp.exp(jax.random.uniform(ks[7], (NUM_HEADS,), jnp.float32) * (np.float32(np.log(0.1)) - np.float32(np.log(0.001))) + np.float32(np.log(0.001)))
        dt = jnp.maximum(dt, 0.0001)
        dt_bias = dt + jnp.log(-jnp.expm1(-dt))
        conv_q_w = jax.random.normal(ks[8], (KEY_DIM, 1, CONV), jnp.float32) * 0.1
        conv_k_w = jax.random.normal(ks[9], (KEY_DIM * NUM_HH, 1, CONV), jnp.float32) * 0.1
        conv_v_w = jax.random.normal(ks[10], (KEY_DIM * NUM_HH, 1, CONV), jnp.float32) * 0.1
        Wg = jax.random.normal(ks[11], (HIDDEN, KEY_DIM), jnp.float32) * s
        norm_w = jnp.ones((HEAD_DIM,), jnp.float32)
        Wo = jax.random.normal(ks[12], (KEY_DIM, HIDDEN), jnp.float32) * s
        return dict(x=x, Wq=Wq, Wk=Wk, Wv=Wv, Wb=Wb, Wa=Wa, A_log=A_log, dt_bias=dt_bias, conv_q_w=conv_q_w, conv_k_w=conv_k_w, conv_v_w=conv_v_w, Wg=Wg, norm_w=norm_w, Wo=Wo)
    _L0_attn_all = _L0_attn_setup()
    _L0_attn_in = {k: v for k, v in _L0_attn_all.items() if k in ('Wq', 'Wk', 'Wv', 'Wb', 'Wa', 'A_log', 'dt_bias', 'conv_q_w', 'conv_k_w', 'conv_v_w', 'Wg', 'norm_w', 'Wo')}
    del _L0_attn_all

    def _L0_ffn_setup():
        import jax, jax.numpy as jnp
        import numpy as np
        NUM_EXPERTS = 64
        TOP_K = 8
        HIDDEN = 512
        INTER = 256
        key = jax.random.key(seed)
        k1, k2, k3, k4 = jax.random.split(key, 4)
        scale = 1.0 / np.sqrt(HIDDEN)
        hidden_states = jax.random.normal(k1, (4, 512, HIDDEN), dtype=jnp.float32)
        gate_w = jax.random.normal(k2, (NUM_EXPERTS, HIDDEN), dtype=jnp.float32) * scale
        w13 = jax.random.normal(k3, (NUM_EXPERTS, 2 * INTER, HIDDEN), dtype=jnp.float32) * scale
        w2 = jax.random.normal(k4, (NUM_EXPERTS, HIDDEN, INTER), dtype=jnp.float32) * (1.0 / np.sqrt(INTER))
        return {'hidden_states': hidden_states, 'gate_w': gate_w, 'w13': w13, 'w2': w2}
    _L0_ffn_all = _L0_ffn_setup()
    _L0_ffn_in = {k: v for k, v in _L0_ffn_all.items() if k in ('gate_w', 'w13', 'w2')}
    del _L0_ffn_all

    def _L1_xattn_setup():
        import jax, jax.numpy as jnp
        import numpy as np
        B, S, L = (2, 256, 256)
        DIM_Q, H, K, D_C, D_CQ, R = (512, 16, 128, 128, 384, 64)

        def _rope_tables(length, dim):
            inv = 1.0 / 10000.0 ** (jnp.arange(0, dim, 2, dtype=jnp.float32) / dim)
            f = jnp.arange(length, dtype=jnp.float32)[:, None] * inv[None, :]
            sin = jnp.repeat(jnp.sin(f), 2, axis=-1)
            cos = jnp.repeat(jnp.cos(f), 2, axis=-1)
            return (sin, cos)

        def _rotate_half(x):
            half = x.shape[-1] // 2
            return jnp.concatenate([-x[..., half:], x[..., :half]], axis=-1)

        def _apply_rope(x, sin, cos):
            return x * cos + _rotate_half(x) * sin
        key = jax.random.key(seed)
        ks = jax.random.split(key, 8)
        return {'hidden_q': jax.random.normal(ks[0], (B, S, DIM_Q), jnp.float32), 'kv_c': jax.random.normal(ks[1], (B, L, D_C), jnp.float32), 'Wq': jax.random.normal(ks[2], (H * K, DIM_Q), jnp.float32) / np.sqrt(DIM_Q).astype(np.float32), 'w_kc_q': jax.random.normal(ks[3], (H, K, D_CQ), jnp.float32) / np.sqrt(K).astype(np.float32), 'w_kc_kv': jax.random.normal(ks[4], (H, K, D_C), jnp.float32) / np.sqrt(K).astype(np.float32), 'W_qr': jax.random.normal(ks[5], (H, D_CQ, R), jnp.float32) / np.float32(np.sqrt(D_CQ) * np.sqrt(R)), 'W_kr': jax.random.normal(ks[6], (H, D_C, R), jnp.float32) / np.sqrt(D_C).astype(np.float32), 'Wo': jax.random.normal(ks[7], (DIM_Q, H * K), jnp.float32) / np.sqrt(H * K).astype(np.float32)}
    _L1_xattn_all = _L1_xattn_setup()
    _L1_xattn_in = {k: v for k, v in _L1_xattn_all.items() if k in ('Wq', 'w_kc_q', 'w_kc_kv', 'W_qr', 'W_kr', 'Wo')}
    del _L1_xattn_all

    def _L1_attn_setup():
        import jax, jax.numpy as jnp
        import numpy as np
        B_, S_, E_ = (2, 512, 512)
        H_, P_, N_, G_, K_, CH_ = (64, 64, 128, 1, 4, 64)
        INTER = H_ * P_
        CONV_DIM = INTER + 2 * G_ * N_
        PROJ = INTER + CONV_DIM + H_
        EPS = 1e-05

        def segsum(x):
            T = x.shape[-1]
            xe = jnp.broadcast_to(x[..., None], x.shape + (T,))
            m_excl = jnp.tril(jnp.ones((T, T), bool), -1)
            s = jnp.cumsum(jnp.where(m_excl, xe, 0.0), axis=-2)
            m_incl = jnp.tril(jnp.ones((T, T), bool), 0)
            return jnp.where(m_incl, s, -jnp.inf)

        def ssm_forward(input_states, in_proj_w, conv_w, conv_b, A_log, dt_bias, D, norm_w, out_proj_w):
            b, s, _ = input_states.shape
            proj = input_states @ in_proj_w.T
            gate, hBC, dt = jnp.split(proj, [INTER, INTER + CONV_DIM], axis=-1)
            x = hBC.transpose(0, 2, 1)
            x = jax.lax.conv_general_dilated(x, conv_w, (1,), [(K_ - 1, 0)], dimension_numbers=('NCH', 'OIH', 'NCH'), feature_group_count=CONV_DIM)
            hBC = jax.nn.silu((x + conv_b[None, :, None]).transpose(0, 2, 1))
            hs, Bmat, Cmat = jnp.split(hBC, [INTER, INTER + G_ * N_], axis=-1)
            A = -jnp.exp(A_log)
            dt = jax.nn.softplus(dt + dt_bias)
            xh = hs.reshape(b, s, H_, P_)
            Bf = jnp.repeat(Bmat.reshape(b, s, G_, N_), H_ // G_, axis=2)
            Cf = jnp.repeat(Cmat.reshape(b, s, G_, N_), H_ // G_, axis=2)
            D_res = D[:, None] * xh
            xh = xh * dt[..., None]
            Adt = A[None, None, :] * dt
            nch = s // CH_
            xc = xh.reshape(b, nch, CH_, H_, P_)
            Bc = Bf.reshape(b, nch, CH_, H_, N_)
            Cc = Cf.reshape(b, nch, CH_, H_, N_)
            Ac = Adt.reshape(b, nch, CH_, H_).transpose(0, 3, 1, 2)
            A_cum = jnp.cumsum(Ac, axis=-1)
            L = jnp.exp(segsum(Ac))
            Gm = jnp.einsum('bclhn,bcshn->bclsh', Cc, Bc)
            M = Gm * L.transpose(0, 2, 3, 4, 1)
            Y_diag = jnp.einsum('bclsh,bcshp->bclhp', M, xc)
            decay_states = jnp.exp(A_cum[..., -1:] - A_cum)
            states = jnp.einsum('bclhn,bhcl,bclhp->bchpn', Bc, decay_states, xc)
            states = jnp.concatenate([jnp.zeros_like(states[:, :1]), states], axis=1)
            A_last = jnp.pad(A_cum[..., -1], ((0, 0), (0, 0), (1, 0)))
            decay_chunk = jnp.exp(segsum(A_last))
            new_states = jnp.einsum('bhij,bjhpn->bihpn', decay_chunk, states)
            states = new_states[:, :-1]
            state_decay = jnp.exp(A_cum)
            Y_off = jnp.einsum('bclhn,bchpn,bhcl->bclhp', Cc, states, state_decay)
            y = (Y_diag + Y_off).reshape(b, s, H_, P_) + D_res
            y = y.reshape(b, s, INTER)
            yg = y * jax.nn.silu(gate)
            var = jnp.mean(yg * yg, axis=-1, keepdims=True)
            yn = norm_w * (yg * jax.lax.rsqrt(var + EPS))
            return yn @ out_proj_w.T
        key = jax.random.key(seed)
        ks = jax.random.split(key, 4)
        return {'input_states': jax.random.normal(ks[0], (B_, S_, E_), jnp.float32), 'mask': jnp.ones((B_, 1, S_), jnp.int32), 'in_proj_w': jax.random.normal(ks[1], (PROJ, E_), jnp.float32) * 0.02, 'conv_w': jax.random.normal(ks[2], (CONV_DIM, 1, K_), jnp.float32) * 0.2, 'conv_b': jnp.zeros((CONV_DIM,), jnp.float32), 'A_log': jnp.log(jnp.arange(1, H_ + 1, dtype=jnp.float32)), 'dt_bias': jnp.ones((H_,), jnp.float32), 'D': jnp.ones((H_,), jnp.float32), 'norm_w': jnp.ones((INTER,), jnp.float32), 'out_proj_w': jax.random.normal(ks[3], (E_, INTER), jnp.float32) * 0.02}
    _L1_attn_all = _L1_attn_setup()
    _L1_attn_in = {k: v for k, v in _L1_attn_all.items() if k in ('mask', 'in_proj_w', 'conv_w', 'conv_b', 'A_log', 'dt_bias', 'D', 'norm_w', 'out_proj_w')}
    del _L1_attn_all

    def _L1_ffn_setup():
        import jax, jax.numpy as jnp
        import numpy as np
        NUM_EXPERTS = 8
        TOP_K = 2
        FFN_DIM = 512
        HIDDEN_DIM = 1024
        key = jax.random.key(seed)
        k0, k1, k2, k3, k4 = jax.random.split(key, 5)
        scale = 0.02
        return {'hidden_states': jax.random.normal(k0, (2, 256, FFN_DIM), dtype=jnp.float32), 'gate_w': jax.random.normal(k1, (NUM_EXPERTS, FFN_DIM), dtype=jnp.float32) * scale, 'w1': jax.random.normal(k2, (NUM_EXPERTS, FFN_DIM, HIDDEN_DIM), dtype=jnp.float32) * scale, 'w2': jax.random.normal(k3, (NUM_EXPERTS, HIDDEN_DIM, FFN_DIM), dtype=jnp.float32) * scale, 'w3': jax.random.normal(k4, (NUM_EXPERTS, FFN_DIM, HIDDEN_DIM), dtype=jnp.float32) * scale}
    _L1_ffn_all = _L1_ffn_setup()
    _L1_ffn_in = {k: v for k, v in _L1_ffn_all.items() if k in ('gate_w', 'w1', 'w2', 'w3')}
    del _L1_ffn_all
    return {'x': x, 'ctx_512': ctx_512, 'L0_xattn_Wq': _L0_xattn_in['Wq'], 'L0_xattn_Wkv_expand': _L0_xattn_in['Wkv_expand'], 'L0_xattn_Wout': _L0_xattn_in['Wout'], 'L0_attn_Wq': _L0_attn_in['Wq'], 'L0_attn_Wk': _L0_attn_in['Wk'], 'L0_attn_Wv': _L0_attn_in['Wv'], 'L0_attn_Wb': _L0_attn_in['Wb'], 'L0_attn_Wa': _L0_attn_in['Wa'], 'L0_attn_A_log': _L0_attn_in['A_log'], 'L0_attn_dt_bias': _L0_attn_in['dt_bias'], 'L0_attn_conv_q_w': _L0_attn_in['conv_q_w'], 'L0_attn_conv_k_w': _L0_attn_in['conv_k_w'], 'L0_attn_conv_v_w': _L0_attn_in['conv_v_w'], 'L0_attn_Wg': _L0_attn_in['Wg'], 'L0_attn_norm_w': _L0_attn_in['norm_w'], 'L0_attn_Wo': _L0_attn_in['Wo'], 'L0_ffn_gate_w': _L0_ffn_in['gate_w'], 'L0_ffn_w13': _L0_ffn_in['w13'], 'L0_ffn_w2': _L0_ffn_in['w2'], 'L1_xattn_Wq': _L1_xattn_in['Wq'], 'L1_xattn_w_kc_q': _L1_xattn_in['w_kc_q'], 'L1_xattn_w_kc_kv': _L1_xattn_in['w_kc_kv'], 'L1_xattn_W_qr': _L1_xattn_in['W_qr'], 'L1_xattn_W_kr': _L1_xattn_in['W_kr'], 'L1_xattn_Wo': _L1_xattn_in['Wo'], 'L1_attn_mask': _L1_attn_in['mask'], 'L1_attn_in_proj_w': _L1_attn_in['in_proj_w'], 'L1_attn_conv_w': _L1_attn_in['conv_w'], 'L1_attn_conv_b': _L1_attn_in['conv_b'], 'L1_attn_A_log': _L1_attn_in['A_log'], 'L1_attn_dt_bias': _L1_attn_in['dt_bias'], 'L1_attn_D': _L1_attn_in['D'], 'L1_attn_norm_w': _L1_attn_in['norm_w'], 'L1_attn_out_proj_w': _L1_attn_in['out_proj_w'], 'L1_ffn_gate_w': _L1_ffn_in['gate_w'], 'L1_ffn_w1': _L1_ffn_in['w1'], 'L1_ffn_w2': _L1_ffn_in['w2'], 'L1_ffn_w3': _L1_ffn_in['w3']}

def reference(x, ctx_512, L0_xattn_Wq, L0_xattn_Wkv_expand, L0_xattn_Wout, L0_attn_Wq, L0_attn_Wk, L0_attn_Wv, L0_attn_Wb, L0_attn_Wa, L0_attn_A_log, L0_attn_dt_bias, L0_attn_conv_q_w, L0_attn_conv_k_w, L0_attn_conv_v_w, L0_attn_Wg, L0_attn_norm_w, L0_attn_Wo, L0_ffn_gate_w, L0_ffn_w13, L0_ffn_w2, L1_xattn_Wq, L1_xattn_w_kc_q, L1_xattn_w_kc_kv, L1_xattn_W_qr, L1_xattn_W_kr, L1_xattn_Wo, L1_attn_mask, L1_attn_in_proj_w, L1_attn_conv_w, L1_attn_conv_b, L1_attn_A_log, L1_attn_dt_bias, L1_attn_D, L1_attn_norm_w, L1_attn_out_proj_w, L1_ffn_gate_w, L1_ffn_w1, L1_ffn_w2, L1_ffn_w3):
    import jax
    import jax.numpy as jnp

    def _L0_xattn_ref(q, latent_kv, Wq, Wkv_expand, Wout):
        import jax, jax.numpy as jnp
        import numpy as np
        B, S, H, NH, L = (2, 512, 512, 16, 128)
        HD = H // NH
        b, sq, _ = q.shape
        sk = latent_kv.shape[1]
        qp = q @ Wq.T
        kv = latent_kv @ Wkv_expand.T
        k, v = jnp.split(kv, 2, axis=-1)
        qh = qp.reshape(b, sq, NH, HD).transpose(0, 2, 1, 3)
        kh = k.reshape(b, sk, NH, HD).transpose(0, 2, 1, 3)
        vh = v.reshape(b, sk, NH, HD).transpose(0, 2, 1, 3)
        inv_sqrt_d = 1.0 / jnp.sqrt(jnp.float32(HD))
        scores = jnp.einsum('bhqd,bhkd->bhqk', qh, kh) * inv_sqrt_d
        causal = jnp.tril(jnp.ones((sq, sk), dtype=bool))
        scores = jnp.where(causal, scores, jnp.finfo(scores.dtype).min)
        attn = jax.nn.softmax(scores, axis=-1)
        out = jnp.einsum('bhqk,bhkd->bhqd', attn, vh)
        out = out.transpose(0, 2, 1, 3).reshape(b, sq, H)
        return out @ Wout.T

    def _L0_attn_ref(x, Wq, Wk, Wv, Wb, Wa, A_log, dt_bias, conv_q_w, conv_k_w, conv_v_w, Wg, norm_w, Wo):
        import jax, jax.numpy as jnp
        import numpy as np
        HIDDEN = 512
        HEAD_DIM = 128
        NUM_HEADS = 8
        NUM_HH = 2
        CONV = 4
        EPS = 1e-05
        KEY_DIM = NUM_HEADS * HEAD_DIM

        def _causal_conv_silu(x, w):
            y = jax.lax.conv_general_dilated(jnp.swapaxes(x, 1, 2), w, window_strides=(1,), padding=[(w.shape[-1] - 1, 0)], feature_group_count=w.shape[0], dimension_numbers=('NCH', 'OIH', 'NCH'))
            return jnp.swapaxes(jax.nn.silu(y), 1, 2)

        def _l2norm(x):
            n = jnp.sqrt(jnp.sum(x * x, axis=-1, keepdims=True))
            return x / jnp.maximum(n, 1e-12)

        def _reference_tuple_inner(x, Wq, Wk, Wv, Wb, Wa, A_log, dt_bias, conv_q_w, conv_k_w, conv_v_w, Wg, norm_w, Wo):
            B, L, _ = x.shape
            H, Dh, nh = (NUM_HEADS, HEAD_DIM, NUM_HH)
            q = _causal_conv_silu(x @ Wq, conv_q_w).reshape(B, L, H, Dh)
            k = _causal_conv_silu(x @ Wk, conv_k_w).reshape(B, L, nh, H, Dh)
            v = _causal_conv_silu(x @ Wv, conv_v_w).reshape(B, L, nh, H, Dh)
            q = _l2norm(q) / np.float32(np.sqrt(Dh))
            k = _l2norm(k)
            beta = 2.0 * jax.nn.sigmoid(x @ Wb).reshape(B, L, nh, H)
            g = -jnp.exp(A_log) * jax.nn.softplus(x @ Wa + dt_bias)

            def step(state, inp):
                q_t, k_t, v_t, b_t, g_t = inp
                state = state * jnp.exp(g_t)[..., None, None]
                for j in range(nh):
                    kj = k_t[:, j]
                    corr = jnp.einsum('bhk,bhkv->bhv', kj, state)
                    u = (v_t[:, j] - corr) * b_t[:, j][..., None]
                    state = state + jnp.einsum('bhk,bhv->bhkv', kj, u)
                o_t = jnp.einsum('bhk,bhkv->bhv', q_t, state)
                return (state, o_t)
            state0 = jnp.zeros((B, H, Dh, Dh), x.dtype)
            xs = (jnp.moveaxis(q, 1, 0), jnp.moveaxis(k, 1, 0), jnp.moveaxis(v, 1, 0), jnp.moveaxis(beta, 1, 0), jnp.moveaxis(g, 1, 0))
            state, o = jax.lax.scan(step, state0, xs)
            o = jnp.moveaxis(o, 0, 1)
            gate = (x @ Wg).reshape(B, L, H, Dh)
            o = o * jax.lax.rsqrt(jnp.mean(o * o, axis=-1, keepdims=True) + EPS)
            o = o * norm_w * jax.nn.silu(gate)
            out = o.reshape(B, L, H * Dh) @ Wo
            return (out, state)
        return _reference_tuple_inner(x, Wq, Wk, Wv, Wb, Wa, A_log, dt_bias, conv_q_w, conv_k_w, conv_v_w, Wg, norm_w, Wo)[0]

    def _L0_ffn_ref(hidden_states, gate_w, w13, w2):
        import jax, jax.numpy as jnp
        import numpy as np
        NUM_EXPERTS = 64
        TOP_K = 8
        HIDDEN = 512
        INTER = 256
        orig_shape = hidden_states.shape
        x = hidden_states.reshape(-1, HIDDEN)
        logits = jnp.einsum('th,eh->te', x, gate_w)
        probs = jax.nn.softmax(logits, axis=-1)
        topk_w, topk_idx = jax.lax.top_k(probs, TOP_K)
        combine = (jax.nn.one_hot(topk_idx, NUM_EXPERTS, dtype=x.dtype) * topk_w[..., None]).sum(axis=1)

        def step(acc, inp):
            w13_e, w2_e, c = inp
            g = x @ w13_e[:INTER].T
            u = x @ w13_e[INTER:].T
            h = jax.nn.silu(g) * u
            o = h @ w2_e.T
            return (acc + c[:, None] * o, None)
        out0 = jnp.zeros_like(x)
        out, _ = jax.lax.scan(step, out0, (w13, w2, combine.T))
        return out.reshape(orig_shape)

    def _L1_xattn_ref(hidden_q, kv_c, Wq, w_kc_q, w_kc_kv, W_qr, W_kr, Wo):
        import jax, jax.numpy as jnp
        import numpy as np
        B, S, L = (2, 256, 256)
        DIM_Q, H, K, D_C, D_CQ, R = (512, 16, 128, 128, 384, 64)

        def _rope_tables(length, dim):
            inv = 1.0 / 10000.0 ** (jnp.arange(0, dim, 2, dtype=jnp.float32) / dim)
            f = jnp.arange(length, dtype=jnp.float32)[:, None] * inv[None, :]
            sin = jnp.repeat(jnp.sin(f), 2, axis=-1)
            cos = jnp.repeat(jnp.cos(f), 2, axis=-1)
            return (sin, cos)

        def _rotate_half(x):
            half = x.shape[-1] // 2
            return jnp.concatenate([-x[..., half:], x[..., :half]], axis=-1)

        def _apply_rope(x, sin, cos):
            return x * cos + _rotate_half(x) * sin
        Bv, Sv, _ = hidden_q.shape
        _, Lv, _ = kv_c.shape
        q_hk = (hidden_q @ Wq.T).reshape(Bv, Sv, H, K)
        q_big = jnp.einsum('bshk,hkq->bshq', q_hk, w_kc_q)
        sin_q, cos_q = _rope_tables(Sv, D_CQ)
        q_big = _apply_rope(q_big, sin_q[None, :, None, :], cos_q[None, :, None, :])
        sin_k, cos_k = _rope_tables(Lv, D_C)
        kv_r = _apply_rope(kv_c, sin_k[None], cos_k[None])
        q_r = jnp.einsum('bshq,hqr->bhsr', q_big, W_qr)
        k_r = jnp.einsum('bld,hdr->bhlr', kv_r, W_kr)
        scores = jnp.einsum('bhsr,bhlr->bhsl', q_r, k_r)
        attn = jax.nn.softmax(scores, axis=-1)
        ctx_c = jnp.einsum('bhsl,bld->bhsd', attn, kv_r)
        ctx_lat = jnp.einsum('bhsd,hkd->bhsk', ctx_c, w_kc_kv)
        ctx = ctx_lat.transpose(0, 2, 1, 3).reshape(Bv, Sv, H * K)
        return ctx @ Wo.T

    def _L1_attn_ref(input_states, mask, in_proj_w, conv_w, conv_b, A_log, dt_bias, D, norm_w, out_proj_w):
        import jax, jax.numpy as jnp
        import numpy as np
        B_, S_, E_ = (2, 512, 512)
        H_, P_, N_, G_, K_, CH_ = (64, 64, 128, 1, 4, 64)
        INTER = H_ * P_
        CONV_DIM = INTER + 2 * G_ * N_
        PROJ = INTER + CONV_DIM + H_
        EPS = 1e-05

        def segsum(x):
            T = x.shape[-1]
            xe = jnp.broadcast_to(x[..., None], x.shape + (T,))
            m_excl = jnp.tril(jnp.ones((T, T), bool), -1)
            s = jnp.cumsum(jnp.where(m_excl, xe, 0.0), axis=-2)
            m_incl = jnp.tril(jnp.ones((T, T), bool), 0)
            return jnp.where(m_incl, s, -jnp.inf)

        def ssm_forward(input_states, in_proj_w, conv_w, conv_b, A_log, dt_bias, D, norm_w, out_proj_w):
            b, s, _ = input_states.shape
            proj = input_states @ in_proj_w.T
            gate, hBC, dt = jnp.split(proj, [INTER, INTER + CONV_DIM], axis=-1)
            x = hBC.transpose(0, 2, 1)
            x = jax.lax.conv_general_dilated(x, conv_w, (1,), [(K_ - 1, 0)], dimension_numbers=('NCH', 'OIH', 'NCH'), feature_group_count=CONV_DIM)
            hBC = jax.nn.silu((x + conv_b[None, :, None]).transpose(0, 2, 1))
            hs, Bmat, Cmat = jnp.split(hBC, [INTER, INTER + G_ * N_], axis=-1)
            A = -jnp.exp(A_log)
            dt = jax.nn.softplus(dt + dt_bias)
            xh = hs.reshape(b, s, H_, P_)
            Bf = jnp.repeat(Bmat.reshape(b, s, G_, N_), H_ // G_, axis=2)
            Cf = jnp.repeat(Cmat.reshape(b, s, G_, N_), H_ // G_, axis=2)
            D_res = D[:, None] * xh
            xh = xh * dt[..., None]
            Adt = A[None, None, :] * dt
            nch = s // CH_
            xc = xh.reshape(b, nch, CH_, H_, P_)
            Bc = Bf.reshape(b, nch, CH_, H_, N_)
            Cc = Cf.reshape(b, nch, CH_, H_, N_)
            Ac = Adt.reshape(b, nch, CH_, H_).transpose(0, 3, 1, 2)
            A_cum = jnp.cumsum(Ac, axis=-1)
            L = jnp.exp(segsum(Ac))
            Gm = jnp.einsum('bclhn,bcshn->bclsh', Cc, Bc)
            M = Gm * L.transpose(0, 2, 3, 4, 1)
            Y_diag = jnp.einsum('bclsh,bcshp->bclhp', M, xc)
            decay_states = jnp.exp(A_cum[..., -1:] - A_cum)
            states = jnp.einsum('bclhn,bhcl,bclhp->bchpn', Bc, decay_states, xc)
            states = jnp.concatenate([jnp.zeros_like(states[:, :1]), states], axis=1)
            A_last = jnp.pad(A_cum[..., -1], ((0, 0), (0, 0), (1, 0)))
            decay_chunk = jnp.exp(segsum(A_last))
            new_states = jnp.einsum('bhij,bjhpn->bihpn', decay_chunk, states)
            states = new_states[:, :-1]
            state_decay = jnp.exp(A_cum)
            Y_off = jnp.einsum('bclhn,bchpn,bhcl->bclhp', Cc, states, state_decay)
            y = (Y_diag + Y_off).reshape(b, s, H_, P_) + D_res
            y = y.reshape(b, s, INTER)
            yg = y * jax.nn.silu(gate)
            var = jnp.mean(yg * yg, axis=-1, keepdims=True)
            yn = norm_w * (yg * jax.lax.rsqrt(var + EPS))
            return yn @ out_proj_w.T
        return ssm_forward(input_states, in_proj_w, conv_w, conv_b, A_log, dt_bias, D, norm_w, out_proj_w)

    def _L1_ffn_ref(hidden_states, gate_w, w1, w2, w3):
        import jax, jax.numpy as jnp
        import numpy as np
        NUM_EXPERTS = 8
        TOP_K = 2
        FFN_DIM = 512
        HIDDEN_DIM = 1024
        origin_shape = hidden_states.shape
        x = hidden_states.reshape(-1, FFN_DIM)
        n_tokens = x.shape[0]
        router_logits = x @ gate_w.T
        routing_probs = jax.nn.softmax(router_logits.astype(jnp.float32), axis=-1)
        topk_w, topk_idx = jax.lax.top_k(routing_probs, TOP_K)
        topk_w = topk_w / jnp.sum(topk_w, axis=-1, keepdims=True)
        topk_w = topk_w.astype(x.dtype)
        token_ids = jnp.arange(n_tokens)[:, None]
        full_w = jnp.zeros((n_tokens, NUM_EXPERTS), dtype=x.dtype)
        full_w = full_w.at[token_ids, topk_idx].add(topk_w)
        h = jax.nn.silu(jnp.einsum('nf,efh->enh', x, w1)) * jnp.einsum('nf,efh->enh', x, w3)
        y = jnp.einsum('enh,ehf->enf', h, w2)
        out = jnp.einsum('enf,ne->nf', y, full_w)
        return out.reshape(origin_shape)
    x = x + _L0_xattn_ref(_layernorm(x, axis=-1), ctx_512, L0_xattn_Wq, L0_xattn_Wkv_expand, L0_xattn_Wout)
    x = x + _L0_attn_ref(_layernorm(x, axis=-1), L0_attn_Wq, L0_attn_Wk, L0_attn_Wv, L0_attn_Wb, L0_attn_Wa, L0_attn_A_log, L0_attn_dt_bias, L0_attn_conv_q_w, L0_attn_conv_k_w, L0_attn_conv_v_w, L0_attn_Wg, L0_attn_norm_w, L0_attn_Wo)
    x = x + _L0_ffn_ref(_layernorm(x, axis=-1), L0_ffn_gate_w, L0_ffn_w13, L0_ffn_w2)
    x = x + _L1_xattn_ref(_layernorm(x, axis=-1), ctx_512, L1_xattn_Wq, L1_xattn_w_kc_q, L1_xattn_w_kc_kv, L1_xattn_W_qr, L1_xattn_W_kr, L1_xattn_Wo)
    x = x + _L1_attn_ref(_layernorm(x, axis=-1), L1_attn_mask, L1_attn_in_proj_w, L1_attn_conv_w, L1_attn_conv_b, L1_attn_A_log, L1_attn_dt_bias, L1_attn_D, L1_attn_norm_w, L1_attn_out_proj_w)
    x = x + _L1_ffn_ref(_layernorm(x, axis=-1), L1_ffn_gate_w, L1_ffn_w1, L1_ffn_w2, L1_ffn_w3)
    return x

_drawn_inputs = setup_inputs


def setup_inputs(seed=0):
    import zlib

    import numpy as np

    out = dict(_drawn_inputs(seed))
    spreads = {'L0_attn_norm_w': (1.0, 0.6),
     'L1_attn_conv_b': (0.0, 0.1),
     'L1_attn_dt_bias': (1.0, 0.6),
     'L1_attn_D': (1.0, 0.2),
     'L1_attn_norm_w': (1.0, 0.2)}
    factors = {'L0_xattn_Wq': 8.0, 'L0_attn_Wa': 8.0, 'L1_attn_A_log': 7.231}
    for name, (base, spread) in spreads.items():
        noise = np.random.default_rng([zlib.crc32(name.encode()), seed]).standard_normal(out[name].shape)
        drawn = base * np.exp(spread * noise) if base else spread * noise
        out[name] = jnp.asarray(drawn.astype(out[name].dtype))
    for name, factor in factors.items():
        out[name] = (out[name] * factor).astype(out[name].dtype)
    return out
```

```python
from contextlib import ExitStack

import numpy as np
import concourse.bass as bass
from concourse import mybir

F32 = mybir.dt.float32
ACT = mybir.ActivationFunctionType
ALU = mybir.AluOpType
AX_X = mybir.AxisListType.X

P = 128
TOK = 256
TT = TOK // P
D = 512
KT = D // P
CTX = 4096
CT = CTX // P
EPS = 1e-5
LOWEST = -3.0e38

RING = 4
SLOT = 3072
N_L0X, N_L0A, N_L0F, N_L1X, N_L1A, N_L1F = 2, 10, 64, 12, 22, 32
FIRST_SLOT = {}
_at = 0
for _name, _n in (("L0x", N_L0X), ("L0a", N_L0A), ("L0f", N_L0F), ("L1x", N_L1X), ("L1a", N_L1A), ("L1f", N_L1F)):
    FIRST_SLOT[_name] = (_at, _n)
    _at += _n
SLOTS = _at

C_ID = 0
C_LEVEL = C_ID + 4 * P
C_CAUSAL = C_LEVEL + 7 * P
C_ONES = C_CAUSAL + 2 * P
C_EPS = C_ONES + P
C_PICK = C_EPS + 1
C_N = C_PICK + 64

S_ACONV = 0
S_AAB = S_ACONV + 160
S_ANORM = S_AAB + 96
S_AHEAD = S_ANORM + 1
S_F0 = S_AHEAD + 2
S_F1 = S_F0 + KT * 64
S_MCONV = S_F1 + KT * 8
S_MBIAS = S_MCONV + 136
S_MDT = S_MBIAS + 34
S_MHEAD = S_MDT + KT * 64
S_MD = S_MHEAD + 2
S_MNORM = S_MD + 64
S_N = S_MNORM + 32


class Chain:

    def __init__(self, eng, sem):
        self.eng, self.sem, self.n = eng, sem, 0

    def did(self, ins):
        ins.then_inc(self.sem, 1)
        self.n += 1
        return self.n

    def wait(self):
        self.eng.wait_ge(self.sem, self.n)


class Env:
    pass


def bcast_last(ap, shape):
    return ap.unsqueeze(len(shape) - 1).broadcast_to(shape)


def open_env(nc, ctx, io):
    e = Env()
    e.nc, e.io = nc, io

    def sb(name, shape):
        return ctx.enter_context(nc.sbuf_tensor("sb_" + name, shape, F32))

    e.ps = ctx.enter_context(nc.psum_tensor("banks", [P, 8, 512], F32))
    e.fixed = sb("fixed", [P, C_N])
    e.small = sb("small", [P, S_N])
    e.xres = sb("xres", [P, TT, D])
    e.xnbuf = sb("xnbuf", [P, 2 * TT * D])
    e.xn = e.xnbuf[:, 0:TT * D].rearrange("p (t d) -> p t d", t=TT)
    e.xnT = e.xnbuf[:, TT * D:2 * TT * D].rearrange("p (k t) -> p k t", k=KT)
    e.stats = sb("stats", [P, TT, 6])
    e.mv = sb("mv", [P, TT, 2])
    e.std = sb("std", [P, TT])
    e.ring = sb("ring", [P, RING, SLOT])
    e.ident = e.fixed[:, C_ID:C_ID + P]
    e.ident4 = e.fixed[:, C_ID:C_ID + 4 * P]
    e.ones = e.fixed[:, C_ONES:C_ONES + P]
    e.eps = e.fixed[:, C_EPS:C_EPS + 1]
    e.w_in = [ctx.enter_context(nc.semaphore(f"w_in{i}")) for i in range(RING)]
    e.w_used = ctx.enter_context(nc.semaphore("w_used"))
    e.boot = ctx.enter_context(nc.semaphore("boot"))
    e.n0 = 0
    e.slots = 0
    e.preloaded = False
    return e


def layer_sems(nc, ctx, tag, names):
    return {n: ctx.enter_context(nc.semaphore(f"{tag}_{n}")) for n in names}


def clear_sems(nc, s):
    ids = sorted(x.num for x in s.values())
    runs = []
    for i in ids:
        if runs and runs[-1][1] == i:
            runs[-1][1] = i + 1
        else:
            runs.append([i, i + 1])
    with nc.Block(no_gpsimd_drain=True) as block:
        @block.gpsimd
        def _(pool):
            for lo, hi in runs:
                pool.sem_clear(range(lo, hi))


LN_OWN = 3
LN_SEMS = ["ln_self", "ln_stats", "ln_std", "ln_xn", "ln_turned", "ln_done"]


def stream(sp, e, first, count):
    lo = first + RING if first or e.preloaded else 0
    hi = min(first + count + RING, e.slots)
    for n in range(lo, min(hi, RING)):
        sp.dma_start(e.ring[:, n, :], e.io["wall"][n]).then_inc(e.w_in[n], 16)
    lo = max(lo, RING)
    while lo < hi and lo % RING:
        load_slot(sp, e, lo, lo % RING)
        lo += 1
    turns = (hi - lo) // RING
    if turns > 1:
        with sp.Fori(0, turns) as i:
            for u in range(RING):
                sp.wait_ge(e.w_used, i * RING + (lo + u - RING + 1))
                sp.dma_start(e.ring[:, u, :], e.io["wall"][bass.ds(i * RING + (lo + u), 1)].rearrange("a p n -> (a p) n"))\
                    .then_inc(e.w_in[u], 16)
        lo += turns * RING
    while lo < hi:
        load_slot(sp, e, lo, lo % RING)
        lo += 1


def load_slot(sp, e, n, u):
    sp.wait_ge(e.w_used, n - RING + 1)
    sp.dma_start(e.ring[:, u, :], e.io["wall"][n]).then_inc(e.w_in[u], 16)


def slot_in(eng, e, n):
    eng.wait_ge(e.w_in[n % RING], 16 * (n // RING + 1))
    return e.ring[:, n % RING, :]



def ln_vector(dve, e, s):
    me = Chain(dve, s["ln_self"])
    for t in range(TT):
        me.did(dve.bn_stats(e.stats[:, t, :], e.xres[:, t, :]))
    me.wait()
    for t in range(TT):
        dve.bn_aggr(e.mv[:, t, :], e.stats[:, t, :]).then_inc(s["ln_stats"], 1)
    dve.wait_ge(s["ln_std"], 1)
    me.did(dve.reciprocal(e.std[:, :], e.std[:, :]))
    me.wait()
    for t in range(TT):
        dve.tensor_scalar(e.xn[:, t, :], e.xres[:, t, :], e.mv[:, t, 0:1], e.std[:, t:t + 1],
                          ALU.subtract, ALU.mult).then_inc(s["ln_xn"], 1)
    dve.wait_ge(s["ln_turned"], 1)
    dve.tensor_copy(e.xnT[:, 0:2, :], e.ps[:, 0, :].rearrange("p (k t) -> p k t", k=2)).then_inc(s["ln_done"], 1)


def ln_scalar(act, e, s):
    act.wait_ge(s["ln_stats"], TT)
    act.activation(e.std[:, :], e.mv[:, :, 1], ACT.Sqrt, bias=e.eps).then_inc(s["ln_std"], 1)
    act.wait_ge(s["ln_turned"], 2)
    act.activation(e.xnT[:, 2:4, :], e.ps[:, 1, :].rearrange("p (k t) -> p k t", k=2), ACT.Copy)\
        .then_inc(s["ln_done"], 1)


def ln_tensor(pe, e, s):
    for k in range(KT):
        for t in range(TT):
            if k == 0:
                pe.wait_ge(s["ln_xn"], t + 1)
            at = (k % 2) * TOK + t * P
            last = pe.transpose(e.ps[:, k // 2, at:at + P], e.xn[:, t, k * P:(k + 1) * P], e.ident)
        if k % 2:
            last.then_inc(s["ln_turned"], 1)
    pe.wait_ge(s["ln_done"], 2)



def layer_l0x(e, first_layer=True):
    nc, ps, fixed = e.nc, e.ps, e.fixed
    NH, HD = 16, 32
    G = 4
    SCALE = float(np.float32(1.0) / np.sqrt(np.float32(HD)))
    n0 = e.n0
    with ExitStack() as ctx:
        def sb(name, shape):
            return ctx.enter_context(nc.sbuf_tensor("l0x_" + name, shape, F32))
        s = layer_sems(nc, ctx, "l0x", LN_SEMS + [
            "k_mm", "v_mm", "q_mm", "kqv", "score_mm", "masked", "top", "prob", "turn_mm", "turned", "o_mm",
            "o_sb", "oT_mm", "oT_sb", "out_mm", "dve_self"])
        ctxT = sb("ctxT", [P, TOK])
        kT = sb("kT", [P, 4, TOK])
        v = sb("v", [P, TT, D])
        qT = sb("qT", [P, 4, TOK])
        sc = sb("sc", [P, G, 3 * P])
        pT = sb("pT", [P, G, 3, P])
        ntop = sb("ntop", [P, 4, 2 * G])
        rsum = sb("rsum", [P, TT, NH])
        o = sb("o", [P, TT, D])
        oT = sb("oT", [P, KT, TOK])
        causal = fixed[:, C_CAUSAL:C_CAUSAL + 2 * P]

        with nc.Block(no_gpsimd_drain=True) as block:
            @block.sync
            def _(sp):
                sp.dma_start(e.xres[:, :, :], e.io["x"].rearrange("(t p) d -> p t d", p=P)).then_inc(e.boot, 16)
                sp.dma_start(fixed[:, :], e.io["fixed"]).then_inc(e.boot, 16)
                sp.dma_start(ctxT[:, :], e.io["ctxT"]).then_inc(e.boot, 16)
                sp.dma_start(e.small[:, :], e.io["small"]).then_inc(e.boot, 16)
                stream(sp, e, n0, N_L0X)

            @block.tensor
            def _(pe):
                pe.wait_ge(e.boot, 64)
                w = slot_in(pe, e, n0)
                for m in range(4):
                    last = pe.matmul(ps[:, 2 + m // 2, (m % 2) * TOK:(m % 2 + 1) * TOK],
                                     w[:, 2048 + m * P:2048 + (m + 1) * P], ctxT[:, :], start=True, stop=True)
                last.then_inc(s["k_mm"], 1)
                for t in range(TT):
                    last = pe.matmul(ps[:, 4 + t, :], ctxT[:, t * P:(t + 1) * P], w[:, 2560:3072],
                                     start=True, stop=True)
                last.then_inc(s["v_mm"], 1)
                ln_tensor(pe, e, s)
                for m in range(4):
                    for k in range(KT):
                        last = pe.matmul(ps[:, 6 + m // 2, (m % 2) * TOK:(m % 2 + 1) * TOK],
                                         w[:, k * D + m * P:k * D + (m + 1) * P], e.xnT[:, k, :],
                                         start=(k == 0), stop=(k == KT - 1))
                last.then_inc(s["q_mm"], 1)
                pe.wait_ge(s["kqv"], 3)
                pe.nop().then_inc(e.w_used, 1)
                for g in range(4):
                    r = slice(32 * g, 32 * g + 32)
                    if g:
                        pe.wait_ge(s["masked"], 2 * g)
                    for m in range(G):
                        pe.matmul(ps[:, 0, m * P:(m + 1) * P], qT[r, m, 0:P], kT[r, m, 0:P], start=True, stop=True)
                        last = pe.matmul(ps[:, 1 + m // 2, (m % 2) * TOK:(m % 2 + 1) * TOK], qT[r, m, P:TOK],
                                         kT[r, m, :], start=True, stop=True)
                    last.then_inc(s["score_mm"], 1)
                    pe.wait_ge(s["prob"], 2 * G * (g + 1))
                    if g:
                        pe.wait_ge(s["turned"], 2 * g)
                    for m in range(G):
                        for b in range(3):
                            at = (m * 3 + b) * P
                            last = pe.transpose(ps[:, 3 + at // 512, at % 512:at % 512 + P],
                                                sc[:, m, b * P:(b + 1) * P], e.ident)
                    last.then_inc(s["turn_mm"], 1)
                    pe.wait_ge(s["turned"], 2 * (g + 1))
                    for m in range(G):
                        h = 4 * m + g
                        hs = slice(HD * h, HD * (h + 1))
                        pe.matmul(ps[:, 6, hs], pT[:, m, 0, :], v[:, 0, hs], start=True, stop=True)
                        pe.matmul(ps[:, 7, hs], pT[:, m, 1, :], v[:, 0, hs], start=True, stop=False)
                        last = pe.matmul(ps[:, 7, hs], pT[:, m, 2, :], v[:, 1, hs], start=False, stop=True)
                last.then_inc(s["o_mm"], 1)
                pe.wait_ge(s["o_sb"], 2)
                for k in range(KT):
                    for t in range(TT):
                        last = pe.transpose(ps[:, k // 2, (k % 2) * TOK + t * P:(k % 2) * TOK + (t + 1) * P],
                                            o[:, t, k * P:(k + 1) * P], e.ident)
                last.then_inc(s["oT_mm"], 1)
                pe.wait_ge(s["oT_sb"], 1)
                w = slot_in(pe, e, n0 + 1)
                for t in range(TT):
                    for k in range(KT):
                        last = pe.matmul(ps[:, 2 + t, :], oT[:, k, t * P:(t + 1) * P], w[:, k * D:(k + 1) * D],
                                         start=(k == 0), stop=(k == KT - 1))
                    last.then_inc(s["out_mm"], 1)
                pe.wait_ge(s["out_mm"], TT)
                pe.nop().then_inc(e.w_used, 1)

            @block.scalar
            def _(act):
                act.wait_ge(e.boot, 64)
                ln_scalar(act, e, s)
                act.wait_ge(s["v_mm"], 1)
                act.activation(v[:, :, :], ps[:, 4:6, :], ACT.Copy).then_inc(s["kqv"], 1)
                act.wait_ge(s["q_mm"], 1)
                act.activation(qT[:, :, :].rearrange("p a b -> p (a b)"),
                               ps[:, 6:8, :].rearrange("p a b -> p (a b)"), ACT.Copy).then_inc(s["kqv"], 1)
                for g in range(4):
                    act.wait_ge(s["top"], g + 1)
                    for m in range(G):
                        h = 4 * m + g
                        act.activation(sc[:, m, 0:P], sc[:, m, 0:P], ACT.Exp, bias=ntop[:, g, m:m + 1],
                                       accum_out=rsum[:, 0, h:h + 1]).then_inc(s["prob"], 1)
                        act.activation(sc[:, m, P:3 * P], sc[:, m, P:3 * P], ACT.Exp,
                                       bias=ntop[:, g, G + m:G + m + 1],
                                       accum_out=rsum[:, 1, h:h + 1]).then_inc(s["prob"], 1)
                    act.wait_ge(s["turn_mm"], g + 1)
                    act.activation(pT[:, :, :, :].rearrange("p a b c -> p (a b c)")[:, 1024:1536],
                                   ps[:, 5, :], ACT.Copy)\
                        .then_inc(s["turned"], 1)

            @block.vector
            def _(dve):
                me = Chain(dve, s["dve_self"])
                dve.wait_ge(e.boot, 64)
                ln_vector(dve, e, s)
                dve.wait_ge(s["k_mm"], 1)
                dve.tensor_copy(kT[:, :, :].rearrange("p a b -> p (a b)"),
                                ps[:, 2:4, :].rearrange("p a b -> p (a b)")).then_inc(s["kqv"], 1)
                for g in range(4):
                    dve.wait_ge(s["score_mm"], g + 1)
                    if g:
                        dve.wait_ge(s["turn_mm"], g)
                    dve.scalar_tensor_tensor(
                        out=sc[:, :, 0:P], in0=ps[:, 0, :].rearrange("p (m k) -> p m k", m=G), scalar=SCALE,
                        in1=causal[:, P:2 * P].unsqueeze(1).broadcast_to((P, G, P)), op0=ALU.mult, op1=ALU.add)\
                        .then_inc(s["masked"], 1)
                    dve.scalar_tensor_tensor(
                        out=sc[:, :, P:3 * P], in0=ps[:, 1:3, :].rearrange("p a (m k) -> p (a m) k", m=2),
                        scalar=SCALE, in1=causal.unsqueeze(1).broadcast_to((P, G, 2 * P)),
                        op0=ALU.mult, op1=ALU.add).then_inc(s["masked"], 1)
                    dve.wait_ge(s["masked"], 2 * (g + 1))
                    me.did(dve.tensor_reduce(ntop[:, g, 0:G], sc[:, :, 0:P], AX_X, ALU.max))
                    me.did(dve.tensor_reduce(ntop[:, g, G:2 * G], sc[:, :, P:3 * P], AX_X, ALU.max))
                    me.wait()
                    dve.tensor_scalar(ntop[:, g, :], ntop[:, g, :], -1.0, None, ALU.mult).then_inc(s["top"], 1)
                    dve.wait_ge(s["turn_mm"], g + 1)
                    dve.tensor_copy(pT[:, :, :, :].rearrange("p a b c -> p (a b c)")[:, 0:1024],
                                    ps[:, 3:5, :].rearrange("p a b -> p (a b)"))\
                        .then_inc(s["turned"], 1)
                dve.wait_ge(s["prob"], 8 * G)
                me.did(dve.reciprocal(rsum[:, :, :], rsum[:, :, :]))
                me.wait()
                dve.wait_ge(s["o_mm"], 1)
                for t in range(TT):
                    dve.tensor_tensor(o[:, t, :].rearrange("p (h d) -> p h d", h=NH),
                                      ps[:, 6 + t, :].rearrange("p (h d) -> p h d", h=NH),
                                      bcast_last(rsum[:, t, :], (P, NH, HD)), ALU.mult).then_inc(s["o_sb"], 1)
                dve.wait_ge(s["oT_mm"], 1)
                dve.tensor_copy(oT[:, :, :].rearrange("p a b -> p (a b)"),
                                ps[:, 0:2, :].rearrange("p a b -> p (a b)")).then_inc(s["oT_sb"], 1)
                for t in range(TT):
                    dve.wait_ge(s["out_mm"], t + 1)
                    me.did(dve.tensor_tensor(e.xres[:, t, :], e.xres[:, t, :], ps[:, 2 + t, :], ALU.add))
        clear_sems(nc, s)
    e.n0 += N_L0X



def layer_moe(e, tag, n_experts, parts, top_k, router_at):
    nc, ps = e.nc, e.ps
    n0 = e.n0
    steps = n_experts * parts
    assert n0 % RING == 0 or steps % RING == 0
    INNER = 256
    W2 = KT * 2 * INNER
    NV = max(n_experts, 8) + (8 - top_k)
    with ExitStack() as ctx:
        def sb(name, shape):
            return ctx.enter_context(nc.sbuf_tensor(f"{tag}_{name}", shape, F32))
        s = layer_sems(nc, ctx, tag, LN_SEMS + [
            "dve_self", "logits", "ltop", "exps", "router", "first_mm", "silu", "inner", "second_mm", "added"])
        prob = sb("prob", [P, TT, NV])
        left = sb("left", [P, TT, NV])
        comb = sb("comb", [P, TT, n_experts])
        top = sb("top", [P, TT, 8])
        nmax = sb("nmax", [P, TT])
        total = sb("total", [P, TT])
        silu = sb("silu", [P, 2, 2 * TOK])
        hT = sb("hT", [P, 2, 2, TOK])

        def first_half(pe, turn, u):
            b = u % 2
            slot = (n0 + u) % RING
            w = e.ring[:, slot, :]
            pe.wait_ge(e.w_in[slot], turn * 16 + 16 * ((n0 + u) // RING + 1))
            early = isinstance(turn, int) and turn * RING + u < 2
            if not early:
                pe.wait_ge(s["inner"], turn * RING + (u - 1))
            for f in range(4):
                for k in range(KT):
                    last = pe.matmul(ps[:, 2 * b + f // 2, (f % 2) * TOK:(f % 2 + 1) * TOK],
                                     w[:, k * 2 * INNER + f * P:k * 2 * INNER + (f + 1) * P], e.xnT[:, k, :],
                                     start=(k == 0), stop=(k == KT - 1))
                    if f == 0 and k == 0 and not early:
                        last.then_inc(e.w_used, 1)
                if f % 2:
                    last.then_inc(s["first_mm"], 1)

        def second_half(pe, turn, u):
            b = u % 2
            w = e.ring[:, (n0 + u) % RING, :]
            pe.wait_ge(s["inner"], turn * RING + (u + 1))
            if not (isinstance(turn, int) and turn * RING + u < 2):
                pe.wait_ge(s["added"], turn * (2 * RING) + 2 * (u - 1))
            for t in range(TT):
                for k in range(2):
                    last = pe.matmul(ps[:, 4 + 2 * b + t, :], hT[:, b, k, t * P:(t + 1) * P],
                                     w[:, W2 + k * D:W2 + (k + 1) * D], start=(k == 0), stop=(k == 1))
                last.then_inc(s["second_mm"], 1)

        def activate(act, turn, u):
            b = u % 2
            act.wait_ge(s["first_mm"], turn * (2 * RING) + (2 * u + 1))
            if not (isinstance(turn, int) and turn * RING + u < 2):
                act.wait_ge(s["inner"], turn * RING + (u - 1))
            act.activation(silu[:, b, :], ps[:, 2 * b, :], ACT.Silu).then_inc(s["silu"], 1)

        def multiply(dve, turn, u):
            b = u % 2
            dve.wait_ge(s["first_mm"], turn * (2 * RING) + (2 * u + 2))
            dve.wait_ge(s["silu"], turn * RING + (u + 1))
            if not (isinstance(turn, int) and turn * RING + u < 2):
                dve.wait_ge(s["second_mm"], turn * (2 * RING) + 2 * (u - 1))
            dve.tensor_tensor(hT[:, b, :, :].rearrange("p k t -> p (k t)"), silu[:, b, :], ps[:, 2 * b + 1, :],
                              ALU.mult).then_inc(s["inner"], 1)

        def add(dve, turn, u):
            b = u % 2
            for t in range(TT):
                if parts == 1:
                    at = turn * RING + u
                    weight = comb[:, t, at:at + 1] if isinstance(turn, int) else comb[:, t, bass.ds(at, 1)]
                else:
                    weight = comb[:, t, turn:turn + 1] if isinstance(turn, int) else comb[:, t, bass.ds(turn, 1)]
                dve.wait_ge(s["second_mm"], turn * (2 * RING) + (2 * u + t + 1))
                if not (isinstance(turn, int) and turn * RING + u < 1):
                    dve.wait_ge(s["added"], turn * (2 * RING) + (2 * u + t - 1))
                dve.scalar_tensor_tensor(out=e.xres[:, t, :], in0=ps[:, 4 + 2 * b + t, :], scalar=weight,
                                         in1=e.xres[:, t, :], op0=ALU.mult, op1=ALU.add).then_inc(s["added"], 1)

        TURNS = steps // RING
        with nc.Block(no_gpsimd_drain=True) as block:
            @block.sync
            def _(sp):
                if tag == "l0f":
                    rope_sync(sp, e)
                stream(sp, e, n0, steps)

            if tag == "l0f":
                @block.gpsimd
                def _(pool):
                    rope_pool(pool, e)

            @block.tensor
            def _(pe):
                ln_tensor(pe, e, s)
                for t in range(TT):
                    for k in range(KT):
                        last = pe.matmul(ps[:, 7, t * 64:t * 64 + n_experts], e.xnT[:, k, t * P:(t + 1) * P],
                                         e.small[:, router_at + k * n_experts:router_at + (k + 1) * n_experts],
                                         start=(k == 0), stop=(k == KT - 1))
                last.then_inc(s["logits"], 1)
                first_half(pe, 0, 0)
                for u in range(RING):
                    if u == 1:
                        pe.wait_ge(s["exps"], TT)
                    first_half(pe, 0, u + 1) if u < RING - 1 else first_half(pe, 1, 0)
                    second_half(pe, 0, u)
                with pe.Fori(1, TURNS - 1) as i:
                    for u in range(RING):
                        first_half(pe, i, u + 1) if u < RING - 1 else first_half(pe, i + 1, 0)
                        second_half(pe, i, u)
                for u in range(RING):
                    if u < RING - 1:
                        first_half(pe, TURNS - 1, u + 1)
                    second_half(pe, TURNS - 1, u)
                pe.wait_ge(s["second_mm"], 2 * steps)
                for _ in range(2):
                    pe.nop().then_inc(e.w_used, 1)

            @block.scalar
            def _(act):
                ln_scalar(act, e, s)
                act.wait_ge(s["ltop"], 1)
                for t in range(TT):
                    act.activation(prob[:, t, 0:n_experts], ps[:, 7, t * 64:t * 64 + n_experts], ACT.Exp,
                                   bias=nmax[:, t:t + 1], accum_out=total[:, t:t + 1]).then_inc(s["exps"], 1)
                for u in range(RING):
                    activate(act, 0, u)
                with act.Fori(1, TURNS) as i:
                    for u in range(RING):
                        activate(act, i, u)

            @block.vector
            def _(dve):
                me = Chain(dve, s["dve_self"])
                me.did(dve.memset(prob[:, :, :], -1.0))
                ln_vector(dve, e, s)
                dve.wait_ge(s["logits"], 1)
                lg = ps[:, 7, 0:TT * 64].rearrange("p (t x) -> p t x", t=TT)[:, :, 0:n_experts]
                me.did(dve.tensor_reduce(nmax[:, :], lg, AX_X, ALU.max))
                me.wait()
                dve.tensor_scalar(nmax[:, :], nmax[:, :], -1.0, None, ALU.mult).then_inc(s["ltop"], 1)
                dve.wait_ge(s["exps"], TT)
                me.did(dve.reciprocal(total[:, :], total[:, :]))
                me.wait()
                for t in range(TT):
                    me.did(dve.tensor_scalar(prob[:, t, 0:n_experts], prob[:, t, 0:n_experts], total[:, t:t + 1],
                                             None, ALU.mult))
                me.wait()
                for t in range(TT):
                    me.did(dve.max(top[:, t, :], prob[:, t, :]))
                me.wait()
                if top_k < 8:
                    me.did(dve.tensor_reduce(total[:, :], top[:, :, 0:top_k], AX_X, ALU.add))
                    me.did(dve.memset(top[:, :, top_k:8], -1.0))
                    me.wait()
                    me.did(dve.reciprocal(total[:, :], total[:, :]))
                    me.wait()
                for t in range(TT):
                    me.did(dve.match_replace(left[:, t, :], top[:, t, :], prob[:, t, :], 0.0))
                me.wait()
                me.did(dve.tensor_tensor(comb[:, :, :], prob[:, :, 0:n_experts], left[:, :, 0:n_experts],
                                         ALU.subtract))
                me.wait()
                if top_k < 8:
                    for t in range(TT):
                        me.did(dve.tensor_scalar(comb[:, t, :], comb[:, t, :], total[:, t:t + 1], None, ALU.mult))
                    me.wait()
                multiply(dve, 0, 0)
                for u in range(RING):
                    multiply(dve, 0, u + 1) if u < RING - 1 else multiply(dve, 1, 0)
                    add(dve, 0, u)
                with dve.Fori(1, TURNS - 1) as i:
                    for u in range(RING):
                        multiply(dve, i, u + 1) if u < RING - 1 else multiply(dve, i + 1, 0)
                        add(dve, i, u)
                for u in range(RING):
                    if u < RING - 1:
                        multiply(dve, TURNS - 1, u + 1)
                    add(dve, TURNS - 1, u)
        clear_sems(nc, s)
    e.n0 += steps


def layer_l0f(e):
    layer_moe(e, "l0f", 64, 1, 8, S_F0)


def layer_l1f(e):
    layer_moe(e, "l1f", 8, 4, 2, S_F1)



def softplus_vector(dve, me, x, a, y, z, s, out):
    dve.scalar_tensor_tensor(out=a, in0=x, scalar=-1.0, in1=x, op0=ALU.mult, op1=ALU.max).then_inc(s["sp_abs"], 1)
    dve.wait_ge(s["sp_abs"], 1)
    me.did(dve.tensor_scalar(x, x, 0.0, None, ALU.max))
    dve.wait_ge(s["sp_exp"], 1)
    me.did(dve.tensor_scalar(a, y, 2.0, None, ALU.add))
    me.wait()
    me.did(dve.reciprocal(a, a))
    me.wait()
    me.did(dve.tensor_tensor(z, y, a, ALU.mult))
    me.wait()
    me.did(dve.tensor_tensor(y, z, z, ALU.mult))
    me.wait()
    me.did(dve.tensor_scalar(a, y, 1.0 / 15.0, None, ALU.mult))
    for n in range(6, 0, -1):
        me.wait()
        me.did(dve.scalar_tensor_tensor(out=a, in0=a, scalar=1.0 / (2 * n + 1), in1=y, op0=ALU.add, op1=ALU.mult))
    me.wait()
    me.did(dve.scalar_tensor_tensor(out=a, in0=a, scalar=1.0, in1=z, op0=ALU.add, op1=ALU.mult))
    me.wait()
    dve.scalar_tensor_tensor(out=out, in0=a, scalar=2.0, in1=x, op0=ALU.mult, op1=ALU.add)\
        .then_inc(s["sp_done"], 1)


def softplus_scalar(act, a, y, s):
    act.wait_ge(s["sp_abs"], 1)
    act.activation(y, a, ACT.Exp, scale=-1.0).then_inc(s["sp_exp"], 1)



def layer_l0a(e):
    nc, ps = e.nc, e.ps
    n0 = e.n0
    NH, NJ = 8, 2
    STEPS = NJ * TOK
    NC = STEPS // P
    CTOK = P // NJ
    CONV_TILES, TILES = 40, 48
    LEVELS = 7
    with ExitStack() as ctx:
        def sb(name, shape):
            return ctx.enter_context(nc.sbuf_tensor("l0a_" + name, shape, F32))
        s = layer_sems(nc, ctx, "l0a", LN_SEMS + [
            "dve_self", "act_self", "pool_self", "rows_mm", "tile_mm", "tile_ev", "pads", "conv", "silu", "sp_abs",
            "sp_exp", "sp_done", "decay", "beta", "rows", "cols_mm", "cols", "eb_mm", "scan", "kt_mm", "kt_sb",
            "vt_mm", "vt_sb", "qt_mm", "qt_sb", "norms", "normed", "kn_mm", "kn_d", "kn_a", "kb", "kb_mm", "kb_d",
            "kb_a", "qn_mm", "qn_sb", "qc", "qc_mm", "qc_sb", "g_mm", "g_sb", "p_mm", "p_sb", "kd", "ct", "y_mm",
            "y_sb", "pp_mm", "x_up", "xt_up", "ks_mm", "r_sb", "u_mm", "u_sb", "ds_mm", "sc", "s_new", "o_mm", "o_sb",
            "sq", "ss_mm", "rms", "rinv", "rb_mm", "gated", "y", "out_mm"])
        big = [sb(f"big{i}", [P, 4096]) for i in range(6)]
        mid = [sb(f"mid{i}", [P, 2048]) for i in range(4)]
        cols = sb("cols", [P, 128])
        junk = sb("junk", [P, P])

        def hs(buf):
            return buf[:, 0:4096].rearrange("p (h r) -> p h r", h=NH)

        def hc(buf):
            return buf[:, 0:4096].rearrange("p (h c d) -> p h c d", h=NH, c=NC)
        kraw, keyT = hs(big[0]), hs(big[0])
        vraw, kb, AT = hs(big[1]), hc(big[1]), hc(big[1])
        ktm = hc(big[2])
        bV = hc(big[3])
        KbT, XT = hs(big[4]), hc(big[4])
        DT, X = hs(big[5]), hc(big[5])
        qraw = mid[0][:, :].rearrange("p (h t) -> p h t", h=NH)
        QT = qraw
        qtm = mid[1][:, :].rearrange("p (h t d) -> p h t d", h=NH, t=TT)
        PT = mid[1][:, :].rearrange("p (h c t) -> p h c t", h=NH, c=NC)
        QcT = mid[2][:, :].rearrange("p (h t) -> p h t", h=NH)
        gate = mid[3][:, :].rearrange("p (h t) -> p h t", h=NH)
        OT = e.xnbuf[:, :].rearrange("p (h t) -> p h t", h=NH)
        pad = big[3][:, 0:2 * 259].rearrange("p (b n) -> p b n", b=2)
        conv = big[3][:, 1024:1536].rearrange("p (b n) -> p b n", b=2)
        rows = big[4][0:8, :]
        r_x, r_a, r_y, r_z = (rows[:, i * TOK:(i + 1) * TOK] for i in range(4))
        r_e, r_e0, r_c, r_b = (rows[:, 1024 + i * STEPS:1024 + (i + 1) * STEPS] for i in range(4))
        r_0 = rows[:, 3072:3072 + P]
        r_negA = rows[:, 3200:3201]
        CTm = mid[0][:, 0:1024].rearrange("p (b c n) -> p b c n", b=2, c=NC)
        Y = mid[0][:, 1024:2048].rearrange("p (b c n) -> p b c n", b=2, c=NC)
        R = big[1][:, 0:1024].rearrange("p (h d) -> p h d", h=NH)
        U = big[1][:, 1024:2048].rearrange("p (h d) -> p h d", h=NH)
        S = big[1][:, 2048:4096].rearrange("p (b h d) -> p b h d", b=2, h=NH)
        sq = big[3][:, 0:2048].rearrange("p (h t) -> p h t", h=NH)
        yT = big[3][:, 2048:4096].rearrange("p (h t) -> p h t", h=NH)
        beta = cols[:, 0:32].rearrange("p (c h) -> p c h", h=NH)
        cum = cols[:, 32:64].rearrange("p (c h) -> p c h", h=NH)
        ctok = cols[:, 64:80].rearrange("p (t h) -> p t h", h=NH)
        cend = cols[:, 80:112].rearrange("p (h c) -> p h c", h=NH)
        nbc = sb("nbc", [P, NC, NH])
        knorm = sb("knorm", [P, NH, NC])
        qnorm = sb("qnorm", [P, NH, TT])
        dend = sb("dend", [P, NH, NC])
        srow = sb("srow", [8, 2 * TOK])
        ident, ident4, small = e.ident, e.ident4, e.small

        def taps(i, j):
            return small[:, S_ACONV + 4 * i + j:S_ACONV + 4 * i + j + 1]

        def conv_out(i):
            if i < 8:
                return qraw[:, i, :]
            raw, i = (kraw, i - 8) if i < 24 else (vraw, i - 24)
            return raw[:, i % NH, :].rearrange("p (t j) -> p j t", j=NJ)[:, i // NH, :]

        with nc.Block(no_gpsimd_drain=True) as block:
            @block.sync
            def _(sp):
                stream(sp, e, n0, N_L0A)

            @block.tensor
            def _(pe):
                ln_tensor(pe, e, s)
                for j in range(3):
                    for k in range(KT):
                        last = pe.matmul(ps[0:8, min(4 + j, 5), (j // 2) * TOK:(j // 2 + 1) * TOK],
                                         small[:, S_AAB + 24 * k + 8 * j:S_AAB + 24 * k + 8 * j + 8],
                                         e.xnT[:, k, :], start=(k == 0), stop=(k == KT - 1))
                last.then_inc(s["rows_mm"], 1)
                for i in range(TILES):
                    w = slot_in(pe, e, n0 + i // 6)
                    if i >= 4:
                        pe.wait_ge(s["tile_ev"], i - 3)
                    for k in range(KT):
                        last = pe.matmul(ps[:, i % 4, 0:TOK], w[:, k * 768 + (i % 6) * P:k * 768 + (i % 6 + 1) * P],
                                         e.xnT[:, k, :], start=(k == 0), stop=(k == KT - 1))
                        if k == 0 and i and i % 6 == 0:
                            last.then_inc(e.w_used, 1)
                    last.then_inc(s["tile_mm"], 1)
                pe.wait_ge(s["silu"], TILES)
                pe.nop().then_inc(e.w_used, 1)
                pe.wait_ge(s["rows"], 2)
                for c in range(NC):
                    pe.transpose(ps[:, 5, 8 * c:8 * c + 8], r_b[:, c * P:(c + 1) * P], ident[0:8, 0:8])
                    pe.transpose(ps[:, 5, 32 + 8 * c:40 + 8 * c], r_c[:, c * P:(c + 1) * P], ident[0:8, 0:8])
                for t in range(TT):
                    at = t * NJ * P
                    pe.transpose(ps[:, 5, 64 + 8 * t:72 + 8 * t], r_c[:, at + 1:at + NJ * P:NJ], ident[0:8, 0:8])
                for h in range(NH):
                    last = pe.matmul(ps[:, 5, 80 + 4 * h:84 + 4 * h], ident[0:8, h:h + 1].broadcast_to((8, P)),
                                     r_c[:, P - 1:STEPS:P], start=True, stop=True)
                last.then_inc(s["cols_mm"], 1)
                for h in range(NH):
                    if h >= 2:
                        pe.wait_ge(s["scan"], h - 1)
                    pe.matmul(ps[:, 6 + h % 2, :], ident[0:8, h:h + 1].broadcast_to((8, P)), r_e0,
                              start=True, stop=True).then_inc(s["eb_mm"], 1)
                for h in range(NH):
                    if h >= 2:
                        pe.wait_ge(s["kt_sb"], h - 1)
                    for c in range(NC):
                        last = pe.transpose(ps[:, h % 2, c * P:(c + 1) * P], kraw[:, h, c * P:(c + 1) * P], ident)
                    last.then_inc(s["kt_mm"], 1)
                    if h % 2 == 0:
                        if h >= 4:
                            pe.wait_ge(s["qt_sb"], h // 2 - 1)
                        for x in range(2):
                            for t in range(TT):
                                last = pe.transpose(ps[:, 2 + h // 2 % 2, (2 * x + t) * P:(2 * x + t + 1) * P],
                                                    qraw[:, h + x, t * P:(t + 1) * P], ident)
                        last.then_inc(s["qt_mm"], 1)
                    if h == 0:
                        pe.wait_ge(s["cols"], 1)
                    if h >= 2:
                        pe.wait_ge(s["vt_sb"], h - 1)
                    for c in range(NC):
                        last = pe.transpose(ps[:, 4 + h % 2, c * P:(c + 1) * P], vraw[:, h, c * P:(c + 1) * P],
                                            ident)
                    last.then_inc(s["vt_mm"], 1)
                pe.wait_ge(s["normed"], 1)
                for h in range(NH):
                    if h >= 2:
                        pe.wait_ge(s["kn_a" if h % 2 else "kn_d"], h // 2)
                    for c in range(NC):
                        last = pe.transpose(ps[:, h % 2, c * P:(c + 1) * P], ktm[:, h, c, :], ident)
                    last.then_inc(s["kn_mm"], 1)
                pe.wait_ge(s["normed"], 2)
                for h in range(0, NH, 2):
                    if h >= 4:
                        pe.wait_ge(s["qn_sb"], h // 2 - 1)
                    for x in range(2):
                        for t in range(TT):
                            last = pe.transpose(ps[:, 2 + h // 2 % 2, (2 * x + t) * P:(2 * x + t + 1) * P],
                                                qtm[:, h + x, t, :], ident)
                    last.then_inc(s["qn_mm"], 1)
                pe.wait_ge(s["kb"], 1)
                for h in range(NH):
                    if h >= 2:
                        pe.wait_ge(s["kb_a" if h % 2 else "kb_d"], h // 2)
                    for c in range(NC):
                        last = pe.transpose(ps[:, 4 + h % 2, c * P:(c + 1) * P], kb[:, h, c, :], ident)
                    last.then_inc(s["kb_mm"], 1)
                pe.wait_ge(s["qc"], 1)
                pe.wait_ge(s["kn_a"], 4)
                pe.wait_ge(s["kn_d"], 4)
                for h in range(0, NH, 2):
                    if h >= 4:
                        pe.wait_ge(s["qc_sb"], h // 2 - 1)
                    for x in range(2):
                        for t in range(TT):
                            last = pe.transpose(ps[:, h // 2 % 2, (2 * x + t) * P:(2 * x + t + 1) * P],
                                                qtm[:, h + x, t, :], ident)
                    last.then_inc(s["qc_mm"], 1)
                pe.wait_ge(s["qn_sb"], 4)
                pe.wait_ge(s["kb_a"], 4)
                pe.wait_ge(s["kb_d"], 4)
                for h in range(NH):
                    if h >= 2:
                        pe.wait_ge(s["g_sb"], h - 1)
                    for c in range(NC):
                        at = slice(c * P, (c + 1) * P)
                        last = pe.matmul(ps[:, 2 + h % 2, at], keyT[:, h, at], KbT[:, h, at], start=True, stop=True)
                    last.then_inc(s["g_mm"], 1)
                    if h % 2:
                        if h >= 5:
                            pe.wait_ge(s["p_sb"], h // 2 - 1)
                        for x in range(2):
                            for c in range(NC):
                                last = pe.matmul(ps[:, 6 + h // 2 % 2, (x * NC + c) * CTOK:(x * NC + c + 1) * CTOK],
                                                 keyT[:, h - 1 + x, c * P:(c + 1) * P],
                                                 QT[:, h - 1 + x, c * CTOK:(c + 1) * CTOK], start=True, stop=True)
                        last.then_inc(s["p_mm"], 1)
                pe.wait_ge(s["g_sb"], NH)
                pe.wait_ge(s["qc_sb"], 4)

                def level_y(n):
                    l, h = divmod(n, NH)
                    pe.wait_ge(s["ct"], n + 1)
                    if l:
                        pe.wait_ge(s["x_up"], n - NH + 1)
                    if n >= 2:
                        pe.wait_ge(s["x_up" if n - 2 < NH else "y_sb"], n - 1 if n - 2 < NH else n - 1 - NH)
                    for c in range(NC):
                        last = pe.matmul(ps[:, n % 2, c * P:(c + 1) * P], CTm[:, n % 2, c, :],
                                         X[:, h, c, :] if l else ident, start=True, stop=True)
                    last.then_inc(s["y_mm"], 1)

                def level_xy(n):
                    l, h = divmod(n, NH)
                    if not l:
                        return
                    pe.wait_ge(s["y_sb"], n - NH + 1)
                    pe.wait_ge(s["xt_up"], n - NH + 1)
                    if n - NH >= 2:
                        pe.wait_ge(s["xt_up"], n - 1)
                        pe.wait_ge(s["x_up"], min(n - 1, NH * (LEVELS - 1)))
                    for c in range(NC):
                        at = slice(c * P, (c + 1) * P)
                        if l < LEVELS - 1:
                            pe.matmul(ps[:, 2 + n % 2, at], XT[:, h, c, :], Y[:, n % 2, c, :], start=True, stop=True)
                        last = pe.matmul(ps[:, 4 + n % 2, at], Y[:, n % 2, c, :], XT[:, h, c, :],
                                         start=True, stop=True)
                    last.then_inc(s["pp_mm"], 1)

                for n in range(NH * LEVELS + 2):
                    if n < NH * LEVELS:
                        level_y(n)
                    if n >= 2:
                        level_xy(n - 2)
                pe.wait_ge(s["xt_up"], NH * LEVELS)
                pe.wait_ge(s["kd"], 1)

                for c in range(NC):
                    at = slice(c * P, (c + 1) * P)
                    for x in range(2):
                        if c:
                            pe.wait_ge(s["s_new"], 2 * (c - 1) + x + 1)
                            for h in range(4 * x, 4 * x + 4):
                                last = pe.matmul(ps[:, x, (h % 4) * P:(h % 4 + 1) * P], keyT[:, h, at],
                                                 S[:, c % 2, h, :], start=True, stop=True)
                            last.then_inc(s["ks_mm"], 1)
                    for x in range(2):
                        pe.wait_ge(s["r_sb"], 2 * c + x + 1)
                        for h in range(4 * x, 4 * x + 4):
                            last = pe.matmul(ps[:, 2 + x, (h % 4) * P:(h % 4 + 1) * P], XT[:, h, c, :], R[:, h, :],
                                             start=True, stop=True)
                        last.then_inc(s["u_mm"], 1)
                    for x in range(2):
                        pe.wait_ge(s["u_sb"], 2 * c + x + 1)
                        if c < NC - 1:
                            for h in range(4 * x, 4 * x + 4):
                                last = pe.matmul(ps[:, 4 + x, (h % 4) * P:(h % 4 + 1) * P], ktm[:, h, c, :],
                                                 U[:, h, :], start=True, stop=True)
                            last.then_inc(s["ds_mm"], 1)
                    if c >= 2:
                        pe.wait_ge(s["o_sb"], c - 1)
                    for h in range(NH):
                        o = ps[:, 6 + c % 2, h * CTOK:(h + 1) * CTOK]
                        if c:
                            pe.matmul(o, S[:, c % 2, h, :], QcT[:, h, c * CTOK:(c + 1) * CTOK],
                                      start=True, stop=False)
                        last = pe.matmul(o, U[:, h, :], PT[:, h, c, :], start=(c == 0), stop=True)
                    last.then_inc(s["o_mm"], 1)
                pe.wait_ge(s["sq"], 1)
                for h in range(NH):
                    last = pe.matmul(ps[0:8, 0, 0:TOK], e.fixed[:, C_PICK + 8 * h:C_PICK + 8 * h + 8], sq[:, h, :],
                                     start=(h == 0), stop=(h == NH - 1))
                last.then_inc(s["ss_mm"], 1)
                pe.wait_ge(s["rinv"], 1)
                for h in range(NH):
                    last = pe.matmul(ps[:, 2 + h // 2, (h % 2) * TOK:(h % 2 + 1) * TOK],
                                     ident[0:8, h:h + 1].broadcast_to((8, P)), srow[:, TOK:2 * TOK],
                                     start=True, stop=True)
                last.then_inc(s["rb_mm"], 1)
                pe.wait_ge(s["y"], 1)
                for t in range(TT):
                    for h in range(NH):
                        w = slot_in(pe, e, n0 + 8 + h // 4)
                        last = pe.matmul(ps[:, 6 + t, :], yT[:, h, t * P:(t + 1) * P],
                                         w[:, (h % 4) * D:(h % 4 + 1) * D], start=(h == 0), stop=(h == NH - 1))
                    last.then_inc(s["out_mm"], 1)
                pe.wait_ge(s["out_mm"], TT)
                for _ in range(2):
                    pe.nop().then_inc(e.w_used, 1)

            @block.scalar
            def _(act):
                me = Chain(act, s["act_self"])
                ln_scalar(act, e, s)

                def silu(i):
                    act.wait_ge(s["conv"], i + 1)
                    act.activation(conv_out(i), conv[:, i % 2, :], ACT.Silu).then_inc(s["silu"], 1)

                act.wait_ge(s["pads"], 1)
                for i in range(CONV_TILES):
                    act.wait_ge(s["tile_mm"], i + 1)
                    if i >= 2:
                        act.wait_ge(s["conv"], i - 1)
                    act.activation(pad[:, i % 2, 3:3 + TOK], ps[:, i % 4, 0:TOK], ACT.Copy).then_inc(s["tile_ev"], 1)
                    if i:
                        silu(i - 1)
                silu(CONV_TILES - 1)
                for i in range(CONV_TILES, TILES):
                    act.wait_ge(s["tile_mm"], i + 1)
                    act.wait_ge(s["silu"], i)
                    act.activation(gate[:, i - CONV_TILES, :], ps[:, i % 4, 0:TOK], ACT.Silu).then_inc(s["silu"], 1)
                    if i < TILES - 4:
                        act.wait_ge(s["silu"], i + 1)
                        act.nop().then_inc(s["tile_ev"], 1)
                act.wait_ge(s["rows_mm"], 1)
                rb = r_b.rearrange("p (t j) -> p j t", j=NJ)
                act.activation(rb[:, 0, :], ps[0:8, 5, 0:TOK], ACT.Sigmoid).then_inc(s["beta"], 1)
                act.activation(rb[:, 1, :], ps[0:8, 5, TOK:2 * TOK], ACT.Sigmoid).then_inc(s["beta"], 1)
                me.did(act.activation(r_negA, small[0:8, S_AHEAD:S_AHEAD + 1], ACT.Exp))
                me.wait()
                me.did(act.activation(r_negA, r_negA, ACT.Copy, scale=-1.0))
                softplus_scalar(act, r_a, r_y, s)
                act.wait_ge(s["sp_done"], 1)
                me.wait()
                act.activation(r_e.rearrange("p (t j) -> p j t", j=NJ)[:, 0, :], r_z, ACT.Exp, scale=r_negA)\
                    .then_inc(s["decay"], 1)
                act.wait_ge(s["cols_mm"], 1)
                act.activation(cols[:, 0:112], ps[:, 5, 0:112], ACT.Copy).then_inc(s["cols"], 1)
                for h in range(NH):
                    act.wait_ge(s["kt_mm"], h + 1)
                    for c in range(NC):
                        if me.n > 2:
                            me.wait()
                        me.did(act.activation(junk[:, :], ps[:, h % 2, c * P:(c + 1) * P], ACT.Square,
                                              accum_out=knorm[:, h, c:c + 1]))
                    act.activation(ktm[:, h, :, :].rearrange("p c d -> p (c d)"), ps[:, h % 2, :], ACT.Copy)\
                        .then_inc(s["kt_sb"], 1)
                    if h % 2 == 0:
                        act.wait_ge(s["qt_mm"], h // 2 + 1)
                        for x in range(2):
                            for t in range(TT):
                                me.wait()
                                me.did(act.activation(junk[:, :],
                                                      ps[:, 2 + h // 2 % 2, (2 * x + t) * P:(2 * x + t + 1) * P],
                                                      ACT.Square, accum_out=qnorm[:, h + x, t:t + 1]))
                        act.activation(qtm[:, h:h + 2, :, :].rearrange("p h t d -> p (h t d)"),
                                       ps[:, 2 + h // 2 % 2, :], ACT.Copy).then_inc(s["qt_sb"], 1)
                me.wait()
                act.activation(knorm[:, :, :], knorm[:, :, :], ACT.Sqrt).then_inc(s["norms"], 1)
                act.activation(qnorm[:, :, :], qnorm[:, :, :], ACT.Sqrt).then_inc(s["norms"], 1)
                for h in range(1, NH, 2):
                    act.wait_ge(s["kn_mm"], h + 1)
                    act.activation(keyT[:, h, :], ps[:, 1, :], ACT.Copy).then_inc(s["kn_a"], 1)
                for j in range(4):
                    act.wait_ge(s["qn_mm"], j + 1)
                    act.activation(QT[:, 2 * j:2 * j + 2, :].rearrange("p h t -> p (h t)"), ps[:, 2 + j % 2, :],
                                   ACT.Copy).then_inc(s["qn_sb"], 1)
                act.wait_ge(s["scan"], NH)
                for h in range(1, NH, 2):
                    act.wait_ge(s["kb_mm"], h + 1)
                    act.activation(KbT[:, h, :], ps[:, 5, :], ACT.Copy).then_inc(s["kb_a"], 1)
                for j in range(4):
                    act.wait_ge(s["qc_mm"], j + 1)
                    act.activation(QcT[:, 2 * j:2 * j + 2, :].rearrange("p h t -> p (h t)"), ps[:, j % 2, :],
                                   ACT.Copy).then_inc(s["qc_sb"], 1)
                for n in range(NH, NH * LEVELS):
                    act.wait_ge(s["y_mm"], n + 1)
                    if n == NH:
                        act.wait_ge(s["p_mm"], 4)
                    if n - NH >= 2:
                        act.wait_ge(s["pp_mm"], n - NH - 1)
                    act.activation(Y[:, n % 2, :, :].rearrange("p c d -> p (c d)"), ps[:, n % 2, :], ACT.Copy)\
                        .then_inc(s["y_sb"], 1)
                for c in range(NC):
                    for x in range(2):
                        act.wait_ge(s["u_mm"], 2 * c + x + 1)
                        if c:
                            act.wait_ge(s["o_mm"], c)
                        act.activation(U[:, 4 * x:4 * x + 4, :].rearrange("p h d -> p (h d)"), ps[:, 2 + x, :],
                                       ACT.Copy).then_inc(s["u_sb"], 1)
                    act.wait_ge(s["o_mm"], c + 1)
                    act.activation(OT[:, :, c * CTOK:(c + 1) * CTOK],
                                   ps[:, 6 + c % 2, :].rearrange("p (h t) -> p h t", h=NH), ACT.Copy)\
                        .then_inc(s["o_sb"], 1)
                act.wait_ge(s["o_sb"], NC)
                act.wait_ge(s["r_sb"], 2 * NC)
                act.activation(sq[:, :, :], OT[:, :, :], ACT.Square).then_inc(s["sq"], 1)
                act.wait_ge(s["ss_mm"], 1)
                act.activation(srow[:, 0:TOK], ps[0:8, 0, 0:TOK], ACT.Sqrt, bias=e.eps[0:8, :], scale=1.0 / P)\
                    .then_inc(s["rms"], 1)

            @block.gpsimd
            def _(pool):
                pool.wait_ge(s["normed"], 1)
                pool.wait_ge(s["vt_mm"], NH)
                for c in range(NC):
                    last = pool.tensor_tensor(kb[:, :, c, :], ktm[:, :, c, :], bcast_last(beta[:, c, :], (P, NH, P)),
                                              ALU.mult)
                    last.then_inc(s["pool_self"], 1)
                pool.wait_ge(s["pool_self"], NC)
                pool.nop().then_inc(s["kb"], 1)
                pool.wait_ge(s["qn_mm"], 4)
                for t in range(TT):
                    pool.tensor_tensor(qtm[:, :, t, :], qtm[:, :, t, :], bcast_last(ctok[:, t, :], (P, NH, P)),
                                       ALU.mult).then_inc(s["pool_self"], 1)
                pool.wait_ge(s["pool_self"], NC + TT)
                pool.nop().then_inc(s["qc"], 1)
                for n in range(NH * LEVELS):
                    l, h = divmod(n, NH)
                    pool.wait_ge(s["g_sb"], h + 1)
                    if n == 0:
                        pool.wait_ge(s["p_mm"], 4)
                    if n >= 2:
                        pool.wait_ge(s["y_mm"], n - 1)
                        if n - 2 < NH:
                            pool.wait_ge(s["xt_up"], n - 1)
                    level = e.fixed[:, C_LEVEL + l * P:C_LEVEL + (l + 1) * P]
                    pool.tensor_tensor(CTm[:, n % 2, :, :], AT[:, h, :, :],
                                       level.unsqueeze(1).broadcast_to((P, NC, P)), ALU.mult).then_inc(s["ct"], 1)
                for c in range(1, NC - 1):
                    for x in range(2):
                        pool.wait_ge(s["s_new"], 2 * (c - 1) + x + 1)
                        if c >= 2:
                            pool.wait_ge(s["o_mm"], c)
                        hh = slice(4 * x, 4 * x + 4)
                        pool.tensor_tensor(S[:, (c + 1) % 2, hh, :], S[:, c % 2, hh, :],
                                           bcast_last(cend[:, hh, c], (P, 4, P)), ALU.mult).then_inc(s["sc"], 1)

            @block.vector
            def _(dve):
                me = Chain(dve, s["dve_self"])
                ln_vector(dve, e, s)
                dve.memset(pad[:, :, :], 0.0).then_inc(s["pads"], 1)
                for i in range(CONV_TILES):
                    dve.wait_ge(s["tile_ev"], i + 1)
                    if i >= 2:
                        dve.wait_ge(s["silu"], i - 1)
                    x, y = pad[:, i % 2, :], conv[:, i % 2, :]
                    me.did(dve.tensor_scalar(y, x[:, 0:TOK], taps(i, 0), None, ALU.mult))
                    for j in range(1, 4):
                        me.wait()
                        last = dve.scalar_tensor_tensor(out=y, in0=x[:, j:j + TOK], scalar=taps(i, j), in1=y,
                                                        op0=ALU.mult, op1=ALU.add)
                        if j < 3:
                            me.did(last)
                    last.then_inc(s["conv"], 1)
                dve.wait_ge(s["rows_mm"], 1)
                me.did(dve.memset(r_e, 1.0))
                me.did(dve.memset(r_0, 0.0))
                me.did(dve.tensor_scalar(r_x, ps[0:8, 4, 0:TOK], small[0:8, S_AHEAD + 1:S_AHEAD + 2], None, ALU.add))
                me.wait()
                softplus_vector(dve, me, r_x, r_a, r_y, r_z, s, r_z)
                dve.wait_ge(s["beta"], 2)
                dve.tensor_scalar(r_b, r_b, 2.0, None, ALU.mult).then_inc(s["rows"], 1)
                dve.wait_ge(s["decay"], 1)
                me.did(dve.tensor_copy(r_e0, r_e))
                me.wait()
                me.did(dve.memset(r_e0[:, 0:STEPS:P], 0.0))
                for c in range(NC):
                    at = slice(c * P, (c + 1) * P)
                    me.did(dve.tensor_tensor_scan(r_c[:, at], r_e[:, at], r_0, 1.0, ALU.mult, ALU.add))
                me.wait()
                dve.nop().then_inc(s["rows"], 1)
                for h in range(NH):
                    dve.wait_ge(s["eb_mm"], h + 1)
                    dve.tensor_tensor_scan(DT[:, h, :], ps[:, 6 + h % 2, :], ident4, 0.0, ALU.mult, ALU.add)\
                        .then_inc(s["scan"], 1)
                dve.wait_ge(s["cols"], 1)
                me.did(dve.scalar_tensor_tensor(out=nbc[:, :, :], in0=beta, scalar=-1.0, in1=cum, op0=ALU.mult,
                                                op1=ALU.mult))
                dve.wait_ge(s["scan"], NH)
                me.did(dve.tensor_copy(dend[:, :, :], DT[:, :, P - 1:STEPS:P]))
                for h in range(NH):
                    dve.wait_ge(s["vt_mm"], h + 1)
                    dve.tensor_tensor(bV[:, h, :, :], ps[:, 4 + h % 2, :].rearrange("p (c d) -> p c d", c=NC),
                                      bcast_last(beta[:, :, h], (P, NC, P)), ALU.mult).then_inc(s["vt_sb"], 1)
                dve.wait_ge(s["norms"], 2)
                for v, f in ((knorm, 1.0), (qnorm, 1.0 / float(np.sqrt(P)))):
                    me.did(dve.tensor_scalar(v[:, :, :], v[:, :, :], 1e-12, None, ALU.max))
                    me.wait()
                    me.did(dve.reciprocal(v[:, :, :], v[:, :, :]))
                    me.wait()
                    if f != 1.0:
                        me.did(dve.tensor_scalar(v[:, :, :], v[:, :, :], f, None, ALU.mult))
                        me.wait()
                dve.wait_ge(s["kt_sb"], NH)
                dve.tensor_tensor(ktm[:, :, :, :].rearrange("p h c d -> p (h c) d"),
                                  ktm[:, :, :, :].rearrange("p h c d -> p (h c) d"),
                                  bcast_last(knorm[:, :, :].rearrange("p h c -> p (h c)"), (P, NH * NC, P)),
                                  ALU.mult).then_inc(s["normed"], 1)
                dve.wait_ge(s["qt_sb"], 4)
                dve.tensor_tensor(qtm[:, :, :, :].rearrange("p h c d -> p (h c) d"),
                                  qtm[:, :, :, :].rearrange("p h c d -> p (h c) d"),
                                  bcast_last(qnorm[:, :, :].rearrange("p h c -> p (h c)"), (P, NH * TT, P)),
                                  ALU.mult).then_inc(s["normed"], 1)
                for h in range(0, NH, 2):
                    dve.wait_ge(s["kn_mm"], h + 1)
                    dve.tensor_copy(keyT[:, h, :], ps[:, 0, :]).then_inc(s["kn_d"], 1)
                for h in range(0, NH, 2):
                    dve.wait_ge(s["kb_mm"], h + 1)
                    dve.tensor_copy(KbT[:, h, :], ps[:, 4, :]).then_inc(s["kb_d"], 1)
                dve.wait_ge(s["kn_mm"], NH)
                dve.wait_ge(s["kb"], 1)
                me.wait()
                dve.wait_ge(s["normed"], 1)
                dve.tensor_tensor(ktm[:, :, :, :].rearrange("p h c d -> p (h c) d"),
                                  ktm[:, :, :, :].rearrange("p h c d -> p (h c) d"),
                                  bcast_last(dend[:, :, :].rearrange("p h c -> p (h c)"), (P, NH * NC, P)),
                                  ALU.mult).then_inc(s["kd"], 1)
                for h in range(NH):
                    dve.wait_ge(s["g_mm"], h + 1)
                    if h == 0:
                        dve.wait_ge(s["kb_mm"], NH)
                    dve.tensor_tensor(AT[:, h, :, :].rearrange("p c d -> p (c d)"), ps[:, 2 + h % 2, :], DT[:, h, :],
                                      ALU.mult).then_inc(s["g_sb"], 1)
                    if h % 2:
                        dve.wait_ge(s["p_mm"], h // 2 + 1)
                        if h == 1:
                            dve.wait_ge(s["qc_mm"], 4)
                        dve.tensor_tensor(
                            PT[:, h - 1:h + 1, :, :].rearrange("p h c t -> p (h c) t"),
                            ps[:, 6 + h // 2 % 2, :].rearrange("p (a t) -> p a t", t=CTOK),
                            DT[:, h - 1:h + 1, :].rearrange("p h (c t j) -> p (h c) t j", c=NC, j=NJ)[:, :, :, 1],
                            ALU.mult).then_inc(s["p_sb"], 1)
                dve.wait_ge(s["g_sb"], NH)
                dve.wait_ge(s["p_sb"], 4)
                for n in range(NH * LEVELS):
                    l, h = divmod(n, NH)
                    x, xt = (v[:, h, :, :].rearrange("p c d -> p (c d)") for v in (X, XT))
                    if l == 0:
                        dve.wait_ge(s["y_mm"], n + 1)
                        dve.tensor_tensor(x, ident4, ps[:, n % 2, :], ALU.subtract).then_inc(s["x_up"], 1)
                        dve.wait_ge(s["g_mm"], NH)
                        dve.tensor_tensor(xt, ident4, CTm[:, n % 2, :, :].rearrange("p c d -> p (c d)"),
                                          ALU.subtract).then_inc(s["xt_up"], 1)
                        continue
                    dve.wait_ge(s["pp_mm"], n - NH + 1)
                    dve.wait_ge(s["xt_up"], n - NH + 1)
                    if l < LEVELS - 1:
                        dve.wait_ge(s["x_up"], n - NH + 1)
                        dve.tensor_tensor(x, x, ps[:, 2 + n % 2, :], ALU.subtract).then_inc(s["x_up"], 1)
                    dve.tensor_tensor(xt, xt, ps[:, 4 + n % 2, :], ALU.subtract).then_inc(s["xt_up"], 1)
                dve.wait_ge(s["ct"], NH * LEVELS)
                for c in range(NC):
                    for x in range(2):
                        hh = slice(4 * x, 4 * x + 4)
                        if c == 0:
                            dve.tensor_copy(R[:, hh, :], bV[:, hh, c, :]).then_inc(s["r_sb"], 1)
                            continue
                        dve.wait_ge(s["ks_mm"], 2 * (c - 1) + x + 1)
                        dve.wait_ge(s["u_mm"], 2 * (c - 1) + x + 1)
                        me.did(dve.tensor_tensor(R[:, hh, :], ps[:, x, :].rearrange("p (h d) -> p h d", h=4),
                                                 bcast_last(nbc[:, c, hh], (P, 4, P)), ALU.mult))
                        me.wait()
                        dve.tensor_tensor(R[:, hh, :], R[:, hh, :], bV[:, hh, c, :], ALU.add).then_inc(s["r_sb"], 1)
                    if c == NC - 1:
                        continue
                    for x in range(2):
                        hh = slice(4 * x, 4 * x + 4)
                        dve.wait_ge(s["ds_mm"], 2 * c + x + 1)
                        new = S[:, (c + 1) % 2, hh, :]
                        add = ps[:, 4 + x, :].rearrange("p (h d) -> p h d", h=4)
                        if c == 0:
                            dve.tensor_copy(new, add).then_inc(s["s_new"], 1)
                            continue
                        dve.wait_ge(s["sc"], 2 * (c - 1) + x + 1)
                        dve.tensor_tensor(new, new, add, ALU.add).then_inc(s["s_new"], 1)
                dve.wait_ge(s["o_sb"], NC)
                dve.wait_ge(s["r_sb"], 2 * NC)
                dve.scalar_tensor_tensor(out=yT[:, :, :], in0=OT[:, :, :], scalar=small[:, S_ANORM:S_ANORM + 1],
                                         in1=gate[:, :, :], op0=ALU.mult, op1=ALU.mult).then_inc(s["gated"], 1)
                dve.wait_ge(s["rms"], 1)
                dve.reciprocal(srow[:, TOK:2 * TOK], srow[:, 0:TOK]).then_inc(s["rinv"], 1)
                dve.wait_ge(s["rb_mm"], 1)
                dve.wait_ge(s["gated"], 1)
                flat = yT[:, :, :].rearrange("p h t -> p (h t)")
                dve.tensor_tensor(flat, flat, ps[:, 2:6, :].rearrange("p a n -> p (a n)"), ALU.mult)\
                    .then_inc(s["y"], 1)
                for t in range(TT):
                    dve.wait_ge(s["out_mm"], t + 1)
                    me.did(dve.tensor_tensor(e.xres[:, t, :], e.xres[:, t, :], ps[:, 6 + t, :], ALU.add))
        clear_sems(nc, s)
    e.n0 += N_L0A



Q_BIG = 384
HALF = Q_BIG // 2
_c = np.arange(Q_BIG)
Q_TILES = [_c[0:128], _c[192:320], np.concatenate([_c[128:192], _c[320:384]])]
Q_TURNED = np.concatenate([_c[320:384], _c[128:192]])
L1X_WQ, L1X_WKC, L1X_WQR, L1X_WKR = 0, 512, 1024, 1216
L1X_HEAD = 1344


def open_rope(e, ctx):
    nc = e.nc

    def sb(name, shape):
        return ctx.enter_context(nc.sbuf_tensor("rope_" + name, shape, F32))
    e.rbuf = sb("buf", [P, 2 * CTX])
    e.kvr = sb("kvr", [P, CT, P])
    e.rope = {n: ctx.enter_context(nc.semaphore("rope_" + n)) for n in ("in", "cos", "sin", "done")}


def rope_sync(sp, e):
    sp.dma_start(e.rbuf[:, 0:4096], e.io["ctx"]).then_inc(e.rope["in"], 16)
    sp.dma_start(e.rbuf[:, 4096:8192], e.io["rope_k"]).then_inc(e.rope["in"], 16)


def rope_pool(pool, e):
    raw = e.rbuf[:, 0:4096].rearrange("p (t d) -> p t d", d=P)
    cos = e.rbuf[:, 4096:6144].rearrange("p (t f) -> p t f", f=64)
    sin = e.rbuf[:, 6144:8192].rearrange("p (t f) -> p t f", f=64)
    H = P // 2

    def pairs(ap):
        return ap.rearrange("p t (f two) -> p t f two", two=2)
    pool.wait_ge(e.rope["in"], 32)
    pool.tensor_tensor(pairs(e.kvr[:, :, :]), pairs(raw), bcast_last(cos, (P, CT, 64, 2)), ALU.mult)\
        .then_inc(e.rope["cos"], 1)
    pool.wait_ge(e.rope["cos"], 1)
    prod = e.rbuf[:, 4096:6144].rearrange("p (t f) -> p t f", f=H)
    pool.tensor_tensor(pairs(prod), pairs(raw[:, :, H:P]), bcast_last(sin[:, :, 0:32], (P, CT, 32, 2)), ALU.mult)\
        .then_inc(e.rope["sin"], 1)
    pool.wait_ge(e.rope["sin"], 1)
    pool.tensor_tensor(e.kvr[:, :, 0:H], e.kvr[:, :, 0:H], prod, ALU.add).then_inc(e.rope["done"], 1)
    pool.wait_ge(e.rope["done"], 1)
    pool.tensor_tensor(pairs(prod), pairs(raw[:, :, 0:H]), bcast_last(sin[:, :, 32:64], (P, CT, 32, 2)), ALU.mult)\
        .then_inc(e.rope["sin"], 1)
    pool.wait_ge(e.rope["sin"], 2)
    pool.tensor_tensor(e.kvr[:, :, H:P], e.kvr[:, :, H:P], prod, ALU.add).then_inc(e.rope["done"], 1)


def layer_l1x(e):
    nc, ps = e.nc, e.ps
    n0 = e.n0
    NH = 16
    KB = 4
    HT = CT // 2
    SUBS = 8
    PAIRS = NH // 2
    with ExitStack() as ctx:
        def sb(name, shape):
            return ctx.enter_context(nc.sbuf_tensor("l1x_" + name, shape, F32))
        s = layer_sems(nc, ctx, "l1x", LN_SEMS + [
            "dve_self", "tables", "kvT_mm", "kvT_a", "kvT_d", "q_mm", "q_sb", "big_mm", "big_d", "rotated", "qr_mm", "qr_sb",
            "q2_mm", "q2_sb", "cur", "score_mm", "top", "exp", "turn_mm", "turned_d", "turned_a", "ctx_mm",
            "taken", "rescale", "cT_mm", "cT_sb", "lat_mm", "lat_sb", "out_mm"])
        kvT = sb("kvT", [P, CTX])
        rope_q = sb("rope_q", [P, 2, 3, TOK])
        wlat = sb("wlat", [P, NH * P])
        q1 = sb("q1", [P, 2, TOK])
        rc = sb("rc", [P, 3, TOK])
        rs = sb("rs", [P, 2, 3, TOK])
        qr = sb("qr", [64, 2, TOK])
        q2T = sb("q2T", [P, NH, TOK])
        cur = sb("cur", [P, 2, TOK])
        cn = sb("cn", [P, NH, TT, P])
        tops = sb("tops", [P, 5])
        tmax = sb("tmax", [P, TT, 2])
        ntop = sb("ntop", [P, TT, 2])
        sums = sb("sums", [P, TT, 2])
        scale = sb("scale", [P, TT])
        den = sb("den", [P, TT])
        c1 = sb("c1", [P, TT, P])
        prob = e.rbuf[:, 0:4096].rearrange("p (b n) -> p b n", b=2)
        probT = e.rbuf[:, 4096:8192].rearrange("p (b t n) -> p b t n", b=2, n=P)
        ccT = rs
        cx = q2T

        def head(w, h):
            return w[:, (h % 2) * L1X_HEAD:(h % 2 + 1) * L1X_HEAD]

        with nc.Block(no_gpsimd_drain=True) as block:
            @block.sync
            def _(sp):
                sp.dma_start(rope_q[:, :, :, :].rearrange("p a b c -> p (a b c)"), e.io["rope_q"])\
                    .then_inc(s["tables"], 16)
                sp.dma_start(wlat[:, :], e.io["wlat"]).then_inc(s["tables"], 16)
                stream(sp, e, n0, N_L1X)

            @block.tensor
            def _(pe):
                pe.wait_ge(e.rope["done"], 2)
                for g in range(CT // 4):
                    if g >= 6:
                        pe.wait_ge(s["kvT_a" if g % 2 else "kvT_d"], (g - 6) // 2 + 1)
                    for j in range(4):
                        last = pe.transpose(ps[:, 2 + g % 6, j * P:(j + 1) * P], e.kvr[:, 4 * g + j, :], e.ident)
                    last.then_inc(s["kvT_mm"], 1)
                ln_tensor(pe, e, s)
                pe.wait_ge(s["kvT_d"], 4)
                pe.wait_ge(s["kvT_a"], 4)
                used = [False]

                def q_of(h):
                    w = head(slot_in(pe, e, n0 + h // 2), h)
                    if h >= 2:
                        pe.wait_ge(s["q_sb"], h - 1)
                    for k in range(KT):
                        last = pe.matmul(ps[:, h % 2, 0:TOK], w[:, L1X_WQ + k * P:L1X_WQ + (k + 1) * P],
                                         e.xnT[:, k, :], start=(k == 0), stop=(k == KT - 1))
                        if k == 0 and used[0]:
                            last.then_inc(e.w_used, 1)
                            used[0] = False
                    last.then_inc(s["q_mm"], 1)

                def big_of(h):
                    w = head(e.ring[:, (n0 + h // 2) % RING, :], h)
                    pe.wait_ge(s["q_sb"], h + 1)
                    if h:
                        pe.wait_ge(s["big_d"], h)
                    for f in range(4):
                        last = pe.matmul(ps[:, 2 + f // 2, (f % 2) * TOK:(f % 2 + 1) * TOK],
                                         w[:, L1X_WKC + f * P:L1X_WKC + (f + 1) * P], q1[:, h % 2, :],
                                         start=True, stop=True)
                    last.then_inc(s["big_mm"], 1)

                def qr_of(h):
                    w = head(e.ring[:, (n0 + h // 2) % RING, :], h)
                    pe.wait_ge(s["rotated"], h + 1)
                    if h >= 2:
                        pe.wait_ge(s["qr_sb"], h - 1)
                    for f in range(3):
                        last = pe.matmul(ps[0:64, 4 + h % 2, 0:TOK], w[:, L1X_WQR + f * 64:L1X_WQR + (f + 1) * 64],
                                         rs[:, h % 2, f, :], start=(f == 0), stop=(f == 2))
                    last.then_inc(s["qr_mm"], 1)

                def q2_of(h):
                    w = head(e.ring[:, (n0 + h // 2) % RING, :], h)
                    pe.wait_ge(s["qr_sb"], h + 1)
                    if h >= 2:
                        pe.wait_ge(s["q2_sb"], h - 1)
                    pe.matmul(ps[:, 6 + h % 2, 0:TOK], w[0:64, L1X_WKR:L1X_WKR + P], qr[:, h % 2, :],
                              start=True, stop=True).then_inc(s["q2_mm"], 1)
                    if h % 2:
                        used[0] = True

                for h in range(NH + 3):
                    if h < NH:
                        q_of(h)
                    if 1 <= h <= NH:
                        big_of(h - 1)
                    if 2 <= h <= NH + 1:
                        qr_of(h - 2)
                    if h >= 3:
                        if used[0]:
                            pe.wait_ge(s["q2_mm"], h - 3)
                            pe.nop().then_inc(e.w_used, 1)
                            used[0] = False
                        q2_of(h - 3)
                pe.wait_ge(s["q2_mm"], NH)
                pe.nop().then_inc(e.w_used, 1)
                pe.wait_ge(s["q2_sb"], NH)

                def scores(turn, u):
                    g = turn * SUBS + u
                    hh, qt, half = u // 4, u // 2 % 2, u % 2
                    if u % 4 == 0:
                        pe.wait_ge(s["cur"], turn * 2 + (hh + 1))
                    if not (isinstance(turn, int) and g == 0):
                        pe.wait_ge(s["exp"], g)
                    for b in range(KB):
                        at = half * 2048 + b * 512
                        pe.matmul(ps[:, b, :], cur[:, hh, qt * P:(qt + 1) * P], kvT[:, at:at + 512],
                                  start=True, stop=True).then_inc(s["score_mm"], 1)

                def output(turn, u):
                    g = turn * SUBS + u
                    static = isinstance(turn, int)
                    half = u % 2

                    def turn_group(q):
                        name = "turned_a" if q % 2 else "turned_d"
                        if not (static and g * 2 + q // 2 == 0):
                            pe.wait_ge(s[name], g * 2 + q // 2)
                        for j in range(4):
                            t = 4 * q + j
                            last = pe.transpose(ps[:, 4 + q % 2, j * P:(j + 1) * P],
                                                prob[:, u % 2, t * P:(t + 1) * P], e.ident)
                        last.then_inc(s["turn_mm"], 1)

                    def ctx_group(q):
                        pe.wait_ge(s["turned_a" if q % 2 else "turned_d"], g * 2 + (q // 2 + 1))
                        if q == 0 and not (static and g < 2):
                            pe.wait_ge(s["taken"], g - 1)
                        for j in range(4):
                            t = 4 * q + j
                            last = pe.matmul(ps[:, 6 + half, 0:P], probT[:, u % 2, t, :], e.kvr[:, half * HT + t, :],
                                             start=(t == 0), stop=(t == HT - 1))
                        if q == 3:
                            last.then_inc(s["ctx_mm"], 1)

                    if u == 0 and static:
                        pe.wait_ge(s["exp"], 1)
                    turn_group(0)
                    turn_group(1)
                    ctx_group(0)
                    turn_group(2)
                    ctx_group(1)
                    turn_group(3)
                    ctx_group(2)
                    ctx_group(3)

                scores(0, 0)
                for u in range(1, SUBS):
                    scores(0, u)
                    output(0, u - 1)
                with pe.Fori(1, PAIRS) as i:
                    scores(i, 0)
                    output(i - 1, SUBS - 1)
                    for u in range(1, SUBS):
                        scores(i, u)
                        output(i, u - 1)
                pe.wait_ge(s["exp"], PAIRS * SUBS)
                output(PAIRS - 1, SUBS - 1)

                def turn_pair(j):
                    if j >= 2:
                        pe.wait_ge(s["cT_sb"], j - 1)
                    for x in range(2):
                        for t in range(TT):
                            last = pe.transpose(ps[:, j % 2, x * TOK + t * P:x * TOK + (t + 1) * P],
                                                cn[:, 2 * j + x, t, :], e.ident)
                    last.then_inc(s["cT_mm"], 1)

                def latent(j):
                    pe.wait_ge(s["cT_sb"], j + 1)
                    if j >= 2:
                        pe.wait_ge(s["lat_sb"], j - 1)
                    for x in range(2):
                        h = 2 * j + x
                        last = pe.matmul(ps[:, 2 + j % 2, x * TOK:(x + 1) * TOK], wlat[:, h * P:(h + 1) * P],
                                         ccT[:, j % 2, x, :], start=True, stop=True)
                    last.then_inc(s["lat_mm"], 1)

                def project(j):
                    pe.wait_ge(s["lat_sb"], j + 1)
                    w = slot_in(pe, e, n0 + PAIRS + j // 2)
                    for x in range(2):
                        h = 2 * j + x
                        for t in range(TT):
                            last = pe.matmul(ps[:, 6 + t, :], cx[:, h, t * P:(t + 1) * P],
                                             w[:, (h % 4) * D:(h % 4 + 1) * D], start=(h == 0), stop=(h == NH - 1))
                            if j % 2 == 0 and x == 0 and t == 0 and j:
                                last.then_inc(e.w_used, 1)
                    if j == PAIRS - 1:
                        last.then_inc(s["out_mm"], 1)

                pe.wait_ge(s["ln_self"], LN_OWN + 12 * PAIRS)
                for j in range(PAIRS + 2):
                    if j < PAIRS:
                        turn_pair(j)
                    if 1 <= j <= PAIRS:
                        latent(j - 1)
                    if j >= 2:
                        project(j - 2)
                pe.wait_ge(s["out_mm"], 1)
                pe.nop().then_inc(e.w_used, 1)

            @block.scalar
            def _(act):
                for g in range(1, CT // 4, 2):
                    act.wait_ge(s["kvT_mm"], g + 1)
                    act.activation(kvT[:, g * 512:(g + 1) * 512], ps[:, 2 + g % 6, :], ACT.Copy)\
                        .then_inc(s["kvT_a"], 1)
                ln_scalar(act, e, s)
                for h in range(NH + 3):
                    if h < NH:
                        act.wait_ge(s["q_mm"], h + 1)
                        if h >= 2:
                            act.wait_ge(s["big_mm"], h - 1)
                        act.activation(q1[:, h % 2, :], ps[:, h % 2, 0:TOK], ACT.Copy).then_inc(s["q_sb"], 1)
                    if 2 <= h <= NH + 1:
                        x = h - 2
                        act.wait_ge(s["qr_mm"], x + 1)
                        if x >= 2:
                            act.wait_ge(s["q2_mm"], x - 1)
                        act.activation(qr[:, x % 2, :], ps[0:64, 4 + x % 2, 0:TOK], ACT.Copy)\
                            .then_inc(s["qr_sb"], 1)
                    if h >= 3:
                        x = h - 3
                        act.wait_ge(s["q2_mm"], x + 1)
                        act.activation(q2T[:, x, :], ps[:, 6 + x % 2, 0:TOK], ACT.Copy).then_inc(s["q2_sb"], 1)

                def turned(turn, u, q):
                    g = turn * SUBS + u
                    act.wait_ge(s["turn_mm"], g * 4 + (q + 1))
                    if not (isinstance(turn, int) and g < 2):
                        act.wait_ge(s["ctx_mm"], g - 1)
                    act.activation(probT[:, u % 2, 4 * q:4 * q + 4, :].rearrange("p a b -> p (a b)"), ps[:, 5, :],
                                   ACT.Copy).then_inc(s["turned_a"], 1)

                def exps(turn, u):
                    g = turn * SUBS + u
                    qt, half = u // 2 % 2, u % 2
                    act.wait_ge(s["top"], g + 1)
                    act.activation(prob[:, u % 2, :], ps[:, 0:KB, :].rearrange("p a b -> p (a b)"), ACT.Exp,
                                   bias=ntop[:, qt, half:half + 1], accum_out=sums[:, qt, half:half + 1])\
                        .then_inc(s["exp"], 1)
                    if half:
                        act.activation(scale[:, qt:qt + 1], tmax[:, qt, 0:1], ACT.Exp, bias=ntop[:, qt, 1:2])\
                            .then_inc(s["rescale"], 1)

                exps(0, 0)
                for u in range(1, SUBS):
                    turned(0, u - 1, 1)
                    exps(0, u)
                    turned(0, u - 1, 3)
                with act.Fori(1, PAIRS) as i:
                    turned(i - 1, SUBS - 1, 1)
                    exps(i, 0)
                    turned(i - 1, SUBS - 1, 3)
                    for u in range(1, SUBS):
                        turned(i, u - 1, 1)
                        exps(i, u)
                        turned(i, u - 1, 3)
                turned(PAIRS - 1, SUBS - 1, 1)
                turned(PAIRS - 1, SUBS - 1, 3)
                for j in range(PAIRS):
                    act.wait_ge(s["lat_mm"], j + 1)
                    act.activation(cx[:, 2 * j:2 * j + 2, :].rearrange("p a b -> p (a b)"), ps[:, 2 + j % 2, :],
                                   ACT.Copy).then_inc(s["lat_sb"], 1)

            @block.gpsimd
            def _(pool):
                pool.wait_ge(s["q2_sb"], NH)
                for x in range(2):
                    pool.tensor_copy(cur[:, x, :], q2T[:, x, :]).then_inc(s["cur"], 1)
                with pool.Fori(1, PAIRS) as i:
                    for x in range(2):
                        pool.wait_ge(s["score_mm"], i * (4 * SUBS) + (x - 1) * 16)
                        pool.tensor_copy(cur[:, x, :], q2T[:, bass.ds(i * 2 + x, 1), :].rearrange("p a b -> p (a b)"))\
                            .then_inc(s["cur"], 1)

            @block.vector
            def _(dve):
                me = Chain(dve, s["dve_self"])
                for g in range(0, CT // 4, 2):
                    dve.wait_ge(s["kvT_mm"], g + 1)
                    dve.tensor_copy(kvT[:, g * 512:(g + 1) * 512], ps[:, 2 + g % 6, :]).then_inc(s["kvT_d"], 1)
                ln_vector(dve, e, s)
                dve.wait_ge(s["tables"], 32)
                for h in range(NH):
                    dve.wait_ge(s["big_mm"], h + 1)
                    if h:
                        dve.wait_ge(s["rotated"], h)
                    x01, x22 = ps[:, 2, :].rearrange("p (a n) -> p a n", a=2), ps[:, 3, :].rearrange("p (a n) -> p a n", a=2)
                    if h >= 2:
                        dve.wait_ge(s["qr_mm"], h - 1)
                    me.did(dve.tensor_tensor(rc[:, :, :].rearrange("p a n -> p (a n)"),
                                             ps[:, 2:4, :].rearrange("p a n -> p (a n)")[:, 0:3 * TOK],
                                             rope_q[:, 0, :, :].rearrange("p a n -> p (a n)"), ALU.mult))
                    me.did(dve.tensor_tensor(rs[:, h % 2, 0, :], x01[:, 1, :], rope_q[:, 1, 0, :], ALU.mult))
                    me.did(dve.tensor_tensor(rs[:, h % 2, 1, :], x01[:, 0, :], rope_q[:, 1, 1, :], ALU.mult))
                    dve.tensor_tensor(rs[:, h % 2, 2, :], x22[:, 1, :], rope_q[:, 1, 2, :], ALU.mult)\
                        .then_inc(s["big_d"], 1)
                    me.wait()
                    dve.wait_ge(s["big_d"], h + 1)
                    dve.tensor_tensor(rs[:, h % 2, :, :], rs[:, h % 2, :, :], rc[:, :, :], ALU.add)\
                        .then_inc(s["rotated"], 1)
                dve.wait_ge(s["rotated"], NH)
                base = me.n

                OWN = 6

                def maxima(turn, u):
                    g = turn * SUBS + u
                    qt, half = u // 2 % 2, u % 2
                    for b in range(KB):
                        dve.wait_ge(s["score_mm"], g * 4 + (b + 1))
                        dve.tensor_reduce(tops[:, b:b + 1], ps[:, b, :], AX_X, ALU.max).then_inc(s["dve_self"], 1)
                    dve.wait_ge(s["dve_self"], base + g * OWN + 4)
                    dve.tensor_reduce(tmax[:, qt, half:half + 1], tops[:, 0:KB + half], AX_X, ALU.max)\
                        .then_inc(s["dve_self"], 1)
                    dve.wait_ge(s["dve_self"], base + g * OWN + 5)
                    if not half:
                        dve.tensor_copy(tops[:, KB:KB + 1], tmax[:, qt, 0:1]).then_inc(s["dve_self"], 1)
                    else:
                        dve.nop().then_inc(s["dve_self"], 1)
                    dve.tensor_scalar(ntop[:, qt, half:half + 1], tmax[:, qt, half:half + 1], -1.0, None, ALU.mult)\
                        .then_inc(s["top"], 1)

                def turned(turn, u, q):
                    g = turn * SUBS + u
                    dve.wait_ge(s["turn_mm"], g * 4 + (q + 1))
                    if not (isinstance(turn, int) and g < 2):
                        dve.wait_ge(s["ctx_mm"], g - 1)
                    dve.tensor_copy(probT[:, u % 2, 4 * q:4 * q + 4, :].rearrange("p a b -> p (a b)"), ps[:, 4, :])\
                        .then_inc(s["turned_d"], 1)

                def take(turn, u):
                    g = turn * SUBS + u
                    hh, qt, half = u // 4, u // 2 % 2, u % 2
                    dve.wait_ge(s["ctx_mm"], g + 1)
                    if not half:
                        dve.tensor_copy(c1[:, qt, :], ps[:, 6, 0:P]).then_inc(s["taken"], 1)
                        return
                    dve.wait_ge(s["rescale"], turn * 4 + (u // 2 + 1))
                    dve.wait_ge(s["taken"], g)
                    dve.scalar_tensor_tensor(out=c1[:, qt, :], in0=c1[:, qt, :], scalar=scale[:, qt:qt + 1],
                                             in1=ps[:, 7, 0:P], op0=ALU.mult, op1=ALU.add).then_inc(s["taken"], 1)
                    dve.scalar_tensor_tensor(out=den[:, qt:qt + 1], in0=sums[:, qt, 0:1], scalar=scale[:, qt:qt + 1],
                                             in1=sums[:, qt, 1:2], op0=ALU.mult, op1=ALU.add)\
                        .then_inc(s["ln_self"], 1)
                    dve.wait_ge(s["ln_self"], LN_OWN + turn * 12 + (u // 2) * 3 + 1)
                    dve.reciprocal(den[:, qt:qt + 1], den[:, qt:qt + 1]).then_inc(s["ln_self"], 1)
                    dve.wait_ge(s["ln_self"], LN_OWN + turn * 12 + (u // 2) * 3 + 2)
                    at = turn * 2 + hh
                    out = cn[:, at, qt, :] if isinstance(turn, int) else \
                        cn[:, bass.ds(at, 1), qt, :].rearrange("p a b -> p (a b)")
                    dve.wait_ge(s["taken"], g + 1)
                    dve.tensor_scalar(out, c1[:, qt, :], den[:, qt:qt + 1], None, ALU.mult).then_inc(s["ln_self"], 1)

                maxima(0, 0)
                for u in range(1, SUBS):
                    maxima(0, u)
                    turned(0, u - 1, 0)
                    turned(0, u - 1, 2)
                    take(0, u - 1)
                with dve.Fori(1, PAIRS) as i:
                    for u in range(SUBS):
                        maxima(i, u)
                        v = (i - 1, SUBS - 1) if u == 0 else (i, u - 1)
                        turned(*v, 0)
                        turned(*v, 2)
                        take(*v)
                turned(PAIRS - 1, SUBS - 1, 0)
                turned(PAIRS - 1, SUBS - 1, 2)
                take(PAIRS - 1, SUBS - 1)
                dve.wait_ge(s["ln_self"], LN_OWN + PAIRS * 12)
                for j in range(PAIRS):
                    dve.wait_ge(s["cT_mm"], j + 1)
                    if j >= 2:
                        dve.wait_ge(s["lat_mm"], j - 1)
                    dve.tensor_copy(ccT[:, j % 2, 0:2, :].rearrange("p a b -> p (a b)"), ps[:, j % 2, :])\
                        .then_inc(s["cT_sb"], 1)
                dve.wait_ge(s["out_mm"], 1)
                for t in range(TT):
                    dve.tensor_tensor(e.xres[:, t, :], e.xres[:, t, :], ps[:, 6 + t, :], ALU.add)\
                        .then_inc(s["cT_sb"], 1)
        clear_sems(nc, s)
    e.n0 += N_L1X



def layer_l1a(e):
    nc, ps = e.nc, e.ps
    n0 = e.n0
    NH, HD = 64, 64
    INNER = NH * HD
    F = INNER // P
    CONV_TILES = 2 + F
    GROUPS = 8
    GH = NH // GROUPS
    PAIRS = NH // 2
    with ExitStack() as ctx:
        def sb(name, shape):
            return ctx.enter_context(nc.sbuf_tensor("l1a_" + name, shape, F32))
        s = layer_sems(nc, ctx, "l1a", LN_SEMS + [
            "dve_self", "act_self", "dt_mm", "tile_mm", "tile_ev", "pads", "conv", "silu", "xt_mm", "xt_sb", "sp_abs",
            "sp_exp", "sp_done", "decay", "rows", "cols_mm", "cols", "gt_mm", "gt_sb", "btm_sb", "eb_mm", "scan",
            "m", "ends", "xdt", "xd", "xs", "diag_mm", "st_mm", "st_sb", "off_mm", "off_read", "gate_mm", "gate",
            "t_step", "y", "diag_read", "turn_mm", "yT", "squared", "out_mm"])
        xh = sb("xh", [P, TT, INNER])
        xdt = sb("xdt", [P, TT, INNER])
        ybuf = sb("ybuf", [P, F, TOK])
        BC = sb("BC", [P, 2, TOK])
        Bt = sb("Bt", [P, P])
        GT = sb("GT", [P, TT, P])
        L = sb("L", [P, 2, 2, TT, P])
        M = sb("M", [P, 2, 2, TT, P])
        st = sb("st", [P, 512])
        sg = sb("sg", [P, TT, 512])
        y = sb("y", [P, TT, 512])
        dtm = sb("dtm", [P, 3, NH])
        dend = sb("dend", [P, NH])
        ssq = sb("ssq", [P, TT, GROUPS])
        rms = sb("rms", [P, TT])
        small, ident, ident4 = e.small, e.ident, e.ident4
        flat = ybuf[:, :, :].rearrange("p f t -> p (f t)")
        pad = flat[:, 4096:4096 + 2 * 259].rearrange("p (b n) -> p b n", b=2)
        conv = flat[:, 4700:4700 + 512].rearrange("p (b n) -> p b n", b=2)
        xf = flat[:, 5220:5220 + 1024].rearrange("p (b n) -> p b n", b=4)
        r_x, r_a, r_y, r_z, r_e = (flat[0:64, 6272 + i * TOK:6272 + (i + 1) * TOK] for i in range(5))
        r_0 = flat[0:64, 7552:7680]
        r_c = flat[0:64, 7680:7808]
        r_negA = flat[0:64, 7808:7809]
        rowbuf = sb("rowbuf", [64, TOK])
        xsg = sb("xsg", [P, 2, 512])
        junk = e.xn[:, 0, :]

        def taps(i, j):
            return small[:, S_MCONV + 4 * i + j:S_MCONV + 4 * i + j + 1]

        def squares(act, g, me):
            for c in range(TT):
                act.wait_ge(s["y"], 2 * g + c + 1)
                if 2 * g + c:
                    act.wait_ge(s["squared"], 2 * g + c)
                act.activation(junk[:, :], y[:, c, :], ACT.Square, accum_out=ssq[:, c, g:g + 1])\
                    .then_inc(s["squared"], 1)

        with nc.Block(no_gpsimd_drain=True) as block:
            @block.sync
            def _(sp):
                stream(sp, e, n0, N_L1A)

            @block.tensor
            def _(pe):
                ln_tensor(pe, e, s)
                for k in range(KT):
                    last = pe.matmul(ps[0:64, 4, 0:TOK], small[:, S_MDT + 64 * k:S_MDT + 64 * k + 64], e.xnT[:, k, :],
                                     start=(k == 0), stop=(k == KT - 1))
                last.then_inc(s["dt_mm"], 1)

                def turn_x(j):
                    pe.wait_ge(s["silu"], 2 * j + 4)
                    if j >= 2:
                        pe.wait_ge(s["xt_sb"], j - 1)
                    for t in range(TT):
                        for x in range(2):
                            last = pe.transpose(ps[:, 6 + j % 2, t * 256 + x * P:t * 256 + (x + 1) * P],
                                                xf[:, (2 * j + x) % 4, t * P:(t + 1) * P], ident)
                    last.then_inc(s["xt_mm"], 1)

                for i in range(CONV_TILES):
                    w = slot_in(pe, e, n0 + i // 6)
                    if i >= 4:
                        pe.wait_ge(s["tile_ev"], i - 3)
                    for k in range(KT):
                        last = pe.matmul(ps[:, i % 4, 0:TOK], w[:, k * 768 + (i % 6) * P:k * 768 + (i % 6 + 1) * P],
                                         e.xnT[:, k, :], start=(k == 0), stop=(k == KT - 1))
                        if k == 0 and i and i % 6 == 0:
                            last.then_inc(e.w_used, 1)
                    last.then_inc(s["tile_mm"], 1)
                    if i >= 6 and i % 2 == 0:
                        turn_x((i - 6) // 2)
                for j in range((CONV_TILES - 6) // 2, F // 2):
                    turn_x(j)
                pe.nop().then_inc(e.w_used, 1)
                for c in range(TT):
                    at = slice(c * P, (c + 1) * P)
                    pe.matmul(ps[:, 5, at], BC[:, 0, at], BC[:, 1, at], start=True, stop=True)
                pe.transpose(ps[:, 5, 2 * P:3 * P], BC[:, 0, 0:P], ident).then_inc(s["gt_mm"], 1)
                pe.wait_ge(s["rows"], 1)
                for c in range(TT):
                    pe.transpose(ps[:, 4, c * NH:(c + 1) * NH], r_z[:, c * P:(c + 1) * P], ident[0:64, 0:64])
                pe.transpose(ps[:, 4, 2 * NH:3 * NH], r_c, ident[0:64, 0:64]).then_inc(s["cols_mm"], 1)
                pe.wait_ge(s["cols"], 1)
                pe.wait_ge(s["gt_sb"], 2)

                def decays(q):
                    if q >= 2:
                        pe.wait_ge(s["scan"], q - 1)
                    for x in range(2):
                        h = 2 * q + x
                        last = pe.matmul(ps[:, q % 2, x * TOK:(x + 1) * TOK],
                                         ident[0:64, h:h + 1].broadcast_to((64, P)), rowbuf[:, :],
                                         start=True, stop=True)
                    last.then_inc(s["eb_mm"], 1)

                def diagonal(q):
                    g = q // 4
                    pe.wait_ge(s["m"], q + 1)
                    if q % 4 == 0:
                        pe.wait_ge(s["xdt"], 2 * g + 2)
                        if g:
                            pe.wait_ge(s["diag_read"], 2 * g)
                    for x in range(2):
                        h = 2 * q + x
                        for c in range(TT):
                            last = pe.matmul(ps[:, 2 + c, (h % GH) * HD:(h % GH + 1) * HD], M[:, q % 2, x, c, :],
                                             xdt[:, c, h * HD:(h + 1) * HD], start=True, stop=True)
                    last.then_inc(s["diag_mm"], 1)

                def gates(g, c):
                    w = slot_in(pe, e, n0 + 6 + g)
                    n = 2 * g + c
                    if n:
                        pe.wait_ge(s["gate"], n)
                    for k in range(KT):
                        last = pe.matmul(ps[:, 5, :], e.xnT[:, k, c * P:(c + 1) * P], w[:, k * 512:(k + 1) * 512],
                                         start=(k == 0), stop=(k == KT - 1))
                        if k == 0 and c == 0 and g:
                            last.then_inc(e.w_used, 1)
                    last.then_inc(s["gate_mm"], 1)

                def state(g):
                    pe.wait_ge(s["xs"], g + 1)
                    if g:
                        pe.wait_ge(s["off_read"], g)
                    pe.matmul(ps[:, 4, :], Bt[:, :], xsg[:, g % 2, :], start=True, stop=True).then_inc(s["st_mm"], 1)

                def off(g):
                    pe.wait_ge(s["st_sb"], g + 1)
                    pe.matmul(ps[:, 4, :], BC[:, 1, P:TOK], st[:, :], start=True, stop=True).then_inc(s["off_mm"], 1)

                def turn_y(g):
                    for c in range(TT):
                        pe.wait_ge(s["y"], 2 * g + c + 1)
                        if g:
                            pe.wait_ge(s["yT"], 2 * g + c - 1)
                        for j in range(4):
                            last = pe.transpose(ps[:, 6 + c, j * P:(j + 1) * P], y[:, c, j * P:(j + 1) * P], ident)
                        last.then_inc(s["turn_mm"], 1)

                decays(0)
                decays(1)
                for g in range(GROUPS):
                    gates(g, 0)
                    for q in range(4 * g, 4 * g + 4):
                        diagonal(q)
                        if q + 2 < PAIRS:
                            decays(q + 2)
                        if q == 4 * g + 1 and g:
                            turn_y(g - 1)
                    gates(g, 1)
                    state(g)
                    off(g)
                turn_y(GROUPS - 1)
                pe.wait_ge(s["yT"], 2 * GROUPS)
                for f in range(F):
                    w = slot_in(pe, e, n0 + 6 + GROUPS + f // 4)
                    for t in range(TT):
                        last = pe.matmul(ps[:, t, :], ybuf[:, f, t * P:(t + 1) * P], w[:, (f % 4) * D:(f % 4 + 1) * D],
                                         start=(f == 0), stop=(f == F - 1))
                        if f % 4 == 0 and t == 0:
                            last.then_inc(e.w_used, 1)
                last.then_inc(s["out_mm"], 1)
                pe.wait_ge(s["out_mm"], 1)
                pe.nop().then_inc(e.w_used, 1)

            @block.scalar
            def _(act):
                me = Chain(act, s["act_self"])
                ln_scalar(act, e, s)

                def silu(i):
                    act.wait_ge(s["conv"], i + 1)
                    if i >= 6:
                        act.wait_ge(s["xt_mm"], (i - 4) // 2)
                    out = BC[:, i, :] if i < 2 else xf[:, (i - 2) % 4, :]
                    act.activation(out, conv[:, i % 2, :], ACT.Silu, bias=small[:, S_MBIAS + i:S_MBIAS + i + 1])\
                        .then_inc(s["silu"], 1)

                def turned_x(j):
                    act.wait_ge(s["xt_mm"], j + 1)
                    act.activation(xh[:, :, j * 256:(j + 1) * 256], ps[:, 6 + j % 2, :].rearrange("p (t n) -> p t n", t=TT),
                                   ACT.Copy).then_inc(s["xt_sb"], 1)

                act.wait_ge(s["pads"], 1)
                done = 0
                for i in range(CONV_TILES):
                    act.wait_ge(s["tile_mm"], i + 1)
                    if i >= 2:
                        act.wait_ge(s["conv"], i - 1)
                    act.activation(pad[:, i % 2, 3:3 + TOK], ps[:, i % 4, 0:TOK], ACT.Copy).then_inc(s["tile_ev"], 1)
                    if i:
                        silu(i - 1)
                    if i >= 8 and i % 2 == 0:
                        turned_x(done)
                        done += 1
                silu(CONV_TILES - 1)
                while done < F // 2:
                    turned_x(done)
                    done += 1
                act.wait_ge(s["gt_mm"], 1)
                act.activation(GT[:, :, :].rearrange("p c n -> p (c n)"), ps[:, 5, 0:TOK], ACT.Copy).then_inc(s["gt_sb"], 1)
                act.activation(Bt[:, :], ps[:, 5, 2 * P:3 * P], ACT.Copy).then_inc(s["gt_sb"], 1)
                me.did(act.activation(r_negA, small[0:64, S_MHEAD:S_MHEAD + 1], ACT.Exp))
                me.wait()
                me.did(act.activation(r_negA, r_negA, ACT.Copy, scale=-1.0))
                softplus_scalar(act, r_a, r_y, s)
                act.wait_ge(s["sp_done"], 1)
                me.wait()
                act.activation(r_e, r_z, ACT.Exp, scale=r_negA).then_inc(s["decay"], 1)
                act.wait_ge(s["cols_mm"], 1)
                act.activation(dtm[:, :, :].rearrange("p c h -> p (c h)"), ps[:, 4, 0:3 * NH], ACT.Copy)\
                    .then_inc(s["cols"], 1)
                for g in range(GROUPS):
                    for c in range(TT):
                        act.wait_ge(s["gate_mm"], 2 * g + c + 1)
                        if g:
                            act.wait_ge(s["y"], 2 * g + c - 1)
                        act.activation(sg[:, c, :], ps[:, 5, :], ACT.Silu).then_inc(s["gate"], 1)
                        if g and c == 0:
                            squares(act, g - 1, me)
                    act.wait_ge(s["st_mm"], g + 1)
                    if g:
                        act.wait_ge(s["off_mm"], g)
                    act.activation(st[:, :], ps[:, 4, :], ACT.Copy).then_inc(s["st_sb"], 1)
                squares(act, GROUPS - 1, me)
                act.wait_ge(s["ln_xn"], TT + 1)
                act.activation(rms[:, :], rms[:, :], ACT.Sqrt, bias=e.eps, scale=1.0 / INNER).then_inc(s["ln_std"], 1)

            @block.gpsimd
            def _(pool):
                pool.wait_ge(s["cols"], 1)
                pool.wait_ge(s["xt_sb"], F // 2)
                for g in range(GROUPS):
                    at, hh = slice(g * 512, (g + 1) * 512), slice(g * GH, (g + 1) * GH)

                    def by_head(ap):
                        return ap.rearrange("p (h d) -> p h d", d=HD)
                    for c in range(TT):
                        pool.tensor_tensor(by_head(xdt[:, c, at]), by_head(xh[:, c, at]),
                                           bcast_last(dtm[:, c, hh], (P, GH, HD)), ALU.mult).then_inc(s["xdt"], 1)
                    pool.wait_ge(s["xdt"], 2 * g + 2)
                    for c in range(TT):
                        pool.tensor_tensor(by_head(xh[:, c, at]), by_head(xh[:, c, at]),
                                           bcast_last(small[:, S_MD + g * GH:S_MD + (g + 1) * GH], (P, GH, HD)),
                                           ALU.mult).then_inc(s["xd"], 1)
                    pool.wait_ge(s["ends"], 4 * g + 4)
                    if g >= 2:
                        pool.wait_ge(s["st_mm"], g - 1)
                    pool.tensor_tensor(by_head(xsg[:, g % 2, :]), by_head(xdt[:, 0, at]),
                                       bcast_last(dend[:, hh], (P, GH, HD)), ALU.mult).then_inc(s["xs"], 1)

            @block.vector
            def _(dve):
                me = Chain(dve, s["dve_self"])
                ln_vector(dve, e, s)
                dve.memset(pad[:, :, :], 0.0).then_inc(s["pads"], 1)
                for i in range(CONV_TILES):
                    dve.wait_ge(s["tile_ev"], i + 1)
                    if i >= 2:
                        dve.wait_ge(s["silu"], i - 1)
                    x, z = pad[:, i % 2, :], conv[:, i % 2, :]
                    me.did(dve.tensor_scalar(z, x[:, 0:TOK], taps(i, 0), None, ALU.mult))
                    for j in range(1, 4):
                        me.wait()
                        last = dve.scalar_tensor_tensor(out=z, in0=x[:, j:j + TOK], scalar=taps(i, j), in1=z,
                                                        op0=ALU.mult, op1=ALU.add)
                        if j < 3:
                            me.did(last)
                    last.then_inc(s["conv"], 1)
                dve.wait_ge(s["dt_mm"], 1)
                me.did(dve.memset(r_0, 0.0))
                me.did(dve.tensor_scalar(r_x, ps[0:64, 4, 0:TOK], small[0:64, S_MHEAD + 1:S_MHEAD + 2], None, ALU.add))
                me.wait()
                softplus_vector(dve, me, r_x, r_a, r_y, r_z, s, r_z)
                dve.wait_ge(s["decay"], 1)
                me.did(dve.tensor_copy(rowbuf[:, :], r_e))
                me.did(dve.tensor_tensor_scan(r_c, r_e[:, P:TOK], r_0, 1.0, ALU.mult, ALU.add))
                me.wait()
                me.did(dve.memset(rowbuf[:, 0:TOK:P], 0.0))
                me.wait()
                dve.nop().then_inc(s["rows"], 1)
                dve.wait_ge(s["gt_sb"], 2)

                def pair(q):
                    dve.wait_ge(s["eb_mm"], q + 1)
                    if q >= 2:
                        dve.wait_ge(s["m"], q - 1)
                        dve.wait_ge(s["ends"], q - 1)
                    d = L[:, q % 2, :, :, :]
                    dve.tensor_tensor_scan(d.rearrange("p h c n -> p (h c n)"), ps[:, q % 2, :], ident4, 0.0,
                                           ALU.mult, ALU.add).then_inc(s["scan"], 1)
                    dve.wait_ge(s["scan"], q + 1)
                    if q >= 2:
                        dve.wait_ge(s["diag_mm"], q - 1)
                    dve.tensor_copy(dend[:, 2 * q:2 * q + 2], d[:, :, 0, P - 1]).then_inc(s["ends"], 1)
                    dve.tensor_tensor(M[:, q % 2, :, :, :].rearrange("p h c n -> p h (c n)"),
                                      d.rearrange("p h c n -> p h (c n)"),
                                      GT[:, :, :].rearrange("p c n -> p (c n)").unsqueeze(1).broadcast_to((P, 2, TOK)),
                                      ALU.mult).then_inc(s["m"], 1)

                def by_head(ap):
                    return ap.rearrange("p (h d) -> p h d", d=HD)

                def outputs(g):
                    at, hh = slice(g * 512, (g + 1) * 512), slice(g * GH, (g + 1) * GH)
                    base = 5 * g
                    dve.wait_ge(s["diag_mm"], 4 * g + 4)
                    dve.wait_ge(s["xd"], 2 * g + 2)
                    if g:
                        dve.wait_ge(s["turn_mm"], 2 * g)
                        dve.wait_ge(s["squared"], 2 * g)
                    dve.tensor_tensor(y[:, 0, :], ps[:, 2, :], xh[:, 0, at], ALU.add).then_inc(s["diag_read"], 1)
                    dve.tensor_tensor(xh[:, 1, at], ps[:, 3, :], xh[:, 1, at], ALU.add).then_inc(s["diag_read"], 1)
                    dve.wait_ge(s["gate"], 2 * g + 1)
                    dve.wait_ge(s["diag_read"], 2 * g + 2)
                    dve.tensor_tensor(y[:, 0, :], y[:, 0, :], sg[:, 0, :], ALU.mult).then_inc(s["y"], 1)
                    dve.wait_ge(s["off_mm"], g + 1)
                    dve.tensor_tensor(by_head(y[:, 1, :]), by_head(ps[:, 4, :]), bcast_last(dtm[:, 2, hh], (P, GH, HD)),
                                      ALU.mult).then_inc(s["off_read"], 1)
                    dve.wait_ge(s["off_read"], g + 1)
                    dve.tensor_tensor(y[:, 1, :], y[:, 1, :], xh[:, 1, at], ALU.add).then_inc(s["t_step"], 1)
                    dve.wait_ge(s["t_step"], g + 1)
                    dve.wait_ge(s["gate"], 2 * g + 2)
                    dve.tensor_tensor(y[:, 1, :], y[:, 1, :], sg[:, 1, :], ALU.mult).then_inc(s["y"], 1)

                def turned_y(g):
                    for c in range(TT):
                        dve.wait_ge(s["turn_mm"], 2 * g + c + 1)
                        dve.tensor_tensor(ybuf[:, 4 * g:4 * g + 4, c * P:(c + 1) * P],
                                          ps[:, 6 + c, :].rearrange("p (f n) -> p f n", n=P),
                                          bcast_last(small[:, S_MNORM + 4 * g:S_MNORM + 4 * g + 4], (P, 4, P)),
                                          ALU.mult).then_inc(s["yT"], 1)

                dve.wait_ge(s["cols_mm"], 1)
                for g in range(GROUPS):
                    for q in range(4 * g, 4 * g + 4):
                        pair(q)
                        if q == 4 * g + 2 and g:
                            turned_y(g - 1)
                    outputs(g)
                turned_y(GROUPS - 1)
                dve.wait_ge(s["squared"], 2 * GROUPS)
                me.did(dve.tensor_reduce(rms[:, :], ssq[:, :, :], AX_X, ALU.add))
                me.wait()
                dve.nop().then_inc(s["ln_xn"], 1)
                dve.wait_ge(s["ln_std"], 2)
                me.did(dve.reciprocal(rms[:, :], rms[:, :]))
                me.wait()
                dve.wait_ge(s["out_mm"], 1)
                for t in range(TT):
                    me.did(dve.scalar_tensor_tensor(out=e.xres[:, t, :], in0=ps[:, t, :], scalar=rms[:, t:t + 1],
                                                    in1=e.xres[:, t, :], op0=ALU.mult, op1=ALU.add))
        clear_sems(nc, s)
    e.n0 += N_L1A



def _ktiles(wT):
    k, n = wT.shape
    return wT.reshape(k // P, P, n).transpose(1, 0, 2).reshape(P, -1)


def _slot(*parts):
    out = np.zeros((P, SLOT), np.float32)
    at = 0
    for a in parts:
        out[:a.shape[0], at:at + a.shape[1]] = a
        at += a.shape[1]
    return out


def slots_l0x(i):
    wq = np.asarray(i["L0_xattn_Wq"]).T
    wkv = np.asarray(i["L0_xattn_Wkv_expand"]).T
    wout = np.asarray(i["L0_xattn_Wout"]).T
    return [_slot(_ktiles(wq), wkv), _slot(_ktiles(wout))]


def fixed_columns():
    out = np.zeros((P, C_N), np.float32)
    for r in range(4):
        out[:, C_ID + r * P:C_ID + (r + 1) * P] = np.eye(P)
    a = np.arange(P)
    for l in range(7):
        b = 1 << l
        s, r = a[:, None], a[None, :]
        out[:, C_LEVEL + l * P:C_LEVEL + (l + 1) * P] = \
            (s // (2 * b) == r // (2 * b)) & (s % (2 * b) < b) & (r % (2 * b) >= b)
    out[:, C_CAUSAL + P:C_CAUSAL + 2 * P] = np.where(a[None, :] <= a[:, None], 0.0, LOWEST)
    out[:, C_ONES:C_ONES + P] = 1.0
    out[:, C_EPS] = EPS
    for h in range(8):
        out[:, C_PICK + 9 * h] = 1.0
    return out


def small_columns(i):
    out = np.zeros((P, S_N), np.float32)
    g = lambda n: np.asarray(i[n])
    conv = np.concatenate([g("L0_attn_conv_q_w"), g("L0_attn_conv_k_w"), g("L0_attn_conv_v_w")])[:, 0, :]
    out[:, S_ACONV:S_ACONV + 160] = conv.reshape(40, P, 4).transpose(1, 0, 2).reshape(P, 160)
    out[:, S_AAB:S_AAB + 96] = _ktiles(np.concatenate([g("L0_attn_Wa"), g("L0_attn_Wb")], axis=1))
    out[:, S_ANORM] = g("L0_attn_norm_w")
    out[:8, S_AHEAD] = g("L0_attn_A_log")
    out[:8, S_AHEAD + 1] = g("L0_attn_dt_bias")
    out[:, S_F0:S_F0 + 256] = _ktiles(g("L0_ffn_gate_w").T)
    out[:, S_F1:S_F1 + 32] = _ktiles(g("L1_ffn_gate_w").T)
    order = np.concatenate([np.arange(4096, 4352), np.arange(4096)])
    out[:, S_MCONV:S_MCONV + 136] = g("L1_attn_conv_w")[order, 0, :].reshape(34, P, 4).transpose(1, 0, 2).reshape(P, 136)
    out[:, S_MBIAS:S_MBIAS + 34] = g("L1_attn_conv_b")[order].reshape(34, P).T
    out[:, S_MDT:S_MDT + 256] = _ktiles(g("L1_attn_in_proj_w")[4096 + 4352:].T)
    out[:64, S_MHEAD] = g("L1_attn_A_log")
    out[:64, S_MHEAD + 1] = g("L1_attn_dt_bias")
    out[:, S_MD:S_MD + 64] = g("L1_attn_D")[None, :]
    out[:, S_MNORM:S_MNORM + 32] = g("L1_attn_norm_w").reshape(32, P).T
    return out


def slots_l0f(i):
    w13, w2 = np.asarray(i["L0_ffn_w13"]), np.asarray(i["L0_ffn_w2"])
    return [_slot(_ktiles(w13[x].T), _ktiles(w2[x].T)) for x in range(w13.shape[0])]


def slots_l1f(i):
    w1, w2, w3 = (np.asarray(i["L1_ffn_" + n]) for n in ("w1", "w2", "w3"))
    return [_slot(_ktiles(np.concatenate([w1[x][:, c:c + 256], w3[x][:, c:c + 256]], axis=1)), _ktiles(w2[x][c:c + 256]))
            for x in range(w1.shape[0]) for c in range(0, 1024, 256)]


def slots_l1x(i):
    g = lambda n: np.asarray(i["L1_xattn_" + n])
    wq, wkc, wqr, wkr, wo = g("Wq"), g("w_kc_q"), g("W_qr"), g("W_kr"), g("Wo")
    out = []
    for pair in range(8):
        parts = []
        for h in (2 * pair, 2 * pair + 1):
            parts += [_ktiles(wq[h * P:(h + 1) * P].T),
                      *[wkc[h][:, c] for c in Q_TILES + [Q_TURNED]],
                      *[wqr[h][c] for c in Q_TILES],
                      np.pad(wkr[h].T, ((0, 64), (0, 0)))]
        out.append(_slot(*parts))
    return out + [_slot(_ktiles(wo.T[c:c + 4 * P])) for c in range(0, 16 * P, 4 * P)]


def rope_tables(length, dim):
    f32 = np.float32
    inv = f32(1.0) / np.power(f32(10000.0), np.arange(0, dim, 2, dtype=f32) / f32(dim)).astype(f32)
    f = np.arange(length, dtype=f32)[:, None] * inv[None, :]
    return np.sin(f).astype(f32), np.cos(f).astype(f32)


def extra_inputs(i):
    ctx = np.asarray(i["ctx_512"])[0]
    wlat = np.asarray(i["L1_xattn_w_kc_kv"])
    sin_k, cos_k = rope_tables(CTX, P)
    sin_q, cos_q = (np.repeat(t, 2, axis=-1).T for t in rope_tables(TOK, Q_BIG))
    sign_k = np.where(np.arange(64) < 32, -1.0, 1.0).astype(np.float32)
    sign_q = np.where(np.arange(Q_BIG) < HALF, -1.0, 1.0).astype(np.float32)[:, None]

    def rows(a):
        return a.reshape(CT, P, -1).transpose(1, 0, 2).reshape(P, -1)
    return {
        "ctxT": ctx[:TOK].T,
        "ctx": rows(ctx),
        "rope_k": np.concatenate([rows(cos_k), rows(sin_k * sign_k)], axis=1),
        "rope_q": np.concatenate([cos_q[c] for c in Q_TILES] + [(sin_q * sign_q)[c] for c in Q_TILES], axis=1),
        "wlat": wlat.transpose(2, 0, 1).reshape(P, 16 * P),
    }


def slots_l0a(i):
    g = lambda n: np.asarray(i["L0_attn_" + n])
    w = np.concatenate([g("Wq"), g("Wk"), g("Wv"), g("Wg")], axis=1)
    wo = g("Wo")
    return [_slot(_ktiles(w[:, c:c + 768])) for c in range(0, 6144, 768)] + \
        [_slot(_ktiles(wo[c:c + 4 * P])) for c in (0, 4 * P)]


def slots_l1a(i):
    w = np.asarray(i["L1_attn_in_proj_w"]).T
    gate, conv = w[:, :4096], w[:, 4096:8448]
    conv = np.concatenate([conv[:, 4096:], conv[:, :4096]], axis=1)
    wo = np.asarray(i["L1_attn_out_proj_w"]).T
    out = [_slot(_ktiles(np.pad(conv[:, c:c + 768], ((0, 0), (0, max(0, c + 768 - conv.shape[1]))))))
           for c in range(0, conv.shape[1], 768)]
    out += [_slot(_ktiles(gate[:, c:c + 512])) for c in range(0, 4096, 512)]
    return out + [_slot(_ktiles(wo[c:c + 4 * P])) for c in range(0, 4096, 4 * P)]



def build_program(nc, io):
    with ExitStack() as ctx:
        e = open_env(nc, ctx, io)
        e.slots = SLOTS
        layer_l0x(e)
        layer_l0a(e)
        with ExitStack() as rope:
            open_rope(e, rope)
            layer_l0f(e)
            layer_l1x(e)
        layer_l1a(e)
        layer_l1f(e)
        stored = ctx.enter_context(nc.semaphore("stored"))
        with nc.Block(no_gpsimd_drain=True) as block:
            @block.sync
            def _(sp):
                sp.dma_start(io["out"].rearrange("(t p) d -> p t d", p=P), e.xres[:, :, :]).then_inc(stored, 16)
                sp.wait_ge(stored, 16)



def kernel(**inputs):
    import concourse.bacc as bacc
    from concourse.bass_utils import run_bass_kernel_spmd

    slots = []
    for part in (slots_l0x, slots_l0a, slots_l0f, slots_l1x, slots_l1a, slots_l1f):
        slots += part(inputs)
    arrays = {"x": np.asarray(inputs["x"])[0], "fixed": fixed_columns(), "small": small_columns(inputs),
              "wall": np.stack(slots), **extra_inputs(inputs)}
    arrays = {name: np.ascontiguousarray(a) for name, a in arrays.items()}
    nc = bacc.Bacc("TRN2", target_bir_lowering=False, num_devices=1)
    io = {name: nc.dram_tensor(name, a.shape, mybir.dt.from_np(a.dtype), kind="ExternalInput").ap()
          for name, a in arrays.items()}
    io["out"] = nc.dram_tensor("out", (TOK, D), F32, kind="ExternalOutput").ap()
    build_program(nc, io)
    r = run_bass_kernel_spmd(nc, [arrays], core_ids=[0])
    return r.results[0]["out"].reshape(1, TOK, D)
```

```python
from contextlib import ExitStack

import numpy as np
import concourse.bass as bass
from concourse import mybir

F32 = mybir.dt.float32
F32R = mybir.dt.float32r
ACT = mybir.ActivationFunctionType
ALU = mybir.AluOpType
AX_X = mybir.AxisListType.X

P = 128
TOK = 256
TT = TOK // P
D = 512
KT = D // P
CTX = 4096
CT = CTX // P
EPS = 1e-5
LOWEST = -3.0e38

RING = 4
SLOT = 3072
N_L0X, N_L0A, N_L0F, N_L1X, N_L1A, N_L1F = 2, 10, 64, 12, 22, 32
FIRST_SLOT = {}
_at = 0
for _name, _n in (("L0x", N_L0X), ("L0a", N_L0A), ("L0f", N_L0F), ("L1x", N_L1X), ("L1a", N_L1A), ("L1f", N_L1F)):
    FIRST_SLOT[_name] = (_at, _n)
    _at += _n
SLOTS = _at

C_ID = 0
C_LEVEL = C_ID + 4 * P
C_CAUSAL = C_LEVEL + 7 * P
C_ONES = C_CAUSAL + 2 * P
C_EPS = C_ONES + P
C_PICK = C_EPS + 1
C_N = C_PICK + 64

S_ACONV = 0
S_AAB = S_ACONV + 160
S_ANORM = S_AAB + 96
S_AHEAD = S_ANORM + 1
S_F0 = S_AHEAD + 2
S_F1 = S_F0 + KT * 64
S_MCONV = S_F1 + KT * 8
S_MBIAS = S_MCONV + 136
S_MDT = S_MBIAS + 34
S_MHEAD = S_MDT + KT * 64
S_MD = S_MHEAD + 2
S_MNORM = S_MD + 64
S_N = S_MNORM + 32


class Chain:

    def __init__(self, eng, sem):
        self.eng, self.sem, self.n = eng, sem, 0

    def did(self, ins):
        ins.then_inc(self.sem, 1)
        self.n += 1
        return self.n

    def wait(self):
        self.eng.wait_ge(self.sem, self.n)


class Env:
    pass


def bcast_last(ap, shape):
    return ap.unsqueeze(len(shape) - 1).broadcast_to(shape)


def open_env(nc, ctx, io):
    e = Env()
    e.nc, e.io = nc, io

    def sb(name, shape):
        return ctx.enter_context(nc.sbuf_tensor("sb_" + name, shape, F32))

    e.ps = ctx.enter_context(nc.psum_tensor("banks", [P, 8, 512], F32))
    e.fixed = sb("fixed", [P, C_N])
    e.small = sb("small", [P, S_N])
    e.xres = sb("xres", [P, TT, D])
    e.xnbuf = sb("xnbuf", [P, 2 * TT * D])
    e.xn = e.xnbuf[:, 0:TT * D].rearrange("p (t d) -> p t d", t=TT)
    e.xnT = e.xnbuf[:, TT * D:2 * TT * D].rearrange("p (k t) -> p k t", k=KT)
    e.stats = sb("stats", [P, TT, 6])
    e.mv = sb("mv", [P, TT, 2])
    e.std = sb("std", [P, TT])
    e.ring = sb("ring", [P, RING, SLOT])
    e.ident = e.fixed[:, C_ID:C_ID + P]
    e.ident4 = e.fixed[:, C_ID:C_ID + 4 * P]
    e.ones = e.fixed[:, C_ONES:C_ONES + P]
    e.eps = e.fixed[:, C_EPS:C_EPS + 1]
    e.w_in = [ctx.enter_context(nc.semaphore(f"w_in{i}")) for i in range(RING)]
    e.w_used = ctx.enter_context(nc.semaphore("w_used"))
    e.boot = ctx.enter_context(nc.semaphore("boot"))
    e.n0 = 0
    e.slots = 0
    e.preloaded = False
    return e


def layer_sems(nc, ctx, tag, names):
    return {n: ctx.enter_context(nc.semaphore(f"{tag}_{n}")) for n in names}


def clear_sems(nc, s):
    ids = sorted(x.num for x in s.values())
    runs = []
    for i in ids:
        if runs and runs[-1][1] == i:
            runs[-1][1] = i + 1
        else:
            runs.append([i, i + 1])
    with nc.Block(no_gpsimd_drain=True) as block:
        @block.gpsimd
        def _(pool):
            for lo, hi in runs:
                pool.sem_clear(range(lo, hi))


LN_OWN = 3
LN_SEMS = ["ln_self", "ln_stats", "ln_std", "ln_xn", "ln_turned", "ln_done"]


def stream(sp, e, first, count):
    lo = first + RING if first or e.preloaded else 0
    hi = min(first + count + RING, e.slots)
    for n in range(lo, min(hi, RING)):
        sp.dma_start(e.ring[:, n, :], e.io["wall"][n]).then_inc(e.w_in[n], 16)
    lo = max(lo, RING)
    while lo < hi and lo % RING:
        load_slot(sp, e, lo, lo % RING)
        lo += 1
    turns = (hi - lo) // RING
    if turns > 1:
        with sp.Fori(0, turns) as i:
            for u in range(RING):
                sp.wait_ge(e.w_used, i * RING + (lo + u - RING + 1))
                sp.dma_start(e.ring[:, u, :], e.io["wall"][bass.ds(i * RING + (lo + u), 1)].rearrange("a p n -> (a p) n"))\
                    .then_inc(e.w_in[u], 16)
        lo += turns * RING
    while lo < hi:
        load_slot(sp, e, lo, lo % RING)
        lo += 1


def load_slot(sp, e, n, u):
    sp.wait_ge(e.w_used, n - RING + 1)
    sp.dma_start(e.ring[:, u, :], e.io["wall"][n]).then_inc(e.w_in[u], 16)


def slot_in(eng, e, n):
    eng.wait_ge(e.w_in[n % RING], 16 * (n // RING + 1))
    return e.ring[:, n % RING, :]



def ln_vector(dve, e, s):
    me = Chain(dve, s["ln_self"])
    for t in range(TT):
        me.did(dve.bn_stats(e.stats[:, t, :], e.xres[:, t, :]))
    me.wait()
    for t in range(TT):
        dve.bn_aggr(e.mv[:, t, :], e.stats[:, t, :]).then_inc(s["ln_stats"], 1)
    dve.wait_ge(s["ln_std"], 1)
    me.did(dve.reciprocal(e.std[:, :], e.std[:, :]))
    me.wait()
    for t in range(TT):
        dve.tensor_scalar(e.xn[:, t, :], e.xres[:, t, :], e.mv[:, t, 0:1], e.std[:, t:t + 1],
                          ALU.subtract, ALU.mult).then_inc(s["ln_xn"], 1)
    dve.wait_ge(s["ln_turned"], 1)
    dve.tensor_copy(e.xnT[:, 0:2, :], e.ps[:, 0, :].rearrange("p (k t) -> p k t", k=2)).then_inc(s["ln_done"], 1)


def ln_scalar(act, e, s):
    act.wait_ge(s["ln_stats"], TT)
    act.activation(e.std[:, :], e.mv[:, :, 1], ACT.Sqrt, bias=e.eps).then_inc(s["ln_std"], 1)
    act.wait_ge(s["ln_turned"], 2)
    act.activation(e.xnT[:, 2:4, :], e.ps[:, 1, :].rearrange("p (k t) -> p k t", k=2), ACT.Copy)\
        .then_inc(s["ln_done"], 1)


def ln_tensor(pe, e, s):
    for k in range(KT):
        for t in range(TT):
            if k == 0:
                pe.wait_ge(s["ln_xn"], t + 1)
            at = (k % 2) * TOK + t * P
            last = pe.transpose(e.ps[:, k // 2, at:at + P], e.xn[:, t, k * P:(k + 1) * P], e.ident)
        if k % 2:
            last.then_inc(s["ln_turned"], 1)
    pe.wait_ge(s["ln_done"], 2)



def layer_l0x(e, first_layer=True):
    nc, ps, fixed = e.nc, e.ps, e.fixed
    NH, HD = 16, 32
    G = 4
    SCALE = float(np.float32(1.0) / np.sqrt(np.float32(HD)))
    n0 = e.n0
    with ExitStack() as ctx:
        def sb(name, shape):
            return ctx.enter_context(nc.sbuf_tensor("l0x_" + name, shape, F32))
        s = layer_sems(nc, ctx, "l0x", LN_SEMS + [
            "k_mm", "v_mm", "q_mm", "kqv", "score_mm", "masked", "top", "prob", "turn_mm", "turned", "o_mm",
            "o_sb", "oT_mm", "oT_sb", "out_mm", "dve_self"])
        ctxT = sb("ctxT", [P, TOK])
        kT = sb("kT", [P, 4, TOK])
        v = sb("v", [P, TT, D])
        qT = sb("qT", [P, 4, TOK])
        sc = sb("sc", [P, G, 3 * P])
        pT = sb("pT", [P, G, 3, P])
        ntop = sb("ntop", [P, 4, 2 * G])
        rsum = sb("rsum", [P, TT, NH])
        o = sb("o", [P, TT, D])
        oT = sb("oT", [P, KT, TOK])
        causal = fixed[:, C_CAUSAL:C_CAUSAL + 2 * P]

        with nc.Block(no_gpsimd_drain=True) as block:
            @block.sync
            def _(sp):
                sp.dma_start(e.xres[:, :, :], e.io["x"].rearrange("(t p) d -> p t d", p=P)).then_inc(e.boot, 16)
                sp.dma_start(fixed[:, :], e.io["fixed"]).then_inc(e.boot, 16)
                sp.dma_start(ctxT[:, :], e.io["ctxT"]).then_inc(e.boot, 16)
                sp.dma_start(e.small[:, :], e.io["small"]).then_inc(e.boot, 16)
                stream(sp, e, n0, N_L0X)

            @block.tensor
            def _(pe):
                pe.wait_ge(e.boot, 64)
                w = slot_in(pe, e, n0)
                for m in range(4):
                    last = pe.matmul(ps[:, 2 + m // 2, (m % 2) * TOK:(m % 2 + 1) * TOK],
                                     w[:, 2048 + m * P:2048 + (m + 1) * P], ctxT[:, :], start=True, stop=True)
                last.then_inc(s["k_mm"], 1)
                for t in range(TT):
                    last = pe.matmul(ps[:, 4 + t, :], ctxT[:, t * P:(t + 1) * P], w[:, 2560:3072],
                                     start=True, stop=True)
                last.then_inc(s["v_mm"], 1)
                ln_tensor(pe, e, s)
                for m in range(4):
                    for k in range(KT):
                        last = pe.matmul(ps[:, 6 + m // 2, (m % 2) * TOK:(m % 2 + 1) * TOK],
                                         w[:, k * D + m * P:k * D + (m + 1) * P], e.xnT[:, k, :],
                                         start=(k == 0), stop=(k == KT - 1))
                last.then_inc(s["q_mm"], 1)
                pe.wait_ge(s["kqv"], 3)
                pe.nop().then_inc(e.w_used, 1)
                for g in range(4):
                    r = slice(32 * g, 32 * g + 32)
                    if g:
                        pe.wait_ge(s["masked"], 2 * g)
                    for m in range(G):
                        pe.matmul(ps[:, 0, m * P:(m + 1) * P], qT[r, m, 0:P], kT[r, m, 0:P], start=True, stop=True)
                        last = pe.matmul(ps[:, 1 + m // 2, (m % 2) * TOK:(m % 2 + 1) * TOK], qT[r, m, P:TOK],
                                         kT[r, m, :], start=True, stop=True)
                    last.then_inc(s["score_mm"], 1)
                    pe.wait_ge(s["prob"], 2 * G * (g + 1))
                    if g:
                        pe.wait_ge(s["turned"], 2 * g)
                    for m in range(G):
                        for b in range(3):
                            at = (m * 3 + b) * P
                            last = pe.transpose(ps[:, 3 + at // 512, at % 512:at % 512 + P],
                                                sc[:, m, b * P:(b + 1) * P], e.ident)
                    last.then_inc(s["turn_mm"], 1)
                    pe.wait_ge(s["turned"], 2 * (g + 1))
                    for m in range(G):
                        h = 4 * m + g
                        hs = slice(HD * h, HD * (h + 1))
                        pe.matmul(ps[:, 6, hs], pT[:, m, 0, :], v[:, 0, hs], start=True, stop=True)
                        pe.matmul(ps[:, 7, hs], pT[:, m, 1, :], v[:, 0, hs], start=True, stop=False)
                        last = pe.matmul(ps[:, 7, hs], pT[:, m, 2, :], v[:, 1, hs], start=False, stop=True)
                last.then_inc(s["o_mm"], 1)
                pe.wait_ge(s["o_sb"], 2)
                for k in range(KT):
                    for t in range(TT):
                        last = pe.transpose(ps[:, k // 2, (k % 2) * TOK + t * P:(k % 2) * TOK + (t + 1) * P],
                                            o[:, t, k * P:(k + 1) * P], e.ident)
                last.then_inc(s["oT_mm"], 1)
                pe.wait_ge(s["oT_sb"], 1)
                w = slot_in(pe, e, n0 + 1)
                for t in range(TT):
                    for k in range(KT):
                        last = pe.matmul(ps[:, 2 + t, :], oT[:, k, t * P:(t + 1) * P], w[:, k * D:(k + 1) * D],
                                         start=(k == 0), stop=(k == KT - 1))
                    last.then_inc(s["out_mm"], 1)
                pe.wait_ge(s["out_mm"], TT)
                pe.nop().then_inc(e.w_used, 1)

            @block.scalar
            def _(act):
                act.wait_ge(e.boot, 64)
                ln_scalar(act, e, s)
                act.wait_ge(s["v_mm"], 1)
                act.activation(v[:, :, :], ps[:, 4:6, :], ACT.Copy).then_inc(s["kqv"], 1)
                act.wait_ge(s["q_mm"], 1)
                act.activation(qT[:, :, :].rearrange("p a b -> p (a b)"),
                               ps[:, 6:8, :].rearrange("p a b -> p (a b)"), ACT.Copy).then_inc(s["kqv"], 1)
                for g in range(4):
                    act.wait_ge(s["top"], g + 1)
                    for m in range(G):
                        h = 4 * m + g
                        act.activation(sc[:, m, 0:P], sc[:, m, 0:P], ACT.Exp, bias=ntop[:, g, m:m + 1],
                                       accum_out=rsum[:, 0, h:h + 1]).then_inc(s["prob"], 1)
                        act.activation(sc[:, m, P:3 * P], sc[:, m, P:3 * P], ACT.Exp,
                                       bias=ntop[:, g, G + m:G + m + 1],
                                       accum_out=rsum[:, 1, h:h + 1]).then_inc(s["prob"], 1)
                    act.wait_ge(s["turn_mm"], g + 1)
                    act.activation(pT[:, :, :, :].rearrange("p a b c -> p (a b c)")[:, 1024:1536],
                                   ps[:, 5, :], ACT.Copy)\
                        .then_inc(s["turned"], 1)

            @block.vector
            def _(dve):
                me = Chain(dve, s["dve_self"])
                dve.wait_ge(e.boot, 64)
                ln_vector(dve, e, s)
                dve.wait_ge(s["k_mm"], 1)
                dve.tensor_copy(kT[:, :, :].rearrange("p a b -> p (a b)"),
                                ps[:, 2:4, :].rearrange("p a b -> p (a b)")).then_inc(s["kqv"], 1)
                for g in range(4):
                    dve.wait_ge(s["score_mm"], g + 1)
                    if g:
                        dve.wait_ge(s["turn_mm"], g)
                    dve.scalar_tensor_tensor(
                        out=sc[:, :, 0:P], in0=ps[:, 0, :].rearrange("p (m k) -> p m k", m=G), scalar=SCALE,
                        in1=causal[:, P:2 * P].unsqueeze(1).broadcast_to((P, G, P)), op0=ALU.mult, op1=ALU.add)\
                        .then_inc(s["masked"], 1)
                    dve.scalar_tensor_tensor(
                        out=sc[:, :, P:3 * P], in0=ps[:, 1:3, :].rearrange("p a (m k) -> p (a m) k", m=2),
                        scalar=SCALE, in1=causal.unsqueeze(1).broadcast_to((P, G, 2 * P)),
                        op0=ALU.mult, op1=ALU.add).then_inc(s["masked"], 1)
                    dve.wait_ge(s["masked"], 2 * (g + 1))
                    me.did(dve.tensor_reduce(ntop[:, g, 0:G], sc[:, :, 0:P], AX_X, ALU.max))
                    me.did(dve.tensor_reduce(ntop[:, g, G:2 * G], sc[:, :, P:3 * P], AX_X, ALU.max))
                    me.wait()
                    dve.tensor_scalar(ntop[:, g, :], ntop[:, g, :], -1.0, None, ALU.mult).then_inc(s["top"], 1)
                    dve.wait_ge(s["turn_mm"], g + 1)
                    dve.tensor_copy(pT[:, :, :, :].rearrange("p a b c -> p (a b c)")[:, 0:1024],
                                    ps[:, 3:5, :].rearrange("p a b -> p (a b)"))\
                        .then_inc(s["turned"], 1)
                dve.wait_ge(s["prob"], 8 * G)
                me.did(dve.reciprocal(rsum[:, :, :], rsum[:, :, :]))
                me.wait()
                dve.wait_ge(s["o_mm"], 1)
                for t in range(TT):
                    dve.tensor_tensor(o[:, t, :].rearrange("p (h d) -> p h d", h=NH),
                                      ps[:, 6 + t, :].rearrange("p (h d) -> p h d", h=NH),
                                      bcast_last(rsum[:, t, :], (P, NH, HD)), ALU.mult).then_inc(s["o_sb"], 1)
                dve.wait_ge(s["oT_mm"], 1)
                dve.tensor_copy(oT[:, :, :].rearrange("p a b -> p (a b)"),
                                ps[:, 0:2, :].rearrange("p a b -> p (a b)")).then_inc(s["oT_sb"], 1)
                for t in range(TT):
                    dve.wait_ge(s["out_mm"], t + 1)
                    me.did(dve.tensor_tensor(e.xres[:, t, :], e.xres[:, t, :], ps[:, 2 + t, :], ALU.add))
        clear_sems(nc, s)
    e.n0 += N_L0X



def layer_moe(e, tag, n_experts, parts, top_k, router_at):
    nc, ps = e.nc, e.ps
    n0 = e.n0
    steps = n_experts * parts
    TURNS = steps // RING
    assert steps % RING == 0 and TURNS >= 3
    INNER = 256
    W2 = KT * 2 * INNER
    NV = max(n_experts, 8) + (8 - top_k)
    with ExitStack() as ctx:
        def sb(name, shape, dt=F32):
            return ctx.enter_context(nc.sbuf_tensor(f"{tag}_{name}", shape, dt))
        s = layer_sems(nc, ctx, tag, LN_SEMS + [
            "dve_self", "logits", "ltop", "exps", "router", "x_hi", "x_lo", "w1_hi", "w1_lo", "w2_hi", "first_mm",
            "silu", "inner", "h_hi", "h_lo", "second_mm", "added"])
        if tag == "l0f":
            open_rope_tables(e, ctx)
        prob = sb("prob", [P, TT, NV])
        left = sb("left", [P, TT, NV])
        comb = sb("comb", [P, TT, n_experts])
        top = sb("top", [P, TT, 8])
        nmax = sb("nmax", [P, TT])
        total = sb("total", [P, TT])
        x_hi, x_lo = sb("x_hi", [P, KT, TOK], F32R), sb("x_lo", [P, KT, TOK], F32R)
        w1_hi, w1_lo = sb("w1_hi", [P, 2, W2], F32R), sb("w1_lo", [P, 2, W2], F32R)
        w2_hi, w2_lo = sb("w2_hi", [P, 2, 2 * D], F32R), sb("w2_lo", [P, 2, 2 * D], F32R)
        silu = sb("silu", [P, 2, 2 * TOK])
        h = sb("h", [P, 2, 2 * TOK])
        h_hi, h_lo = sb("h_hi", [P, 2, 2, TOK], F32R), sb("h_lo", [P, 2, 2, TOK], F32R)

        def early(at, steps_back):
            turn, u = at
            return isinstance(turn, int) and turn * RING + u < steps_back

        def count(at, c, k):
            turn, u = at
            return turn * (c * RING) + (c * u + k)

        def after(at, d):
            turn, u = at
            return turn + (u + d) // RING, (u + d) % RING

        def first_hi(act, at):
            b, slot = at[1] % 2, (n0 + at[1]) % RING
            act.wait_ge(e.w_in[slot], at[0] * 16 + 16 * ((n0 + at[1]) // RING + 1))
            if not early(at, 2):
                act.wait_ge(s["first_mm"], count(at, 2, -2))
            act.activation(w1_hi[:, b, :], e.ring[:, slot, 0:W2], ACT.Copy).then_inc(s["w1_hi"], 1)

        def first_lo(dve, at):
            b, slot = at[1] % 2, (n0 + at[1]) % RING
            dve.wait_ge(s["w1_hi"], count(at, 1, 1))
            dve.tensor_tensor(w1_lo[:, b, :], e.ring[:, slot, 0:W2], w1_hi[:, b, :].bitcast(F32), ALU.subtract)\
                .then_inc(s["w1_lo"], 1)

        def second_hi(act, at):
            b, slot = at[1] % 2, (n0 + at[1]) % RING
            if not early(at, 2):
                act.wait_ge(s["second_mm"], count(at, 2, -2))
            act.activation(w2_hi[:, b, :], e.ring[:, slot, W2:SLOT], ACT.Copy).then_inc(s["w2_hi"], 1)

        def second_lo(dve, at):
            b, slot = at[1] % 2, (n0 + at[1]) % RING
            dve.wait_ge(s["w2_hi"], count(at, 1, 1))
            dve.tensor_tensor(w2_lo[:, b, :], e.ring[:, slot, W2:SLOT], w2_hi[:, b, :].bitcast(F32), ALU.subtract)\
                .then_inc(e.w_used, 1)

        def first_half(pe, at):
            b = at[1] % 2
            pe.wait_ge(s["w1_lo"], count(at, 1, 1))
            if not early(at, 2):
                pe.wait_ge(s["inner"], count(at, 1, -1))
            for f in range(4):
                out = ps[:, 2 * b + f // 2, (f % 2) * TOK:(f % 2 + 1) * TOK]
                for k in range(KT):
                    w = slice(k * 2 * INNER + f * P, k * 2 * INNER + (f + 1) * P)
                    pe.matmul(out, w1_hi[:, b, w], x_hi[:, k, :], start=(k == 0), stop=False)
                    pe.matmul(out, w1_hi[:, b, w], x_lo[:, k, :], start=False, stop=False)
                    last = pe.matmul(out, w1_lo[:, b, w], x_hi[:, k, :], start=False, stop=(k == KT - 1))
                if f % 2:
                    last.then_inc(s["first_mm"], 1)

        def second_half(pe, at):
            b = at[1] % 2
            pe.wait_ge(s["h_lo"], count(at, 1, 1))
            pe.wait_ge(e.w_used, count(at, 1, n0 + 1))
            if not early(at, 2):
                pe.wait_ge(s["added"], count(at, 2, -2))
            for t in range(TT):
                out, tok = ps[:, 4 + 2 * b + t, :], slice(t * P, (t + 1) * P)
                for k in range(2):
                    w = slice(k * D, (k + 1) * D)
                    pe.matmul(out, h_hi[:, b, k, tok], w2_hi[:, b, w], start=(k == 0), stop=False)
                    pe.matmul(out, h_hi[:, b, k, tok], w2_lo[:, b, w], start=False, stop=False)
                    last = pe.matmul(out, h_lo[:, b, k, tok], w2_hi[:, b, w], start=False, stop=(k == 1))
                last.then_inc(s["second_mm"], 1)

        def activate(act, at):
            b = at[1] % 2
            act.wait_ge(s["first_mm"], count(at, 2, 1))
            if not early(at, 2):
                act.wait_ge(s["inner"], count(at, 1, -1))
            act.activation(silu[:, b, :], ps[:, 2 * b, :], ACT.Silu).then_inc(s["silu"], 1)

        def multiply(dve, at):
            b = at[1] % 2
            dve.wait_ge(s["first_mm"], count(at, 2, 2))
            dve.wait_ge(s["silu"], count(at, 1, 1))
            if not early(at, 2):
                dve.wait_ge(s["h_lo"], count(at, 1, -1))
            dve.tensor_tensor(h[:, b, :], silu[:, b, :], ps[:, 2 * b + 1, :], ALU.mult).then_inc(s["inner"], 1)

        def inner_hi(act, at):
            b = at[1] % 2
            act.wait_ge(s["inner"], count(at, 1, 1))
            if not early(at, 2):
                act.wait_ge(s["second_mm"], count(at, 2, -2))
            act.activation(h_hi[:, b, :, :].rearrange("p k t -> p (k t)"), h[:, b, :], ACT.Copy)\
                .then_inc(s["h_hi"], 1)

        def inner_lo(dve, at):
            b = at[1] % 2
            dve.wait_ge(s["h_hi"], count(at, 1, 1))
            dve.tensor_tensor(h_lo[:, b, :, :].rearrange("p k t -> p (k t)"), h[:, b, :],
                              h_hi[:, b, :, :].rearrange("p k t -> p (k t)").bitcast(F32), ALU.subtract)\
                .then_inc(s["h_lo"], 1)

        def add(dve, at):
            turn, u = at
            b = u % 2
            expert = turn if parts == RING else turn * RING + u
            for t in range(TT):
                weight = comb[:, t, expert:expert + 1] if isinstance(turn, int) else comb[:, t, bass.ds(expert, 1)]
                dve.wait_ge(s["second_mm"], count(at, 2, t + 1))
                if not early(at, 1):
                    dve.wait_ge(s["added"], count(at, 2, t - 1))
                dve.scalar_tensor_tensor(out=e.xres[:, t, :], in0=ps[:, 4 + 2 * b + t, :], scalar=weight,
                                         in1=e.xres[:, t, :], op0=ALU.mult, op1=ALU.add).then_inc(s["added"], 1)

        def within(at, d):
            turn, u = at
            return not isinstance(turn, int) or turn * RING + u + d < steps

        def pe_step(pe, at):
            if within(at, 1):
                first_half(pe, after(at, 1))
            second_half(pe, at)

        def act_step(act, at):
            if within(at, 1):
                activate(act, after(at, 1))
                inner_hi(act, after(at, 1))
            if within(at, 3):
                first_hi(act, after(at, 3))
            if within(at, 2):
                second_hi(act, after(at, 2))

        def dve_step(dve, at):
            if within(at, 1):
                multiply(dve, after(at, 1))
                inner_lo(dve, after(at, 1))
            add(dve, at)
            if within(at, 3):
                first_lo(dve, after(at, 3))
            if within(at, 2):
                second_lo(dve, after(at, 2))

        def all_steps(eng, step):
            for u in range(RING):
                step(eng, (0, u))
            with eng.Fori(1, TURNS - 1) as i:
                for u in range(RING):
                    step(eng, (i, u))
            for u in range(RING):
                step(eng, (TURNS - 1, u))

        with nc.Block(no_gpsimd_drain=True) as block:
            @block.sync
            def _(sp):
                if tag == "l0f":
                    rope_sync(sp, e)
                stream(sp, e, n0, steps)

            if tag == "l0f":
                @block.gpsimd
                def _(pool):
                    rope_pool(pool, e)

            @block.tensor
            def _(pe):
                ln_tensor(pe, e, s)
                for t in range(TT):
                    for k in range(KT):
                        last = pe.matmul(ps[:, 7, t * 64:t * 64 + n_experts], e.xnT[:, k, t * P:(t + 1) * P],
                                         e.small[:, router_at + k * n_experts:router_at + (k + 1) * n_experts],
                                         start=(k == 0), stop=(k == KT - 1))
                last.then_inc(s["logits"], 1)
                pe.wait_ge(s["x_lo"], 1)
                first_half(pe, (0, 0))
                pe.wait_ge(s["exps"], TT)
                all_steps(pe, pe_step)

            @block.scalar
            def _(act):
                first_hi(act, (0, 0))
                first_hi(act, (0, 1))
                ln_scalar(act, e, s)
                act.wait_ge(s["ln_done"], 2)
                act.activation(x_hi[:, :, :], e.xnT, ACT.Copy).then_inc(s["x_hi"], 1)
                act.wait_ge(s["ltop"], 1)
                for t in range(TT):
                    act.activation(prob[:, t, 0:n_experts], ps[:, 7, t * 64:t * 64 + n_experts], ACT.Exp,
                                   bias=nmax[:, t:t + 1], accum_out=total[:, t:t + 1]).then_inc(s["exps"], 1)
                second_hi(act, (0, 0))
                second_hi(act, (0, 1))
                activate(act, (0, 0))
                inner_hi(act, (0, 0))
                first_hi(act, (0, 2))
                all_steps(act, act_step)

            @block.vector
            def _(dve):
                me = Chain(dve, s["dve_self"])
                me.did(dve.memset(prob[:, :, :], -1.0))
                ln_vector(dve, e, s)
                first_lo(dve, (0, 0))
                dve.wait_ge(s["x_hi"], 1)
                dve.tensor_tensor(x_lo[:, :, :], e.xnT, x_hi[:, :, :].bitcast(F32), ALU.subtract)\
                    .then_inc(s["x_lo"], 1)
                dve.wait_ge(s["logits"], 1)
                lg = ps[:, 7, 0:TT * 64].rearrange("p (t x) -> p t x", t=TT)[:, :, 0:n_experts]
                me.did(dve.tensor_reduce(nmax[:, :], lg, AX_X, ALU.max))
                me.wait()
                dve.tensor_scalar(nmax[:, :], nmax[:, :], -1.0, None, ALU.mult).then_inc(s["ltop"], 1)
                first_lo(dve, (0, 1))
                second_lo(dve, (0, 0))
                second_lo(dve, (0, 1))
                multiply(dve, (0, 0))
                inner_lo(dve, (0, 0))
                first_lo(dve, (0, 2))
                dve.wait_ge(s["exps"], TT)
                me.did(dve.reciprocal(total[:, :], total[:, :]))
                me.wait()
                for t in range(TT):
                    me.did(dve.tensor_scalar(prob[:, t, 0:n_experts], prob[:, t, 0:n_experts], total[:, t:t + 1],
                                             None, ALU.mult))
                me.wait()
                for t in range(TT):
                    me.did(dve.max(top[:, t, :], prob[:, t, :]))
                me.wait()
                if top_k < 8:
                    me.did(dve.tensor_reduce(total[:, :], top[:, :, 0:top_k], AX_X, ALU.add))
                    me.did(dve.memset(top[:, :, top_k:8], -1.0))
                    me.wait()
                    me.did(dve.reciprocal(total[:, :], total[:, :]))
                    me.wait()
                for t in range(TT):
                    me.did(dve.match_replace(left[:, t, :], top[:, t, :], prob[:, t, :], 0.0))
                me.wait()
                me.did(dve.tensor_tensor(comb[:, :, :], prob[:, :, 0:n_experts], left[:, :, 0:n_experts],
                                         ALU.subtract))
                me.wait()
                if top_k < 8:
                    for t in range(TT):
                        me.did(dve.tensor_scalar(comb[:, t, :], comb[:, t, :], total[:, t:t + 1], None, ALU.mult))
                    me.wait()
                all_steps(dve, dve_step)
        clear_sems(nc, s)
    e.n0 += steps


def layer_l0f(e):
    layer_moe(e, "l0f", 64, 1, 8, S_F0)


def layer_l1f(e):
    layer_moe(e, "l1f", 8, 4, 2, S_F1)



def softplus_vector(dve, me, x, a, y, z, s, out):
    dve.scalar_tensor_tensor(out=a, in0=x, scalar=-1.0, in1=x, op0=ALU.mult, op1=ALU.max).then_inc(s["sp_abs"], 1)
    dve.wait_ge(s["sp_abs"], 1)
    me.did(dve.tensor_scalar(x, x, 0.0, None, ALU.max))
    dve.wait_ge(s["sp_exp"], 1)
    me.did(dve.tensor_scalar(a, y, 2.0, None, ALU.add))
    me.wait()
    me.did(dve.reciprocal(a, a))
    me.wait()
    me.did(dve.tensor_tensor(z, y, a, ALU.mult))
    me.wait()
    me.did(dve.tensor_tensor(y, z, z, ALU.mult))
    me.wait()
    me.did(dve.tensor_scalar(a, y, 1.0 / 15.0, None, ALU.mult))
    for n in range(6, 0, -1):
        me.wait()
        me.did(dve.scalar_tensor_tensor(out=a, in0=a, scalar=1.0 / (2 * n + 1), in1=y, op0=ALU.add, op1=ALU.mult))
    me.wait()
    me.did(dve.scalar_tensor_tensor(out=a, in0=a, scalar=1.0, in1=z, op0=ALU.add, op1=ALU.mult))
    me.wait()
    dve.scalar_tensor_tensor(out=out, in0=a, scalar=2.0, in1=x, op0=ALU.mult, op1=ALU.add)\
        .then_inc(s["sp_done"], 1)


def softplus_scalar(act, a, y, s):
    act.wait_ge(s["sp_abs"], 1)
    act.activation(y, a, ACT.Exp, scale=-1.0).then_inc(s["sp_exp"], 1)



def layer_l0a(e):
    nc, ps = e.nc, e.ps
    n0 = e.n0
    NH, NJ = 8, 2
    STEPS = NJ * TOK
    NC = STEPS // P
    CTOK = P // NJ
    CONV_TILES, TILES = 40, 48
    LEVELS = 7
    with ExitStack() as ctx:
        def sb(name, shape):
            return ctx.enter_context(nc.sbuf_tensor("l0a_" + name, shape, F32))
        s = layer_sems(nc, ctx, "l0a", LN_SEMS + [
            "dve_self", "act_self", "pool_self", "rows_mm", "tile_mm", "tile_ev", "pads", "conv", "silu", "sp_abs",
            "sp_exp", "sp_done", "decay", "beta", "rows", "cols_mm", "cols", "eb_mm", "scan", "kt_mm", "kt_sb",
            "vt_mm", "vt_sb", "qt_mm", "qt_sb", "norms", "normed", "kn_mm", "kn_d", "kn_a", "kb", "kb_mm", "kb_d",
            "kb_a", "qn_mm", "qn_sb", "qc", "qc_mm", "qc_sb", "g_mm", "g_sb", "p_mm", "p_sb", "kd", "ct", "y_mm",
            "y_sb", "pp_mm", "x_up", "xt_up", "ks_mm", "r_sb", "u_mm", "u_sb", "ds_mm", "sc", "s_new", "o_mm", "o_sb",
            "sq", "ss_mm", "rms", "rinv", "rb_mm", "gated", "y", "out_mm"])
        big = [sb(f"big{i}", [P, 4096]) for i in range(6)]
        mid = [sb(f"mid{i}", [P, 2048]) for i in range(4)]
        cols = sb("cols", [P, 128])
        junk = sb("junk", [P, P])

        def hs(buf):
            return buf[:, 0:4096].rearrange("p (h r) -> p h r", h=NH)

        def hc(buf):
            return buf[:, 0:4096].rearrange("p (h c d) -> p h c d", h=NH, c=NC)
        kraw, keyT = hs(big[0]), hs(big[0])
        vraw, kb, AT = hs(big[1]), hc(big[1]), hc(big[1])
        ktm = hc(big[2])
        bV = hc(big[3])
        KbT, XT = hs(big[4]), hc(big[4])
        DT, X = hs(big[5]), hc(big[5])
        qraw = mid[0][:, :].rearrange("p (h t) -> p h t", h=NH)
        QT = qraw
        qtm = mid[1][:, :].rearrange("p (h t d) -> p h t d", h=NH, t=TT)
        PT = mid[1][:, :].rearrange("p (h c t) -> p h c t", h=NH, c=NC)
        QcT = mid[2][:, :].rearrange("p (h t) -> p h t", h=NH)
        gate = mid[3][:, :].rearrange("p (h t) -> p h t", h=NH)
        OT = e.xnbuf[:, :].rearrange("p (h t) -> p h t", h=NH)
        pad = big[3][:, 0:2 * 259].rearrange("p (b n) -> p b n", b=2)
        conv = big[3][:, 1024:1536].rearrange("p (b n) -> p b n", b=2)
        rows = big[4][0:8, :]
        r_x, r_a, r_y, r_z = (rows[:, i * TOK:(i + 1) * TOK] for i in range(4))
        r_e, r_e0, r_c, r_b = (rows[:, 1024 + i * STEPS:1024 + (i + 1) * STEPS] for i in range(4))
        r_0 = rows[:, 3072:3072 + P]
        r_negA = rows[:, 3200:3201]
        CTm = mid[0][:, 0:1024].rearrange("p (b c n) -> p b c n", b=2, c=NC)
        Y = mid[0][:, 1024:2048].rearrange("p (b c n) -> p b c n", b=2, c=NC)
        R = big[1][:, 0:1024].rearrange("p (h d) -> p h d", h=NH)
        U = big[1][:, 1024:2048].rearrange("p (h d) -> p h d", h=NH)
        S = big[1][:, 2048:4096].rearrange("p (b h d) -> p b h d", b=2, h=NH)
        sq = big[3][:, 0:2048].rearrange("p (h t) -> p h t", h=NH)
        yT = big[3][:, 2048:4096].rearrange("p (h t) -> p h t", h=NH)
        beta = cols[:, 0:32].rearrange("p (c h) -> p c h", h=NH)
        cum = cols[:, 32:64].rearrange("p (c h) -> p c h", h=NH)
        ctok = cols[:, 64:80].rearrange("p (t h) -> p t h", h=NH)
        cend = cols[:, 80:112].rearrange("p (h c) -> p h c", h=NH)
        nbc = sb("nbc", [P, NC, NH])
        knorm = sb("knorm", [P, NH, NC])
        qnorm = sb("qnorm", [P, NH, TT])
        dend = sb("dend", [P, NH, NC])
        srow = sb("srow", [8, 2 * TOK])
        ident, ident4, small = e.ident, e.ident4, e.small

        def taps(i, j):
            return small[:, S_ACONV + 4 * i + j:S_ACONV + 4 * i + j + 1]

        def conv_out(i):
            if i < 8:
                return qraw[:, i, :]
            raw, i = (kraw, i - 8) if i < 24 else (vraw, i - 24)
            return raw[:, i % NH, :].rearrange("p (t j) -> p j t", j=NJ)[:, i // NH, :]

        with nc.Block(no_gpsimd_drain=True) as block:
            @block.sync
            def _(sp):
                stream(sp, e, n0, N_L0A)

            @block.tensor
            def _(pe):
                ln_tensor(pe, e, s)
                for j in range(3):
                    for k in range(KT):
                        last = pe.matmul(ps[0:8, min(4 + j, 5), (j // 2) * TOK:(j // 2 + 1) * TOK],
                                         small[:, S_AAB + 24 * k + 8 * j:S_AAB + 24 * k + 8 * j + 8],
                                         e.xnT[:, k, :], start=(k == 0), stop=(k == KT - 1))
                last.then_inc(s["rows_mm"], 1)
                for i in range(TILES):
                    w = slot_in(pe, e, n0 + i // 6)
                    if i >= 4:
                        pe.wait_ge(s["tile_ev"], i - 3)
                    for k in range(KT):
                        last = pe.matmul(ps[:, i % 4, 0:TOK], w[:, k * 768 + (i % 6) * P:k * 768 + (i % 6 + 1) * P],
                                         e.xnT[:, k, :], start=(k == 0), stop=(k == KT - 1))
                        if k == 0 and i and i % 6 == 0:
                            last.then_inc(e.w_used, 1)
                    last.then_inc(s["tile_mm"], 1)
                pe.wait_ge(s["silu"], TILES)
                pe.nop().then_inc(e.w_used, 1)
                pe.wait_ge(s["rows"], 2)
                for c in range(NC):
                    pe.transpose(ps[:, 5, 8 * c:8 * c + 8], r_b[:, c * P:(c + 1) * P], ident[0:8, 0:8])
                    pe.transpose(ps[:, 5, 32 + 8 * c:40 + 8 * c], r_c[:, c * P:(c + 1) * P], ident[0:8, 0:8])
                for t in range(TT):
                    at = t * NJ * P
                    pe.transpose(ps[:, 5, 64 + 8 * t:72 + 8 * t], r_c[:, at + 1:at + NJ * P:NJ], ident[0:8, 0:8])
                for h in range(NH):
                    last = pe.matmul(ps[:, 5, 80 + 4 * h:84 + 4 * h], ident[0:8, h:h + 1].broadcast_to((8, P)),
                                     r_c[:, P - 1:STEPS:P], start=True, stop=True)
                last.then_inc(s["cols_mm"], 1)
                for h in range(NH):
                    if h >= 2:
                        pe.wait_ge(s["scan"], h - 1)
                    pe.matmul(ps[:, 6 + h % 2, :], ident[0:8, h:h + 1].broadcast_to((8, P)), r_e0,
                              start=True, stop=True).then_inc(s["eb_mm"], 1)
                for h in range(NH):
                    if h >= 2:
                        pe.wait_ge(s["kt_sb"], h - 1)
                    for c in range(NC):
                        last = pe.transpose(ps[:, h % 2, c * P:(c + 1) * P], kraw[:, h, c * P:(c + 1) * P], ident)
                    last.then_inc(s["kt_mm"], 1)
                    if h % 2 == 0:
                        if h >= 4:
                            pe.wait_ge(s["qt_sb"], h // 2 - 1)
                        for x in range(2):
                            for t in range(TT):
                                last = pe.transpose(ps[:, 2 + h // 2 % 2, (2 * x + t) * P:(2 * x + t + 1) * P],
                                                    qraw[:, h + x, t * P:(t + 1) * P], ident)
                        last.then_inc(s["qt_mm"], 1)
                    if h == 0:
                        pe.wait_ge(s["cols"], 1)
                    if h >= 2:
                        pe.wait_ge(s["vt_sb"], h - 1)
                    for c in range(NC):
                        last = pe.transpose(ps[:, 4 + h % 2, c * P:(c + 1) * P], vraw[:, h, c * P:(c + 1) * P],
                                            ident)
                    last.then_inc(s["vt_mm"], 1)
                pe.wait_ge(s["normed"], 1)
                for h in range(NH):
                    if h >= 2:
                        pe.wait_ge(s["kn_a" if h % 2 else "kn_d"], h // 2)
                    for c in range(NC):
                        last = pe.transpose(ps[:, h % 2, c * P:(c + 1) * P], ktm[:, h, c, :], ident)
                    last.then_inc(s["kn_mm"], 1)
                pe.wait_ge(s["normed"], 2)
                for h in range(0, NH, 2):
                    if h >= 4:
                        pe.wait_ge(s["qn_sb"], h // 2 - 1)
                    for x in range(2):
                        for t in range(TT):
                            last = pe.transpose(ps[:, 2 + h // 2 % 2, (2 * x + t) * P:(2 * x + t + 1) * P],
                                                qtm[:, h + x, t, :], ident)
                    last.then_inc(s["qn_mm"], 1)
                pe.wait_ge(s["kb"], 1)
                for h in range(NH):
                    if h >= 2:
                        pe.wait_ge(s["kb_a" if h % 2 else "kb_d"], h // 2)
                    for c in range(NC):
                        last = pe.transpose(ps[:, 4 + h % 2, c * P:(c + 1) * P], kb[:, h, c, :], ident)
                    last.then_inc(s["kb_mm"], 1)
                pe.wait_ge(s["qc"], 1)
                pe.wait_ge(s["kn_a"], 4)
                pe.wait_ge(s["kn_d"], 4)
                for h in range(0, NH, 2):
                    if h >= 4:
                        pe.wait_ge(s["qc_sb"], h // 2 - 1)
                    for x in range(2):
                        for t in range(TT):
                            last = pe.transpose(ps[:, h // 2 % 2, (2 * x + t) * P:(2 * x + t + 1) * P],
                                                qtm[:, h + x, t, :], ident)
                    last.then_inc(s["qc_mm"], 1)
                pe.wait_ge(s["qn_sb"], 4)
                pe.wait_ge(s["kb_a"], 4)
                pe.wait_ge(s["kb_d"], 4)
                for h in range(NH):
                    if h >= 2:
                        pe.wait_ge(s["g_sb"], h - 1)
                    for c in range(NC):
                        at = slice(c * P, (c + 1) * P)
                        last = pe.matmul(ps[:, 2 + h % 2, at], keyT[:, h, at], KbT[:, h, at], start=True, stop=True)
                    last.then_inc(s["g_mm"], 1)
                    if h % 2:
                        if h >= 5:
                            pe.wait_ge(s["p_sb"], h // 2 - 1)
                        for x in range(2):
                            for c in range(NC):
                                last = pe.matmul(ps[:, 6 + h // 2 % 2, (x * NC + c) * CTOK:(x * NC + c + 1) * CTOK],
                                                 keyT[:, h - 1 + x, c * P:(c + 1) * P],
                                                 QT[:, h - 1 + x, c * CTOK:(c + 1) * CTOK], start=True, stop=True)
                        last.then_inc(s["p_mm"], 1)
                pe.wait_ge(s["g_sb"], NH)
                pe.wait_ge(s["qc_sb"], 4)

                def level_y(n):
                    l, h = divmod(n, NH)
                    pe.wait_ge(s["ct"], n + 1)
                    if l:
                        pe.wait_ge(s["x_up"], n - NH + 1)
                    if n >= 2:
                        pe.wait_ge(s["x_up" if n - 2 < NH else "y_sb"], n - 1 if n - 2 < NH else n - 1 - NH)
                    for c in range(NC):
                        last = pe.matmul(ps[:, n % 2, c * P:(c + 1) * P], CTm[:, n % 2, c, :],
                                         X[:, h, c, :] if l else ident, start=True, stop=True)
                    last.then_inc(s["y_mm"], 1)

                def level_xy(n):
                    l, h = divmod(n, NH)
                    if not l:
                        return
                    pe.wait_ge(s["y_sb"], n - NH + 1)
                    pe.wait_ge(s["xt_up"], n - NH + 1)
                    if n - NH >= 2:
                        pe.wait_ge(s["xt_up"], n - 1)
                        pe.wait_ge(s["x_up"], min(n - 1, NH * (LEVELS - 1)))
                    for c in range(NC):
                        at = slice(c * P, (c + 1) * P)
                        if l < LEVELS - 1:
                            pe.matmul(ps[:, 2 + n % 2, at], XT[:, h, c, :], Y[:, n % 2, c, :], start=True, stop=True)
                        last = pe.matmul(ps[:, 4 + n % 2, at], Y[:, n % 2, c, :], XT[:, h, c, :],
                                         start=True, stop=True)
                    last.then_inc(s["pp_mm"], 1)

                for n in range(NH * LEVELS + 2):
                    if n < NH * LEVELS:
                        level_y(n)
                    if n >= 2:
                        level_xy(n - 2)
                pe.wait_ge(s["xt_up"], NH * LEVELS)
                pe.wait_ge(s["kd"], 1)

                for c in range(NC):
                    at = slice(c * P, (c + 1) * P)
                    for x in range(2):
                        if c:
                            pe.wait_ge(s["s_new"], 2 * (c - 1) + x + 1)
                            for h in range(4 * x, 4 * x + 4):
                                last = pe.matmul(ps[:, x, (h % 4) * P:(h % 4 + 1) * P], keyT[:, h, at],
                                                 S[:, c % 2, h, :], start=True, stop=True)
                            last.then_inc(s["ks_mm"], 1)
                    for x in range(2):
                        pe.wait_ge(s["r_sb"], 2 * c + x + 1)
                        for h in range(4 * x, 4 * x + 4):
                            last = pe.matmul(ps[:, 2 + x, (h % 4) * P:(h % 4 + 1) * P], XT[:, h, c, :], R[:, h, :],
                                             start=True, stop=True)
                        last.then_inc(s["u_mm"], 1)
                    for x in range(2):
                        pe.wait_ge(s["u_sb"], 2 * c + x + 1)
                        if c < NC - 1:
                            for h in range(4 * x, 4 * x + 4):
                                last = pe.matmul(ps[:, 4 + x, (h % 4) * P:(h % 4 + 1) * P], ktm[:, h, c, :],
                                                 U[:, h, :], start=True, stop=True)
                            last.then_inc(s["ds_mm"], 1)
                    if c >= 2:
                        pe.wait_ge(s["o_sb"], c - 1)
                    for h in range(NH):
                        o = ps[:, 6 + c % 2, h * CTOK:(h + 1) * CTOK]
                        if c:
                            pe.matmul(o, S[:, c % 2, h, :], QcT[:, h, c * CTOK:(c + 1) * CTOK],
                                      start=True, stop=False)
                        last = pe.matmul(o, U[:, h, :], PT[:, h, c, :], start=(c == 0), stop=True)
                    last.then_inc(s["o_mm"], 1)
                pe.wait_ge(s["sq"], 1)
                for h in range(NH):
                    last = pe.matmul(ps[0:8, 0, 0:TOK], e.fixed[:, C_PICK + 8 * h:C_PICK + 8 * h + 8], sq[:, h, :],
                                     start=(h == 0), stop=(h == NH - 1))
                last.then_inc(s["ss_mm"], 1)
                pe.wait_ge(s["rinv"], 1)
                for h in range(NH):
                    last = pe.matmul(ps[:, 2 + h // 2, (h % 2) * TOK:(h % 2 + 1) * TOK],
                                     ident[0:8, h:h + 1].broadcast_to((8, P)), srow[:, TOK:2 * TOK],
                                     start=True, stop=True)
                last.then_inc(s["rb_mm"], 1)
                pe.wait_ge(s["y"], 1)
                for t in range(TT):
                    for h in range(NH):
                        w = slot_in(pe, e, n0 + 8 + h // 4)
                        last = pe.matmul(ps[:, 6 + t, :], yT[:, h, t * P:(t + 1) * P],
                                         w[:, (h % 4) * D:(h % 4 + 1) * D], start=(h == 0), stop=(h == NH - 1))
                    last.then_inc(s["out_mm"], 1)
                pe.wait_ge(s["out_mm"], TT)
                for _ in range(2):
                    pe.nop().then_inc(e.w_used, 1)

            @block.scalar
            def _(act):
                me = Chain(act, s["act_self"])
                ln_scalar(act, e, s)

                def silu(i):
                    act.wait_ge(s["conv"], i + 1)
                    act.activation(conv_out(i), conv[:, i % 2, :], ACT.Silu).then_inc(s["silu"], 1)

                act.wait_ge(s["pads"], 1)
                for i in range(CONV_TILES):
                    act.wait_ge(s["tile_mm"], i + 1)
                    if i >= 2:
                        act.wait_ge(s["conv"], i - 1)
                    act.activation(pad[:, i % 2, 3:3 + TOK], ps[:, i % 4, 0:TOK], ACT.Copy).then_inc(s["tile_ev"], 1)
                    if i:
                        silu(i - 1)
                silu(CONV_TILES - 1)
                for i in range(CONV_TILES, TILES):
                    act.wait_ge(s["tile_mm"], i + 1)
                    act.wait_ge(s["silu"], i)
                    act.activation(gate[:, i - CONV_TILES, :], ps[:, i % 4, 0:TOK], ACT.Silu).then_inc(s["silu"], 1)
                    if i < TILES - 4:
                        act.wait_ge(s["silu"], i + 1)
                        act.nop().then_inc(s["tile_ev"], 1)
                act.wait_ge(s["rows_mm"], 1)
                rb = r_b.rearrange("p (t j) -> p j t", j=NJ)
                act.activation(rb[:, 0, :], ps[0:8, 5, 0:TOK], ACT.Sigmoid).then_inc(s["beta"], 1)
                act.activation(rb[:, 1, :], ps[0:8, 5, TOK:2 * TOK], ACT.Sigmoid).then_inc(s["beta"], 1)
                me.did(act.activation(r_negA, small[0:8, S_AHEAD:S_AHEAD + 1], ACT.Exp))
                me.wait()
                me.did(act.activation(r_negA, r_negA, ACT.Copy, scale=-1.0))
                softplus_scalar(act, r_a, r_y, s)
                act.wait_ge(s["sp_done"], 1)
                me.wait()
                act.activation(r_e.rearrange("p (t j) -> p j t", j=NJ)[:, 0, :], r_z, ACT.Exp, scale=r_negA)\
                    .then_inc(s["decay"], 1)
                act.wait_ge(s["cols_mm"], 1)
                act.activation(cols[:, 0:112], ps[:, 5, 0:112], ACT.Copy).then_inc(s["cols"], 1)
                for h in range(NH):
                    act.wait_ge(s["kt_mm"], h + 1)
                    for c in range(NC):
                        if me.n > 2:
                            me.wait()
                        me.did(act.activation(junk[:, :], ps[:, h % 2, c * P:(c + 1) * P], ACT.Square,
                                              accum_out=knorm[:, h, c:c + 1]))
                    act.activation(ktm[:, h, :, :].rearrange("p c d -> p (c d)"), ps[:, h % 2, :], ACT.Copy)\
                        .then_inc(s["kt_sb"], 1)
                    if h % 2 == 0:
                        act.wait_ge(s["qt_mm"], h // 2 + 1)
                        for x in range(2):
                            for t in range(TT):
                                me.wait()
                                me.did(act.activation(junk[:, :],
                                                      ps[:, 2 + h // 2 % 2, (2 * x + t) * P:(2 * x + t + 1) * P],
                                                      ACT.Square, accum_out=qnorm[:, h + x, t:t + 1]))
                        act.activation(qtm[:, h:h + 2, :, :].rearrange("p h t d -> p (h t d)"),
                                       ps[:, 2 + h // 2 % 2, :], ACT.Copy).then_inc(s["qt_sb"], 1)
                me.wait()
                act.activation(knorm[:, :, :], knorm[:, :, :], ACT.Sqrt).then_inc(s["norms"], 1)
                act.activation(qnorm[:, :, :], qnorm[:, :, :], ACT.Sqrt).then_inc(s["norms"], 1)
                for h in range(1, NH, 2):
                    act.wait_ge(s["kn_mm"], h + 1)
                    act.activation(keyT[:, h, :], ps[:, 1, :], ACT.Copy).then_inc(s["kn_a"], 1)
                for j in range(4):
                    act.wait_ge(s["qn_mm"], j + 1)
                    act.activation(QT[:, 2 * j:2 * j + 2, :].rearrange("p h t -> p (h t)"), ps[:, 2 + j % 2, :],
                                   ACT.Copy).then_inc(s["qn_sb"], 1)
                act.wait_ge(s["scan"], NH)
                for h in range(1, NH, 2):
                    act.wait_ge(s["kb_mm"], h + 1)
                    act.activation(KbT[:, h, :], ps[:, 5, :], ACT.Copy).then_inc(s["kb_a"], 1)
                for j in range(4):
                    act.wait_ge(s["qc_mm"], j + 1)
                    act.activation(QcT[:, 2 * j:2 * j + 2, :].rearrange("p h t -> p (h t)"), ps[:, j % 2, :],
                                   ACT.Copy).then_inc(s["qc_sb"], 1)
                for n in range(NH, NH * LEVELS):
                    act.wait_ge(s["y_mm"], n + 1)
                    if n == NH:
                        act.wait_ge(s["p_mm"], 4)
                    if n - NH >= 2:
                        act.wait_ge(s["pp_mm"], n - NH - 1)
                    act.activation(Y[:, n % 2, :, :].rearrange("p c d -> p (c d)"), ps[:, n % 2, :], ACT.Copy)\
                        .then_inc(s["y_sb"], 1)
                for c in range(NC):
                    for x in range(2):
                        act.wait_ge(s["u_mm"], 2 * c + x + 1)
                        if c:
                            act.wait_ge(s["o_mm"], c)
                        act.activation(U[:, 4 * x:4 * x + 4, :].rearrange("p h d -> p (h d)"), ps[:, 2 + x, :],
                                       ACT.Copy).then_inc(s["u_sb"], 1)
                    act.wait_ge(s["o_mm"], c + 1)
                    act.activation(OT[:, :, c * CTOK:(c + 1) * CTOK],
                                   ps[:, 6 + c % 2, :].rearrange("p (h t) -> p h t", h=NH), ACT.Copy)\
                        .then_inc(s["o_sb"], 1)
                act.wait_ge(s["o_sb"], NC)
                act.wait_ge(s["r_sb"], 2 * NC)
                act.activation(sq[:, :, :], OT[:, :, :], ACT.Square).then_inc(s["sq"], 1)
                act.wait_ge(s["ss_mm"], 1)
                act.activation(srow[:, 0:TOK], ps[0:8, 0, 0:TOK], ACT.Sqrt, bias=e.eps[0:8, :], scale=1.0 / P)\
                    .then_inc(s["rms"], 1)

            @block.gpsimd
            def _(pool):
                pool.wait_ge(s["normed"], 1)
                pool.wait_ge(s["vt_mm"], NH)
                for c in range(NC):
                    last = pool.tensor_tensor(kb[:, :, c, :], ktm[:, :, c, :], bcast_last(beta[:, c, :], (P, NH, P)),
                                              ALU.mult)
                    last.then_inc(s["pool_self"], 1)
                pool.wait_ge(s["pool_self"], NC)
                pool.nop().then_inc(s["kb"], 1)
                pool.wait_ge(s["qn_mm"], 4)
                for t in range(TT):
                    pool.tensor_tensor(qtm[:, :, t, :], qtm[:, :, t, :], bcast_last(ctok[:, t, :], (P, NH, P)),
                                       ALU.mult).then_inc(s["pool_self"], 1)
                pool.wait_ge(s["pool_self"], NC + TT)
                pool.nop().then_inc(s["qc"], 1)
                for n in range(NH * LEVELS):
                    l, h = divmod(n, NH)
                    pool.wait_ge(s["g_sb"], h + 1)
                    if n == 0:
                        pool.wait_ge(s["p_mm"], 4)
                    if n >= 2:
                        pool.wait_ge(s["y_mm"], n - 1)
                        if n - 2 < NH:
                            pool.wait_ge(s["xt_up"], n - 1)
                    level = e.fixed[:, C_LEVEL + l * P:C_LEVEL + (l + 1) * P]
                    pool.tensor_tensor(CTm[:, n % 2, :, :], AT[:, h, :, :],
                                       level.unsqueeze(1).broadcast_to((P, NC, P)), ALU.mult).then_inc(s["ct"], 1)
                for c in range(1, NC - 1):
                    for x in range(2):
                        pool.wait_ge(s["s_new"], 2 * (c - 1) + x + 1)
                        if c >= 2:
                            pool.wait_ge(s["o_mm"], c)
                        hh = slice(4 * x, 4 * x + 4)
                        pool.tensor_tensor(S[:, (c + 1) % 2, hh, :], S[:, c % 2, hh, :],
                                           bcast_last(cend[:, hh, c], (P, 4, P)), ALU.mult).then_inc(s["sc"], 1)

            @block.vector
            def _(dve):
                me = Chain(dve, s["dve_self"])
                ln_vector(dve, e, s)
                dve.memset(pad[:, :, :], 0.0).then_inc(s["pads"], 1)
                for i in range(CONV_TILES):
                    dve.wait_ge(s["tile_ev"], i + 1)
                    if i >= 2:
                        dve.wait_ge(s["silu"], i - 1)
                    x, y = pad[:, i % 2, :], conv[:, i % 2, :]
                    me.did(dve.tensor_scalar(y, x[:, 0:TOK], taps(i, 0), None, ALU.mult))
                    for j in range(1, 4):
                        me.wait()
                        last = dve.scalar_tensor_tensor(out=y, in0=x[:, j:j + TOK], scalar=taps(i, j), in1=y,
                                                        op0=ALU.mult, op1=ALU.add)
                        if j < 3:
                            me.did(last)
                    last.then_inc(s["conv"], 1)
                dve.wait_ge(s["rows_mm"], 1)
                me.did(dve.memset(r_e, 1.0))
                me.did(dve.memset(r_0, 0.0))
                me.did(dve.tensor_scalar(r_x, ps[0:8, 4, 0:TOK], small[0:8, S_AHEAD + 1:S_AHEAD + 2], None, ALU.add))
                me.wait()
                softplus_vector(dve, me, r_x, r_a, r_y, r_z, s, r_z)
                dve.wait_ge(s["beta"], 2)
                dve.tensor_scalar(r_b, r_b, 2.0, None, ALU.mult).then_inc(s["rows"], 1)
                dve.wait_ge(s["decay"], 1)
                me.did(dve.tensor_copy(r_e0, r_e))
                me.wait()
                me.did(dve.memset(r_e0[:, 0:STEPS:P], 0.0))
                for c in range(NC):
                    at = slice(c * P, (c + 1) * P)
                    me.did(dve.tensor_tensor_scan(r_c[:, at], r_e[:, at], r_0, 1.0, ALU.mult, ALU.add))
                me.wait()
                dve.nop().then_inc(s["rows"], 1)
                for h in range(NH):
                    dve.wait_ge(s["eb_mm"], h + 1)
                    dve.tensor_tensor_scan(DT[:, h, :], ps[:, 6 + h % 2, :], ident4, 0.0, ALU.mult, ALU.add)\
                        .then_inc(s["scan"], 1)
                dve.wait_ge(s["cols"], 1)
                me.did(dve.scalar_tensor_tensor(out=nbc[:, :, :], in0=beta, scalar=-1.0, in1=cum, op0=ALU.mult,
                                                op1=ALU.mult))
                dve.wait_ge(s["scan"], NH)
                me.did(dve.tensor_copy(dend[:, :, :], DT[:, :, P - 1:STEPS:P]))
                for h in range(NH):
                    dve.wait_ge(s["vt_mm"], h + 1)
                    dve.tensor_tensor(bV[:, h, :, :], ps[:, 4 + h % 2, :].rearrange("p (c d) -> p c d", c=NC),
                                      bcast_last(beta[:, :, h], (P, NC, P)), ALU.mult).then_inc(s["vt_sb"], 1)
                dve.wait_ge(s["norms"], 2)
                for v, f in ((knorm, 1.0), (qnorm, 1.0 / float(np.sqrt(P)))):
                    me.did(dve.tensor_scalar(v[:, :, :], v[:, :, :], 1e-12, None, ALU.max))
                    me.wait()
                    me.did(dve.reciprocal(v[:, :, :], v[:, :, :]))
                    me.wait()
                    if f != 1.0:
                        me.did(dve.tensor_scalar(v[:, :, :], v[:, :, :], f, None, ALU.mult))
                        me.wait()
                dve.wait_ge(s["kt_sb"], NH)
                dve.tensor_tensor(ktm[:, :, :, :].rearrange("p h c d -> p (h c) d"),
                                  ktm[:, :, :, :].rearrange("p h c d -> p (h c) d"),
                                  bcast_last(knorm[:, :, :].rearrange("p h c -> p (h c)"), (P, NH * NC, P)),
                                  ALU.mult).then_inc(s["normed"], 1)
                dve.wait_ge(s["qt_sb"], 4)
                dve.tensor_tensor(qtm[:, :, :, :].rearrange("p h c d -> p (h c) d"),
                                  qtm[:, :, :, :].rearrange("p h c d -> p (h c) d"),
                                  bcast_last(qnorm[:, :, :].rearrange("p h c -> p (h c)"), (P, NH * TT, P)),
                                  ALU.mult).then_inc(s["normed"], 1)
                for h in range(0, NH, 2):
                    dve.wait_ge(s["kn_mm"], h + 1)
                    dve.tensor_copy(keyT[:, h, :], ps[:, 0, :]).then_inc(s["kn_d"], 1)
                for h in range(0, NH, 2):
                    dve.wait_ge(s["kb_mm"], h + 1)
                    dve.tensor_copy(KbT[:, h, :], ps[:, 4, :]).then_inc(s["kb_d"], 1)
                dve.wait_ge(s["kn_mm"], NH)
                dve.wait_ge(s["kb"], 1)
                me.wait()
                dve.wait_ge(s["normed"], 1)
                dve.tensor_tensor(ktm[:, :, :, :].rearrange("p h c d -> p (h c) d"),
                                  ktm[:, :, :, :].rearrange("p h c d -> p (h c) d"),
                                  bcast_last(dend[:, :, :].rearrange("p h c -> p (h c)"), (P, NH * NC, P)),
                                  ALU.mult).then_inc(s["kd"], 1)
                for h in range(NH):
                    dve.wait_ge(s["g_mm"], h + 1)
                    if h == 0:
                        dve.wait_ge(s["kb_mm"], NH)
                    dve.tensor_tensor(AT[:, h, :, :].rearrange("p c d -> p (c d)"), ps[:, 2 + h % 2, :], DT[:, h, :],
                                      ALU.mult).then_inc(s["g_sb"], 1)
                    if h % 2:
                        dve.wait_ge(s["p_mm"], h // 2 + 1)
                        if h == 1:
                            dve.wait_ge(s["qc_mm"], 4)
                        dve.tensor_tensor(
                            PT[:, h - 1:h + 1, :, :].rearrange("p h c t -> p (h c) t"),
                            ps[:, 6 + h // 2 % 2, :].rearrange("p (a t) -> p a t", t=CTOK),
                            DT[:, h - 1:h + 1, :].rearrange("p h (c t j) -> p (h c) t j", c=NC, j=NJ)[:, :, :, 1],
                            ALU.mult).then_inc(s["p_sb"], 1)
                dve.wait_ge(s["g_sb"], NH)
                dve.wait_ge(s["p_sb"], 4)
                for n in range(NH * LEVELS):
                    l, h = divmod(n, NH)
                    x, xt = (v[:, h, :, :].rearrange("p c d -> p (c d)") for v in (X, XT))
                    if l == 0:
                        dve.wait_ge(s["y_mm"], n + 1)
                        dve.tensor_tensor(x, ident4, ps[:, n % 2, :], ALU.subtract).then_inc(s["x_up"], 1)
                        dve.wait_ge(s["g_mm"], NH)
                        dve.tensor_tensor(xt, ident4, CTm[:, n % 2, :, :].rearrange("p c d -> p (c d)"),
                                          ALU.subtract).then_inc(s["xt_up"], 1)
                        continue
                    dve.wait_ge(s["pp_mm"], n - NH + 1)
                    dve.wait_ge(s["xt_up"], n - NH + 1)
                    if l < LEVELS - 1:
                        dve.wait_ge(s["x_up"], n - NH + 1)
                        dve.tensor_tensor(x, x, ps[:, 2 + n % 2, :], ALU.subtract).then_inc(s["x_up"], 1)
                    dve.tensor_tensor(xt, xt, ps[:, 4 + n % 2, :], ALU.subtract).then_inc(s["xt_up"], 1)
                dve.wait_ge(s["ct"], NH * LEVELS)
                for c in range(NC):
                    for x in range(2):
                        hh = slice(4 * x, 4 * x + 4)
                        if c == 0:
                            dve.tensor_copy(R[:, hh, :], bV[:, hh, c, :]).then_inc(s["r_sb"], 1)
                            continue
                        dve.wait_ge(s["ks_mm"], 2 * (c - 1) + x + 1)
                        dve.wait_ge(s["u_mm"], 2 * (c - 1) + x + 1)
                        me.did(dve.tensor_tensor(R[:, hh, :], ps[:, x, :].rearrange("p (h d) -> p h d", h=4),
                                                 bcast_last(nbc[:, c, hh], (P, 4, P)), ALU.mult))
                        me.wait()
                        dve.tensor_tensor(R[:, hh, :], R[:, hh, :], bV[:, hh, c, :], ALU.add).then_inc(s["r_sb"], 1)
                    if c == NC - 1:
                        continue
                    for x in range(2):
                        hh = slice(4 * x, 4 * x + 4)
                        dve.wait_ge(s["ds_mm"], 2 * c + x + 1)
                        new = S[:, (c + 1) % 2, hh, :]
                        add = ps[:, 4 + x, :].rearrange("p (h d) -> p h d", h=4)
                        if c == 0:
                            dve.tensor_copy(new, add).then_inc(s["s_new"], 1)
                            continue
                        dve.wait_ge(s["sc"], 2 * (c - 1) + x + 1)
                        dve.tensor_tensor(new, new, add, ALU.add).then_inc(s["s_new"], 1)
                dve.wait_ge(s["o_sb"], NC)
                dve.wait_ge(s["r_sb"], 2 * NC)
                dve.scalar_tensor_tensor(out=yT[:, :, :], in0=OT[:, :, :], scalar=small[:, S_ANORM:S_ANORM + 1],
                                         in1=gate[:, :, :], op0=ALU.mult, op1=ALU.mult).then_inc(s["gated"], 1)
                dve.wait_ge(s["rms"], 1)
                dve.reciprocal(srow[:, TOK:2 * TOK], srow[:, 0:TOK]).then_inc(s["rinv"], 1)
                dve.wait_ge(s["rb_mm"], 1)
                dve.wait_ge(s["gated"], 1)
                flat = yT[:, :, :].rearrange("p h t -> p (h t)")
                dve.tensor_tensor(flat, flat, ps[:, 2:6, :].rearrange("p a n -> p (a n)"), ALU.mult)\
                    .then_inc(s["y"], 1)
                for t in range(TT):
                    dve.wait_ge(s["out_mm"], t + 1)
                    me.did(dve.tensor_tensor(e.xres[:, t, :], e.xres[:, t, :], ps[:, 6 + t, :], ALU.add))
        clear_sems(nc, s)
    e.n0 += N_L0A



Q_BIG = 384
HALF = Q_BIG // 2
_c = np.arange(Q_BIG)
Q_TILES = [_c[0:128], _c[192:320], np.concatenate([_c[128:192], _c[320:384]])]
Q_TURNED = np.concatenate([_c[320:384], _c[128:192]])
L1X_WQ, L1X_WKC, L1X_WQR, L1X_WKR = 0, 512, 1024, 1216
L1X_HEAD = 1344


def open_rope(e, ctx):
    nc = e.nc

    def sb(name, shape):
        return ctx.enter_context(nc.sbuf_tensor("rope_" + name, shape, F32))
    e.kvr = sb("kvr", [P, CT, P])
    e.rope = {n: ctx.enter_context(nc.semaphore("rope_" + n)) for n in ("in", "cos", "sin", "done")}


def open_rope_tables(e, ctx):
    e.rbuf = ctx.enter_context(e.nc.sbuf_tensor("rope_buf", [P, 2 * CTX], F32))


def rope_sync(sp, e):
    sp.dma_start(e.rbuf[:, 0:4096], e.io["ctx"]).then_inc(e.rope["in"], 16)
    sp.dma_start(e.rbuf[:, 4096:8192], e.io["rope_k"]).then_inc(e.rope["in"], 16)


def rope_pool(pool, e):
    raw = e.rbuf[:, 0:4096].rearrange("p (t d) -> p t d", d=P)
    cos = e.rbuf[:, 4096:6144].rearrange("p (t f) -> p t f", f=64)
    sin = e.rbuf[:, 6144:8192].rearrange("p (t f) -> p t f", f=64)
    H = P // 2

    def pairs(ap):
        return ap.rearrange("p t (f two) -> p t f two", two=2)
    pool.wait_ge(e.rope["in"], 32)
    pool.tensor_tensor(pairs(e.kvr[:, :, :]), pairs(raw), bcast_last(cos, (P, CT, 64, 2)), ALU.mult)\
        .then_inc(e.rope["cos"], 1)
    pool.wait_ge(e.rope["cos"], 1)
    prod = e.rbuf[:, 4096:6144].rearrange("p (t f) -> p t f", f=H)
    pool.tensor_tensor(pairs(prod), pairs(raw[:, :, H:P]), bcast_last(sin[:, :, 0:32], (P, CT, 32, 2)), ALU.mult)\
        .then_inc(e.rope["sin"], 1)
    pool.wait_ge(e.rope["sin"], 1)
    pool.tensor_tensor(e.kvr[:, :, 0:H], e.kvr[:, :, 0:H], prod, ALU.add).then_inc(e.rope["done"], 1)
    pool.wait_ge(e.rope["done"], 1)
    pool.tensor_tensor(pairs(prod), pairs(raw[:, :, 0:H]), bcast_last(sin[:, :, 32:64], (P, CT, 32, 2)), ALU.mult)\
        .then_inc(e.rope["sin"], 1)
    pool.wait_ge(e.rope["sin"], 2)
    pool.tensor_tensor(e.kvr[:, :, H:P], e.kvr[:, :, H:P], prod, ALU.add).then_inc(e.rope["done"], 1)


def layer_l1x(e):
    nc, ps = e.nc, e.ps
    n0 = e.n0
    NH = 16
    KB = 4
    HT = CT // 2
    SUBS = 8
    PAIRS = NH // 2
    with ExitStack() as ctx:
        def sb(name, shape, dt=F32, scope=ctx):
            return scope.enter_context(nc.sbuf_tensor("l1x_" + name, shape, dt))
        s = layer_sems(nc, ctx, "l1x", LN_SEMS + [
            "dve_self", "tables", "kvT_mm", "kvT_hi", "kvT_lo", "kv_hi", "kv_lo", "q_mm", "q_sb", "big_mm", "big_d", "rotated", "qr_mm", "qr_sb",
            "q2_mm", "q2_sb", "cur_in", "cur", "score_mm", "tops", "top", "exp", "turn_mm", "p_hi", "p_lo", "ctx_mm",
            "taken", "take", "rescale", "cT_mm", "cT_sb", "lat_mm", "lat_sb", "out_mm"])
        kvT_hi, kvT_lo = sb("kvT_hi", [P, CTX], F32R), sb("kvT_lo", [P, CTX], F32R)
        kv = sb("kv", [P, CT, 2, P], F32R)
        with ExitStack() as scope:
            rope_q = sb("rope_q", [P, 2, 3, TOK], scope=scope)
            q1 = sb("q1", [P, 2, TOK], scope=scope)
            rc = sb("rc", [P, 3, TOK], scope=scope)
            qr = sb("qr", [64, 2, TOK], scope=scope)
        pT_hi, pT_lo = sb("pT_hi", [P, 4, 4, P], F32R), sb("pT_lo", [P, 4, 4, P], F32R)
        rs = sb("rs", [P, 2, 3, TOK])
        q2T = sb("q2T", [P, NH, TOK])
        cur = sb("cur", [P, 2, TOK])
        cur_hi, cur_lo = sb("cur_hi", [P, 2, TOK], F32R), sb("cur_lo", [P, 2, TOK], F32R)
        cn = q2T[:, :, :].rearrange("p h (t d) -> p h t d", t=TT)
        tops = sb("tops", [P, 5])
        tmax = sb("tmax", [P, TT, 2])
        ntop = sb("ntop", [P, TT, 2])
        sums = sb("sums", [P, TT, 2, 2])
        ssum = sb("ssum", [P, 2])
        scale = sb("scale", [P, TT])
        den = sb("den", [P, TT])
        c1 = sb("c1", [P, TT, P])
        prob = e.kvr[:, :, :].rearrange("p t d -> p (t d)").rearrange("p (b n) -> p b n", b=2)
        ccT = rs
        cx = e.kvr[:, :, :].rearrange("p t d -> p (t d)").rearrange("p (h t) -> p h t", h=NH)

        TAKE = 6

        def all_steps(eng, step):
            steps = [None, None] + [(0, u) for u in range(SUBS)]
            for u in range(SUBS):
                step(steps[u + 2], steps[u + 1], steps[u])
            with eng.Fori(1, PAIRS) as i:
                steps = [(i - 1, SUBS - 2), (i - 1, SUBS - 1)] + [(i, u) for u in range(SUBS)]
                for u in range(SUBS):
                    step(steps[u + 2], steps[u + 1], steps[u])
            last = PAIRS - 1
            step(None, (last, SUBS - 1), (last, SUBS - 2))
            step(None, None, (last, SUBS - 1))

        def head(w, h):
            return w[:, (h % 2) * L1X_HEAD:(h % 2 + 1) * L1X_HEAD]

        with nc.Block(no_gpsimd_drain=True) as block:
            @block.sync
            def _(sp):
                sp.dma_start(rope_q[:, :, :, :].rearrange("p a b c -> p (a b c)"), e.io["rope_q"])\
                    .then_inc(s["tables"], 16)
                stream(sp, e, n0, N_L1X)

            @block.tensor
            def _(pe):
                pe.wait_ge(e.rope["done"], 2)
                for g in range(CT // 4):
                    if g >= 6:
                        pe.wait_ge(s["kvT_lo"], g - 5)
                    for j in range(4):
                        last = pe.transpose(ps[:, 2 + g % 6, j * P:(j + 1) * P], e.kvr[:, 4 * g + j, :], e.ident)
                    last.then_inc(s["kvT_mm"], 1)
                ln_tensor(pe, e, s)
                pe.wait_ge(s["kvT_lo"], CT // 4)
                used = [False]

                def q_of(h):
                    w = head(slot_in(pe, e, n0 + h // 2), h)
                    if h >= 2:
                        pe.wait_ge(s["q_sb"], h - 1)
                    for k in range(KT):
                        last = pe.matmul(ps[:, h % 2, 0:TOK], w[:, L1X_WQ + k * P:L1X_WQ + (k + 1) * P],
                                         e.xnT[:, k, :], start=(k == 0), stop=(k == KT - 1))
                        if k == 0 and used[0]:
                            last.then_inc(e.w_used, 1)
                            used[0] = False
                    last.then_inc(s["q_mm"], 1)

                def big_of(h):
                    w = head(e.ring[:, (n0 + h // 2) % RING, :], h)
                    pe.wait_ge(s["q_sb"], h + 1)
                    if h:
                        pe.wait_ge(s["big_d"], h)
                    for f in range(4):
                        last = pe.matmul(ps[:, 2 + f // 2, (f % 2) * TOK:(f % 2 + 1) * TOK],
                                         w[:, L1X_WKC + f * P:L1X_WKC + (f + 1) * P], q1[:, h % 2, :],
                                         start=True, stop=True)
                    last.then_inc(s["big_mm"], 1)

                def qr_of(h):
                    w = head(e.ring[:, (n0 + h // 2) % RING, :], h)
                    pe.wait_ge(s["rotated"], h + 1)
                    if h >= 2:
                        pe.wait_ge(s["qr_sb"], h - 1)
                    for f in range(3):
                        last = pe.matmul(ps[0:64, 4 + h % 2, 0:TOK], w[:, L1X_WQR + f * 64:L1X_WQR + (f + 1) * 64],
                                         rs[:, h % 2, f, :], start=(f == 0), stop=(f == 2))
                    last.then_inc(s["qr_mm"], 1)

                def q2_of(h):
                    w = head(e.ring[:, (n0 + h // 2) % RING, :], h)
                    pe.wait_ge(s["qr_sb"], h + 1)
                    if h >= 2:
                        pe.wait_ge(s["q2_sb"], h - 1)
                    pe.matmul(ps[:, 6 + h % 2, 0:TOK], w[0:64, L1X_WKR:L1X_WKR + P], qr[:, h % 2, :],
                              start=True, stop=True).then_inc(s["q2_mm"], 1)
                    if h % 2:
                        used[0] = True

                for h in range(NH + 3):
                    if h < NH:
                        q_of(h)
                    if 1 <= h <= NH:
                        big_of(h - 1)
                    if 2 <= h <= NH + 1:
                        qr_of(h - 2)
                    if h >= 3:
                        if used[0]:
                            pe.wait_ge(s["q2_mm"], h - 3)
                            pe.nop().then_inc(e.w_used, 1)
                            used[0] = False
                        q2_of(h - 3)
                pe.wait_ge(s["q2_mm"], NH)
                pe.nop().then_inc(e.w_used, 1)
                pe.wait_ge(s["q2_sb"], NH)

                def score(at, b):
                    turn, u = at
                    g = turn * SUBS + u
                    hh, qt, half = u // 4, u // 2 % 2, u % 2
                    if b == 0 and u % 4 == 0:
                        pe.wait_ge(s["cur"], turn * 2 + (hh + 1))
                    if b % 2 == 0 and not (isinstance(turn, int) and g == 0):
                        pe.wait_ge(s["exp"], g * 2 - 1 + b // 2)
                    out, q = ps[:, b, :], slice(qt * P, (qt + 1) * P)
                    k = slice(half * 2048 + b * 512, half * 2048 + (b + 1) * 512)
                    pe.matmul(out, cur_hi[:, hh, q], kvT_hi[:, k], start=True, stop=False)
                    pe.matmul(out, cur_hi[:, hh, q], kvT_lo[:, k], start=False, stop=False)
                    pe.matmul(out, cur_lo[:, hh, q], kvT_hi[:, k], start=False, stop=True)\
                        .then_inc(s["score_mm"], 1)

                def turn_group(at, q):
                    turn, u = at
                    n = (turn * SUBS + u) * 4 + q
                    if not (isinstance(turn, int) and n < 2):
                        pe.wait_ge(s["p_lo"], n - 1)
                    pe.wait_ge(s["exp"], (turn * SUBS + u) * 2 + 1 + q // 2)
                    for j in range(4):
                        t = 4 * q + j
                        last = pe.transpose(ps[:, 4 + q % 2, j * P:(j + 1) * P], prob[:, u % 2, t * P:(t + 1) * P],
                                            e.ident)
                    last.then_inc(s["turn_mm"], 1)

                def ctx_group(at, q):
                    turn, u = at
                    g = turn * SUBS + u
                    pe.wait_ge(s["p_lo"], g * 4 + (q + 1))
                    if q == 0 and not (isinstance(turn, int) and g < 2):
                        pe.wait_ge(s["taken"], g - 1)
                    if q == 0 and isinstance(turn, int) and g == 0:
                        pe.wait_ge(s["kv_lo"], 1)
                    for j in range(4):
                        t = 4 * q + j
                        k = (u % 2) * HT + t
                        pe.matmul(ps[:, 6 + u % 2, 0:2 * P], pT_hi[:, q, j, :],
                                  kv[:, k, :, :].rearrange("p a d -> p (a d)"), start=(t == 0), stop=False,
                                  skip_group_check=True)
                        last = pe.matmul(ps[:, 6 + u % 2, 0:P], pT_lo[:, q, j, :], kv[:, k, 0, :],
                                         start=False, stop=(t == HT - 1), skip_group_check=True)
                    last.then_inc(s["ctx_mm"], 1)

                def pe_step(at, before, before2):
                    if at:
                        score(at, 0)
                        score(at, 1)
                    if before2:
                        ctx_group(before2, 3)
                    if before:
                        turn_group(before, 0)
                    if at:
                        score(at, 2)
                    if before:
                        turn_group(before, 1)
                    if at:
                        score(at, 3)
                    if before:
                        ctx_group(before, 0)
                        turn_group(before, 2)
                        ctx_group(before, 1)
                        turn_group(before, 3)
                        ctx_group(before, 2)

                all_steps(pe, pe_step)

                def turn_pair(j):
                    if j >= 2:
                        pe.wait_ge(s["cT_sb"], j - 1)
                    for x in range(2):
                        for t in range(TT):
                            last = pe.transpose(ps[:, j % 2, x * TOK + t * P:x * TOK + (t + 1) * P],
                                                cn[:, 2 * j + x, t, :], e.ident)
                    last.then_inc(s["cT_mm"], 1)

                def latent(j):
                    w = slot_in(pe, e, n0 + PAIRS + j // 2)
                    pe.wait_ge(s["cT_sb"], j + 1)
                    if j >= 2:
                        pe.wait_ge(s["lat_sb"], j - 1)
                    for x in range(2):
                        h = 2 * j + x
                        at = 4 * D + (h % 4) * P
                        last = pe.matmul(ps[:, 2 + j % 2, x * TOK:(x + 1) * TOK], w[:, at:at + P],
                                         ccT[:, j % 2, x, :], start=True, stop=True)
                    last.then_inc(s["lat_mm"], 1)

                def project(j):
                    pe.wait_ge(s["lat_sb"], j + 1)
                    w = slot_in(pe, e, n0 + PAIRS + j // 2)
                    for x in range(2):
                        h = 2 * j + x
                        for t in range(TT):
                            last = pe.matmul(ps[:, 6 + t, :], cx[:, h, t * P:(t + 1) * P],
                                             w[:, (h % 4) * D:(h % 4 + 1) * D], start=(h == 0), stop=(h == NH - 1))
                            if j % 2 == 0 and x == 0 and t == 0 and j:
                                last.then_inc(e.w_used, 1)
                    if j == PAIRS - 1:
                        last.then_inc(s["out_mm"], 1)

                pe.wait_ge(s["take"], TAKE * 4 * PAIRS)
                for j in range(PAIRS + 2):
                    if j < PAIRS:
                        turn_pair(j)
                    if 1 <= j <= PAIRS:
                        latent(j - 1)
                    if j >= 2:
                        project(j - 2)
                pe.wait_ge(s["out_mm"], 1)
                pe.nop().then_inc(e.w_used, 1)

            @block.scalar
            def _(act):
                for g in range(CT // 4):
                    act.wait_ge(s["kvT_mm"], g + 1)
                    act.activation(kvT_hi[:, g * 512:(g + 1) * 512], ps[:, 2 + g % 6, :], ACT.Copy)\
                        .then_inc(s["kvT_hi"], 1)
                ln_scalar(act, e, s)
                for h in range(NH + 3):
                    if h == 4:
                        act.activation(kv[:, :, 0, :], e.kvr[:, :, :], ACT.Copy).then_inc(s["kv_hi"], 1)
                    if h < NH:
                        act.wait_ge(s["q_mm"], h + 1)
                        if h >= 2:
                            act.wait_ge(s["big_mm"], h - 1)
                        act.activation(q1[:, h % 2, :], ps[:, h % 2, 0:TOK], ACT.Copy).then_inc(s["q_sb"], 1)
                    if 2 <= h <= NH + 1:
                        x = h - 2
                        act.wait_ge(s["qr_mm"], x + 1)
                        if x >= 2:
                            act.wait_ge(s["q2_mm"], x - 1)
                        act.activation(qr[:, x % 2, :], ps[0:64, 4 + x % 2, 0:TOK], ACT.Copy)\
                            .then_inc(s["qr_sb"], 1)
                    if h >= 3:
                        x = h - 3
                        act.wait_ge(s["q2_mm"], x + 1)
                        act.activation(q2T[:, x, :], ps[:, 6 + x % 2, 0:TOK], ACT.Copy).then_inc(s["q2_sb"], 1)

                def hi(at, q):
                    turn, u = at
                    n = (turn * SUBS + u) * 4 + q
                    act.wait_ge(s["turn_mm"], n + 1)
                    if not (isinstance(turn, int) and n < 4):
                        act.wait_ge(s["ctx_mm"], n - 3)
                    act.activation(pT_hi[:, q, :, :].rearrange("p a b -> p (a b)"), ps[:, 4 + q % 2, :], ACT.Copy)\
                        .then_inc(s["p_hi"], 1)

                def exps(at, part):
                    turn, u = at
                    g = turn * SUBS + u
                    qt, half = u // 2 % 2, u % 2
                    act.wait_ge(s["top"], g + 1)
                    act.activation(prob[:, u % 2, part * 1024:(part + 1) * 1024],
                                   ps[:, 2 * part:2 * part + 2, :].rearrange("p a b -> p (a b)"), ACT.Exp,
                                   bias=ntop[:, qt, half:half + 1], accum_out=sums[:, qt, half, part:part + 1])\
                        .then_inc(s["exp"], 1)
                    if half and part:
                        act.activation(scale[:, qt:qt + 1], tmax[:, qt, 0:1], ACT.Exp, bias=ntop[:, qt, 1:2])\
                            .then_inc(s["rescale"], 1)

                def act_step(at, before, before2):
                    if before:
                        hi(before, 0)
                        hi(before, 1)
                        hi(before, 2)
                    if at:
                        exps(at, 0)
                    if before:
                        hi(before, 3)
                    if at:
                        exps(at, 1)

                act.wait_ge(s["kv_lo"], 1)
                all_steps(act, act_step)
                for j in range(PAIRS):
                    act.wait_ge(s["lat_mm"], j + 1)
                    act.activation(cx[:, 2 * j:2 * j + 2, :].rearrange("p a b -> p (a b)"), ps[:, 2 + j % 2, :],
                                   ACT.Copy).then_inc(s["lat_sb"], 1)

            @block.gpsimd
            def _(pool):
                def fetch(x, source):
                    pool.tensor_copy(cur[:, x, :], source).then_inc(s["cur_in"], 1)
                    pool.tensor_copy(cur_hi[:, x, :], source).then_inc(s["cur_in"], 1)

                def rest(x):
                    pool.tensor_tensor(cur_lo[:, x, :], cur[:, x, :], cur_hi[:, x, :].bitcast(F32), ALU.subtract)\
                        .then_inc(s["cur"], 1)

                pool.wait_ge(s["q2_sb"], NH)
                for x in range(2):
                    fetch(x, q2T[:, x, :])
                    pool.wait_ge(s["cur_in"], 2 * (x + 1))
                    rest(x)
                with pool.Fori(1, PAIRS) as i:
                    for x in range(2):
                        pool.wait_ge(s["score_mm"], i * (4 * SUBS) + (x - 1) * 16)
                        pool.wait_ge(s["cur"], i * 2 + x)
                        fetch(x, q2T[:, bass.ds(i * 2 + x, 1), :].rearrange("p a b -> p (a b)"))
                        pool.wait_ge(s["cur_in"], i * 4 + (2 * x + 2))
                        rest(x)

            @block.vector
            def _(dve):
                me = Chain(dve, s["dve_self"])
                for g in range(CT // 4):
                    dve.wait_ge(s["kvT_hi"], g + 1)
                    dve.tensor_tensor(kvT_lo[:, g * 512:(g + 1) * 512], ps[:, 2 + g % 6, :],
                                      kvT_hi[:, g * 512:(g + 1) * 512].bitcast(F32), ALU.subtract)\
                        .then_inc(s["kvT_lo"], 1)
                ln_vector(dve, e, s)
                dve.wait_ge(s["tables"], 16)
                for h in range(NH):
                    if h == 4:
                        dve.wait_ge(s["kv_hi"], 1)
                        dve.tensor_tensor(kv[:, :, 1, :], e.kvr[:, :, :], kv[:, :, 0, :].bitcast(F32), ALU.subtract)\
                            .then_inc(s["kv_lo"], 1)
                    dve.wait_ge(s["big_mm"], h + 1)
                    if h:
                        dve.wait_ge(s["rotated"], h)
                    x01, x22 = ps[:, 2, :].rearrange("p (a n) -> p a n", a=2), ps[:, 3, :].rearrange("p (a n) -> p a n", a=2)
                    if h >= 2:
                        dve.wait_ge(s["qr_mm"], h - 1)
                    me.did(dve.tensor_tensor(rc[:, :, :].rearrange("p a n -> p (a n)"),
                                             ps[:, 2:4, :].rearrange("p a n -> p (a n)")[:, 0:3 * TOK],
                                             rope_q[:, 0, :, :].rearrange("p a n -> p (a n)"), ALU.mult))
                    me.did(dve.tensor_tensor(rs[:, h % 2, 0, :], x01[:, 1, :], rope_q[:, 1, 0, :], ALU.mult))
                    me.did(dve.tensor_tensor(rs[:, h % 2, 1, :], x01[:, 0, :], rope_q[:, 1, 1, :], ALU.mult))
                    dve.tensor_tensor(rs[:, h % 2, 2, :], x22[:, 1, :], rope_q[:, 1, 2, :], ALU.mult)\
                        .then_inc(s["big_d"], 1)
                    me.wait()
                    dve.wait_ge(s["big_d"], h + 1)
                    dve.tensor_tensor(rs[:, h % 2, :, :], rs[:, h % 2, :, :], rc[:, :, :], ALU.add)\
                        .then_inc(s["rotated"], 1)
                dve.wait_ge(s["rotated"], NH)

                def maximum(at, b):
                    g = at[0] * SUBS + at[1]
                    dve.wait_ge(s["score_mm"], g * 4 + (b + 1))
                    if b == 0 and not (isinstance(at[0], int) and g == 0):
                        dve.wait_ge(s["top"], g)
                    dve.tensor_reduce(tops[:, b:b + 1], ps[:, b, :], AX_X, ALU.max).then_inc(s["tops"], 1)

                def overall(at):
                    turn, u = at
                    g = turn * SUBS + u
                    qt, half = u // 2 % 2, u % 2
                    dve.wait_ge(s["tops"], g * 6 + 4)
                    dve.tensor_reduce(tmax[:, qt, half:half + 1], tops[:, 0:KB + half], AX_X, ALU.max)\
                        .then_inc(s["tops"], 1)
                    dve.wait_ge(s["tops"], g * 6 + 5)
                    if not half:
                        dve.tensor_copy(tops[:, KB:KB + 1], tmax[:, qt, 0:1]).then_inc(s["tops"], 1)
                    else:
                        dve.nop().then_inc(s["tops"], 1)
                    dve.tensor_scalar(ntop[:, qt, half:half + 1], tmax[:, qt, half:half + 1], -1.0, None, ALU.mult)\
                        .then_inc(s["top"], 1)

                def lo(at, q):
                    n = (at[0] * SUBS + at[1]) * 4 + q
                    dve.wait_ge(s["p_hi"], n + 1)
                    dve.tensor_tensor(pT_lo[:, q, :, :].rearrange("p a b -> p (a b)"), ps[:, 4 + q % 2, :],
                                      pT_hi[:, q, :, :].rearrange("p a b -> p (a b)").bitcast(F32), ALU.subtract)\
                        .then_inc(s["p_lo"], 1)

                def take(at):
                    turn, u = at
                    g = turn * SUBS + u
                    hh, qt, half = u // 4, u // 2 % 2, u % 2
                    done = turn * (4 * TAKE) + (u // 2) * TAKE
                    out = c1[:, qt, :]
                    dve.wait_ge(s["ctx_mm"], g * 4 + 4)
                    if not half:
                        if not (isinstance(turn, int) and g == 0):
                            dve.wait_ge(s["take"], done)
                        dve.tensor_copy(out, ps[:, 6, 0:P]).then_inc(s["take"], 1)
                        dve.wait_ge(s["take"], done + 1)
                        dve.tensor_tensor(out, out, ps[:, 6, P:2 * P], ALU.add).then_inc(s["taken"], 1)
                        return
                    dve.wait_ge(s["rescale"], turn * 4 + (u // 2 + 1))
                    dve.wait_ge(s["taken"], g)
                    dve.scalar_tensor_tensor(out=out, in0=out, scalar=scale[:, qt:qt + 1], in1=ps[:, 7, 0:P],
                                             op0=ALU.mult, op1=ALU.add).then_inc(s["take"], 1)
                    dve.tensor_tensor(ssum[:, :], sums[:, qt, :, 0], sums[:, qt, :, 1], ALU.add)\
                        .then_inc(s["take"], 1)
                    dve.wait_ge(s["take"], done + 3)
                    dve.tensor_tensor(out, out, ps[:, 7, P:2 * P], ALU.add).then_inc(s["taken"], 1)
                    dve.scalar_tensor_tensor(out=den[:, qt:qt + 1], in0=ssum[:, 0:1], scalar=scale[:, qt:qt + 1],
                                             in1=ssum[:, 1:2], op0=ALU.mult, op1=ALU.add).then_inc(s["take"], 1)
                    dve.wait_ge(s["take"], done + 4)
                    dve.reciprocal(den[:, qt:qt + 1], den[:, qt:qt + 1]).then_inc(s["take"], 1)
                    dve.wait_ge(s["take"], done + 5)
                    dve.wait_ge(s["taken"], g + 1)
                    head = turn * 2 + hh
                    to = cn[:, head, qt, :] if isinstance(turn, int) else \
                        cn[:, bass.ds(head, 1), qt, :].rearrange("p a b -> p (a b)")
                    dve.tensor_scalar(to, out, den[:, qt:qt + 1], None, ALU.mult).then_inc(s["take"], 1)

                def dve_step(at, before, before2):
                    if at:
                        maximum(at, 0)
                        maximum(at, 1)
                    if before2:
                        take(before2)
                    if before:
                        lo(before, 0)
                    if at:
                        maximum(at, 2)
                    if before:
                        lo(before, 1)
                    if at:
                        maximum(at, 3)
                        overall(at)
                    if before:
                        lo(before, 2)
                        lo(before, 3)

                all_steps(dve, dve_step)
                dve.wait_ge(s["take"], TAKE * 4 * PAIRS)
                for j in range(PAIRS):
                    dve.wait_ge(s["cT_mm"], j + 1)
                    if j >= 2:
                        dve.wait_ge(s["lat_mm"], j - 1)
                    dve.tensor_copy(ccT[:, j % 2, 0:2, :].rearrange("p a b -> p (a b)"), ps[:, j % 2, :])\
                        .then_inc(s["cT_sb"], 1)
                dve.wait_ge(s["out_mm"], 1)
                for t in range(TT):
                    dve.tensor_tensor(e.xres[:, t, :], e.xres[:, t, :], ps[:, 6 + t, :], ALU.add)\
                        .then_inc(s["cT_sb"], 1)
        clear_sems(nc, s)
    e.n0 += N_L1X



def layer_l1a(e):
    nc, ps = e.nc, e.ps
    n0 = e.n0
    NH, HD = 64, 64
    INNER = NH * HD
    F = INNER // P
    CONV_TILES = 2 + F
    GROUPS = 8
    GH = NH // GROUPS
    PAIRS = NH // 2
    with ExitStack() as ctx:
        def sb(name, shape):
            return ctx.enter_context(nc.sbuf_tensor("l1a_" + name, shape, F32))
        s = layer_sems(nc, ctx, "l1a", LN_SEMS + [
            "dve_self", "act_self", "dt_mm", "tile_mm", "tile_ev", "pads", "conv", "silu", "xt_mm", "xt_sb", "sp_abs",
            "sp_exp", "sp_done", "decay", "rows", "cols_mm", "cols", "gt_mm", "gt_sb", "btm_sb", "eb_mm", "scan",
            "m", "ends", "xdt", "xd", "xs", "diag_mm", "st_mm", "st_sb", "off_mm", "off_read", "gate_mm", "gate",
            "t_step", "y", "diag_read", "turn_mm", "yT", "squared", "out_mm"])
        xh = sb("xh", [P, TT, INNER])
        xdt = sb("xdt", [P, TT, INNER])
        ybuf = sb("ybuf", [P, F, TOK])
        BC = sb("BC", [P, 2, TOK])
        Bt = sb("Bt", [P, P])
        GT = sb("GT", [P, TT, P])
        L = sb("L", [P, 2, 2, TT, P])
        M = sb("M", [P, 2, 2, TT, P])
        st = sb("st", [P, 512])
        sg = sb("sg", [P, TT, 512])
        y = sb("y", [P, TT, 512])
        dtm = sb("dtm", [P, 3, NH])
        dend = sb("dend", [P, NH])
        ssq = sb("ssq", [P, TT, GROUPS])
        rms = sb("rms", [P, TT])
        small, ident, ident4 = e.small, e.ident, e.ident4
        flat = ybuf[:, :, :].rearrange("p f t -> p (f t)")
        pad = flat[:, 4096:4096 + 2 * 259].rearrange("p (b n) -> p b n", b=2)
        conv = flat[:, 4700:4700 + 512].rearrange("p (b n) -> p b n", b=2)
        xf = flat[:, 5220:5220 + 1024].rearrange("p (b n) -> p b n", b=4)
        r_x, r_a, r_y, r_z, r_e = (flat[0:64, 6272 + i * TOK:6272 + (i + 1) * TOK] for i in range(5))
        r_0 = flat[0:64, 7552:7680]
        r_c = flat[0:64, 7680:7808]
        r_negA = flat[0:64, 7808:7809]
        rowbuf = sb("rowbuf", [64, TOK])
        xsg = sb("xsg", [P, 2, 512])
        junk = e.xn[:, 0, :]

        def taps(i, j):
            return small[:, S_MCONV + 4 * i + j:S_MCONV + 4 * i + j + 1]

        def squares(act, g, me):
            for c in range(TT):
                act.wait_ge(s["y"], 2 * g + c + 1)
                if 2 * g + c:
                    act.wait_ge(s["squared"], 2 * g + c)
                act.activation(junk[:, :], y[:, c, :], ACT.Square, accum_out=ssq[:, c, g:g + 1])\
                    .then_inc(s["squared"], 1)

        with nc.Block(no_gpsimd_drain=True) as block:
            @block.sync
            def _(sp):
                stream(sp, e, n0, N_L1A)

            @block.tensor
            def _(pe):
                ln_tensor(pe, e, s)
                for k in range(KT):
                    last = pe.matmul(ps[0:64, 4, 0:TOK], small[:, S_MDT + 64 * k:S_MDT + 64 * k + 64], e.xnT[:, k, :],
                                     start=(k == 0), stop=(k == KT - 1))
                last.then_inc(s["dt_mm"], 1)

                def turn_x(j):
                    pe.wait_ge(s["silu"], 2 * j + 4)
                    if j >= 2:
                        pe.wait_ge(s["xt_sb"], j - 1)
                    for t in range(TT):
                        for x in range(2):
                            last = pe.transpose(ps[:, 6 + j % 2, t * 256 + x * P:t * 256 + (x + 1) * P],
                                                xf[:, (2 * j + x) % 4, t * P:(t + 1) * P], ident)
                    last.then_inc(s["xt_mm"], 1)

                for i in range(CONV_TILES):
                    w = slot_in(pe, e, n0 + i // 6)
                    if i >= 4:
                        pe.wait_ge(s["tile_ev"], i - 3)
                    for k in range(KT):
                        last = pe.matmul(ps[:, i % 4, 0:TOK], w[:, k * 768 + (i % 6) * P:k * 768 + (i % 6 + 1) * P],
                                         e.xnT[:, k, :], start=(k == 0), stop=(k == KT - 1))
                        if k == 0 and i and i % 6 == 0:
                            last.then_inc(e.w_used, 1)
                    last.then_inc(s["tile_mm"], 1)
                    if i >= 6 and i % 2 == 0:
                        turn_x((i - 6) // 2)
                for j in range((CONV_TILES - 6) // 2, F // 2):
                    turn_x(j)
                pe.nop().then_inc(e.w_used, 1)
                for c in range(TT):
                    at = slice(c * P, (c + 1) * P)
                    pe.matmul(ps[:, 5, at], BC[:, 0, at], BC[:, 1, at], start=True, stop=True)
                pe.transpose(ps[:, 5, 2 * P:3 * P], BC[:, 0, 0:P], ident).then_inc(s["gt_mm"], 1)
                pe.wait_ge(s["rows"], 1)
                for c in range(TT):
                    pe.transpose(ps[:, 4, c * NH:(c + 1) * NH], r_z[:, c * P:(c + 1) * P], ident[0:64, 0:64])
                pe.transpose(ps[:, 4, 2 * NH:3 * NH], r_c, ident[0:64, 0:64]).then_inc(s["cols_mm"], 1)
                pe.wait_ge(s["cols"], 1)
                pe.wait_ge(s["gt_sb"], 2)

                def decays(q):
                    if q >= 2:
                        pe.wait_ge(s["scan"], q - 1)
                    for x in range(2):
                        h = 2 * q + x
                        last = pe.matmul(ps[:, q % 2, x * TOK:(x + 1) * TOK],
                                         ident[0:64, h:h + 1].broadcast_to((64, P)), rowbuf[:, :],
                                         start=True, stop=True)
                    last.then_inc(s["eb_mm"], 1)

                def diagonal(q):
                    g = q // 4
                    pe.wait_ge(s["m"], q + 1)
                    if q % 4 == 0:
                        pe.wait_ge(s["xdt"], 2 * g + 2)
                        if g:
                            pe.wait_ge(s["diag_read"], 2 * g)
                    for x in range(2):
                        h = 2 * q + x
                        for c in range(TT):
                            last = pe.matmul(ps[:, 2 + c, (h % GH) * HD:(h % GH + 1) * HD], M[:, q % 2, x, c, :],
                                             xdt[:, c, h * HD:(h + 1) * HD], start=True, stop=True)
                    last.then_inc(s["diag_mm"], 1)

                def gates(g, c):
                    w = slot_in(pe, e, n0 + 6 + g)
                    n = 2 * g + c
                    if n:
                        pe.wait_ge(s["gate"], n)
                    for k in range(KT):
                        last = pe.matmul(ps[:, 5, :], e.xnT[:, k, c * P:(c + 1) * P], w[:, k * 512:(k + 1) * 512],
                                         start=(k == 0), stop=(k == KT - 1))
                        if k == 0 and c == 0 and g:
                            last.then_inc(e.w_used, 1)
                    last.then_inc(s["gate_mm"], 1)

                def state(g):
                    pe.wait_ge(s["xs"], g + 1)
                    if g:
                        pe.wait_ge(s["off_read"], g)
                    pe.matmul(ps[:, 4, :], Bt[:, :], xsg[:, g % 2, :], start=True, stop=True).then_inc(s["st_mm"], 1)

                def off(g):
                    pe.wait_ge(s["st_sb"], g + 1)
                    pe.matmul(ps[:, 4, :], BC[:, 1, P:TOK], st[:, :], start=True, stop=True).then_inc(s["off_mm"], 1)

                def turn_y(g):
                    for c in range(TT):
                        pe.wait_ge(s["y"], 2 * g + c + 1)
                        if g:
                            pe.wait_ge(s["yT"], 2 * g + c - 1)
                        for j in range(4):
                            last = pe.transpose(ps[:, 6 + c, j * P:(j + 1) * P], y[:, c, j * P:(j + 1) * P], ident)
                        last.then_inc(s["turn_mm"], 1)

                decays(0)
                decays(1)
                for g in range(GROUPS):
                    gates(g, 0)
                    for q in range(4 * g, 4 * g + 4):
                        diagonal(q)
                        if q + 2 < PAIRS:
                            decays(q + 2)
                        if q == 4 * g + 1 and g:
                            turn_y(g - 1)
                    gates(g, 1)
                    state(g)
                    off(g)
                turn_y(GROUPS - 1)
                pe.wait_ge(s["yT"], 2 * GROUPS)
                for f in range(F):
                    w = slot_in(pe, e, n0 + 6 + GROUPS + f // 4)
                    for t in range(TT):
                        last = pe.matmul(ps[:, t, :], ybuf[:, f, t * P:(t + 1) * P], w[:, (f % 4) * D:(f % 4 + 1) * D],
                                         start=(f == 0), stop=(f == F - 1))
                        if f % 4 == 0 and t == 0:
                            last.then_inc(e.w_used, 1)
                last.then_inc(s["out_mm"], 1)
                pe.wait_ge(s["out_mm"], 1)
                pe.nop().then_inc(e.w_used, 1)

            @block.scalar
            def _(act):
                me = Chain(act, s["act_self"])
                ln_scalar(act, e, s)

                def silu(i):
                    act.wait_ge(s["conv"], i + 1)
                    if i >= 6:
                        act.wait_ge(s["xt_mm"], (i - 4) // 2)
                    out = BC[:, i, :] if i < 2 else xf[:, (i - 2) % 4, :]
                    act.activation(out, conv[:, i % 2, :], ACT.Silu, bias=small[:, S_MBIAS + i:S_MBIAS + i + 1])\
                        .then_inc(s["silu"], 1)

                def turned_x(j):
                    act.wait_ge(s["xt_mm"], j + 1)
                    act.activation(xh[:, :, j * 256:(j + 1) * 256], ps[:, 6 + j % 2, :].rearrange("p (t n) -> p t n", t=TT),
                                   ACT.Copy).then_inc(s["xt_sb"], 1)

                act.wait_ge(s["pads"], 1)
                done = 0
                for i in range(CONV_TILES):
                    act.wait_ge(s["tile_mm"], i + 1)
                    if i >= 2:
                        act.wait_ge(s["conv"], i - 1)
                    act.activation(pad[:, i % 2, 3:3 + TOK], ps[:, i % 4, 0:TOK], ACT.Copy).then_inc(s["tile_ev"], 1)
                    if i:
                        silu(i - 1)
                    if i >= 8 and i % 2 == 0:
                        turned_x(done)
                        done += 1
                silu(CONV_TILES - 1)
                while done < F // 2:
                    turned_x(done)
                    done += 1
                act.wait_ge(s["gt_mm"], 1)
                act.activation(GT[:, :, :].rearrange("p c n -> p (c n)"), ps[:, 5, 0:TOK], ACT.Copy).then_inc(s["gt_sb"], 1)
                act.activation(Bt[:, :], ps[:, 5, 2 * P:3 * P], ACT.Copy).then_inc(s["gt_sb"], 1)
                me.did(act.activation(r_negA, small[0:64, S_MHEAD:S_MHEAD + 1], ACT.Exp))
                me.wait()
                me.did(act.activation(r_negA, r_negA, ACT.Copy, scale=-1.0))
                softplus_scalar(act, r_a, r_y, s)
                act.wait_ge(s["sp_done"], 1)
                me.wait()
                act.activation(r_e, r_z, ACT.Exp, scale=r_negA).then_inc(s["decay"], 1)
                act.wait_ge(s["cols_mm"], 1)
                act.activation(dtm[:, :, :].rearrange("p c h -> p (c h)"), ps[:, 4, 0:3 * NH], ACT.Copy)\
                    .then_inc(s["cols"], 1)
                for g in range(GROUPS):
                    for c in range(TT):
                        act.wait_ge(s["gate_mm"], 2 * g + c + 1)
                        if g:
                            act.wait_ge(s["y"], 2 * g + c - 1)
                        act.activation(sg[:, c, :], ps[:, 5, :], ACT.Silu).then_inc(s["gate"], 1)
                        if g and c == 0:
                            squares(act, g - 1, me)
                    act.wait_ge(s["st_mm"], g + 1)
                    if g:
                        act.wait_ge(s["off_mm"], g)
                    act.activation(st[:, :], ps[:, 4, :], ACT.Copy).then_inc(s["st_sb"], 1)
                squares(act, GROUPS - 1, me)
                act.wait_ge(s["ln_xn"], TT + 1)
                act.activation(rms[:, :], rms[:, :], ACT.Sqrt, bias=e.eps, scale=1.0 / INNER).then_inc(s["ln_std"], 1)

            @block.gpsimd
            def _(pool):
                pool.wait_ge(s["cols"], 1)
                pool.wait_ge(s["xt_sb"], F // 2)
                for g in range(GROUPS):
                    at, hh = slice(g * 512, (g + 1) * 512), slice(g * GH, (g + 1) * GH)

                    def by_head(ap):
                        return ap.rearrange("p (h d) -> p h d", d=HD)
                    for c in range(TT):
                        pool.tensor_tensor(by_head(xdt[:, c, at]), by_head(xh[:, c, at]),
                                           bcast_last(dtm[:, c, hh], (P, GH, HD)), ALU.mult).then_inc(s["xdt"], 1)
                    pool.wait_ge(s["xdt"], 2 * g + 2)
                    for c in range(TT):
                        pool.tensor_tensor(by_head(xh[:, c, at]), by_head(xh[:, c, at]),
                                           bcast_last(small[:, S_MD + g * GH:S_MD + (g + 1) * GH], (P, GH, HD)),
                                           ALU.mult).then_inc(s["xd"], 1)
                    pool.wait_ge(s["ends"], 4 * g + 4)
                    if g >= 2:
                        pool.wait_ge(s["st_mm"], g - 1)
                    pool.tensor_tensor(by_head(xsg[:, g % 2, :]), by_head(xdt[:, 0, at]),
                                       bcast_last(dend[:, hh], (P, GH, HD)), ALU.mult).then_inc(s["xs"], 1)

            @block.vector
            def _(dve):
                me = Chain(dve, s["dve_self"])
                ln_vector(dve, e, s)
                dve.memset(pad[:, :, :], 0.0).then_inc(s["pads"], 1)
                for i in range(CONV_TILES):
                    dve.wait_ge(s["tile_ev"], i + 1)
                    if i >= 2:
                        dve.wait_ge(s["silu"], i - 1)
                    x, z = pad[:, i % 2, :], conv[:, i % 2, :]
                    me.did(dve.tensor_scalar(z, x[:, 0:TOK], taps(i, 0), None, ALU.mult))
                    for j in range(1, 4):
                        me.wait()
                        last = dve.scalar_tensor_tensor(out=z, in0=x[:, j:j + TOK], scalar=taps(i, j), in1=z,
                                                        op0=ALU.mult, op1=ALU.add)
                        if j < 3:
                            me.did(last)
                    last.then_inc(s["conv"], 1)
                dve.wait_ge(s["dt_mm"], 1)
                me.did(dve.memset(r_0, 0.0))
                me.did(dve.tensor_scalar(r_x, ps[0:64, 4, 0:TOK], small[0:64, S_MHEAD + 1:S_MHEAD + 2], None, ALU.add))
                me.wait()
                softplus_vector(dve, me, r_x, r_a, r_y, r_z, s, r_z)
                dve.wait_ge(s["decay"], 1)
                me.did(dve.tensor_copy(rowbuf[:, :], r_e))
                me.did(dve.tensor_tensor_scan(r_c, r_e[:, P:TOK], r_0, 1.0, ALU.mult, ALU.add))
                me.wait()
                me.did(dve.memset(rowbuf[:, 0:TOK:P], 0.0))
                me.wait()
                dve.nop().then_inc(s["rows"], 1)
                dve.wait_ge(s["gt_sb"], 2)

                def pair(q):
                    dve.wait_ge(s["eb_mm"], q + 1)
                    if q >= 2:
                        dve.wait_ge(s["m"], q - 1)
                        dve.wait_ge(s["ends"], q - 1)
                    d = L[:, q % 2, :, :, :]
                    dve.tensor_tensor_scan(d.rearrange("p h c n -> p (h c n)"), ps[:, q % 2, :], ident4, 0.0,
                                           ALU.mult, ALU.add).then_inc(s["scan"], 1)
                    dve.wait_ge(s["scan"], q + 1)
                    if q >= 2:
                        dve.wait_ge(s["diag_mm"], q - 1)
                    dve.tensor_copy(dend[:, 2 * q:2 * q + 2], d[:, :, 0, P - 1]).then_inc(s["ends"], 1)
                    dve.tensor_tensor(M[:, q % 2, :, :, :].rearrange("p h c n -> p h (c n)"),
                                      d.rearrange("p h c n -> p h (c n)"),
                                      GT[:, :, :].rearrange("p c n -> p (c n)").unsqueeze(1).broadcast_to((P, 2, TOK)),
                                      ALU.mult).then_inc(s["m"], 1)

                def by_head(ap):
                    return ap.rearrange("p (h d) -> p h d", d=HD)

                def outputs(g):
                    at, hh = slice(g * 512, (g + 1) * 512), slice(g * GH, (g + 1) * GH)
                    base = 5 * g
                    dve.wait_ge(s["diag_mm"], 4 * g + 4)
                    dve.wait_ge(s["xd"], 2 * g + 2)
                    if g:
                        dve.wait_ge(s["turn_mm"], 2 * g)
                        dve.wait_ge(s["squared"], 2 * g)
                    dve.tensor_tensor(y[:, 0, :], ps[:, 2, :], xh[:, 0, at], ALU.add).then_inc(s["diag_read"], 1)
                    dve.tensor_tensor(xh[:, 1, at], ps[:, 3, :], xh[:, 1, at], ALU.add).then_inc(s["diag_read"], 1)
                    dve.wait_ge(s["gate"], 2 * g + 1)
                    dve.wait_ge(s["diag_read"], 2 * g + 2)
                    dve.tensor_tensor(y[:, 0, :], y[:, 0, :], sg[:, 0, :], ALU.mult).then_inc(s["y"], 1)
                    dve.wait_ge(s["off_mm"], g + 1)
                    dve.tensor_tensor(by_head(y[:, 1, :]), by_head(ps[:, 4, :]), bcast_last(dtm[:, 2, hh], (P, GH, HD)),
                                      ALU.mult).then_inc(s["off_read"], 1)
                    dve.wait_ge(s["off_read"], g + 1)
                    dve.tensor_tensor(y[:, 1, :], y[:, 1, :], xh[:, 1, at], ALU.add).then_inc(s["t_step"], 1)
                    dve.wait_ge(s["t_step"], g + 1)
                    dve.wait_ge(s["gate"], 2 * g + 2)
                    dve.tensor_tensor(y[:, 1, :], y[:, 1, :], sg[:, 1, :], ALU.mult).then_inc(s["y"], 1)

                def turned_y(g):
                    for c in range(TT):
                        dve.wait_ge(s["turn_mm"], 2 * g + c + 1)
                        dve.tensor_tensor(ybuf[:, 4 * g:4 * g + 4, c * P:(c + 1) * P],
                                          ps[:, 6 + c, :].rearrange("p (f n) -> p f n", n=P),
                                          bcast_last(small[:, S_MNORM + 4 * g:S_MNORM + 4 * g + 4], (P, 4, P)),
                                          ALU.mult).then_inc(s["yT"], 1)

                dve.wait_ge(s["cols_mm"], 1)
                for g in range(GROUPS):
                    for q in range(4 * g, 4 * g + 4):
                        pair(q)
                        if q == 4 * g + 2 and g:
                            turned_y(g - 1)
                    outputs(g)
                turned_y(GROUPS - 1)
                dve.wait_ge(s["squared"], 2 * GROUPS)
                me.did(dve.tensor_reduce(rms[:, :], ssq[:, :, :], AX_X, ALU.add))
                me.wait()
                dve.nop().then_inc(s["ln_xn"], 1)
                dve.wait_ge(s["ln_std"], 2)
                me.did(dve.reciprocal(rms[:, :], rms[:, :]))
                me.wait()
                dve.wait_ge(s["out_mm"], 1)
                for t in range(TT):
                    me.did(dve.scalar_tensor_tensor(out=e.xres[:, t, :], in0=ps[:, t, :], scalar=rms[:, t:t + 1],
                                                    in1=e.xres[:, t, :], op0=ALU.mult, op1=ALU.add))
        clear_sems(nc, s)
    e.n0 += N_L1A



def _ktiles(wT):
    k, n = wT.shape
    return wT.reshape(k // P, P, n).transpose(1, 0, 2).reshape(P, -1)


def _slot(*parts):
    out = np.zeros((P, SLOT), np.float32)
    at = 0
    for a in parts:
        out[:a.shape[0], at:at + a.shape[1]] = a
        at += a.shape[1]
    return out


def slots_l0x(i):
    wq = np.asarray(i["L0_xattn_Wq"]).T
    wkv = np.asarray(i["L0_xattn_Wkv_expand"]).T
    wout = np.asarray(i["L0_xattn_Wout"]).T
    return [_slot(_ktiles(wq), wkv), _slot(_ktiles(wout))]


def fixed_columns():
    out = np.zeros((P, C_N), np.float32)
    for r in range(4):
        out[:, C_ID + r * P:C_ID + (r + 1) * P] = np.eye(P)
    a = np.arange(P)
    for l in range(7):
        b = 1 << l
        s, r = a[:, None], a[None, :]
        out[:, C_LEVEL + l * P:C_LEVEL + (l + 1) * P] = \
            (s // (2 * b) == r // (2 * b)) & (s % (2 * b) < b) & (r % (2 * b) >= b)
    out[:, C_CAUSAL + P:C_CAUSAL + 2 * P] = np.where(a[None, :] <= a[:, None], 0.0, LOWEST)
    out[:, C_ONES:C_ONES + P] = 1.0
    out[:, C_EPS] = EPS
    for h in range(8):
        out[:, C_PICK + 9 * h] = 1.0
    return out


def small_columns(i):
    out = np.zeros((P, S_N), np.float32)
    g = lambda n: np.asarray(i[n])
    conv = np.concatenate([g("L0_attn_conv_q_w"), g("L0_attn_conv_k_w"), g("L0_attn_conv_v_w")])[:, 0, :]
    out[:, S_ACONV:S_ACONV + 160] = conv.reshape(40, P, 4).transpose(1, 0, 2).reshape(P, 160)
    out[:, S_AAB:S_AAB + 96] = _ktiles(np.concatenate([g("L0_attn_Wa"), g("L0_attn_Wb")], axis=1))
    out[:, S_ANORM] = g("L0_attn_norm_w")
    out[:8, S_AHEAD] = g("L0_attn_A_log")
    out[:8, S_AHEAD + 1] = g("L0_attn_dt_bias")
    out[:, S_F0:S_F0 + 256] = _ktiles(g("L0_ffn_gate_w").T)
    out[:, S_F1:S_F1 + 32] = _ktiles(g("L1_ffn_gate_w").T)
    order = np.concatenate([np.arange(4096, 4352), np.arange(4096)])
    out[:, S_MCONV:S_MCONV + 136] = g("L1_attn_conv_w")[order, 0, :].reshape(34, P, 4).transpose(1, 0, 2).reshape(P, 136)
    out[:, S_MBIAS:S_MBIAS + 34] = g("L1_attn_conv_b")[order].reshape(34, P).T
    out[:, S_MDT:S_MDT + 256] = _ktiles(g("L1_attn_in_proj_w")[4096 + 4352:].T)
    out[:64, S_MHEAD] = g("L1_attn_A_log")
    out[:64, S_MHEAD + 1] = g("L1_attn_dt_bias")
    out[:, S_MD:S_MD + 64] = g("L1_attn_D")[None, :]
    out[:, S_MNORM:S_MNORM + 32] = g("L1_attn_norm_w").reshape(32, P).T
    return out


def slots_l0f(i):
    w13, w2 = np.asarray(i["L0_ffn_w13"]), np.asarray(i["L0_ffn_w2"])
    return [_slot(_ktiles(w13[x].T), _ktiles(w2[x].T)) for x in range(w13.shape[0])]


def slots_l1f(i):
    w1, w2, w3 = (np.asarray(i["L1_ffn_" + n]) for n in ("w1", "w2", "w3"))
    return [_slot(_ktiles(np.concatenate([w1[x][:, c:c + 256], w3[x][:, c:c + 256]], axis=1)), _ktiles(w2[x][c:c + 256]))
            for x in range(w1.shape[0]) for c in range(0, 1024, 256)]


def slots_l1x(i):
    g = lambda n: np.asarray(i["L1_xattn_" + n])
    wq, wkc, wqr, wkr, wo = g("Wq"), g("w_kc_q"), g("W_qr"), g("W_kr"), g("Wo")
    out = []
    for pair in range(8):
        parts = []
        for h in (2 * pair, 2 * pair + 1):
            parts += [_ktiles(wq[h * P:(h + 1) * P].T),
                      *[wkc[h][:, c] for c in Q_TILES + [Q_TURNED]],
                      *[wqr[h][c] for c in Q_TILES],
                      np.pad(wkr[h].T, ((0, 64), (0, 0)))]
        out.append(_slot(*parts))
    wlat = g("w_kc_kv").transpose(2, 0, 1).reshape(P, 16 * P)
    return out + [_slot(_ktiles(wo.T[c:c + 4 * P]), wlat[:, c:c + 4 * P]) for c in range(0, 16 * P, 4 * P)]


def rope_tables(length, dim):
    f32 = np.float32
    inv = f32(1.0) / np.power(f32(10000.0), np.arange(0, dim, 2, dtype=f32) / f32(dim)).astype(f32)
    f = np.arange(length, dtype=f32)[:, None] * inv[None, :]
    return np.sin(f).astype(f32), np.cos(f).astype(f32)


def extra_inputs(i):
    ctx = np.asarray(i["ctx_512"])[0]
    sin_k, cos_k = rope_tables(CTX, P)
    sin_q, cos_q = (np.repeat(t, 2, axis=-1).T for t in rope_tables(TOK, Q_BIG))
    sign_k = np.where(np.arange(64) < 32, -1.0, 1.0).astype(np.float32)
    sign_q = np.where(np.arange(Q_BIG) < HALF, -1.0, 1.0).astype(np.float32)[:, None]

    def rows(a):
        return a.reshape(CT, P, -1).transpose(1, 0, 2).reshape(P, -1)
    return {
        "ctxT": ctx[:TOK].T,
        "ctx": rows(ctx),
        "rope_k": np.concatenate([rows(cos_k), rows(sin_k * sign_k)], axis=1),
        "rope_q": np.concatenate([cos_q[c] for c in Q_TILES] + [(sin_q * sign_q)[c] for c in Q_TILES], axis=1),
    }


def slots_l0a(i):
    g = lambda n: np.asarray(i["L0_attn_" + n])
    w = np.concatenate([g("Wq"), g("Wk"), g("Wv"), g("Wg")], axis=1)
    wo = g("Wo")
    return [_slot(_ktiles(w[:, c:c + 768])) for c in range(0, 6144, 768)] + \
        [_slot(_ktiles(wo[c:c + 4 * P])) for c in (0, 4 * P)]


def slots_l1a(i):
    w = np.asarray(i["L1_attn_in_proj_w"]).T
    gate, conv = w[:, :4096], w[:, 4096:8448]
    conv = np.concatenate([conv[:, 4096:], conv[:, :4096]], axis=1)
    wo = np.asarray(i["L1_attn_out_proj_w"]).T
    out = [_slot(_ktiles(np.pad(conv[:, c:c + 768], ((0, 0), (0, max(0, c + 768 - conv.shape[1]))))))
           for c in range(0, conv.shape[1], 768)]
    out += [_slot(_ktiles(gate[:, c:c + 512])) for c in range(0, 4096, 512)]
    return out + [_slot(_ktiles(wo[c:c + 4 * P])) for c in range(0, 4096, 4 * P)]



def build_program(nc, io):
    with ExitStack() as ctx:
        e = open_env(nc, ctx, io)
        e.slots = SLOTS
        layer_l0x(e)
        layer_l0a(e)
        with ExitStack() as rope:
            open_rope(e, rope)
            layer_l0f(e)
            layer_l1x(e)
        layer_l1a(e)
        layer_l1f(e)
        stored = ctx.enter_context(nc.semaphore("stored"))
        with nc.Block(no_gpsimd_drain=True) as block:
            @block.sync
            def _(sp):
                sp.dma_start(io["out"].rearrange("(t p) d -> p t d", p=P), e.xres[:, :, :]).then_inc(stored, 16)
                sp.wait_ge(stored, 16)



def kernel(**inputs):
    import concourse.bacc as bacc
    from concourse.bass_utils import run_bass_kernel_spmd

    slots = []
    for part in (slots_l0x, slots_l0a, slots_l0f, slots_l1x, slots_l1a, slots_l1f):
        slots += part(inputs)
    arrays = {"x": np.asarray(inputs["x"])[0], "fixed": fixed_columns(), "small": small_columns(inputs),
              "wall": np.stack(slots), **extra_inputs(inputs)}
    arrays = {name: np.ascontiguousarray(a) for name, a in arrays.items()}
    nc = bacc.Bacc("TRN2", target_bir_lowering=False, num_devices=1)
    io = {name: nc.dram_tensor(name, a.shape, mybir.dt.from_np(a.dtype), kind="ExternalInput").ap()
          for name, a in arrays.items()}
    io["out"] = nc.dram_tensor("out", (TOK, D), F32, kind="ExternalOutput").ap()
    build_program(nc, io)
    r = run_bass_kernel_spmd(nc, [arrays], core_ids=[0])
    return r.results[0]["out"].reshape(1, TOK, D)
```

```python
from contextlib import ExitStack

import numpy as np
import concourse.bass as bass
from concourse import mybir

F32 = mybir.dt.float32
F32R = mybir.dt.float32r
ACT = mybir.ActivationFunctionType
ALU = mybir.AluOpType
AX_X = mybir.AxisListType.X

P = 128
TOK = 256
TT = TOK // P
D = 512
KT = D // P
CTX = 4096
CT = CTX // P
EPS = 1e-5
LOWEST = -3.0e38

RING = 4
SLOT = 3072
N_L0X, N_L0A, N_L0F, N_L1X, N_L1A, N_L1F = 2, 10, 64, 12, 20, 32
FIRST_SLOT = {}
_at = 0
for _name, _n in (("L0x", N_L0X), ("L0a", N_L0A), ("L0f", N_L0F), ("L1x", N_L1X), ("L1a", N_L1A), ("L1f", N_L1F)):
    FIRST_SLOT[_name] = (_at, _n)
    _at += _n
SLOTS = _at

C_ID = 0
C_LEVEL = C_ID + 4 * P
C_CAUSAL = C_LEVEL + 7 * P
C_ONES = C_CAUSAL + 2 * P
C_EPS = C_ONES + P
C_PICK = C_EPS + 1
C_N = C_PICK + 64

S_ACONV = 0
S_AAB = S_ACONV + 160
S_ANORM = S_AAB + 96
S_AHEAD = S_ANORM + 1
S_F0 = S_AHEAD + 2
S_F1 = S_F0 + KT * 64
S_MCONV = S_F1 + KT * 8
S_MBIAS = S_MCONV + 136
S_MDT = S_MBIAS + 34
S_MHEAD = S_MDT + KT * 64
S_MD = S_MHEAD + 2
S_MNORM = S_MD + 64
S_N = S_MNORM + 32


class Chain:

    def __init__(self, eng, sem):
        self.eng, self.sem, self.n = eng, sem, 0

    def did(self, ins):
        ins.then_inc(self.sem, 1)
        self.n += 1
        return self.n

    def wait(self):
        self.eng.wait_ge(self.sem, self.n)

    def wait_before_last(self):
        self.eng.wait_ge(self.sem, self.n - 1)


class Env:
    pass


def bcast_last(ap, shape):
    return ap.unsqueeze(len(shape) - 1).broadcast_to(shape)


def open_env(nc, ctx, io):
    e = Env()
    e.nc, e.io = nc, io

    def sb(name, shape):
        return ctx.enter_context(nc.sbuf_tensor("sb_" + name, shape, F32))

    e.ps = ctx.enter_context(nc.psum_tensor("banks", [P, 8, 512], F32))
    e.fixed = sb("fixed", [P, C_N])
    e.small = sb("small", [P, S_N])
    e.xres = sb("xres", [P, TT, D])
    e.xnbuf = sb("xnbuf", [P, 2 * TT * D])
    e.xn = e.xnbuf[:, 0:TT * D].rearrange("p (t d) -> p t d", t=TT)
    e.xnT = e.xnbuf[:, TT * D:2 * TT * D].rearrange("p (k t) -> p k t", k=KT)
    e.stats = sb("stats", [P, TT, 6])
    e.mv = sb("mv", [P, TT, 2])
    e.std = sb("std", [P, TT])
    e.ring = sb("ring", [P, RING, SLOT])
    e.ident = e.fixed[:, C_ID:C_ID + P]
    e.ident4 = e.fixed[:, C_ID:C_ID + 4 * P]
    e.ones = e.fixed[:, C_ONES:C_ONES + P]
    e.eps = e.fixed[:, C_EPS:C_EPS + 1]
    e.w_in = [ctx.enter_context(nc.semaphore(f"w_in{i}")) for i in range(RING)]
    e.w_used = ctx.enter_context(nc.semaphore("w_used"))
    e.boot = ctx.enter_context(nc.semaphore("boot"))
    e.n0 = 0
    e.slots = 0
    e.preloaded = False
    return e


def layer_sems(nc, ctx, tag, names):
    return {n: ctx.enter_context(nc.semaphore(f"{tag}_{n}")) for n in names}


def clear_sems(nc, s):
    ids = sorted(x.num for x in s.values())
    runs = []
    for i in ids:
        if runs and runs[-1][1] == i:
            runs[-1][1] = i + 1
        else:
            runs.append([i, i + 1])
    with nc.Block(no_gpsimd_drain=True) as block:
        @block.gpsimd
        def _(pool):
            for lo, hi in runs:
                pool.sem_clear(range(lo, hi))


LN_OWN = 3
LN_SEMS = ["ln_self", "ln_stats", "ln_std", "ln_xn", "ln_turned", "ln_done"]


def stream(sp, e, first, count):
    lo = first + RING if first or e.preloaded else 0
    hi = min(first + count + RING, e.slots)
    for n in range(lo, min(hi, RING)):
        sp.dma_start(e.ring[:, n, :], e.io["wall"][n]).then_inc(e.w_in[n], 16)
    lo = max(lo, RING)
    while lo < hi and lo % RING:
        load_slot(sp, e, lo, lo % RING)
        lo += 1
    turns = (hi - lo) // RING
    if turns > 1:
        with sp.Fori(0, turns) as i:
            for u in range(RING):
                sp.wait_ge(e.w_used, i * RING + (lo + u - RING + 1))
                sp.dma_start(e.ring[:, u, :], e.io["wall"][bass.ds(i * RING + (lo + u), 1)].rearrange("a p n -> (a p) n"))\
                    .then_inc(e.w_in[u], 16)
        lo += turns * RING
    while lo < hi:
        load_slot(sp, e, lo, lo % RING)
        lo += 1


def load_slot(sp, e, n, u):
    sp.wait_ge(e.w_used, n - RING + 1)
    sp.dma_start(e.ring[:, u, :], e.io["wall"][n]).then_inc(e.w_in[u], 16)


def slot_in(eng, e, n):
    eng.wait_ge(e.w_in[n % RING], 16 * (n // RING + 1))
    return e.ring[:, n % RING, :]



def ln_vector(dve, e, s):
    me = Chain(dve, s["ln_self"])
    for t in range(TT):
        me.did(dve.bn_stats(e.stats[:, t, :], e.xres[:, t, :]))
    me.wait()
    for t in range(TT):
        dve.bn_aggr(e.mv[:, t, :], e.stats[:, t, :]).then_inc(s["ln_stats"], 1)
    dve.wait_ge(s["ln_std"], 1)
    me.did(dve.reciprocal(e.std[:, :], e.std[:, :]))
    me.wait()
    for t in range(TT):
        dve.tensor_scalar(e.xn[:, t, :], e.xres[:, t, :], e.mv[:, t, 0:1], e.std[:, t:t + 1],
                          ALU.subtract, ALU.mult).then_inc(s["ln_xn"], 1)
    dve.wait_ge(s["ln_turned"], 1)
    dve.tensor_copy(e.xnT[:, 0:2, :], e.ps[:, 0, :].rearrange("p (k t) -> p k t", k=2)).then_inc(s["ln_done"], 1)


def ln_scalar(act, e, s):
    act.wait_ge(s["ln_stats"], TT)
    act.activation(e.std[:, :], e.mv[:, :, 1], ACT.Sqrt, bias=e.eps).then_inc(s["ln_std"], 1)
    act.wait_ge(s["ln_turned"], 2)
    act.activation(e.xnT[:, 2:4, :], e.ps[:, 1, :].rearrange("p (k t) -> p k t", k=2), ACT.Copy)\
        .then_inc(s["ln_done"], 1)


def ln_tensor(pe, e, s):
    for k in range(KT):
        for t in range(TT):
            if k == 0:
                pe.wait_ge(s["ln_xn"], t + 1)
            at = (k % 2) * TOK + t * P
            last = pe.transpose(e.ps[:, k // 2, at:at + P], e.xn[:, t, k * P:(k + 1) * P], e.ident)
        if k % 2:
            last.then_inc(s["ln_turned"], 1)
    pe.wait_ge(s["ln_done"], 2)



SPLIT_SEMS = ["x_hi", "x_lo", "w_hi", "w_lo"]
AHEAD = 2


def open_split(sb, scope):
    return [sb(n, [P, 4, KT, P], F32R, scope) for n in ("w_hi", "w_lo")] + \
        [sb(n, [P, KT, TOK], F32R, scope) for n in ("x_hi", "x_lo")]


def tile_of(w, i):
    return w.rearrange("p (k n) -> p k n", k=KT)[:, :, (i % 6) * P:(i % 6 + 1) * P]


def split_x_hi(act, e, s, x_hi):
    act.wait_ge(s["ln_done"], 2)
    act.activation(x_hi[:, :, :], e.xnT[:, :, :], ACT.Copy).then_inc(s["x_hi"], 1)


def split_x_lo(dve, e, s, x_hi, x_lo):
    dve.wait_ge(s["x_hi"], 1)
    dve.tensor_tensor(x_lo[:, :, :], e.xnT[:, :, :], x_hi[:, :, :].bitcast(F32), ALU.subtract).then_inc(s["x_lo"], 1)


def split_w_hi(act, e, s, i, w_hi):
    w = slot_in(act, e, e.n0 + i // 6)
    if i >= 4:
        act.wait_ge(s["tile_mm"], i - 3)
    act.activation(w_hi[:, i % 4, :, :], tile_of(w, i), ACT.Copy).then_inc(s["w_hi"], 1)


def split_w_lo(pool, e, s, i, w_hi, w_lo):
    w = slot_in(pool, e, e.n0 + i // 6)
    pool.wait_ge(s["w_hi"], i + 1)
    pool.tensor_tensor(w_lo[:, i % 4, :, :], tile_of(w, i), w_hi[:, i % 4, :, :].bitcast(F32), ALU.subtract)\
        .then_inc(s["w_lo"], 1)


def project_tile(pe, e, s, i, split):
    w_hi, w_lo, x_hi, x_lo = split
    if i == 0:
        pe.wait_ge(s["x_lo"], 1)
    pe.wait_ge(s["w_lo"], i + 1)
    if i >= 4:
        pe.wait_ge(s["tile_ev"], i - 3)
    for k in range(KT):
        out = e.ps[:, i % 4, 0:TOK]
        last = pe.matmul(out, w_hi[:, i % 4, k, :], x_hi[:, k, :], start=(k == 0), stop=False)
        if k == 0 and i and i % 6 == 0:
            last.then_inc(e.w_used, 1)
        pe.matmul(out, w_hi[:, i % 4, k, :], x_lo[:, k, :], start=False, stop=False)
        last = pe.matmul(out, w_lo[:, i % 4, k, :], x_hi[:, k, :], start=False, stop=(k == KT - 1))
    last.then_inc(s["tile_mm"], 1)



CR = 4
SILU_LAG = 3


def tap_scalar(act, s, i, conv, bank, tap):
    if i >= CR:
        act.wait_ge(s["silu"], i - CR + 1)
    act.activation(conv, bank, ACT.Copy, scale=tap).then_inc(s["tap"], 1)


def convolve(dve, me, s, i, pad, conv, taps):
    def step(i, j):
        return dve.scalar_tensor_tensor(out=conv[:, i % CR, :], in0=pad[:, i % CR, j:j + TOK], scalar=taps(i, j),
                                        in1=conv[:, i % CR, :], op0=ALU.mult, op1=ALU.add)

    dve.wait_ge(s["tile_ev"], i + 1)
    if i >= CR:
        dve.wait_ge(s["silu"], i - CR + 1)
    me.did(dve.tensor_scalar(conv[:, i % CR, :], pad[:, i % CR, 3:3 + TOK], taps(i, 3), None, ALU.mult))
    me.wait()
    me.did(step(i, 0))
    dve.wait_ge(s["tap"], i // 2 + 1)
    dve.wait_ge(s["tile_ev"], i + 2)
    me.did(step(i + 1, 0))
    me.wait_before_last()
    me.did(step(i, 1))
    me.wait_before_last()
    me.did(step(i + 1, 1))
    me.wait_before_last()
    step(i, 2).then_inc(s["conv"], 1)
    me.wait()
    step(i + 1, 2).then_inc(s["conv"], 1)



def layer_l0x(e, first_layer=True):
    nc, ps, fixed = e.nc, e.ps, e.fixed
    NH, HD = 16, 32
    G = 4
    SCALE = float(np.float32(1.0) / np.sqrt(np.float32(HD)))
    n0 = e.n0
    with ExitStack() as ctx:
        def sb(name, shape):
            return ctx.enter_context(nc.sbuf_tensor("l0x_" + name, shape, F32))
        s = layer_sems(nc, ctx, "l0x", LN_SEMS + [
            "k_mm", "v_mm", "q_mm", "kqv", "score_mm", "masked", "top", "prob", "turn_mm", "turned", "o_mm",
            "o_sb", "oT_mm", "oT_sb", "out_mm", "dve_self"])
        ctxT = sb("ctxT", [P, TOK])
        kT = sb("kT", [P, 4, TOK])
        v = sb("v", [P, TT, D])
        qT = sb("qT", [P, 4, TOK])
        sc2 = sb("sc", [P, 2, G, 3 * P])
        pT = sb("pT", [P, G, 3, P])
        ntop = sb("ntop", [P, 4, 2 * G])
        rsum = sb("rsum", [P, TT, NH])
        o = sb("o", [P, TT, D])
        oT = sb("oT", [P, KT, TOK])
        causal = fixed[:, C_CAUSAL:C_CAUSAL + 2 * P]

        with nc.Block(no_gpsimd_drain=True) as block:
            @block.sync
            def _(sp):
                sp.dma_start(e.xres[:, :, :], e.io["x"].rearrange("(t p) d -> p t d", p=P)).then_inc(e.boot, 16)
                sp.dma_start(fixed[:, :], e.io["fixed"]).then_inc(e.boot, 16)
                sp.dma_start(ctxT[:, :], e.io["ctxT"]).then_inc(e.boot, 16)
                sp.dma_start(e.small[:, :], e.io["small"]).then_inc(e.boot, 16)
                stream(sp, e, n0, N_L0X)

            @block.tensor
            def _(pe):
                pe.wait_ge(e.boot, 64)
                w = slot_in(pe, e, n0)
                for m in range(4):
                    last = pe.matmul(ps[:, 2 + m // 2, (m % 2) * TOK:(m % 2 + 1) * TOK],
                                     w[:, 2048 + m * P:2048 + (m + 1) * P], ctxT[:, :], start=True, stop=True)
                last.then_inc(s["k_mm"], 1)
                for t in range(TT):
                    last = pe.matmul(ps[:, 4 + t, :], ctxT[:, t * P:(t + 1) * P], w[:, 2560:3072],
                                     start=True, stop=True)
                last.then_inc(s["v_mm"], 1)
                ln_tensor(pe, e, s)
                for m in range(4):
                    for k in range(KT):
                        last = pe.matmul(ps[:, 6 + m // 2, (m % 2) * TOK:(m % 2 + 1) * TOK],
                                         w[:, k * D + m * P:k * D + (m + 1) * P], e.xnT[:, k, :],
                                         start=(k == 0), stop=(k == KT - 1))
                last.then_inc(s["q_mm"], 1)
                pe.wait_ge(s["kqv"], 3)
                pe.nop().then_inc(e.w_used, 1)
                def scores(g):
                    r = slice(32 * g, 32 * g + 32)
                    if g:
                        pe.wait_ge(s["masked"], 2 * g)
                    for m in range(G):
                        pe.matmul(ps[:, 0, m * P:(m + 1) * P], qT[r, m, 0:P], kT[r, m, 0:P], start=True, stop=True)
                        last = pe.matmul(ps[:, 1 + m // 2, (m % 2) * TOK:(m % 2 + 1) * TOK], qT[r, m, P:TOK],
                                         kT[r, m, :], start=True, stop=True)
                    last.then_inc(s["score_mm"], 1)

                scores(0)
                for g in range(4):
                    if g < 3:
                        scores(g + 1)
                    sc = sc2[:, g % 2, :, :]
                    pe.wait_ge(s["prob"], 2 * G * (g + 1))
                    if g:
                        pe.wait_ge(s["turned"], 2 * g)
                    for m in range(G):
                        for b in range(3):
                            at = (m * 3 + b) * P
                            last = pe.transpose(ps[:, 3 + at // 512, at % 512:at % 512 + P],
                                                sc[:, m, b * P:(b + 1) * P], e.ident)
                    last.then_inc(s["turn_mm"], 1)
                    pe.wait_ge(s["turned"], 2 * (g + 1))
                    for m in range(G):
                        h = 4 * m + g
                        hs = slice(HD * h, HD * (h + 1))
                        pe.matmul(ps[:, 6, hs], pT[:, m, 0, :], v[:, 0, hs], start=True, stop=True)
                        pe.matmul(ps[:, 7, hs], pT[:, m, 1, :], v[:, 0, hs], start=True, stop=False)
                        last = pe.matmul(ps[:, 7, hs], pT[:, m, 2, :], v[:, 1, hs], start=False, stop=True)
                last.then_inc(s["o_mm"], 1)
                pe.wait_ge(s["o_sb"], 2)
                for k in range(KT):
                    for t in range(TT):
                        last = pe.transpose(ps[:, k // 2, (k % 2) * TOK + t * P:(k % 2) * TOK + (t + 1) * P],
                                            o[:, t, k * P:(k + 1) * P], e.ident)
                last.then_inc(s["oT_mm"], 1)
                pe.wait_ge(s["oT_sb"], 1)
                w = slot_in(pe, e, n0 + 1)
                for t in range(TT):
                    for k in range(KT):
                        last = pe.matmul(ps[:, 2 + t, :], oT[:, k, t * P:(t + 1) * P], w[:, k * D:(k + 1) * D],
                                         start=(k == 0), stop=(k == KT - 1))
                    last.then_inc(s["out_mm"], 1)
                pe.wait_ge(s["out_mm"], TT)
                pe.nop().then_inc(e.w_used, 1)

            @block.scalar
            def _(act):
                act.wait_ge(e.boot, 64)
                ln_scalar(act, e, s)
                act.wait_ge(s["v_mm"], 1)
                act.activation(v[:, :, :], ps[:, 4:6, :], ACT.Copy).then_inc(s["kqv"], 1)
                act.wait_ge(s["q_mm"], 1)
                act.activation(qT[:, :, :].rearrange("p a b -> p (a b)"),
                               ps[:, 6:8, :].rearrange("p a b -> p (a b)"), ACT.Copy).then_inc(s["kqv"], 1)
                for g in range(4):
                    sc = sc2[:, g % 2, :, :]
                    act.wait_ge(s["top"], g + 1)
                    for m in range(G):
                        h = 4 * m + g
                        act.activation(sc[:, m, 0:P], sc[:, m, 0:P], ACT.Exp, bias=ntop[:, g, m:m + 1],
                                       accum_out=rsum[:, 0, h:h + 1]).then_inc(s["prob"], 1)
                        act.activation(sc[:, m, P:3 * P], sc[:, m, P:3 * P], ACT.Exp,
                                       bias=ntop[:, g, G + m:G + m + 1],
                                       accum_out=rsum[:, 1, h:h + 1]).then_inc(s["prob"], 1)
                    act.wait_ge(s["turn_mm"], g + 1)
                    act.activation(pT[:, :, :, :].rearrange("p a b c -> p (a b c)")[:, 1024:1536],
                                   ps[:, 5, :], ACT.Copy)\
                        .then_inc(s["turned"], 1)

            @block.vector
            def _(dve):
                me = Chain(dve, s["dve_self"])
                dve.wait_ge(e.boot, 64)
                ln_vector(dve, e, s)
                dve.wait_ge(s["k_mm"], 1)
                dve.tensor_copy(kT[:, :, :].rearrange("p a b -> p (a b)"),
                                ps[:, 2:4, :].rearrange("p a b -> p (a b)")).then_inc(s["kqv"], 1)

                def turned(g):
                    dve.wait_ge(s["turn_mm"], g + 1)
                    dve.tensor_copy(pT[:, :, :, :].rearrange("p a b c -> p (a b c)")[:, 0:1024],
                                    ps[:, 3:5, :].rearrange("p a b -> p (a b)"))\
                        .then_inc(s["turned"], 1)

                for g in range(4):
                    sc = sc2[:, g % 2, :, :]
                    dve.wait_ge(s["score_mm"], g + 1)
                    if g >= 2:
                        dve.wait_ge(s["turn_mm"], g - 1)
                    dve.scalar_tensor_tensor(
                        out=sc[:, :, 0:P], in0=ps[:, 0, :].rearrange("p (m k) -> p m k", m=G), scalar=SCALE,
                        in1=causal[:, P:2 * P].unsqueeze(1).broadcast_to((P, G, P)), op0=ALU.mult, op1=ALU.add)\
                        .then_inc(s["masked"], 1)
                    dve.scalar_tensor_tensor(
                        out=sc[:, :, P:3 * P], in0=ps[:, 1:3, :].rearrange("p a (m k) -> p (a m) k", m=2),
                        scalar=SCALE, in1=causal.unsqueeze(1).broadcast_to((P, G, 2 * P)),
                        op0=ALU.mult, op1=ALU.add).then_inc(s["masked"], 1)
                    if g:
                        turned(g - 1)
                    dve.wait_ge(s["masked"], 2 * (g + 1))
                    me.did(dve.tensor_reduce(ntop[:, g, 0:G], sc[:, :, 0:P], AX_X, ALU.max))
                    me.did(dve.tensor_reduce(ntop[:, g, G:2 * G], sc[:, :, P:3 * P], AX_X, ALU.max))
                    me.wait()
                    dve.tensor_scalar(ntop[:, g, :], ntop[:, g, :], -1.0, None, ALU.mult).then_inc(s["top"], 1)
                turned(3)
                dve.wait_ge(s["prob"], 8 * G)
                me.did(dve.reciprocal(rsum[:, :, :], rsum[:, :, :]))
                me.wait()
                dve.wait_ge(s["o_mm"], 1)
                for t in range(TT):
                    dve.tensor_tensor(o[:, t, :].rearrange("p (h d) -> p h d", h=NH),
                                      ps[:, 6 + t, :].rearrange("p (h d) -> p h d", h=NH),
                                      bcast_last(rsum[:, t, :], (P, NH, HD)), ALU.mult).then_inc(s["o_sb"], 1)
                dve.wait_ge(s["oT_mm"], 1)
                dve.tensor_copy(oT[:, :, :].rearrange("p a b -> p (a b)"),
                                ps[:, 0:2, :].rearrange("p a b -> p (a b)")).then_inc(s["oT_sb"], 1)
                for t in range(TT):
                    dve.wait_ge(s["out_mm"], t + 1)
                    me.did(dve.tensor_tensor(e.xres[:, t, :], e.xres[:, t, :], ps[:, 2 + t, :], ALU.add))
        clear_sems(nc, s)
    e.n0 += N_L0X



def layer_moe(e, tag, n_experts, parts, top_k, router_at):
    nc, ps = e.nc, e.ps
    n0 = e.n0
    steps = n_experts * parts
    TURNS = steps // RING
    assert steps % RING == 0 and TURNS >= 3
    INNER = 256
    W2 = KT * 2 * INNER
    NV = max(n_experts, 8) + (8 - top_k)
    with ExitStack() as ctx:
        def sb(name, shape, dt=F32):
            return ctx.enter_context(nc.sbuf_tensor(f"{tag}_{name}", shape, dt))
        s = layer_sems(nc, ctx, tag, LN_SEMS + [
            "dve_self", "logits", "ltop", "exps", "router", "x_hi", "x_lo", "w1_hi", "w1_lo", "w2_hi", "first_mm",
            "silu", "inner", "h_hi", "h_lo", "second_mm", "added"])
        if tag == "l0f":
            open_rope_tables(e, ctx)
        prob = sb("prob", [P, TT, NV])
        left = sb("left", [P, TT, NV])
        comb = sb("comb", [P, TT, n_experts])
        top = sb("top", [P, TT, 8])
        nmax = sb("nmax", [P, TT])
        total = sb("total", [P, TT])
        x_hi, x_lo = sb("x_hi", [P, KT, TOK], F32R), sb("x_lo", [P, KT, TOK], F32R)
        w1_hi, w1_lo = sb("w1_hi", [P, 2, W2], F32R), sb("w1_lo", [P, 2, W2], F32R)
        w2_hi, w2_lo = sb("w2_hi", [P, 2, 2 * D], F32R), sb("w2_lo", [P, 2, 2 * D], F32R)
        silu = sb("silu", [P, 2, 2 * TOK])
        h = sb("h", [P, 2, 2 * TOK])
        h_hi, h_lo = sb("h_hi", [P, 2, 2, TOK], F32R), sb("h_lo", [P, 2, 2, TOK], F32R)

        def early(at, steps_back):
            turn, u = at
            return isinstance(turn, int) and turn * RING + u < steps_back

        def count(at, c, k):
            turn, u = at
            return turn * (c * RING) + (c * u + k)

        def after(at, d):
            turn, u = at
            return turn + (u + d) // RING, (u + d) % RING

        def first_hi(act, at):
            b, slot = at[1] % 2, (n0 + at[1]) % RING
            act.wait_ge(e.w_in[slot], at[0] * 16 + 16 * ((n0 + at[1]) // RING + 1))
            if not early(at, 2):
                act.wait_ge(s["first_mm"], count(at, 2, -2))
            act.activation(w1_hi[:, b, :], e.ring[:, slot, 0:W2], ACT.Copy).then_inc(s["w1_hi"], 1)

        def first_lo(dve, at):
            b, slot = at[1] % 2, (n0 + at[1]) % RING
            dve.wait_ge(s["w1_hi"], count(at, 1, 1))
            dve.tensor_tensor(w1_lo[:, b, :], e.ring[:, slot, 0:W2], w1_hi[:, b, :].bitcast(F32), ALU.subtract)\
                .then_inc(s["w1_lo"], 1)

        def second_hi(act, at):
            b, slot = at[1] % 2, (n0 + at[1]) % RING
            if not early(at, 2):
                act.wait_ge(s["second_mm"], count(at, 2, -2))
            act.activation(w2_hi[:, b, :], e.ring[:, slot, W2:SLOT], ACT.Copy).then_inc(s["w2_hi"], 1)

        def second_lo(dve, at):
            b, slot = at[1] % 2, (n0 + at[1]) % RING
            dve.wait_ge(s["w2_hi"], count(at, 1, 1))
            dve.tensor_tensor(w2_lo[:, b, :], e.ring[:, slot, W2:SLOT], w2_hi[:, b, :].bitcast(F32), ALU.subtract)\
                .then_inc(e.w_used, 1)

        def first_half(pe, at):
            b = at[1] % 2
            pe.wait_ge(s["w1_lo"], count(at, 1, 1))
            if not early(at, 2):
                pe.wait_ge(s["inner"], count(at, 1, -1))
            for f in range(4):
                out = ps[:, 2 * b + f // 2, (f % 2) * TOK:(f % 2 + 1) * TOK]
                for k in range(KT):
                    w = slice(k * 2 * INNER + f * P, k * 2 * INNER + (f + 1) * P)
                    pe.matmul(out, w1_hi[:, b, w], x_hi[:, k, :], start=(k == 0), stop=False)
                    pe.matmul(out, w1_hi[:, b, w], x_lo[:, k, :], start=False, stop=False)
                    last = pe.matmul(out, w1_lo[:, b, w], x_hi[:, k, :], start=False, stop=(k == KT - 1))
                if f % 2:
                    last.then_inc(s["first_mm"], 1)

        def second_half(pe, at):
            b = at[1] % 2
            pe.wait_ge(s["h_lo"], count(at, 1, 1))
            pe.wait_ge(e.w_used, count(at, 1, n0 + 1))
            if not early(at, 2):
                pe.wait_ge(s["added"], count(at, 2, -2))
            for t in range(TT):
                out, tok = ps[:, 4 + 2 * b + t, :], slice(t * P, (t + 1) * P)
                for k in range(2):
                    w = slice(k * D, (k + 1) * D)
                    pe.matmul(out, h_hi[:, b, k, tok], w2_hi[:, b, w], start=(k == 0), stop=False)
                    pe.matmul(out, h_hi[:, b, k, tok], w2_lo[:, b, w], start=False, stop=False)
                    last = pe.matmul(out, h_lo[:, b, k, tok], w2_hi[:, b, w], start=False, stop=(k == 1))
                last.then_inc(s["second_mm"], 1)

        def activate(act, at):
            b = at[1] % 2
            act.wait_ge(s["first_mm"], count(at, 2, 1))
            if not early(at, 2):
                act.wait_ge(s["inner"], count(at, 1, -1))
            act.activation(silu[:, b, :], ps[:, 2 * b, :], ACT.Silu).then_inc(s["silu"], 1)

        def multiply(dve, at):
            b = at[1] % 2
            dve.wait_ge(s["first_mm"], count(at, 2, 2))
            dve.wait_ge(s["silu"], count(at, 1, 1))
            if not early(at, 2):
                dve.wait_ge(s["h_lo"], count(at, 1, -1))
            dve.tensor_tensor(h[:, b, :], silu[:, b, :], ps[:, 2 * b + 1, :], ALU.mult).then_inc(s["inner"], 1)

        def inner_hi(act, at):
            b = at[1] % 2
            act.wait_ge(s["inner"], count(at, 1, 1))
            if not early(at, 2):
                act.wait_ge(s["second_mm"], count(at, 2, -2))
            act.activation(h_hi[:, b, :, :].rearrange("p k t -> p (k t)"), h[:, b, :], ACT.Copy)\
                .then_inc(s["h_hi"], 1)

        def inner_lo(dve, at):
            b = at[1] % 2
            dve.wait_ge(s["h_hi"], count(at, 1, 1))
            dve.tensor_tensor(h_lo[:, b, :, :].rearrange("p k t -> p (k t)"), h[:, b, :],
                              h_hi[:, b, :, :].rearrange("p k t -> p (k t)").bitcast(F32), ALU.subtract)\
                .then_inc(s["h_lo"], 1)

        def add(dve, at):
            turn, u = at
            b = u % 2
            expert = turn if parts == RING else turn * RING + u
            for t in range(TT):
                weight = comb[:, t, expert:expert + 1] if isinstance(turn, int) else comb[:, t, bass.ds(expert, 1)]
                dve.wait_ge(s["second_mm"], count(at, 2, t + 1))
                if not early(at, 1):
                    dve.wait_ge(s["added"], count(at, 2, t - 1))
                dve.scalar_tensor_tensor(out=e.xres[:, t, :], in0=ps[:, 4 + 2 * b + t, :], scalar=weight,
                                         in1=e.xres[:, t, :], op0=ALU.mult, op1=ALU.add).then_inc(s["added"], 1)

        def within(at, d):
            turn, u = at
            return not isinstance(turn, int) or turn * RING + u + d < steps

        def pe_step(pe, at):
            if within(at, 1):
                first_half(pe, after(at, 1))
            second_half(pe, at)

        def act_step(act, at):
            if within(at, 1):
                activate(act, after(at, 1))
                inner_hi(act, after(at, 1))
            if within(at, 3):
                first_hi(act, after(at, 3))
            if within(at, 2):
                second_hi(act, after(at, 2))

        def dve_step(dve, at):
            if within(at, 1):
                multiply(dve, after(at, 1))
                inner_lo(dve, after(at, 1))
            add(dve, at)
            if within(at, 3):
                first_lo(dve, after(at, 3))
            if within(at, 2):
                second_lo(dve, after(at, 2))

        def all_steps(eng, step):
            for u in range(RING):
                step(eng, (0, u))
            with eng.Fori(1, TURNS - 1) as i:
                for u in range(RING):
                    step(eng, (i, u))
            for u in range(RING):
                step(eng, (TURNS - 1, u))

        with nc.Block(no_gpsimd_drain=True) as block:
            @block.sync
            def _(sp):
                if tag == "l0f":
                    rope_sync(sp, e)
                stream(sp, e, n0, steps)

            if tag == "l0f":
                @block.gpsimd
                def _(pool):
                    rope_pool(pool, e)

            @block.tensor
            def _(pe):
                ln_tensor(pe, e, s)
                for t in range(TT):
                    for k in range(KT):
                        last = pe.matmul(ps[:, 7, t * 64:t * 64 + n_experts], e.xnT[:, k, t * P:(t + 1) * P],
                                         e.small[:, router_at + k * n_experts:router_at + (k + 1) * n_experts],
                                         start=(k == 0), stop=(k == KT - 1))
                last.then_inc(s["logits"], 1)
                pe.wait_ge(s["x_lo"], 1)
                first_half(pe, (0, 0))
                pe.wait_ge(s["exps"], TT)
                all_steps(pe, pe_step)

            @block.scalar
            def _(act):
                first_hi(act, (0, 0))
                first_hi(act, (0, 1))
                ln_scalar(act, e, s)
                act.wait_ge(s["ln_done"], 2)
                act.activation(x_hi[:, :, :], e.xnT, ACT.Copy).then_inc(s["x_hi"], 1)
                act.wait_ge(s["ltop"], 1)
                for t in range(TT):
                    act.activation(prob[:, t, 0:n_experts], ps[:, 7, t * 64:t * 64 + n_experts], ACT.Exp,
                                   bias=nmax[:, t:t + 1], accum_out=total[:, t:t + 1]).then_inc(s["exps"], 1)
                second_hi(act, (0, 0))
                second_hi(act, (0, 1))
                activate(act, (0, 0))
                inner_hi(act, (0, 0))
                first_hi(act, (0, 2))
                all_steps(act, act_step)

            @block.vector
            def _(dve):
                me = Chain(dve, s["dve_self"])
                me.did(dve.memset(prob[:, :, :], -1.0))
                ln_vector(dve, e, s)
                first_lo(dve, (0, 0))
                dve.wait_ge(s["x_hi"], 1)
                dve.tensor_tensor(x_lo[:, :, :], e.xnT, x_hi[:, :, :].bitcast(F32), ALU.subtract)\
                    .then_inc(s["x_lo"], 1)
                dve.wait_ge(s["logits"], 1)
                lg = ps[:, 7, 0:TT * 64].rearrange("p (t x) -> p t x", t=TT)[:, :, 0:n_experts]
                me.did(dve.tensor_reduce(nmax[:, :], lg, AX_X, ALU.max))
                me.wait()
                dve.tensor_scalar(nmax[:, :], nmax[:, :], -1.0, None, ALU.mult).then_inc(s["ltop"], 1)
                first_lo(dve, (0, 1))
                second_lo(dve, (0, 0))
                second_lo(dve, (0, 1))
                multiply(dve, (0, 0))
                inner_lo(dve, (0, 0))
                first_lo(dve, (0, 2))
                dve.wait_ge(s["exps"], TT)
                me.did(dve.reciprocal(total[:, :], total[:, :]))
                me.wait()
                for t in range(TT):
                    me.did(dve.tensor_scalar(prob[:, t, 0:n_experts], prob[:, t, 0:n_experts], total[:, t:t + 1],
                                             None, ALU.mult))
                me.wait()
                for t in range(TT):
                    me.did(dve.max(top[:, t, :], prob[:, t, :]))
                me.wait()
                if top_k < 8:
                    me.did(dve.tensor_reduce(total[:, :], top[:, :, 0:top_k], AX_X, ALU.add))
                    me.did(dve.memset(top[:, :, top_k:8], -1.0))
                    me.wait()
                    me.did(dve.reciprocal(total[:, :], total[:, :]))
                    me.wait()
                for t in range(TT):
                    me.did(dve.match_replace(left[:, t, :], top[:, t, :], prob[:, t, :], 0.0))
                me.wait()
                me.did(dve.tensor_tensor(comb[:, :, :], prob[:, :, 0:n_experts], left[:, :, 0:n_experts],
                                         ALU.subtract))
                me.wait()
                if top_k < 8:
                    for t in range(TT):
                        me.did(dve.tensor_scalar(comb[:, t, :], comb[:, t, :], total[:, t:t + 1], None, ALU.mult))
                    me.wait()
                all_steps(dve, dve_step)
        clear_sems(nc, s)
    e.n0 += steps


def layer_l0f(e):
    layer_moe(e, "l0f", 64, 1, 8, S_F0)


def layer_l1f(e):
    layer_moe(e, "l1f", 8, 4, 2, S_F1)



def softplus_vector(dve, me, x, a, s):
    dve.scalar_tensor_tensor(out=a, in0=x, scalar=-1.0, in1=x, op0=ALU.mult, op1=ALU.max).then_inc(s["sp_abs"], 1)
    dve.wait_ge(s["sp_abs"], 1)
    me.did(dve.tensor_scalar(x, x, 0.0, None, ALU.max))


def softplus_vector_end(dve, me, part, x, a, y, z, s, out):
    if part == 0:
        dve.wait_ge(s["sp_exp"], 1)
        me.did(dve.tensor_scalar(a, y, 2.0, None, ALU.add))
        me.wait()
        me.did(dve.reciprocal(a, a))
        me.wait()
        me.did(dve.tensor_tensor(z, y, a, ALU.mult))
        me.wait()
        me.did(dve.tensor_tensor(y, z, z, ALU.mult))
        me.wait()
        me.did(dve.tensor_scalar(a, y, 1.0 / 15.0, None, ALU.mult))
        return
    for n in range(6, 3, -1) if part == 1 else range(3, 0, -1):
        me.wait()
        me.did(dve.scalar_tensor_tensor(out=a, in0=a, scalar=1.0 / (2 * n + 1), in1=y, op0=ALU.add, op1=ALU.mult))
    if part == 2:
        me.wait()
        me.did(dve.scalar_tensor_tensor(out=a, in0=a, scalar=1.0, in1=z, op0=ALU.add, op1=ALU.mult))
        me.wait()
        dve.scalar_tensor_tensor(out=out, in0=a, scalar=2.0, in1=x, op0=ALU.mult, op1=ALU.add)\
            .then_inc(s["sp_done"], 1)


def softplus_scalar(act, a, y, s):
    act.wait_ge(s["sp_abs"], 1)
    act.activation(y, a, ACT.Exp, scale=-1.0).then_inc(s["sp_exp"], 1)



def layer_l0a(e):
    nc, ps = e.nc, e.ps
    n0 = e.n0
    NH, NJ = 8, 2
    STEPS = NJ * TOK
    NC = STEPS // P
    CTOK = P // NJ
    CONV_TILES, TILES = 40, 48
    LEVELS = 7
    HALF = P // 2
    ROWS_MIDDLE, ROWS_END = (8, 14, 20), 28
    with ExitStack() as ctx:
        def sb(name, shape, dt=F32, scope=ctx):
            return scope.enter_context(nc.sbuf_tensor("l0a_" + name, shape, dt))
        s = layer_sems(nc, ctx, "l0a", LN_SEMS + SPLIT_SEMS + [
            "tap",
            "dve_self", "act_self", "rows_mm", "tile_mm", "tile_ev", "pads", "conv", "silu", "sp_abs",
            "sp_exp", "sp_done", "decay", "beta", "rows", "cols_mm", "cols", "eb_mm", "scan", "kt_mm", "kt_sb",
            "vt_mm", "vt_sb", "qt_mm", "qt_sb", "norms", "normed", "squares", "reduced", "kn_mm", "kn_sb", "kb", "kb_dve", "kb_mm", "kb_d",
            "kb_a", "qn_mm", "qn_sb", "qc", "qc_mm", "qc_sb", "g_mm", "g_sb", "p_mm", "p_sb", "kd", "c0", "x0_mm", "x0_up", "ct", "y_mm",
            "y_sb", "pp_mm", "x_up", "xt_up", "ks_mm", "r_sb", "u_mm", "u_sb", "ds_mm", "sc", "s_new", "o_mm", "o_sb",
            "sq", "ss_mm", "rms", "rinv", "rb_mm", "gated", "y", "out_mm"])
        big = {i: sb(f"big{i}", [P, 4096]) for i in (0, 1, 3, 4, 5)}
        mid = {i: sb(f"mid{i}", [P, 2048]) for i in (0, 3)}
        with ExitStack() as scope:
            split = open_split(sb, scope)
        big[2] = sb("big2", [P, 4096])
        mid.update({i: sb(f"mid{i}", [P, 2048]) for i in (1, 2)})
        cols = sb("cols", [P, 128])
        squares = e.xnbuf[:, 0:1024].rearrange("p (b n) -> p b n", b=2)

        def hs(buf):
            return buf[:, 0:4096].rearrange("p (h r) -> p h r", h=NH)

        def hc(buf):
            return buf[:, 0:4096].rearrange("p (h c d) -> p h c d", h=NH, c=NC)
        kraw, keyT = hs(big[0]), hs(big[0])
        vraw, kb, AT = hs(big[1]), hc(big[1]), hc(big[1])
        ktm = hc(big[2])
        bV = hc(big[3])
        KbT, XT = hs(big[4]), hc(big[4])
        DT, X = hs(big[5]), hc(big[5])
        qraw = mid[0][:, :].rearrange("p (h t) -> p h t", h=NH)
        QT = qraw
        qtm = mid[1][:, :].rearrange("p (h t d) -> p h t d", h=NH, t=TT)
        PT = mid[1][:, :].rearrange("p (h c t) -> p h c t", h=NH, c=NC)
        QcT = mid[2][:, :].rearrange("p (h t) -> p h t", h=NH)
        gate = mid[3][:, :].rearrange("p (h t) -> p h t", h=NH)
        OT = e.xnbuf[:, :].rearrange("p (h t) -> p h t", h=NH)
        pad = big[3][:, 0:CR * 259].rearrange("p (b n) -> p b n", b=CR)
        conv = big[3][:, 1536:1536 + CR * TOK].rearrange("p (b n) -> p b n", b=CR)
        rows = big[4][0:8, :]
        r_x, r_a, r_y, r_z = (rows[:, i * TOK:(i + 1) * TOK] for i in range(4))
        r_e, r_e0, r_c, r_b = (rows[:, 1024 + i * STEPS:1024 + (i + 1) * STEPS] for i in range(4))
        r_0 = rows[:, 3072:3072 + P]
        r_negA = rows[:, 3200:3201]
        CTm = e.xnbuf[:, 0:1024].rearrange("p (b c n) -> p b c n", b=2, c=NC)
        Y = e.xnbuf[:, 1024:2048].rearrange("p (b c n) -> p b c n", b=2, c=NC)
        R = big[1][:, 0:1024].rearrange("p (h d) -> p h d", h=NH)
        U = big[1][:, 1024:2048].rearrange("p (h d) -> p h d", h=NH)
        S = big[1][:, 2048:4096].rearrange("p (b h d) -> p b h d", b=2, h=NH)
        sq = big[5][:, 0:2048].rearrange("p (h t) -> p h t", h=NH)
        yT = big[5][:, 2048:4096].rearrange("p (h t) -> p h t", h=NH)
        beta = cols[:, 0:32].rearrange("p (c h) -> p c h", h=NH)
        cum = cols[:, 32:64].rearrange("p (c h) -> p c h", h=NH)
        ctok = cols[:, 64:80].rearrange("p (t h) -> p t h", h=NH)
        cend = cols[:, 80:112].rearrange("p (h c) -> p h c", h=NH)
        nbc = sb("nbc", [P, NC, NH])
        knorm = sb("knorm", [P, NH, NC])
        qnorm = sb("qnorm", [P, NH, TT])
        dend = sb("dend", [P, NH, NC])
        srow = sb("srow", [8, 2 * TOK])
        ident, ident4, small = e.ident, e.ident4, e.small

        def taps(i, j):
            return small[:, S_ACONV + 4 * i + j:S_ACONV + 4 * i + j + 1]

        def conv_out(i):
            if i < 8:
                return qraw[:, i, :]
            raw, i = (kraw, i - 8) if i < 24 else (vraw, i - 24)
            return raw[:, i % NH, :].rearrange("p (t j) -> p j t", j=NJ)[:, i // NH, :]

        with nc.Block(no_gpsimd_drain=True) as block:
            @block.sync
            def _(sp):
                stream(sp, e, n0, N_L0A)

            @block.tensor
            def _(pe):
                ln_tensor(pe, e, s)
                for j in range(3):
                    for k in range(KT):
                        last = pe.matmul(ps[0:8, min(4 + j, 5), (j // 2) * TOK:(j // 2 + 1) * TOK],
                                         small[:, S_AAB + 24 * k + 8 * j:S_AAB + 24 * k + 8 * j + 8],
                                         e.xnT[:, k, :], start=(k == 0), stop=(k == KT - 1))
                last.then_inc(s["rows_mm"], 1)

                def columns():
                    pe.wait_ge(s["rows"], 2)
                    for c in range(NC):
                        pe.transpose(ps[:, 5, 8 * c:8 * c + 8], r_b[:, c * P:(c + 1) * P], ident[0:8, 0:8])
                        pe.transpose(ps[:, 5, 32 + 8 * c:40 + 8 * c], r_c[:, c * P:(c + 1) * P], ident[0:8, 0:8])
                    for t in range(TT):
                        at = t * NJ * P
                        pe.transpose(ps[:, 5, 64 + 8 * t:72 + 8 * t], r_c[:, at + 1:at + NJ * P:NJ], ident[0:8, 0:8])
                    for h in range(NH):
                        last = pe.matmul(ps[:, 5, 80 + 4 * h:84 + 4 * h], ident[0:8, h:h + 1].broadcast_to((8, P)),
                                         r_c[:, P - 1:STEPS:P], start=True, stop=True)
                    last.then_inc(s["cols_mm"], 1)

                def decays(h):
                    if h >= 2:
                        pe.wait_ge(s["scan"], h - 1)
                    pe.matmul(ps[:, 6 + h % 2, :], ident[0:8, h:h + 1].broadcast_to((8, P)), r_e0,
                              start=True, stop=True).then_inc(s["eb_mm"], 1)

                for i in range(TILES):
                    if i == CONV_TILES:
                        columns()
                    if i >= CONV_TILES:
                        decays(i - CONV_TILES)
                    project_tile(pe, e, s, i, split)
                pe.wait_ge(s["silu"], TILES)
                pe.nop().then_inc(e.w_used, 1)
                for h in range(NH):
                    if h >= 2:
                        pe.wait_ge(s["kt_sb"], h - 1)
                    for c in range(NC):
                        last = pe.transpose(ps[:, h % 2, c * P:(c + 1) * P], kraw[:, h, c * P:(c + 1) * P], ident)
                    last.then_inc(s["kt_mm"], 1)
                    if h % 2 == 0:
                        if h >= 4:
                            pe.wait_ge(s["qt_sb"], h // 2 - 1)
                        for x in range(2):
                            for t in range(TT):
                                last = pe.transpose(ps[:, 2 + h // 2 % 2, (2 * x + t) * P:(2 * x + t + 1) * P],
                                                    qraw[:, h + x, t * P:(t + 1) * P], ident)
                        last.then_inc(s["qt_mm"], 1)
                    if h == 0:
                        pe.wait_ge(s["cols"], 1)
                    if h >= 2:
                        pe.wait_ge(s["vt_sb"], h - 1)
                    for c in range(NC):
                        last = pe.transpose(ps[:, 4 + h % 2, c * P:(c + 1) * P], vraw[:, h, c * P:(c + 1) * P],
                                            ident)
                    last.then_inc(s["vt_mm"], 1)
                for m in range(2 * NC):
                    c, x = divmod(m, 2)
                    pe.wait_ge(s["normed"], c + 1)
                    if m >= 2:
                        pe.wait_ge(s["kn_sb"], m - 1)
                    for h in range(4):
                        last = pe.transpose(ps[:, x, h * P:(h + 1) * P], ktm[:, 4 * x + h, c, :], ident)
                    last.then_inc(s["kn_mm"], 1)
                pe.wait_ge(s["normed"], NC + 1)
                for h in range(0, NH, 2):
                    if h >= 4:
                        pe.wait_ge(s["qn_sb"], h // 2 - 1)
                    for x in range(2):
                        for t in range(TT):
                            last = pe.transpose(ps[:, 2 + h // 2 % 2, (2 * x + t) * P:(2 * x + t + 1) * P],
                                                qtm[:, h + x, t, :], ident)
                    last.then_inc(s["qn_mm"], 1)
                for m in range(2 * NC):
                    c, x = divmod(m, 2)
                    pe.wait_ge(s["kb"] if c < NC // 2 else s["kb_dve"], c % (NC // 2) + 1)
                    if m >= 2:
                        pe.wait_ge(s["kb_a" if x else "kb_d"], c)
                    for h in range(4):
                        last = pe.transpose(ps[:, 4 + x, h * P:(h + 1) * P], kb[:, 4 * x + h, c, :], ident)
                    last.then_inc(s["kb_mm"], 1)
                pe.wait_ge(s["qn_sb"], 4)
                pe.wait_ge(s["kb_a"], 4)
                pe.wait_ge(s["kb_d"], 4)
                for h in range(NH):
                    if h >= 2:
                        pe.wait_ge(s["g_sb"], h - 1)
                    for c in range(NC):
                        at = slice(c * P, (c + 1) * P)
                        last = pe.matmul(ps[:, 2 + h % 2, at], keyT[:, h, at], KbT[:, h, at], start=True, stop=True)
                    last.then_inc(s["g_mm"], 1)
                pe.wait_ge(s["qc"], TT)
                pe.wait_ge(s["kn_sb"], 2 * NC)
                for h in range(0, NH, 2):
                    if h >= 4:
                        pe.wait_ge(s["qc_sb"], h // 2 - 1)
                    for x in range(2):
                        for t in range(TT):
                            last = pe.transpose(ps[:, h // 2 % 2, (2 * x + t) * P:(2 * x + t + 1) * P],
                                                qtm[:, h + x, t, :], ident)
                    last.then_inc(s["qc_mm"], 1)
                for h in range(1, NH, 2):
                    if h >= 5:
                        pe.wait_ge(s["p_sb"], h // 2 - 1)
                    for x in range(2):
                        for c in range(NC):
                            last = pe.matmul(ps[:, 6 + h // 2 % 2, (x * NC + c) * CTOK:(x * NC + c + 1) * CTOK],
                                             keyT[:, h - 1 + x, c * P:(c + 1) * P],
                                             QT[:, h - 1 + x, c * CTOK:(c + 1) * CTOK], start=True, stop=True)
                    last.then_inc(s["p_mm"], 1)
                pe.wait_ge(s["g_sb"], NH)
                pe.wait_ge(s["qc_sb"], 4)

                def level_0(h):
                    pe.wait_ge(s["xt_up"], h + 1)
                    if h >= 2:
                        pe.wait_ge(s["x0_up"], h - 1)
                    for c in range(NC):
                        last = pe.transpose(ps[:, h % 2, c * P:(c + 1) * P], XT[:, h, c, :], ident)
                    last.then_inc(s["x0_mm"], 1)

                def level_y(n):
                    l, h = divmod(n, NH)
                    pe.wait_ge(s["ct"], n - NH + 1)
                    if l == 1:
                        pe.wait_ge(s["x0_up"], h + 1)
                    else:
                        pe.wait_ge(s["x_up"], n - 2 * NH + 1)
                    if n - 2 < NH:
                        pe.wait_ge(s["x0_up"], n - 1)
                    else:
                        pe.wait_ge(s["y_sb"], n - 1 - NH)
                    for c in range(NC):
                        last = pe.matmul(ps[:, n % 2, c * P:(c + 1) * P], CTm[:, n % 2, c, :],
                                         X[:, h, c, :], start=True, stop=True)
                    last.then_inc(s["y_mm"], 1)

                def level_xy(n):
                    l, h = divmod(n, NH)
                    pe.wait_ge(s["y_sb"], n - NH + 1)
                    pe.wait_ge(s["xt_up"], n - NH + 1)
                    if n - NH >= 2:
                        pe.wait_ge(s["xt_up"], n - 1)
                        pe.wait_ge(s["x_up"], min(n - 1 - NH, NH * (LEVELS - 2)))
                    for c in range(NC):
                        at = slice(c * P, (c + 1) * P)
                        if l == LEVELS - 1:
                            last = pe.matmul(ps[0:HALF, 4 + n % 2, c * HALF:(c + 1) * HALF],
                                             Y[:, n % 2, c, 0:HALF], XT[:, h, c, HALF:P], start=True, stop=True)
                            continue
                        pe.matmul(ps[:, 2 + n % 2, at], XT[:, h, c, :], Y[:, n % 2, c, :], start=True, stop=True)
                        last = pe.matmul(ps[:, 4 + n % 2, at], Y[:, n % 2, c, :], XT[:, h, c, :],
                                         start=True, stop=True)
                    last.then_inc(s["pp_mm"], 1)

                for h in range(NH):
                    level_0(h)
                for n in range(NH, NH * LEVELS + 2):
                    if n < NH * LEVELS:
                        level_y(n)
                    if n >= NH + 2:
                        level_xy(n - 2)
                pe.wait_ge(s["xt_up"], NH * LEVELS)
                pe.wait_ge(s["kd"], NC)

                for c in range(NC):
                    at = slice(c * P, (c + 1) * P)
                    for x in range(2):
                        if c:
                            pe.wait_ge(s["s_new"], 2 * (c - 1) + x + 1)
                            for h in range(4 * x, 4 * x + 4):
                                last = pe.matmul(ps[:, x, (h % 4) * P:(h % 4 + 1) * P], keyT[:, h, at],
                                                 S[:, c % 2, h, :], start=True, stop=True)
                            last.then_inc(s["ks_mm"], 1)
                    for x in range(2):
                        pe.wait_ge(s["r_sb"], 2 * c + x + 1)
                        for h in range(4 * x, 4 * x + 4):
                            last = pe.matmul(ps[:, 2 + x, (h % 4) * P:(h % 4 + 1) * P], XT[:, h, c, :], R[:, h, :],
                                             start=True, stop=True)
                        last.then_inc(s["u_mm"], 1)
                    for x in range(2):
                        pe.wait_ge(s["u_sb"], 2 * c + x + 1)
                        if c < NC - 1:
                            for h in range(4 * x, 4 * x + 4):
                                last = pe.matmul(ps[:, 4 + x, (h % 4) * P:(h % 4 + 1) * P], ktm[:, h, c, :],
                                                 U[:, h, :], start=True, stop=True)
                            last.then_inc(s["ds_mm"], 1)
                    if c >= 2:
                        pe.wait_ge(s["o_sb"], c - 1)
                    for h in range(NH):
                        o = ps[:, 6 + c % 2, h * CTOK:(h + 1) * CTOK]
                        if c:
                            pe.matmul(o, S[:, c % 2, h, :], QcT[:, h, c * CTOK:(c + 1) * CTOK],
                                      start=True, stop=False)
                        last = pe.matmul(o, U[:, h, :], PT[:, h, c, :], start=(c == 0), stop=True)
                    last.then_inc(s["o_mm"], 1)
                pe.wait_ge(s["sq"], NC)
                for h in range(NH):
                    last = pe.matmul(ps[0:8, 0, 0:TOK], e.fixed[:, C_PICK + 8 * h:C_PICK + 8 * h + 8], sq[:, h, :],
                                     start=(h == 0), stop=(h == NH - 1))
                last.then_inc(s["ss_mm"], 1)
                pe.wait_ge(s["rinv"], 1)
                for h in range(NH):
                    last = pe.matmul(ps[:, 2 + h // 2, (h % 2) * TOK:(h % 2 + 1) * TOK],
                                     ident[0:8, h:h + 1].broadcast_to((8, P)), srow[:, TOK:2 * TOK],
                                     start=True, stop=True)
                last.then_inc(s["rb_mm"], 1)
                for t in range(TT):
                    pe.wait_ge(s["y"], t + 1)
                    for h in range(NH):
                        w = slot_in(pe, e, n0 + 8 + h // 4)
                        last = pe.matmul(ps[:, 6 + t, :], yT[:, h, t * P:(t + 1) * P],
                                         w[:, (h % 4) * D:(h % 4 + 1) * D], start=(h == 0), stop=(h == NH - 1))
                    last.then_inc(s["out_mm"], 1)
                pe.wait_ge(s["out_mm"], TT)
                for _ in range(2):
                    pe.nop().then_inc(e.w_used, 1)

            @block.scalar
            def _(act):
                me = Chain(act, s["act_self"])
                ln_scalar(act, e, s)
                split_x_hi(act, e, s, split[2])
                for i in range(AHEAD):
                    split_w_hi(act, e, s, i, split[0])

                def silu(i):
                    act.wait_ge(s["conv"], i + 1)
                    act.activation(conv_out(i), conv[:, i % CR, :], ACT.Silu).then_inc(s["silu"], 1)

                act.wait_ge(s["rows_mm"], 1)
                rb = r_b.rearrange("p (t j) -> p j t", j=NJ)
                act.activation(rb[:, 0, :], ps[0:8, 5, 0:TOK], ACT.Sigmoid).then_inc(s["beta"], 1)
                act.activation(rb[:, 1, :], ps[0:8, 5, TOK:2 * TOK], ACT.Sigmoid).then_inc(s["beta"], 1)
                me.did(act.activation(r_negA, small[0:8, S_AHEAD:S_AHEAD + 1], ACT.Exp))
                me.wait()
                me.did(act.activation(r_negA, r_negA, ACT.Copy, scale=-1.0))
                softplus_scalar(act, r_a, r_y, s)
                me.wait()
                act.wait_ge(s["pads"], 1)
                for i in range(CONV_TILES):
                    if i + AHEAD < TILES:
                        split_w_hi(act, e, s, i + AHEAD, split[0])
                    act.wait_ge(s["tile_mm"], i + 1)
                    if i % 2:
                        tap_scalar(act, s, i, conv[:, i % CR, :], ps[:, i % 4, 0:TOK], taps(i, 3))
                    if i >= CR:
                        act.wait_ge(s["conv"], i - CR + 1)
                    act.activation(pad[:, i % CR, 3:3 + TOK], ps[:, i % 4, 0:TOK], ACT.Copy).then_inc(s["tile_ev"], 1)
                    if i >= SILU_LAG:
                        silu(i - SILU_LAG)
                    if i == ROWS_MIDDLE[-1] + 2:
                        act.wait_ge(s["sp_done"], 1)
                        act.activation(r_e.rearrange("p (t j) -> p j t", j=NJ)[:, 0, :], r_z, ACT.Exp, scale=r_negA)\
                            .then_inc(s["decay"], 1)
                for i in range(CONV_TILES - SILU_LAG, CONV_TILES):
                    silu(i)
                for i in range(CONV_TILES, TILES):
                    if i + AHEAD < TILES:
                        split_w_hi(act, e, s, i + AHEAD, split[0])
                    act.wait_ge(s["tile_mm"], i + 1)
                    act.wait_ge(s["silu"], i)
                    act.activation(gate[:, i - CONV_TILES, :], ps[:, i % 4, 0:TOK], ACT.Silu).then_inc(s["silu"], 1)
                    if i == CONV_TILES:
                        act.wait_ge(s["cols_mm"], 1)
                        act.activation(cols[:, 0:112], ps[:, 5, 0:112], ACT.Copy).then_inc(s["cols"], 1)
                    if i < TILES - 4:
                        act.wait_ge(s["silu"], i + 1)
                        act.nop().then_inc(s["tile_ev"], 1)
                def squared(n, bank):
                    if n >= 2:
                        act.wait_ge(s["reduced"], n - 1)
                    act.activation(squares[:, n % 2, :], bank, ACT.Square).then_inc(s["squares"], 1)

                n = 0
                for h in range(NH):
                    act.wait_ge(s["kt_mm"], h + 1)
                    squared(n, ps[:, h % 2, :])
                    n += 1
                    act.activation(ktm[:, h, :, :].rearrange("p c d -> p (c d)"), ps[:, h % 2, :], ACT.Copy)\
                        .then_inc(s["kt_sb"], 1)
                    if h % 2 == 0:
                        act.wait_ge(s["qt_mm"], h // 2 + 1)
                        squared(n, ps[:, 2 + h // 2 % 2, :])
                        n += 1
                        act.activation(qtm[:, h:h + 2, :, :].rearrange("p h t d -> p (h t d)"),
                                       ps[:, 2 + h // 2 % 2, :], ACT.Copy).then_inc(s["qt_sb"], 1)
                act.wait_ge(s["reduced"], NH + NH // 2)
                act.activation(knorm[:, :, :], knorm[:, :, :], ACT.Sqrt).then_inc(s["norms"], 1)
                act.activation(qnorm[:, :, :], qnorm[:, :, :], ACT.Sqrt).then_inc(s["norms"], 1)
                for m in range(2 * NC):
                    c, x = divmod(m, 2)
                    act.wait_ge(s["kn_mm"], m + 1)
                    act.activation(keyT[:, 4 * x:4 * x + 4, c * P:(c + 1) * P],
                                   ps[:, x, :].rearrange("p (h r) -> p h r", h=4), ACT.Copy).then_inc(s["kn_sb"], 1)
                for j in range(4):
                    act.wait_ge(s["qn_mm"], j + 1)
                    act.activation(QT[:, 2 * j:2 * j + 2, :].rearrange("p h t -> p (h t)"), ps[:, 2 + j % 2, :],
                                   ACT.Copy).then_inc(s["qn_sb"], 1)
                act.wait_ge(s["scan"], NH)
                for c in range(NC):
                    act.wait_ge(s["kb_mm"], 2 * c + 2)
                    act.activation(KbT[:, 4:8, c * P:(c + 1) * P], ps[:, 5, :].rearrange("p (h r) -> p h r", h=4),
                                   ACT.Copy).then_inc(s["kb_a"], 1)
                for j in range(4):
                    act.wait_ge(s["qc_mm"], j + 1)
                    act.activation(QcT[:, 2 * j:2 * j + 2, :].rearrange("p h t -> p (h t)"), ps[:, j % 2, :],
                                   ACT.Copy).then_inc(s["qc_sb"], 1)
                for h in range(NH):
                    act.wait_ge(s["x0_mm"], h + 1)
                    act.wait_ge(s["p_sb"], h // 2 + 1)
                    act.activation(X[:, h, :, :].rearrange("p c d -> p (c d)"), ps[:, h % 2, :], ACT.Copy)\
                        .then_inc(s["x0_up"], 1)
                for n in range(NH, NH * LEVELS):
                    act.wait_ge(s["y_mm"], n - NH + 1)
                    if n - NH >= 2:
                        act.wait_ge(s["pp_mm"], n - NH - 1)
                    act.activation(Y[:, n % 2, :, :].rearrange("p c d -> p (c d)"), ps[:, n % 2, :], ACT.Copy)\
                        .then_inc(s["y_sb"], 1)
                for c in range(NC):
                    for x in range(2):
                        act.wait_ge(s["u_mm"], 2 * c + x + 1)
                        if c:
                            act.wait_ge(s["o_mm"], c)
                        act.activation(U[:, 4 * x:4 * x + 4, :].rearrange("p h d -> p (h d)"), ps[:, 2 + x, :],
                                       ACT.Copy).then_inc(s["u_sb"], 1)
                    act.wait_ge(s["o_mm"], c + 1)
                    act.activation(OT[:, :, c * CTOK:(c + 1) * CTOK],
                                   ps[:, 6 + c % 2, :].rearrange("p (h t) -> p h t", h=NH), ACT.Copy)\
                        .then_inc(s["o_sb"], 1)
                    act.wait_ge(s["o_sb"], c + 1)
                    ct = slice(c * CTOK, (c + 1) * CTOK)
                    act.activation(sq[:, :, ct], OT[:, :, ct], ACT.Square).then_inc(s["sq"], 1)
                act.wait_ge(s["ss_mm"], 1)
                act.activation(srow[:, 0:TOK], ps[0:8, 0, 0:TOK], ACT.Sqrt, bias=e.eps[0:8, :], scale=1.0 / P)\
                    .then_inc(s["rms"], 1)

            @block.gpsimd
            def _(pool):
                for i in range(TILES):
                    split_w_lo(pool, e, s, i, *split[0:2])
                pool.wait_ge(s["vt_mm"], NH)
                for c in range(NC // 2):
                    pool.wait_ge(s["normed"], c + 1)
                    pool.tensor_tensor(kb[:, :, c, :], ktm[:, :, c, :], bcast_last(beta[:, c, :], (P, NH, P)),
                                       ALU.mult).then_inc(s["kb"], 1)
                def level(l):
                    return e.fixed[:, C_LEVEL + l * P:C_LEVEL + (l + 1) * P].unsqueeze(1).broadcast_to((P, NC, P))

                for h in range(NH):
                    pool.wait_ge(s["g_sb"], h + 1)
                    pool.tensor_tensor(XT[:, h, :, :], AT[:, h, :, :], level(0), ALU.mult).then_inc(s["c0"], 1)
                for n in range(NH, NH * LEVELS):
                    l, h = divmod(n, NH)
                    if n - 2 >= NH:
                        pool.wait_ge(s["y_mm"], n - 1 - NH)
                    pool.tensor_tensor(CTm[:, n % 2, :, :], AT[:, h, :, :], level(l), ALU.mult).then_inc(s["ct"], 1)
                for c in range(1, NC - 1):
                    for x in range(2):
                        pool.wait_ge(s["s_new"], 2 * (c - 1) + x + 1)
                        if c >= 2:
                            pool.wait_ge(s["o_mm"], c)
                        hh = slice(4 * x, 4 * x + 4)
                        pool.tensor_tensor(S[:, (c + 1) % 2, hh, :], S[:, c % 2, hh, :],
                                           bcast_last(cend[:, hh, c], (P, 4, P)), ALU.mult).then_inc(s["sc"], 1)

            @block.vector
            def _(dve):
                me = Chain(dve, s["dve_self"])
                ln_vector(dve, e, s)
                split_x_lo(dve, e, s, split[2], split[3])
                dve.memset(pad[:, :, :], 0.0).then_inc(s["pads"], 1)

                def rows_start():
                    dve.wait_ge(s["rows_mm"], 1)
                    me.did(dve.memset(r_e, 1.0))
                    me.did(dve.memset(r_0, 0.0))
                    me.did(dve.tensor_scalar(r_x, ps[0:8, 4, 0:TOK], small[0:8, S_AHEAD + 1:S_AHEAD + 2], None,
                                             ALU.add))
                    me.wait()
                    softplus_vector(dve, me, r_x, r_a, s)

                def rows_middle(part):
                    softplus_vector_end(dve, me, part, r_x, r_a, r_y, r_z, s, r_z)
                    if part == 0:
                        dve.wait_ge(s["beta"], 2)
                        dve.tensor_scalar(r_b, r_b, 2.0, None, ALU.mult).then_inc(s["rows"], 1)

                def rows_end():
                    dve.wait_ge(s["decay"], 1)
                    me.did(dve.tensor_copy(r_e0, r_e))
                    me.wait()
                    me.did(dve.memset(r_e0[:, 0:STEPS:P], 0.0))
                    for c in range(NC):
                        at = slice(c * P, (c + 1) * P)
                        me.did(dve.tensor_tensor_scan(r_c[:, at], r_e[:, at], r_0, 1.0, ALU.mult, ALU.add))
                    me.wait()
                    dve.nop().then_inc(s["rows"], 1)

                rows_start()
                for i in range(CONV_TILES):
                    if i in ROWS_MIDDLE:
                        rows_middle(ROWS_MIDDLE.index(i))
                    if i == ROWS_END:
                        rows_end()
                    if i % 2 == 0:
                        convolve(dve, me, s, i, pad, conv, taps)
                for h in range(NH):
                    dve.wait_ge(s["eb_mm"], h + 1)
                    dve.tensor_tensor_scan(DT[:, h, :], ps[:, 6 + h % 2, :], ident4, 0.0, ALU.mult, ALU.add)\
                        .then_inc(s["scan"], 1)
                dve.wait_ge(s["cols"], 1)
                me.did(dve.scalar_tensor_tensor(out=nbc[:, :, :], in0=beta, scalar=-1.0, in1=cum, op0=ALU.mult,
                                                op1=ALU.mult))
                dve.wait_ge(s["scan"], NH)
                me.did(dve.tensor_copy(dend[:, :, :], DT[:, :, P - 1:STEPS:P]))
                def norm(n, out, parts):
                    dve.wait_ge(s["squares"], n + 1)
                    dve.tensor_reduce(out, squares[:, n % 2, :].rearrange("p (a d) -> p a d", a=parts), AX_X, ALU.add)\
                        .then_inc(s["reduced"], 1)

                n = 0
                for h in range(NH):
                    norm(n, knorm[:, h, :], NC)
                    n += 1
                    if h % 2 == 0:
                        norm(n, qnorm[:, h:h + 2, :].rearrange("p h t -> p (h t)"), 2 * TT)
                        n += 1
                    dve.wait_ge(s["vt_mm"], h + 1)
                    dve.tensor_tensor(bV[:, h, :, :], ps[:, 4 + h % 2, :].rearrange("p (c d) -> p c d", c=NC),
                                      bcast_last(beta[:, :, h], (P, NC, P)), ALU.mult).then_inc(s["vt_sb"], 1)
                dve.wait_ge(s["norms"], 2)
                for v, f in ((knorm, 1.0), (qnorm, 1.0 / float(np.sqrt(P)))):
                    me.did(dve.tensor_scalar(v[:, :, :], v[:, :, :], 1e-12, None, ALU.max))
                    me.wait()
                    me.did(dve.reciprocal(v[:, :, :], v[:, :, :]))
                    me.wait()
                    if f != 1.0:
                        me.did(dve.tensor_scalar(v[:, :, :], v[:, :, :], f, None, ALU.mult))
                        me.wait()
                dve.wait_ge(s["kt_sb"], NH)
                for c in range(NC):
                    dve.tensor_tensor(ktm[:, :, c, :], ktm[:, :, c, :], bcast_last(knorm[:, :, c], (P, NH, P)),
                                      ALU.mult).then_inc(s["normed"], 1)
                dve.wait_ge(s["qt_sb"], 4)
                dve.tensor_tensor(qtm[:, :, :, :].rearrange("p h c d -> p (h c) d"),
                                  qtm[:, :, :, :].rearrange("p h c d -> p (h c) d"),
                                  bcast_last(qnorm[:, :, :].rearrange("p h c -> p (h c)"), (P, NH * TT, P)),
                                  ALU.mult).then_inc(s["normed"], 1)
                dve.wait_ge(s["vt_mm"], NH)
                for c in range(NC // 2, NC):
                    dve.wait_ge(s["normed"], c + 1)
                    dve.tensor_tensor(kb[:, :, c, :], ktm[:, :, c, :], bcast_last(beta[:, c, :], (P, NH, P)),
                                      ALU.mult).then_inc(s["kb_dve"], 1)
                dve.wait_ge(s["qn_mm"], 4)
                for x in range(TT):
                    dve.tensor_tensor(qtm[:, :, x, :], qtm[:, :, x, :], bcast_last(ctok[:, x, :], (P, NH, P)),
                                      ALU.mult).then_inc(s["qc"], 1)
                for c in range(NC):
                    dve.wait_ge(s["kb_mm"], 2 * c + 1)
                    dve.tensor_copy(KbT[:, 0:4, c * P:(c + 1) * P], ps[:, 4, :].rearrange("p (h r) -> p h r", h=4))\
                        .then_inc(s["kb_d"], 1)

                def end_keys(c):
                    dve.tensor_tensor(ktm[:, :, c, :], ktm[:, :, c, :], bcast_last(dend[:, :, c], (P, NH, P)),
                                      ALU.mult).then_inc(s["kd"], 1)

                def identity_0(h):
                    dve.wait_ge(s["c0"], h + 1)
                    xt = XT[:, h, :, :].rearrange("p c d -> p (c d)")
                    dve.tensor_tensor(xt, xt, ident4, ALU.add).then_inc(s["xt_up"], 1)

                for h in range(NH):
                    dve.wait_ge(s["g_mm"], h + 1)
                    if h == 0:
                        dve.wait_ge(s["kb_mm"], NH)
                    dve.tensor_tensor(AT[:, h, :, :].rearrange("p c d -> p (c d)"), ps[:, 2 + h % 2, :], DT[:, h, :],
                                      ALU.mult).then_inc(s["g_sb"], 1)
                    if h >= 3:
                        identity_0(h - 3)
                for h in range(NH - 3, NH):
                    identity_0(h)
                dve.wait_ge(s["qc_mm"], 4)
                for h in range(1, NH, 2):
                    dve.wait_ge(s["p_mm"], h // 2 + 1)
                    dve.tensor_tensor(
                        PT[:, h - 1:h + 1, :, :].rearrange("p h c t -> p (h c) t"),
                        ps[:, 6 + h // 2 % 2, :].rearrange("p (a t) -> p a t", t=CTOK),
                        DT[:, h - 1:h + 1, :].rearrange("p h (c t j) -> p (h c) t j", c=NC, j=NJ)[:, :, :, 1],
                        ALU.mult).then_inc(s["p_sb"], 1)
                dve.wait_ge(s["g_sb"], NH)
                dve.wait_ge(s["p_sb"], 4)
                for n in range(NH, NH * LEVELS):
                    l, h = divmod(n, NH)
                    x, xt = (v[:, h, :, :].rearrange("p c d -> p (c d)") for v in (X, XT))
                    if h == 0 and l <= NC:
                        end_keys(l - 1)
                    dve.wait_ge(s["pp_mm"], n - NH + 1)
                    dve.wait_ge(s["xt_up"], n - NH + 1)
                    if l < LEVELS - 1:
                        if l == 1:
                            dve.wait_ge(s["x0_up"], h + 1)
                        else:
                            dve.wait_ge(s["x_up"], n - 2 * NH + 1)
                        dve.tensor_tensor(x, x, ps[:, 2 + n % 2, :], ALU.subtract).then_inc(s["x_up"], 1)
                        dve.tensor_tensor(xt, xt, ps[:, 4 + n % 2, :], ALU.subtract).then_inc(s["xt_up"], 1)
                    else:
                        block = XT[0:HALF, h, :, HALF:P]
                        dve.tensor_tensor(block, block, ps[0:HALF, 4 + n % 2, 0:NC * HALF]
                                          .rearrange("p (c n) -> p c n", c=NC), ALU.subtract).then_inc(s["xt_up"], 1)
                def gated(c):
                    dve.wait_ge(s["o_sb"], c + 1)
                    ct = slice(c * CTOK, (c + 1) * CTOK)
                    dve.scalar_tensor_tensor(out=yT[:, :, ct], in0=OT[:, :, ct], scalar=small[:, S_ANORM:S_ANORM + 1],
                                             in1=gate[:, :, ct], op0=ALU.mult, op1=ALU.mult).then_inc(s["gated"], 1)

                dve.wait_ge(s["ct"], NH * (LEVELS - 1))
                for c in range(NC):
                    for x in range(2):
                        hh = slice(4 * x, 4 * x + 4)
                        if c == 0:
                            dve.tensor_copy(R[:, hh, :], bV[:, hh, c, :]).then_inc(s["r_sb"], 1)
                            continue
                        dve.wait_ge(s["ks_mm"], 2 * (c - 1) + x + 1)
                        dve.wait_ge(s["u_mm"], 2 * (c - 1) + x + 1)
                        me.did(dve.tensor_tensor(R[:, hh, :], ps[:, x, :].rearrange("p (h d) -> p h d", h=4),
                                                 bcast_last(nbc[:, c, hh], (P, 4, P)), ALU.mult))
                        me.wait()
                        dve.tensor_tensor(R[:, hh, :], R[:, hh, :], bV[:, hh, c, :], ALU.add).then_inc(s["r_sb"], 1)
                    if c == NC - 1:
                        gated(c - 1)
                        continue
                    if c:
                        gated(c - 1)
                    for x in range(2):
                        hh = slice(4 * x, 4 * x + 4)
                        dve.wait_ge(s["ds_mm"], 2 * c + x + 1)
                        new = S[:, (c + 1) % 2, hh, :]
                        add = ps[:, 4 + x, :].rearrange("p (h d) -> p h d", h=4)
                        if c == 0:
                            dve.tensor_copy(new, add).then_inc(s["s_new"], 1)
                            continue
                        dve.wait_ge(s["sc"], 2 * (c - 1) + x + 1)
                        dve.tensor_tensor(new, new, add, ALU.add).then_inc(s["s_new"], 1)
                gated(NC - 1)
                dve.wait_ge(s["rms"], 1)
                dve.reciprocal(srow[:, TOK:2 * TOK], srow[:, 0:TOK]).then_inc(s["rinv"], 1)
                dve.wait_ge(s["rb_mm"], 1)
                dve.wait_ge(s["gated"], NC)
                for t in range(TT):
                    at = slice(t * P, (t + 1) * P)
                    rms = ps[:, 2:6, :].rearrange("p a (x n) -> p (a x) n", x=2)[:, :, at]
                    dve.tensor_tensor(yT[:, :, at], yT[:, :, at], rms, ALU.mult).then_inc(s["y"], 1)
                for t in range(TT):
                    dve.wait_ge(s["out_mm"], t + 1)
                    me.did(dve.tensor_tensor(e.xres[:, t, :], e.xres[:, t, :], ps[:, 6 + t, :], ALU.add))
        clear_sems(nc, s)
    e.n0 += N_L0A



Q_BIG = 384
HALF = Q_BIG // 2
_c = np.arange(Q_BIG)
Q_TILES = [_c[0:128], _c[192:320], np.concatenate([_c[128:192], _c[320:384]])]
Q_TURNED = np.concatenate([_c[320:384], _c[128:192]])
L1X_WQ, L1X_WKC, L1X_WQR, L1X_WKR = 0, 512, 1024, 1216
L1X_HEAD = 1344


def open_rope(e, ctx):
    nc = e.nc

    def sb(name, shape):
        return ctx.enter_context(nc.sbuf_tensor("rope_" + name, shape, F32))
    e.kvr = sb("kvr", [P, CT, P])
    e.rope = {n: ctx.enter_context(nc.semaphore("rope_" + n)) for n in ("in", "cos", "sin", "done")}


def open_rope_tables(e, ctx):
    e.rbuf = ctx.enter_context(e.nc.sbuf_tensor("rope_buf", [P, 2 * CTX], F32))


def rope_sync(sp, e):
    sp.dma_start(e.rbuf[:, 0:4096], e.io["ctx"]).then_inc(e.rope["in"], 16)
    sp.dma_start(e.rbuf[:, 4096:8192], e.io["rope_k"]).then_inc(e.rope["in"], 16)


def rope_pool(pool, e):
    raw = e.rbuf[:, 0:4096].rearrange("p (t d) -> p t d", d=P)
    cos = e.rbuf[:, 4096:6144].rearrange("p (t f) -> p t f", f=64)
    sin = e.rbuf[:, 6144:8192].rearrange("p (t f) -> p t f", f=64)
    H = P // 2

    def pairs(ap):
        return ap.rearrange("p t (f two) -> p t f two", two=2)
    pool.wait_ge(e.rope["in"], 32)
    pool.tensor_tensor(pairs(e.kvr[:, :, :]), pairs(raw), bcast_last(cos, (P, CT, 64, 2)), ALU.mult)\
        .then_inc(e.rope["cos"], 1)
    pool.wait_ge(e.rope["cos"], 1)
    prod = e.rbuf[:, 4096:6144].rearrange("p (t f) -> p t f", f=H)
    pool.tensor_tensor(pairs(prod), pairs(raw[:, :, H:P]), bcast_last(sin[:, :, 0:32], (P, CT, 32, 2)), ALU.mult)\
        .then_inc(e.rope["sin"], 1)
    pool.wait_ge(e.rope["sin"], 1)
    pool.tensor_tensor(e.kvr[:, :, 0:H], e.kvr[:, :, 0:H], prod, ALU.add).then_inc(e.rope["done"], 1)
    pool.wait_ge(e.rope["done"], 1)
    pool.tensor_tensor(pairs(prod), pairs(raw[:, :, 0:H]), bcast_last(sin[:, :, 32:64], (P, CT, 32, 2)), ALU.mult)\
        .then_inc(e.rope["sin"], 1)
    pool.wait_ge(e.rope["sin"], 2)
    pool.tensor_tensor(e.kvr[:, :, H:P], e.kvr[:, :, H:P], prod, ALU.add).then_inc(e.rope["done"], 1)


def layer_l1x(e):
    nc, ps = e.nc, e.ps
    n0 = e.n0
    NH = 16
    KB = 4
    HT = CT // 2
    SUBS = 8
    PAIRS = NH // 2
    with ExitStack() as ctx:
        def sb(name, shape, dt=F32, scope=ctx):
            return scope.enter_context(nc.sbuf_tensor("l1x_" + name, shape, dt))
        s = layer_sems(nc, ctx, "l1x", LN_SEMS + [
            "dve_self", "tables", "kvT_mm", "kvT_hi", "kvT_lo", "kv_hi", "kv_lo", "q_mm", "q_sb", "big_mm", "big_d", "rotated", "qr_mm", "qr_sb",
            "q2_mm", "q2_sb", "cur_in", "cur", "score_mm", "tops", "top", "exp", "turn_mm", "p_hi", "p_lo", "ctx_mm",
            "taken", "take", "rescale", "cT_mm", "cT_sb", "lat_mm", "lat_sb", "out_mm"])
        kvT_hi, kvT_lo = sb("kvT_hi", [P, CTX], F32R), sb("kvT_lo", [P, CTX], F32R)
        kv = sb("kv", [P, CT, 2, P], F32R)
        with ExitStack() as scope:
            rope_q = sb("rope_q", [P, 2, 3, TOK], scope=scope)
            q1 = sb("q1", [P, 2, TOK], scope=scope)
            rc = sb("rc", [P, 3, TOK], scope=scope)
            qr = sb("qr", [64, 2, TOK], scope=scope)
        pT_hi, pT_lo = sb("pT_hi", [P, 4, 4, P], F32R), sb("pT_lo", [P, 4, 4, P], F32R)
        rs = sb("rs", [P, 2, 3, TOK])
        q2T = sb("q2T", [P, NH, TOK])
        cur = sb("cur", [P, 2, TOK])
        cur_hi, cur_lo = sb("cur_hi", [P, 2, TOK], F32R), sb("cur_lo", [P, 2, TOK], F32R)
        cn = q2T[:, :, :].rearrange("p h (t d) -> p h t d", t=TT)
        tops = sb("tops", [P, 5])
        tmax = sb("tmax", [P, TT, 2])
        ntop = sb("ntop", [P, TT, 2])
        sums = sb("sums", [P, TT, 2, 2])
        ssum = sb("ssum", [P, 2])
        scale = sb("scale", [P, TT])
        den = sb("den", [P, TT])
        c1 = sb("c1", [P, TT, P])
        prob = e.kvr[:, :, :].rearrange("p t d -> p (t d)").rearrange("p (b n) -> p b n", b=2)
        ccT = rs
        cx = e.kvr[:, :, :].rearrange("p t d -> p (t d)").rearrange("p (h t) -> p h t", h=NH)

        TAKE = 6

        def all_steps(eng, step):
            steps = [None, None] + [(0, u) for u in range(SUBS)]
            for u in range(SUBS):
                step(steps[u + 2], steps[u + 1], steps[u])
            with eng.Fori(1, PAIRS) as i:
                steps = [(i - 1, SUBS - 2), (i - 1, SUBS - 1)] + [(i, u) for u in range(SUBS)]
                for u in range(SUBS):
                    step(steps[u + 2], steps[u + 1], steps[u])
            last = PAIRS - 1
            step(None, (last, SUBS - 1), (last, SUBS - 2))
            step(None, None, (last, SUBS - 1))

        def head(w, h):
            return w[:, (h % 2) * L1X_HEAD:(h % 2 + 1) * L1X_HEAD]

        with nc.Block(no_gpsimd_drain=True) as block:
            @block.sync
            def _(sp):
                sp.dma_start(rope_q[:, :, :, :].rearrange("p a b c -> p (a b c)"), e.io["rope_q"])\
                    .then_inc(s["tables"], 16)
                stream(sp, e, n0, N_L1X)

            @block.tensor
            def _(pe):
                pe.wait_ge(e.rope["done"], 2)
                for g in range(CT // 4):
                    if g >= 6:
                        pe.wait_ge(s["kvT_lo"], g - 5)
                    for j in range(4):
                        last = pe.transpose(ps[:, 2 + g % 6, j * P:(j + 1) * P], e.kvr[:, 4 * g + j, :], e.ident)
                    last.then_inc(s["kvT_mm"], 1)
                ln_tensor(pe, e, s)
                pe.wait_ge(s["kvT_lo"], CT // 4)
                used = [False]

                def q_of(h):
                    w = head(slot_in(pe, e, n0 + h // 2), h)
                    if h >= 2:
                        pe.wait_ge(s["q_sb"], h - 1)
                    for k in range(KT):
                        last = pe.matmul(ps[:, h % 2, 0:TOK], w[:, L1X_WQ + k * P:L1X_WQ + (k + 1) * P],
                                         e.xnT[:, k, :], start=(k == 0), stop=(k == KT - 1))
                        if k == 0 and used[0]:
                            last.then_inc(e.w_used, 1)
                            used[0] = False
                    last.then_inc(s["q_mm"], 1)

                def big_of(h):
                    w = head(e.ring[:, (n0 + h // 2) % RING, :], h)
                    pe.wait_ge(s["q_sb"], h + 1)
                    if h:
                        pe.wait_ge(s["big_d"], h)
                    for f in range(4):
                        last = pe.matmul(ps[:, 2 + f // 2, (f % 2) * TOK:(f % 2 + 1) * TOK],
                                         w[:, L1X_WKC + f * P:L1X_WKC + (f + 1) * P], q1[:, h % 2, :],
                                         start=True, stop=True)
                    last.then_inc(s["big_mm"], 1)

                def qr_of(h):
                    w = head(e.ring[:, (n0 + h // 2) % RING, :], h)
                    pe.wait_ge(s["rotated"], h + 1)
                    if h >= 2:
                        pe.wait_ge(s["qr_sb"], h - 1)
                    for f in range(3):
                        last = pe.matmul(ps[0:64, 4 + h % 2, 0:TOK], w[:, L1X_WQR + f * 64:L1X_WQR + (f + 1) * 64],
                                         rs[:, h % 2, f, :], start=(f == 0), stop=(f == 2))
                    last.then_inc(s["qr_mm"], 1)

                def q2_of(h):
                    w = head(e.ring[:, (n0 + h // 2) % RING, :], h)
                    pe.wait_ge(s["qr_sb"], h + 1)
                    if h >= 2:
                        pe.wait_ge(s["q2_sb"], h - 1)
                    pe.matmul(ps[:, 6 + h % 2, 0:TOK], w[0:64, L1X_WKR:L1X_WKR + P], qr[:, h % 2, :],
                              start=True, stop=True).then_inc(s["q2_mm"], 1)
                    if h % 2:
                        used[0] = True

                for h in range(NH + 3):
                    if h < NH:
                        q_of(h)
                    if 1 <= h <= NH:
                        big_of(h - 1)
                    if 2 <= h <= NH + 1:
                        qr_of(h - 2)
                    if h >= 3:
                        if used[0]:
                            pe.wait_ge(s["q2_mm"], h - 3)
                            pe.nop().then_inc(e.w_used, 1)
                            used[0] = False
                        q2_of(h - 3)
                pe.wait_ge(s["q2_mm"], NH)
                pe.nop().then_inc(e.w_used, 1)
                pe.wait_ge(s["q2_sb"], NH)

                def score(at, b):
                    turn, u = at
                    g = turn * SUBS + u
                    hh, qt, half = u // 4, u // 2 % 2, u % 2
                    if b == 0 and u % 4 == 0:
                        pe.wait_ge(s["cur"], turn * 2 + (hh + 1))
                    if b % 2 == 0 and not (isinstance(turn, int) and g == 0):
                        pe.wait_ge(s["exp"], g * 2 - 1 + b // 2)
                    out, q = ps[:, b, :], slice(qt * P, (qt + 1) * P)
                    k = slice(half * 2048 + b * 512, half * 2048 + (b + 1) * 512)
                    pe.matmul(out, cur_hi[:, hh, q], kvT_hi[:, k], start=True, stop=False)
                    pe.matmul(out, cur_hi[:, hh, q], kvT_lo[:, k], start=False, stop=False)
                    pe.matmul(out, cur_lo[:, hh, q], kvT_hi[:, k], start=False, stop=True)\
                        .then_inc(s["score_mm"], 1)

                def turn_group(at, q):
                    turn, u = at
                    n = (turn * SUBS + u) * 4 + q
                    if not (isinstance(turn, int) and n < 2):
                        pe.wait_ge(s["p_lo"], n - 1)
                    pe.wait_ge(s["exp"], (turn * SUBS + u) * 2 + 1 + q // 2)
                    for j in range(4):
                        t = 4 * q + j
                        last = pe.transpose(ps[:, 4 + q % 2, j * P:(j + 1) * P], prob[:, u % 2, t * P:(t + 1) * P],
                                            e.ident)
                    last.then_inc(s["turn_mm"], 1)

                def ctx_group(at, q):
                    turn, u = at
                    g = turn * SUBS + u
                    pe.wait_ge(s["p_lo"], g * 4 + (q + 1))
                    if q == 0 and not (isinstance(turn, int) and g < 2):
                        pe.wait_ge(s["taken"], g - 1)
                    if q == 0 and isinstance(turn, int) and g == 0:
                        pe.wait_ge(s["kv_lo"], 1)
                    for j in range(4):
                        t = 4 * q + j
                        k = (u % 2) * HT + t
                        pe.matmul(ps[:, 6 + u % 2, 0:2 * P], pT_hi[:, q, j, :],
                                  kv[:, k, :, :].rearrange("p a d -> p (a d)"), start=(t == 0), stop=False,
                                  skip_group_check=True)
                        last = pe.matmul(ps[:, 6 + u % 2, 0:P], pT_lo[:, q, j, :], kv[:, k, 0, :],
                                         start=False, stop=(t == HT - 1), skip_group_check=True)
                    last.then_inc(s["ctx_mm"], 1)

                def pe_step(at, before, before2):
                    if at:
                        score(at, 0)
                        score(at, 1)
                    if before2:
                        ctx_group(before2, 3)
                    if before:
                        turn_group(before, 0)
                    if at:
                        score(at, 2)
                    if before:
                        turn_group(before, 1)
                    if at:
                        score(at, 3)
                    if before:
                        turn_group(before, 2)
                        ctx_group(before, 0)
                        turn_group(before, 3)
                        ctx_group(before, 1)
                        ctx_group(before, 2)

                all_steps(pe, pe_step)

                def turn_pair(j):
                    if j >= 2:
                        pe.wait_ge(s["cT_sb"], j - 1)
                    for x in range(2):
                        for t in range(TT):
                            last = pe.transpose(ps[:, j % 2, x * TOK + t * P:x * TOK + (t + 1) * P],
                                                cn[:, 2 * j + x, t, :], e.ident)
                    last.then_inc(s["cT_mm"], 1)

                def latent(j):
                    w = slot_in(pe, e, n0 + PAIRS + j // 2)
                    pe.wait_ge(s["cT_sb"], j + 1)
                    if j >= 2:
                        pe.wait_ge(s["lat_sb"], j - 1)
                    for x in range(2):
                        h = 2 * j + x
                        at = 4 * D + (h % 4) * P
                        last = pe.matmul(ps[:, 2 + j % 2, x * TOK:(x + 1) * TOK], w[:, at:at + P],
                                         ccT[:, j % 2, x, :], start=True, stop=True)
                    last.then_inc(s["lat_mm"], 1)

                def project(j):
                    pe.wait_ge(s["lat_sb"], j + 1)
                    w = slot_in(pe, e, n0 + PAIRS + j // 2)
                    for x in range(2):
                        h = 2 * j + x
                        for t in range(TT):
                            last = pe.matmul(ps[:, 6 + t, :], cx[:, h, t * P:(t + 1) * P],
                                             w[:, (h % 4) * D:(h % 4 + 1) * D], start=(h == 0), stop=(h == NH - 1))
                            if j % 2 == 0 and x == 0 and t == 0 and j:
                                last.then_inc(e.w_used, 1)
                    if j == PAIRS - 1:
                        last.then_inc(s["out_mm"], 1)

                pe.wait_ge(s["take"], TAKE * 4 * PAIRS)
                for j in range(PAIRS + 2):
                    if j < PAIRS:
                        turn_pair(j)
                    if 1 <= j <= PAIRS:
                        latent(j - 1)
                    if j >= 2:
                        project(j - 2)
                pe.wait_ge(s["out_mm"], 1)
                pe.nop().then_inc(e.w_used, 1)

            @block.scalar
            def _(act):
                for g in range(CT // 4):
                    act.wait_ge(s["kvT_mm"], g + 1)
                    act.activation(kvT_hi[:, g * 512:(g + 1) * 512], ps[:, 2 + g % 6, :], ACT.Copy)\
                        .then_inc(s["kvT_hi"], 1)
                ln_scalar(act, e, s)
                for h in range(NH + 3):
                    if h == 4:
                        act.activation(kv[:, :, 0, :], e.kvr[:, :, :], ACT.Copy).then_inc(s["kv_hi"], 1)
                    if h < NH:
                        act.wait_ge(s["q_mm"], h + 1)
                        if h >= 2:
                            act.wait_ge(s["big_mm"], h - 1)
                        act.activation(q1[:, h % 2, :], ps[:, h % 2, 0:TOK], ACT.Copy).then_inc(s["q_sb"], 1)
                    if 2 <= h <= NH + 1:
                        x = h - 2
                        act.wait_ge(s["qr_mm"], x + 1)
                        if x >= 2:
                            act.wait_ge(s["q2_mm"], x - 1)
                        act.activation(qr[:, x % 2, :], ps[0:64, 4 + x % 2, 0:TOK], ACT.Copy)\
                            .then_inc(s["qr_sb"], 1)
                    if h >= 3:
                        x = h - 3
                        act.wait_ge(s["q2_mm"], x + 1)
                        act.activation(q2T[:, x, :], ps[:, 6 + x % 2, 0:TOK], ACT.Copy).then_inc(s["q2_sb"], 1)

                def hi(at, q):
                    turn, u = at
                    n = (turn * SUBS + u) * 4 + q
                    act.wait_ge(s["turn_mm"], n + 1)
                    if not (isinstance(turn, int) and n < 4):
                        act.wait_ge(s["ctx_mm"], n - 3)
                    act.activation(pT_hi[:, q, :, :].rearrange("p a b -> p (a b)"), ps[:, 4 + q % 2, :], ACT.Copy)\
                        .then_inc(s["p_hi"], 1)

                def exps(at, part):
                    turn, u = at
                    g = turn * SUBS + u
                    qt, half = u // 2 % 2, u % 2
                    act.wait_ge(s["top"], g + 1)
                    act.activation(prob[:, u % 2, part * 1024:(part + 1) * 1024],
                                   ps[:, 2 * part:2 * part + 2, :].rearrange("p a b -> p (a b)"), ACT.Exp,
                                   bias=ntop[:, qt, half:half + 1], accum_out=sums[:, qt, half, part:part + 1])\
                        .then_inc(s["exp"], 1)
                    if half and part:
                        act.activation(scale[:, qt:qt + 1], tmax[:, qt, 0:1], ACT.Exp, bias=ntop[:, qt, 1:2])\
                            .then_inc(s["rescale"], 1)

                def act_step(at, before, before2):
                    if before:
                        hi(before, 0)
                        hi(before, 1)
                        hi(before, 2)
                    if at:
                        exps(at, 0)
                    if before:
                        hi(before, 3)
                    if at:
                        exps(at, 1)

                act.wait_ge(s["kv_lo"], 1)
                all_steps(act, act_step)
                for j in range(PAIRS):
                    act.wait_ge(s["lat_mm"], j + 1)
                    act.activation(cx[:, 2 * j:2 * j + 2, :].rearrange("p a b -> p (a b)"), ps[:, 2 + j % 2, :],
                                   ACT.Copy).then_inc(s["lat_sb"], 1)

            @block.gpsimd
            def _(pool):
                def fetch(x, source):
                    pool.tensor_copy(cur[:, x, :], source).then_inc(s["cur_in"], 1)
                    pool.tensor_copy(cur_hi[:, x, :], source).then_inc(s["cur_in"], 1)

                def rest(x):
                    pool.tensor_tensor(cur_lo[:, x, :], cur[:, x, :], cur_hi[:, x, :].bitcast(F32), ALU.subtract)\
                        .then_inc(s["cur"], 1)

                for x in range(2):
                    pool.wait_ge(s["q2_sb"], x + 1)
                    fetch(x, q2T[:, x, :])
                    pool.wait_ge(s["cur_in"], 2 * (x + 1))
                    rest(x)
                with pool.Fori(1, PAIRS) as i:
                    for x in range(2):
                        pool.wait_ge(s["score_mm"], i * (4 * SUBS) + (x - 1) * 16)
                        pool.wait_ge(s["cur"], i * 2 + x)
                        fetch(x, q2T[:, bass.ds(i * 2 + x, 1), :].rearrange("p a b -> p (a b)"))
                        pool.wait_ge(s["cur_in"], i * 4 + (2 * x + 2))
                        rest(x)

            @block.vector
            def _(dve):
                me = Chain(dve, s["dve_self"])
                for g in range(CT // 4):
                    dve.wait_ge(s["kvT_hi"], g + 1)
                    dve.tensor_tensor(kvT_lo[:, g * 512:(g + 1) * 512], ps[:, 2 + g % 6, :],
                                      kvT_hi[:, g * 512:(g + 1) * 512].bitcast(F32), ALU.subtract)\
                        .then_inc(s["kvT_lo"], 1)
                ln_vector(dve, e, s)
                dve.wait_ge(s["tables"], 16)
                for h in range(NH):
                    if h == 4:
                        dve.wait_ge(s["kv_hi"], 1)
                        dve.tensor_tensor(kv[:, :, 1, :], e.kvr[:, :, :], kv[:, :, 0, :].bitcast(F32), ALU.subtract)\
                            .then_inc(s["kv_lo"], 1)
                    dve.wait_ge(s["big_mm"], h + 1)
                    if h:
                        dve.wait_ge(s["rotated"], h)
                    x01, x22 = ps[:, 2, :].rearrange("p (a n) -> p a n", a=2), ps[:, 3, :].rearrange("p (a n) -> p a n", a=2)
                    if h >= 2:
                        dve.wait_ge(s["qr_mm"], h - 1)
                    me.did(dve.tensor_tensor(rc[:, :, :].rearrange("p a n -> p (a n)"),
                                             ps[:, 2:4, :].rearrange("p a n -> p (a n)")[:, 0:3 * TOK],
                                             rope_q[:, 0, :, :].rearrange("p a n -> p (a n)"), ALU.mult))
                    me.did(dve.tensor_tensor(rs[:, h % 2, 0, :], x01[:, 1, :], rope_q[:, 1, 0, :], ALU.mult))
                    me.did(dve.tensor_tensor(rs[:, h % 2, 1, :], x01[:, 0, :], rope_q[:, 1, 1, :], ALU.mult))
                    dve.tensor_tensor(rs[:, h % 2, 2, :], x22[:, 1, :], rope_q[:, 1, 2, :], ALU.mult)\
                        .then_inc(s["big_d"], 1)
                    me.wait()
                    dve.wait_ge(s["big_d"], h + 1)
                    dve.tensor_tensor(rs[:, h % 2, :, :], rs[:, h % 2, :, :], rc[:, :, :], ALU.add)\
                        .then_inc(s["rotated"], 1)
                dve.wait_ge(s["rotated"], NH)

                def maximum(at, b):
                    g = at[0] * SUBS + at[1]
                    dve.wait_ge(s["score_mm"], g * 4 + (b + 1))
                    if b == 0 and not (isinstance(at[0], int) and g == 0):
                        dve.wait_ge(s["top"], g)
                    dve.tensor_reduce(tops[:, b:b + 1], ps[:, b, :], AX_X, ALU.max).then_inc(s["tops"], 1)

                def overall(at):
                    turn, u = at
                    g = turn * SUBS + u
                    qt, half = u // 2 % 2, u % 2
                    dve.wait_ge(s["tops"], g * 6 + 4)
                    dve.tensor_reduce(tmax[:, qt, half:half + 1], tops[:, 0:KB + half], AX_X, ALU.max)\
                        .then_inc(s["tops"], 1)
                    dve.wait_ge(s["tops"], g * 6 + 5)
                    if not half:
                        dve.tensor_copy(tops[:, KB:KB + 1], tmax[:, qt, 0:1]).then_inc(s["tops"], 1)
                    else:
                        dve.nop().then_inc(s["tops"], 1)
                    dve.tensor_scalar(ntop[:, qt, half:half + 1], tmax[:, qt, half:half + 1], -1.0, None, ALU.mult)\
                        .then_inc(s["top"], 1)

                def lo(at, q):
                    n = (at[0] * SUBS + at[1]) * 4 + q
                    dve.wait_ge(s["p_hi"], n + 1)
                    dve.tensor_tensor(pT_lo[:, q, :, :].rearrange("p a b -> p (a b)"), ps[:, 4 + q % 2, :],
                                      pT_hi[:, q, :, :].rearrange("p a b -> p (a b)").bitcast(F32), ALU.subtract)\
                        .then_inc(s["p_lo"], 1)

                def place(at):
                    turn, u = at
                    return turn, u, turn * SUBS + u, u // 2 % 2, turn * (4 * TAKE) + (u // 2) * TAKE

                def take(at):
                    turn, u, g, qt, done = place(at)
                    out = c1[:, qt, :]
                    dve.wait_ge(s["ctx_mm"], g * 4 + 4)
                    if u % 2 == 0:
                        if not (isinstance(turn, int) and g == 0):
                            dve.wait_ge(s["take"], done)
                        dve.tensor_copy(out, ps[:, 6, 0:P]).then_inc(s["take"], 1)
                        dve.wait_ge(s["take"], done + 1)
                        dve.tensor_tensor(out, out, ps[:, 6, P:2 * P], ALU.add).then_inc(s["taken"], 1)
                        return
                    dve.wait_ge(s["rescale"], turn * 4 + (u // 2 + 1))
                    dve.wait_ge(s["taken"], g)
                    dve.scalar_tensor_tensor(out=out, in0=out, scalar=scale[:, qt:qt + 1], in1=ps[:, 7, 0:P],
                                             op0=ALU.mult, op1=ALU.add).then_inc(s["take"], 1)
                    dve.tensor_tensor(ssum[:, :], sums[:, qt, :, 0], sums[:, qt, :, 1], ALU.add)\
                        .then_inc(s["take"], 1)
                    dve.wait_ge(s["take"], done + 3)
                    dve.tensor_tensor(out, out, ps[:, 7, P:2 * P], ALU.add).then_inc(s["taken"], 1)
                    dve.scalar_tensor_tensor(out=den[:, qt:qt + 1], in0=ssum[:, 0:1], scalar=scale[:, qt:qt + 1],
                                             in1=ssum[:, 1:2], op0=ALU.mult, op1=ALU.add).then_inc(s["take"], 1)

                def take_inverse(at):
                    turn, u, g, qt, done = place(at)
                    if u % 2:
                        dve.wait_ge(s["take"], done + 4)
                        dve.reciprocal(den[:, qt:qt + 1], den[:, qt:qt + 1]).then_inc(s["take"], 1)

                def take_output(at):
                    turn, u, g, qt, done = place(at)
                    if u % 2 == 0:
                        return
                    dve.wait_ge(s["take"], done + 5)
                    dve.wait_ge(s["taken"], g + 1)
                    head = turn * 2 + u // 4
                    to = cn[:, head, qt, :] if isinstance(turn, int) else \
                        cn[:, bass.ds(head, 1), qt, :].rearrange("p a b -> p (a b)")
                    dve.tensor_scalar(to, c1[:, qt, :], den[:, qt:qt + 1], None, ALU.mult).then_inc(s["take"], 1)

                def dve_step(at, before, before2):
                    if at:
                        maximum(at, 0)
                        maximum(at, 1)
                    if before2:
                        take(before2)
                    if before:
                        lo(before, 0)
                    if before2:
                        take_inverse(before2)
                    if at:
                        maximum(at, 2)
                    if before2:
                        take_output(before2)
                    if before:
                        lo(before, 1)
                    if at:
                        maximum(at, 3)
                        overall(at)
                    if before:
                        lo(before, 2)
                        lo(before, 3)

                all_steps(dve, dve_step)
                dve.wait_ge(s["take"], TAKE * 4 * PAIRS)
                for j in range(PAIRS):
                    dve.wait_ge(s["cT_mm"], j + 1)
                    if j >= 2:
                        dve.wait_ge(s["lat_mm"], j - 1)
                    dve.tensor_copy(ccT[:, j % 2, 0:2, :].rearrange("p a b -> p (a b)"), ps[:, j % 2, :])\
                        .then_inc(s["cT_sb"], 1)
                dve.wait_ge(s["out_mm"], 1)
                for t in range(TT):
                    dve.tensor_tensor(e.xres[:, t, :], e.xres[:, t, :], ps[:, 6 + t, :], ALU.add)\
                        .then_inc(s["cT_sb"], 1)
        clear_sems(nc, s)
    e.n0 += N_L1X



def layer_l1a(e):
    nc, ps = e.nc, e.ps
    n0 = e.n0
    NH, HD = 64, 64
    INNER = NH * HD
    F = INNER // P
    CONV_TILES = 2 + F
    ROWS_MIDDLE, ROWS_END = (8, 14, 20), 28
    GROUPS = 8
    GH = NH // GROUPS
    PAIRS = NH // 2
    with ExitStack() as ctx:
        def sb(name, shape, dt=F32, scope=ctx):
            return scope.enter_context(nc.sbuf_tensor("l1a_" + name, shape, dt))
        s = layer_sems(nc, ctx, "l1a", LN_SEMS + SPLIT_SEMS + [
            "tap",
            "dve_self", "act_self", "dt_mm", "tile_mm", "tile_ev", "pads", "conv", "silu", "xt_mm", "xt_sb", "sp_abs",
            "sp_exp", "sp_done", "decay", "rows", "cols_mm", "cols", "gt_mm", "gt_sb", "eb_mm", "scan",
            "m", "ends", "xdt", "xd", "xs", "diag_mm", "st_mm", "st_sb", "off_mm", "off_read", "gate_mm", "gate",
            "t_step", "y", "diag_read", "turn_mm", "yT", "squared", "o_hi", "o_lo", "y_hi", "y_lo", "out_mm"])
        xh = sb("xh", [P, TT, INNER])
        ybuf = sb("ybuf", [P, F, TOK])
        BC = sb("BC", [P, 2, TOK])
        Bt = sb("Bt", [P, P])
        GT = sb("GT", [P, TT, P])
        L = sb("L", [P, 2, 2, TT, P])
        M = sb("M", [P, 2, 2, TT, P])
        st = sb("st", [P, 512])
        sg = sb("sg", [P, TT, 512])
        y = sb("y", [P, TT, 512])
        dtm = sb("dtm", [P, 3, NH])
        dend = sb("dend", [P, NH])
        ssq = sb("ssq", [P, TT, GROUPS])
        rms = sb("rms", [P, TT])
        UNITS = F // 2

        def unit_weights(eng, u):
            w = slot_in(eng, e, n0 + 6 + GROUPS + u // 3)
            return w[:, (u % 3) * 2 * D:(u % 3 + 1) * 2 * D].rearrange("p (f n) -> p f n", f=2)

        small, ident, ident4 = e.small, e.ident, e.ident4
        flat = ybuf[:, :, :].rearrange("p f t -> p (f t)")
        pad = flat[:, 0:CR * 259].rearrange("p (b n) -> p b n", b=CR)
        conv = flat[:, 1536:1536 + CR * TOK].rearrange("p (b n) -> p b n", b=CR)
        xf = flat[:, 3072:3072 + 4 * TOK].rearrange("p (b n) -> p b n", b=4)
        r_x, r_a, r_y, r_z, r_e = (flat[0:64, 4096 + i * TOK:4096 + (i + 1) * TOK] for i in range(5))
        r_0 = flat[0:64, 5376:5504]
        r_c = flat[0:64, 5504:5632]
        r_negA = flat[0:64, 5632:5633]
        rowbuf = sb("rowbuf", [64, TOK])
        xsg = sb("xsg", [P, 2, 512])
        with ExitStack() as scope:
            split = open_split(sb, scope)
        with ExitStack() as scope:
            xdt = sb("xdt", [P, TT, INNER], F32, scope)
        OR, EARLY = 4, 2
        o_hi, o_lo = sb("o_hi", [P, OR, D], F32R), sb("o_lo", [P, OR, D], F32R)
        y_hi, y_lo = sb("y_hi", [P, OR, TOK], F32R), sb("y_lo", [P, OR, TOK], F32R)

        def out_weights(eng, f):
            w = slot_in(eng, e, n0 + 6 + GROUPS + f // 6)
            return w[:, (f % 6) * D:(f % 6 + 1) * D]

        junk = e.xn[:, 0, :]

        def taps(i, j):
            return small[:, S_MCONV + 4 * i + j:S_MCONV + 4 * i + j + 1]

        def squares(act, g, me):
            for c in range(TT):
                act.wait_ge(s["y"], 2 * g + c + 1)
                if 2 * g + c:
                    act.wait_ge(s["squared"], 2 * g + c)
                act.activation(junk[:, :], y[:, c, :], ACT.Square, accum_out=ssq[:, c, g:g + 1])\
                    .then_inc(s["squared"], 1)

        with nc.Block(no_gpsimd_drain=True) as block:
            @block.sync
            def _(sp):
                stream(sp, e, n0, N_L1A)

            @block.tensor
            def _(pe):
                ln_tensor(pe, e, s)
                for k in range(KT):
                    last = pe.matmul(ps[0:64, 4, 0:TOK], small[:, S_MDT + 64 * k:S_MDT + 64 * k + 64], e.xnT[:, k, :],
                                     start=(k == 0), stop=(k == KT - 1))
                last.then_inc(s["dt_mm"], 1)

                def turn_x(j):
                    pe.wait_ge(s["silu"], 2 * j + 4)
                    if j >= 2:
                        pe.wait_ge(s["xt_sb"], j - 1)
                    for t in range(TT):
                        for x in range(2):
                            last = pe.transpose(ps[:, 6 + j % 2, t * 256 + x * P:t * 256 + (x + 1) * P],
                                                xf[:, (2 * j + x) % 4, t * P:(t + 1) * P], ident)
                    last.then_inc(s["xt_mm"], 1)

                for i in range(CONV_TILES):
                    project_tile(pe, e, s, i, split)
                    if i >= 8 and i % 2 == 0:
                        turn_x((i - 8) // 2)
                for j in range((CONV_TILES - 8) // 2, F // 2):
                    turn_x(j)
                pe.nop().then_inc(e.w_used, 1)
                for c in range(TT):
                    at = slice(c * P, (c + 1) * P)
                    pe.matmul(ps[:, 5, at], BC[:, 0, at], BC[:, 1, at], start=True, stop=True)
                pe.transpose(ps[:, 5, 2 * P:3 * P], BC[:, 0, 0:P], ident).then_inc(s["gt_mm"], 1)
                pe.wait_ge(s["rows"], 1)
                for c in range(TT):
                    pe.transpose(ps[:, 4, c * NH:(c + 1) * NH], r_z[:, c * P:(c + 1) * P], ident[0:64, 0:64])
                pe.transpose(ps[:, 4, 2 * NH:3 * NH], r_c, ident[0:64, 0:64]).then_inc(s["cols_mm"], 1)
                pe.wait_ge(s["cols"], 1)
                pe.wait_ge(s["gt_sb"], 2)

                def decays(q):
                    if q >= 2:
                        pe.wait_ge(s["scan"], q - 1)
                    for x in range(2):
                        h = 2 * q + x
                        last = pe.matmul(ps[:, q % 2, x * TOK:(x + 1) * TOK],
                                         ident[0:64, h:h + 1].broadcast_to((64, P)), rowbuf[:, :],
                                         start=True, stop=True)
                    last.then_inc(s["eb_mm"], 1)

                def diagonal(q):
                    g = q // 4
                    pe.wait_ge(s["m"], q + 1)
                    if q % 4 == 0:
                        pe.wait_ge(s["xdt"], 2 * g + 2)
                        if g:
                            pe.wait_ge(s["diag_read"], 2 * g)
                    for x in range(2):
                        h = 2 * q + x
                        for c in range(TT):
                            last = pe.matmul(ps[:, 2 + c, (h % GH) * HD:(h % GH + 1) * HD], M[:, q % 2, x, c, :],
                                             xdt[:, c, h * HD:(h + 1) * HD], start=True, stop=True)
                    last.then_inc(s["diag_mm"], 1)

                def gates(g, c):
                    w = slot_in(pe, e, n0 + 6 + g)
                    n = 2 * g + c
                    if n:
                        pe.wait_ge(s["gate"], n)
                    for k in range(KT):
                        last = pe.matmul(ps[:, 5, :], e.xnT[:, k, c * P:(c + 1) * P], w[:, k * 512:(k + 1) * 512],
                                         start=(k == 0), stop=(k == KT - 1))
                        if k == 0 and c == 0 and g:
                            last.then_inc(e.w_used, 1)
                    last.then_inc(s["gate_mm"], 1)

                def state(g):
                    pe.wait_ge(s["xs"], g + 1)
                    if g:
                        pe.wait_ge(s["off_read"], g)
                    pe.matmul(ps[:, 4, :], Bt[:, :], xsg[:, g % 2, :], start=True, stop=True).then_inc(s["st_mm"], 1)

                def off(g):
                    pe.wait_ge(s["st_sb"], g + 1)
                    pe.matmul(ps[:, 4, :], BC[:, 1, P:TOK], st[:, :], start=True, stop=True).then_inc(s["off_mm"], 1)

                def turn_y(g):
                    for c in range(TT):
                        pe.wait_ge(s["y"], 2 * g + c + 1)
                        if g:
                            pe.wait_ge(s["yT"], 2 * g + c - 1)
                        for j in range(4):
                            last = pe.transpose(ps[:, 6 + c, j * P:(j + 1) * P], y[:, c, j * P:(j + 1) * P], ident)
                        last.then_inc(s["turn_mm"], 1)

                decays(0)
                decays(1)
                for g in range(GROUPS):
                    gates(g, 0)
                    for q in range(4 * g, 4 * g + 4):
                        diagonal(q)
                        if q + 2 < PAIRS:
                            decays(q + 2)
                        if q == 4 * g + 1 and g:
                            turn_y(g - 1)
                    state(g)
                    gates(g, 1)
                    off(g)
                for f in range(F):
                    if f == OR:
                        turn_y(GROUPS - 1)
                    pe.wait_ge(s["y_lo"], f + 1)
                    pe.wait_ge(s["o_lo"], f + 1)
                    for t in range(TT):
                        at = slice(t * P, (t + 1) * P)
                        last = pe.matmul(ps[:, t, :], y_hi[:, f % OR, at], o_hi[:, f % OR, :], start=(f == 0),
                                         stop=False)
                        if f % 6 == 0 and t == 0:
                            last.then_inc(e.w_used, 1)
                        pe.matmul(ps[:, t, :], y_hi[:, f % OR, at], o_lo[:, f % OR, :], start=False, stop=False)
                        last = pe.matmul(ps[:, t, :], y_lo[:, f % OR, at], o_hi[:, f % OR, :], start=False,
                                         stop=(f == F - 1))
                    last.then_inc(s["out_mm"], 1)
                pe.wait_ge(s["out_mm"], F)
                pe.nop().then_inc(e.w_used, 1)

            @block.scalar
            def _(act):
                me = Chain(act, s["act_self"])
                ln_scalar(act, e, s)
                split_x_hi(act, e, s, split[2])
                for i in range(AHEAD):
                    split_w_hi(act, e, s, i, split[0])

                def silu(i):
                    act.wait_ge(s["conv"], i + 1)
                    if i >= 6:
                        act.wait_ge(s["xt_mm"], (i - 4) // 2)
                    out = BC[:, i, :] if i < 2 else xf[:, (i - 2) % 4, :]
                    act.activation(out, conv[:, i % CR, :], ACT.Silu, bias=small[:, S_MBIAS + i:S_MBIAS + i + 1])\
                        .then_inc(s["silu"], 1)

                def turned_x(j):
                    act.wait_ge(s["xt_mm"], j + 1)
                    act.activation(xh[:, :, j * 256:(j + 1) * 256], ps[:, 6 + j % 2, :].rearrange("p (t n) -> p t n", t=TT),
                                   ACT.Copy).then_inc(s["xt_sb"], 1)

                me.did(act.activation(r_negA, small[0:64, S_MHEAD:S_MHEAD + 1], ACT.Exp))
                me.wait()
                me.did(act.activation(r_negA, r_negA, ACT.Copy, scale=-1.0))
                softplus_scalar(act, r_a, r_y, s)
                me.wait()
                act.wait_ge(s["pads"], 1)
                done = 0
                for i in range(CONV_TILES):
                    if i + AHEAD < CONV_TILES:
                        split_w_hi(act, e, s, i + AHEAD, split[0])
                    act.wait_ge(s["tile_mm"], i + 1)
                    if i % 2:
                        tap_scalar(act, s, i, conv[:, i % CR, :], ps[:, i % 4, 0:TOK], taps(i, 3))
                    if i >= CR:
                        act.wait_ge(s["conv"], i - CR + 1)
                    act.activation(pad[:, i % CR, 3:3 + TOK], ps[:, i % 4, 0:TOK], ACT.Copy).then_inc(s["tile_ev"], 1)
                    if i >= SILU_LAG:
                        silu(i - SILU_LAG)
                    if i == ROWS_MIDDLE[-1] + 2:
                        act.wait_ge(s["sp_done"], 1)
                        act.activation(r_e, r_z, ACT.Exp, scale=r_negA).then_inc(s["decay"], 1)
                    if i >= 10 and i % 2 == 0:
                        turned_x(done)
                        done += 1
                for i in range(CONV_TILES - SILU_LAG, CONV_TILES):
                    silu(i)
                while done < F // 2:
                    turned_x(done)
                    done += 1
                act.wait_ge(s["gt_mm"], 1)
                act.activation(GT[:, :, :].rearrange("p c n -> p (c n)"), ps[:, 5, 0:TOK], ACT.Copy).then_inc(s["gt_sb"], 1)
                act.activation(Bt[:, :], ps[:, 5, 2 * P:3 * P], ACT.Copy).then_inc(s["gt_sb"], 1)
                act.wait_ge(s["cols_mm"], 1)
                act.activation(dtm[:, :, :].rearrange("p c h -> p (c h)"), ps[:, 4, 0:3 * NH], ACT.Copy)\
                    .then_inc(s["cols"], 1)
                def out_hi(f):
                    w = out_weights(act, f)
                    if f >= OR:
                        act.wait_ge(s["out_mm"], f - OR + 1)
                    act.activation(o_hi[:, f % OR, :], w, ACT.Copy).then_inc(s["o_hi"], 1)
                    act.wait_ge(s["yT"], 2 * (f // 4 + 1))
                    act.activation(y_hi[:, f % OR, :], ybuf[:, f, :], ACT.Copy).then_inc(s["y_hi"], 1)

                for g in range(GROUPS):
                    for c in range(TT):
                        act.wait_ge(s["gate_mm"], 2 * g + c + 1)
                        if g:
                            act.wait_ge(s["y"], 2 * g + c - 1)
                        act.activation(sg[:, c, :], ps[:, 5, :], ACT.Silu).then_inc(s["gate"], 1)
                        if g and c == 0:
                            squares(act, g - 1, me)
                        if c == 0:
                            act.wait_ge(s["st_mm"], g + 1)
                            if g:
                                act.wait_ge(s["off_mm"], g)
                            act.activation(st[:, :], ps[:, 4, :], ACT.Copy).then_inc(s["st_sb"], 1)
                        if g == GROUPS - 1 and c == 0:
                            act.wait_ge(s["diag_mm"], PAIRS)
                            act.wait_ge(s["xs"], GROUPS)
                            for f in range(EARLY):
                                out_hi(f)
                for f in range(EARLY, F):
                    out_hi(f)
                    if f == OR - 1:
                        squares(act, GROUPS - 1, me)
                act.wait_ge(s["ln_xn"], TT + 1)
                act.activation(rms[:, :], rms[:, :], ACT.Sqrt, bias=e.eps, scale=1.0 / INNER).then_inc(s["ln_std"], 1)

            @block.gpsimd
            def _(pool):
                for i in range(CONV_TILES):
                    split_w_lo(pool, e, s, i, *split[0:2])
                pool.wait_ge(s["cols"], 1)
                pool.wait_ge(s["xt_sb"], F // 2)
                for g in range(GROUPS):
                    at, hh = slice(g * 512, (g + 1) * 512), slice(g * GH, (g + 1) * GH)

                    def by_head(ap):
                        return ap.rearrange("p (h d) -> p h d", d=HD)
                    for c in range(TT):
                        pool.tensor_tensor(by_head(xdt[:, c, at]), by_head(xh[:, c, at]),
                                           bcast_last(dtm[:, c, hh], (P, GH, HD)), ALU.mult).then_inc(s["xdt"], 1)
                    pool.wait_ge(s["xdt"], 2 * g + 2)
                    for c in range(TT):
                        pool.tensor_tensor(by_head(xh[:, c, at]), by_head(xh[:, c, at]),
                                           bcast_last(small[:, S_MD + g * GH:S_MD + (g + 1) * GH], (P, GH, HD)),
                                           ALU.mult).then_inc(s["xd"], 1)
                    pool.wait_ge(s["ends"], 4 * g + 4)
                    if g >= 2:
                        pool.wait_ge(s["st_mm"], g - 1)
                    pool.tensor_tensor(by_head(xsg[:, g % 2, :]), by_head(xdt[:, 0, at]),
                                       bcast_last(dend[:, hh], (P, GH, HD)), ALU.mult).then_inc(s["xs"], 1)
            @block.vector
            def _(dve):
                me = Chain(dve, s["dve_self"])
                ln_vector(dve, e, s)
                split_x_lo(dve, e, s, split[2], split[3])
                dve.memset(pad[:, :, :], 0.0).then_inc(s["pads"], 1)

                def rows_start():
                    dve.wait_ge(s["dt_mm"], 1)
                    me.did(dve.memset(r_0, 0.0))
                    me.did(dve.tensor_scalar(r_x, ps[0:64, 4, 0:TOK], small[0:64, S_MHEAD + 1:S_MHEAD + 2], None,
                                             ALU.add))
                    me.wait()
                    softplus_vector(dve, me, r_x, r_a, s)

                def rows_end():
                    dve.wait_ge(s["decay"], 1)
                    me.did(dve.tensor_copy(rowbuf[:, :], r_e))
                    me.did(dve.tensor_tensor_scan(r_c, r_e[:, P:TOK], r_0, 1.0, ALU.mult, ALU.add))
                    me.wait()
                    me.did(dve.memset(rowbuf[:, 0:TOK:P], 0.0))
                    me.wait()
                    dve.nop().then_inc(s["rows"], 1)

                rows_start()
                for i in range(CONV_TILES):
                    if i in ROWS_MIDDLE:
                        softplus_vector_end(dve, me, ROWS_MIDDLE.index(i), r_x, r_a, r_y, r_z, s, r_z)
                    if i == ROWS_END:
                        rows_end()
                    if i % 2 == 0:
                        convolve(dve, me, s, i, pad, conv, taps)
                dve.wait_ge(s["gt_sb"], 2)

                def pair(q):
                    dve.wait_ge(s["eb_mm"], q + 1)
                    if q >= 2:
                        dve.wait_ge(s["m"], q - 1)
                        dve.wait_ge(s["ends"], q - 1)
                    d = L[:, q % 2, :, :, :]
                    dve.tensor_tensor_scan(d.rearrange("p h c n -> p (h c n)"), ps[:, q % 2, :], ident4, 0.0,
                                           ALU.mult, ALU.add).then_inc(s["scan"], 1)
                    dve.wait_ge(s["scan"], q + 1)
                    if q >= 2:
                        dve.wait_ge(s["diag_mm"], q - 1)
                    dve.tensor_copy(dend[:, 2 * q:2 * q + 2], d[:, :, 0, P - 1]).then_inc(s["ends"], 1)
                    dve.tensor_tensor(M[:, q % 2, :, :, :].rearrange("p h c n -> p h (c n)"),
                                      d.rearrange("p h c n -> p h (c n)"),
                                      GT[:, :, :].rearrange("p c n -> p (c n)").unsqueeze(1).broadcast_to((P, 2, TOK)),
                                      ALU.mult).then_inc(s["m"], 1)

                def by_head(ap):
                    return ap.rearrange("p (h d) -> p h d", d=HD)

                def outputs(g):
                    at, hh = slice(g * 512, (g + 1) * 512), slice(g * GH, (g + 1) * GH)
                    base = 5 * g
                    dve.wait_ge(s["diag_mm"], 4 * g + 4)
                    dve.wait_ge(s["xd"], 2 * g + 2)
                    if g:
                        dve.wait_ge(s["turn_mm"], 2 * g)
                        dve.wait_ge(s["squared"], 2 * g)
                    dve.tensor_tensor(y[:, 0, :], ps[:, 2, :], xh[:, 0, at], ALU.add).then_inc(s["diag_read"], 1)
                    dve.tensor_tensor(xh[:, 1, at], ps[:, 3, :], xh[:, 1, at], ALU.add).then_inc(s["diag_read"], 1)
                    dve.wait_ge(s["gate"], 2 * g + 1)
                    dve.wait_ge(s["diag_read"], 2 * g + 2)
                    dve.tensor_tensor(y[:, 0, :], y[:, 0, :], sg[:, 0, :], ALU.mult).then_inc(s["y"], 1)
                    dve.wait_ge(s["off_mm"], g + 1)
                    dve.tensor_tensor(by_head(y[:, 1, :]), by_head(ps[:, 4, :]), bcast_last(dtm[:, 2, hh], (P, GH, HD)),
                                      ALU.mult).then_inc(s["off_read"], 1)
                    dve.wait_ge(s["off_read"], g + 1)
                    dve.tensor_tensor(y[:, 1, :], y[:, 1, :], xh[:, 1, at], ALU.add).then_inc(s["t_step"], 1)
                    dve.wait_ge(s["t_step"], g + 1)
                    dve.wait_ge(s["gate"], 2 * g + 2)
                    dve.tensor_tensor(y[:, 1, :], y[:, 1, :], sg[:, 1, :], ALU.mult).then_inc(s["y"], 1)

                def turned_y(g):
                    for c in range(TT):
                        dve.wait_ge(s["turn_mm"], 2 * g + c + 1)
                        dve.tensor_tensor(ybuf[:, 4 * g:4 * g + 4, c * P:(c + 1) * P],
                                          ps[:, 6 + c, :].rearrange("p (f n) -> p f n", n=P),
                                          bcast_last(small[:, S_MNORM + 4 * g:S_MNORM + 4 * g + 4], (P, 4, P)),
                                          ALU.mult).then_inc(s["yT"], 1)

                def out_lo(f):
                    w = out_weights(dve, f)
                    dve.wait_ge(s["o_hi"], f + 1)
                    dve.tensor_tensor(o_lo[:, f % OR, :], w, o_hi[:, f % OR, :].bitcast(F32), ALU.subtract)\
                        .then_inc(s["o_lo"], 1)
                    dve.wait_ge(s["y_hi"], f + 1)
                    dve.tensor_tensor(y_lo[:, f % OR, :], ybuf[:, f, :], y_hi[:, f % OR, :].bitcast(F32), ALU.subtract)\
                        .then_inc(s["y_lo"], 1)

                dve.wait_ge(s["cols_mm"], 1)
                for g in range(GROUPS):
                    for q in range(4 * g, 4 * g + 4):
                        pair(q)
                        if q == 4 * g + 2 and g:
                            turned_y(g - 1)
                    if g == GROUPS - 1:
                        for f in range(EARLY):
                            out_lo(f)
                    outputs(g)

                for f in range(EARLY, F):
                    if f == OR:
                        turned_y(GROUPS - 1)
                    out_lo(f)
                dve.wait_ge(s["squared"], 2 * GROUPS)
                me.did(dve.tensor_reduce(rms[:, :], ssq[:, :, :], AX_X, ALU.add))
                me.wait()
                dve.nop().then_inc(s["ln_xn"], 1)
                dve.wait_ge(s["ln_std"], 2)
                me.did(dve.reciprocal(rms[:, :], rms[:, :]))
                me.wait()
                dve.wait_ge(s["out_mm"], F)
                for t in range(TT):
                    me.did(dve.scalar_tensor_tensor(out=e.xres[:, t, :], in0=ps[:, t, :], scalar=rms[:, t:t + 1],
                                                    in1=e.xres[:, t, :], op0=ALU.mult, op1=ALU.add))
        clear_sems(nc, s)
    e.n0 += N_L1A



def _ktiles(wT):
    k, n = wT.shape
    return wT.reshape(k // P, P, n).transpose(1, 0, 2).reshape(P, -1)


def _slot(*parts):
    out = np.zeros((P, SLOT), np.float32)
    at = 0
    for a in parts:
        out[:a.shape[0], at:at + a.shape[1]] = a
        at += a.shape[1]
    return out


def slots_l0x(i):
    wq = np.asarray(i["L0_xattn_Wq"]).T
    wkv = np.asarray(i["L0_xattn_Wkv_expand"]).T
    wout = np.asarray(i["L0_xattn_Wout"]).T
    return [_slot(_ktiles(wq), wkv), _slot(_ktiles(wout))]


def fixed_columns():
    out = np.zeros((P, C_N), np.float32)
    for r in range(4):
        out[:, C_ID + r * P:C_ID + (r + 1) * P] = np.eye(P)
    a = np.arange(P)
    for l in range(7):
        b = 1 << l
        s, r = a[:, None], a[None, :]
        out[:, C_LEVEL + l * P:C_LEVEL + (l + 1) * P] = \
            (s // (2 * b) == r // (2 * b)) & (s % (2 * b) < b) & (r % (2 * b) >= b)
    out[:, C_LEVEL:C_LEVEL + P] *= -1.0
    out[:, C_CAUSAL + P:C_CAUSAL + 2 * P] = np.where(a[None, :] <= a[:, None], 0.0, LOWEST)
    out[:, C_ONES:C_ONES + P] = 1.0
    out[:, C_EPS] = EPS
    for h in range(8):
        out[:, C_PICK + 9 * h] = 1.0
    return out


def small_columns(i):
    out = np.zeros((P, S_N), np.float32)
    g = lambda n: np.asarray(i[n])
    conv = np.concatenate([g("L0_attn_conv_q_w"), g("L0_attn_conv_k_w"), g("L0_attn_conv_v_w")])[:, 0, :]
    out[:, S_ACONV:S_ACONV + 160] = conv.reshape(40, P, 4).transpose(1, 0, 2).reshape(P, 160)
    out[:, S_AAB:S_AAB + 96] = _ktiles(np.concatenate([g("L0_attn_Wa"), g("L0_attn_Wb")], axis=1))
    out[:, S_ANORM] = g("L0_attn_norm_w")
    out[:8, S_AHEAD] = g("L0_attn_A_log")
    out[:8, S_AHEAD + 1] = g("L0_attn_dt_bias")
    out[:, S_F0:S_F0 + 256] = _ktiles(g("L0_ffn_gate_w").T)
    out[:, S_F1:S_F1 + 32] = _ktiles(g("L1_ffn_gate_w").T)
    order = np.concatenate([np.arange(4096, 4352), np.arange(4096)])
    out[:, S_MCONV:S_MCONV + 136] = g("L1_attn_conv_w")[order, 0, :].reshape(34, P, 4).transpose(1, 0, 2).reshape(P, 136)
    out[:, S_MBIAS:S_MBIAS + 34] = g("L1_attn_conv_b")[order].reshape(34, P).T
    out[:, S_MDT:S_MDT + 256] = _ktiles(g("L1_attn_in_proj_w")[4096 + 4352:].T)
    out[:64, S_MHEAD] = g("L1_attn_A_log")
    out[:64, S_MHEAD + 1] = g("L1_attn_dt_bias")
    out[:, S_MD:S_MD + 64] = g("L1_attn_D")[None, :]
    out[:, S_MNORM:S_MNORM + 32] = g("L1_attn_norm_w").reshape(32, P).T
    return out


def slots_l0f(i):
    w13, w2 = np.asarray(i["L0_ffn_w13"]), np.asarray(i["L0_ffn_w2"])
    return [_slot(_ktiles(w13[x].T), _ktiles(w2[x].T)) for x in range(w13.shape[0])]


def slots_l1f(i):
    w1, w2, w3 = (np.asarray(i["L1_ffn_" + n]) for n in ("w1", "w2", "w3"))
    return [_slot(_ktiles(np.concatenate([w1[x][:, c:c + 256], w3[x][:, c:c + 256]], axis=1)), _ktiles(w2[x][c:c + 256]))
            for x in range(w1.shape[0]) for c in range(0, 1024, 256)]


def slots_l1x(i):
    g = lambda n: np.asarray(i["L1_xattn_" + n])
    wq, wkc, wqr, wkr, wo = g("Wq"), g("w_kc_q"), g("W_qr"), g("W_kr"), g("Wo")
    out = []
    for pair in range(8):
        parts = []
        for h in (2 * pair, 2 * pair + 1):
            parts += [_ktiles(wq[h * P:(h + 1) * P].T),
                      *[wkc[h][:, c] for c in Q_TILES + [Q_TURNED]],
                      *[wqr[h][c] for c in Q_TILES],
                      np.pad(wkr[h].T, ((0, 64), (0, 0)))]
        out.append(_slot(*parts))
    wlat = g("w_kc_kv").transpose(2, 0, 1).reshape(P, 16 * P)
    return out + [_slot(_ktiles(wo.T[c:c + 4 * P]), wlat[:, c:c + 4 * P]) for c in range(0, 16 * P, 4 * P)]


def rope_tables(length, dim):
    f32 = np.float32
    inv = f32(1.0) / np.power(f32(10000.0), np.arange(0, dim, 2, dtype=f32) / f32(dim)).astype(f32)
    f = np.arange(length, dtype=f32)[:, None] * inv[None, :]
    return np.sin(f).astype(f32), np.cos(f).astype(f32)


def extra_inputs(i):
    ctx = np.asarray(i["ctx_512"])[0]
    sin_k, cos_k = rope_tables(CTX, P)
    sin_q, cos_q = (np.repeat(t, 2, axis=-1).T for t in rope_tables(TOK, Q_BIG))
    sign_k = np.where(np.arange(64) < 32, -1.0, 1.0).astype(np.float32)
    sign_q = np.where(np.arange(Q_BIG) < HALF, -1.0, 1.0).astype(np.float32)[:, None]

    def rows(a):
        return a.reshape(CT, P, -1).transpose(1, 0, 2).reshape(P, -1)
    return {
        "ctxT": ctx[:TOK].T,
        "ctx": rows(ctx),
        "rope_k": np.concatenate([rows(cos_k), rows(sin_k * sign_k)], axis=1),
        "rope_q": np.concatenate([cos_q[c] for c in Q_TILES] + [(sin_q * sign_q)[c] for c in Q_TILES], axis=1),
    }


def slots_l0a(i):
    g = lambda n: np.asarray(i["L0_attn_" + n])
    w = np.concatenate([g("Wq"), g("Wk"), g("Wv"), g("Wg")], axis=1)
    wo = g("Wo")
    return [_slot(_ktiles(w[:, c:c + 768])) for c in range(0, 6144, 768)] + \
        [_slot(_ktiles(wo[c:c + 4 * P])) for c in (0, 4 * P)]


def slots_l1a(i):
    w = np.asarray(i["L1_attn_in_proj_w"]).T
    gate, conv = w[:, :4096], w[:, 4096:8448]
    conv = np.concatenate([conv[:, 4096:], conv[:, :4096]], axis=1)
    wo = np.asarray(i["L1_attn_out_proj_w"]).T
    out = [_slot(_ktiles(np.pad(conv[:, c:c + 768], ((0, 0), (0, max(0, c + 768 - conv.shape[1]))))))
           for c in range(0, conv.shape[1], 768)]
    out += [_slot(_ktiles(gate[:, c:c + 512])) for c in range(0, 4096, 512)]
    return out + [_slot(_ktiles(wo[c:c + 6 * P])) for c in range(0, 4096, 6 * P)]



def build_program(nc, io):
    with ExitStack() as ctx:
        e = open_env(nc, ctx, io)
        e.slots = SLOTS
        layer_l0x(e)
        layer_l0a(e)
        with ExitStack() as rope:
            open_rope(e, rope)
            layer_l0f(e)
            layer_l1x(e)
        layer_l1a(e)
        layer_l1f(e)
        stored = ctx.enter_context(nc.semaphore("stored"))
        with nc.Block(no_gpsimd_drain=True) as block:
            @block.sync
            def _(sp):
                sp.dma_start(io["out"].rearrange("(t p) d -> p t d", p=P), e.xres[:, :, :]).then_inc(stored, 16)
                sp.wait_ge(stored, 16)



def kernel(**inputs):
    import concourse.bacc as bacc
    from concourse.bass_utils import run_bass_kernel_spmd

    slots = []
    for part in (slots_l0x, slots_l0a, slots_l0f, slots_l1x, slots_l1a, slots_l1f):
        slots += part(inputs)
    arrays = {"x": np.asarray(inputs["x"])[0], "fixed": fixed_columns(), "small": small_columns(inputs),
              "wall": np.stack(slots), **extra_inputs(inputs)}
    arrays = {name: np.ascontiguousarray(a) for name, a in arrays.items()}
    nc = bacc.Bacc("TRN2", target_bir_lowering=False, num_devices=1)
    io = {name: nc.dram_tensor(name, a.shape, mybir.dt.from_np(a.dtype), kind="ExternalInput").ap()
          for name, a in arrays.items()}
    io["out"] = nc.dram_tensor("out", (TOK, D), F32, kind="ExternalOutput").ap()
    build_program(nc, io)
    r = run_bass_kernel_spmd(nc, [arrays], core_ids=[0])
    return r.results[0]["out"].reshape(1, TOK, D)
```
